# Optimizing a Trainium2 kernel written in Bass

```python
import numpy as np
import jax
import jax.numpy as jnp

def _softmax(x, axis=-1):
    return jax.nn.softmax(x, axis=axis)

def _gelu(x):
    return jax.nn.gelu(x, approximate=True)

def _silu(x):
    return jax.nn.silu(x)

def _sigmoid(x):
    return jax.nn.sigmoid(x)

def _layernorm(x, axis=-1, eps=1e-05):
    m = jnp.mean(x, axis=axis, keepdims=True)
    v = jnp.var(x, axis=axis, keepdims=True)
    return (x - m) / jnp.sqrt(v + eps)

def _scatter_add(tgt, idx, src, axis=0):
    return tgt.at[idx].add(src)

def _segment_sum(src, seg, n):
    return jax.ops.segment_sum(src, seg, n)
kernel_name = 'mk_perceiver_d4_seqx_r4_ac1f24'

def setup_inputs(seed: int=0):
    np.random.seed(seed)
    _w = jnp.asarray

    def _rec_inputs():
        import jax
        import jax.numpy as jnp
        _rk = jax.random.key(seed)
        x = 7.22e-05 + 1 * jax.random.normal(jax.random.fold_in(_rk, 1), (16, 64, 256), jnp.float32)
        _lenS = 64 - jax.random.randint(jax.random.fold_in(_rk, 7), (16,), 0, max(1, 64 // 4) + 1, jnp.int32)
        _lenS2 = 1024 - jax.random.randint(jax.random.fold_in(_rk, 8), (16,), 0, max(1, 1024 // 4) + 1, jnp.int32)
        _ctx_768P = jax.random.normal(jax.random.fold_in(_rk, 11), (16, 16, 192), jnp.float32)
        _ctx_768c = jax.random.dirichlet(jax.random.fold_in(_rk, 511), 0.3 * jnp.ones((16,), jnp.float32), (16, 1024))
        _ctx_768t = jnp.einsum('bsk,bkd->bsd', _ctx_768c, _ctx_768P)
        _ctx_768t = _ctx_768t * jax.lax.rsqrt(jnp.mean(jnp.square(_ctx_768t)) + 1e-12) * 0.953939
        ctx_768 = -0.000191848 + 0.999787 * (_ctx_768t + 0.3 * jax.random.normal(jax.random.fold_in(_rk, 611), (16, 1024, 192), jnp.float32))
        _validS = jnp.arange(64)[None, :] < _lenS[:, None]
        _validS2 = jnp.arange(1024)[None, :] < _lenS2[:, None]
        _causal = jnp.tril(jnp.ones((64, 64), dtype=bool))
        mask_BxS2_bk0 = jnp.logical_not(jnp.broadcast_to(_validS2[:, :], (16, 1024)))
        return (x, ctx_768, mask_BxS2_bk0)
    x, ctx_768, mask_BxS2_bk0 = _rec_inputs()

    def _L0_xattn_setup():
        import jax, jax.numpy as jnp
        import numpy as np
        Q_DIM = 256
        KV_DIM = 192
        HEADS = 16
        DK = Q_DIM // HEADS
        key = jax.random.key(seed)
        ks = jax.random.split(key, 6)
        B, T_q, T_kv = (4, 512, 512)
        s_q = 1.0 / np.sqrt(Q_DIM)
        s_kv = 1.0 / np.sqrt(KV_DIM)
        return {'q_tokens': jax.random.normal(ks[0], (B, T_q, Q_DIM), jnp.float32), 'kv_tokens': jax.random.normal(ks[1], (B, T_kv, KV_DIM), jnp.float32), 'Wq': jax.random.normal(ks[2], (Q_DIM, Q_DIM), jnp.float32) * s_q, 'Wk': jax.random.normal(ks[3], (Q_DIM, KV_DIM), jnp.float32) * s_kv, 'Wv': jax.random.normal(ks[4], (Q_DIM, KV_DIM), jnp.float32) * s_kv, 'Wo': jax.random.normal(ks[5], (Q_DIM, Q_DIM), jnp.float32) * s_q}
    _L0_xattn_all = _L0_xattn_setup()
    _L0_xattn_in = {k: v for k, v in _L0_xattn_all.items() if k in ('Wq', 'Wk', 'Wv', 'Wo')}
    del _L0_xattn_all

    def _L0_attn_setup():
        import jax, jax.numpy as jnp
        import numpy as np
        D_MODEL, D_STATE, EXPAND, D_CONV, HEADDIM = (256, 128, 2, 4, 64)
        D_INNER = EXPAND * D_MODEL
        NHEADS = D_INNER // HEADDIM
        NGROUPS = 1
        CONV_DIM = D_INNER + 2 * NGROUPS * D_STATE
        D_IN_PROJ = 2 * D_INNER + 2 * NGROUPS * D_STATE + NHEADS
        BATCH, SEQ = (2, 1024)
        EPS = 1e-05

        def _mamba2(u, in_proj_w, conv_w, conv_b, dt_bias, A_log, Dp, norm_w, out_proj_w):
            b, l, _ = u.shape
            zxbcdt = u @ in_proj_w.T
            z, xBC, dt = jnp.split(zxbcdt, [D_INNER, D_INNER + CONV_DIM], axis=-1)
            xBC = jnp.transpose(xBC, (0, 2, 1))
            xBC = jax.lax.conv_general_dilated(xBC, conv_w[:, None, :], window_strides=(1,), padding=[(D_CONV - 1, 0)], feature_group_count=CONV_DIM, dimension_numbers=('NCH', 'OIH', 'NCH'))
            xBC = jax.nn.silu(jnp.transpose(xBC, (0, 2, 1)) + conv_b)
            x, Bm, Cm = jnp.split(xBC, [D_INNER, D_INNER + NGROUPS * D_STATE], axis=-1)
            dt = jax.nn.softplus(dt + dt_bias)
            A = -jnp.exp(A_log)
            xh = x.reshape(b, l, NHEADS, HEADDIM)
            dt_t, x_t = (jnp.moveaxis(dt, 1, 0), jnp.moveaxis(xh, 1, 0))
            B_t, C_t = (jnp.moveaxis(Bm, 1, 0), jnp.moveaxis(Cm, 1, 0))

            def step(h, inputs):
                dtk, xk, Bk, Ck = inputs
                decay = jnp.exp(dtk * A)
                h = h * decay[:, :, None, None] + dtk[:, :, None, None] * xk[..., None] * Bk[:, None, None, :]
                y = jnp.einsum('bhpn,bn->bhp', h, Ck)
                return (h, y)
            h0 = jnp.zeros((b, NHEADS, HEADDIM, D_STATE), u.dtype)
            _, ys = jax.lax.scan(step, h0, (dt_t, x_t, B_t, C_t))
            y = jnp.moveaxis(ys, 0, 1) + Dp[None, None, :, None] * xh
            y = y.reshape(b, l, D_INNER)
            y = y * jax.nn.silu(z)
            y = y * jax.lax.rsqrt(jnp.mean(y * y, axis=-1, keepdims=True) + EPS) * norm_w
            return y @ out_proj_w.T
        key = jax.random.key(seed)
        ks = jax.random.split(key, 6)
        sn = lambda k, shape, sc: jax.random.normal(k, shape, jnp.float32) * sc
        dt = jnp.linspace(0.001, 0.1, NHEADS)
        return {'x': sn(ks[0], (BATCH, SEQ, D_MODEL), 1.0), 'ln_w': jnp.ones((D_MODEL,), jnp.float32), 'ln_b': jnp.zeros((D_MODEL,), jnp.float32), 'in_proj_w': sn(ks[1], (D_IN_PROJ, D_MODEL), D_MODEL ** (-0.5)), 'conv_w': sn(ks[2], (CONV_DIM, D_CONV), D_CONV ** (-0.5)), 'conv_b': jnp.zeros((CONV_DIM,), jnp.float32), 'dt_bias': jnp.log(jnp.expm1(dt)).astype(jnp.float32), 'A_log': jnp.log(jnp.arange(1, NHEADS + 1, dtype=jnp.float32)), 'D': jnp.ones((NHEADS,), jnp.float32), 'norm_w': jnp.ones((D_INNER,), jnp.float32), 'out_proj_w': sn(ks[3], (D_MODEL, D_INNER), D_INNER ** (-0.5))}
    _L0_attn_all = _L0_attn_setup()
    _L0_attn_in = {k: v for k, v in _L0_attn_all.items() if k in ('ln_w', 'ln_b', 'in_proj_w', 'conv_w', 'conv_b', 'dt_bias', 'A_log', 'D', 'norm_w', 'out_proj_w')}
    del _L0_attn_all

    def _L0_ffn_setup():
        import jax, jax.numpy as jnp
        import numpy as np
        D_MODEL = 256
        HIDDEN = 256
        NUM_EXPERTS = 8
        TOP_K = 2
        key = jax.random.key(seed)
        ks = jax.random.split(key, 10)
        s = 0.02
        return {'x': jax.random.normal(ks[0], (2, 512, D_MODEL), dtype=jnp.float32), 'gate_w': jax.random.normal(ks[1], (NUM_EXPERTS, D_MODEL), dtype=jnp.float32) * s, 'up_w': jax.random.normal(ks[2], (NUM_EXPERTS, D_MODEL, HIDDEN), dtype=jnp.float32) * s, 'up_b': jnp.zeros((NUM_EXPERTS, HIDDEN), dtype=jnp.float32), 'down_w': jax.random.normal(ks[3], (NUM_EXPERTS, HIDDEN, D_MODEL), dtype=jnp.float32) * s, 'down_b': jnp.zeros((NUM_EXPERTS, D_MODEL), dtype=jnp.float32), 'sh_up_w': jax.random.normal(ks[4], (D_MODEL, HIDDEN), dtype=jnp.float32) * s, 'sh_up_b': jnp.zeros((HIDDEN,), dtype=jnp.float32), 'sh_down_w': jax.random.normal(ks[5], (HIDDEN, D_MODEL), dtype=jnp.float32) * s, 'sh_down_b': jnp.zeros((D_MODEL,), dtype=jnp.float32)}
    _L0_ffn_all = _L0_ffn_setup()
    _L0_ffn_in = {k: v for k, v in _L0_ffn_all.items() if k in ('gate_w', 'up_w', 'up_b', 'down_w', 'down_b', 'sh_up_w', 'sh_up_b', 'sh_down_w', 'sh_down_b')}
    del _L0_ffn_all

    def _L1_xattn_setup():
        import jax, jax.numpy as jnp
        import numpy as np
        HEADS = 8
        DIM_HEAD = 64
        QUERY_DIM = 256
        CONTEXT_DIM = 192
        INNER = HEADS * DIM_HEAD
        key = jax.random.key(seed)
        ks = jax.random.split(key, 7)
        B, Sq, Skv = (4, 1024, 256)
        x = jax.random.normal(ks[0], (B, Sq, QUERY_DIM), dtype=jnp.float32)
        context = jax.random.normal(ks[1], (B, Skv, CONTEXT_DIM), dtype=jnp.float32)
        Wq = jax.random.normal(ks[2], (QUERY_DIM, INNER), dtype=jnp.float32) * QUERY_DIM ** (-0.5)
        Wk = jax.random.normal(ks[3], (CONTEXT_DIM, INNER), dtype=jnp.float32) * CONTEXT_DIM ** (-0.5)
        Wv = jax.random.normal(ks[4], (CONTEXT_DIM, INNER), dtype=jnp.float32) * CONTEXT_DIM ** (-0.5)
        Wo = jax.random.normal(ks[5], (INNER, QUERY_DIM), dtype=jnp.float32) * INNER ** (-0.5)
        bo = jax.random.normal(ks[6], (QUERY_DIM,), dtype=jnp.float32) * 0.01
        return {'x': x, 'context': context, 'Wq': Wq, 'Wk': Wk, 'Wv': Wv, 'Wo': Wo, 'bo': bo}
    _L1_xattn_all = _L1_xattn_setup()
    _L1_xattn_in = {k: v for k, v in _L1_xattn_all.items() if k in ('Wq', 'Wk', 'Wv', 'Wo', 'bo')}
    del _L1_xattn_all

    def _L1_attn_setup():
        import jax, jax.numpy as jnp
        import numpy as np
        from jax import lax
        B, L, DM = (4, 256, 256)
        DI, N, KC = (512, 16, 4)
        EPS_NORM = 1e-06
        EPS_A = 1e-08

        def _mamba_block(x, norm_w, in_proj_w, in_proj_b, conv_w, conv_b, out_proj_w, out_proj_b, A_log, D_param, dt, B_param, C_param):
            b, l, _ = x.shape
            residual = x
            rms = lax.rsqrt(jnp.mean(x * x, axis=-1, keepdims=True) + EPS_NORM)
            xn = x * rms * norm_w
            xz = xn @ in_proj_w.T + in_proj_b
            x_ssm, gate = jnp.split(xz, 2, axis=-1)
            xc = x_ssm.transpose(0, 2, 1)
            xc = lax.conv_general_dilated(xc, conv_w, (1,), [(KC - 1, KC - 1)], dimension_numbers=('NCH', 'OIH', 'NCH'))
            xc = xc[:, :, :l] + conv_b[None, :, None]
            x_ssm = jax.nn.silu(xc.transpose(0, 2, 1))
            A = -jnp.exp(A_log)
            dts = jax.nn.sigmoid(dt)[:, None]
            A_bar = jnp.exp(dts * A)
            B_bar = (A_bar - 1.0) / (A + EPS_A) * B_param
            l_range = jnp.arange(l, dtype=x.dtype)
            A_pow = A_bar[:, :, None] ** l_range[None, None, :]
            K = jnp.einsum('dn,dn,dnl->dl', C_param, B_bar, A_pow)
            K = jnp.flip(K, axis=1)
            xcv = x_ssm.transpose(0, 2, 1)
            x_padded = jnp.pad(xcv, ((0, 0), (0, 0), (l - 1, 0)))
            ssm = lax.conv_general_dilated(x_padded, K[:, None, :], (1,), 'VALID', feature_group_count=K.shape[0], dimension_numbers=('NCH', 'OIH', 'NCH'))
            ssm = ssm.transpose(0, 2, 1) + x_ssm * D_param
            out = ssm * jax.nn.silu(gate)
            out = out @ out_proj_w.T + out_proj_b
            return residual + out
        key = jax.random.key(seed)
        ks = jax.random.split(key, 6)
        x = jax.random.normal(ks[0], (B, L, DM), jnp.float32)
        norm_w = jnp.ones((DM,), jnp.float32)
        in_proj_w = jax.random.normal(ks[1], (2 * DI, DM), jnp.float32) * 0.02
        in_proj_b = jnp.zeros((2 * DI,), jnp.float32)
        conv_w = jax.random.normal(ks[2], (DI, DI, KC), jnp.float32) * 0.02
        conv_b = jnp.zeros((DI,), jnp.float32)
        out_proj_w = jax.random.normal(ks[3], (DM, DI), jnp.float32) * 0.02
        out_proj_b = jnp.zeros((DM,), jnp.float32)
        A_log = jnp.log(jax.random.uniform(ks[4], (DI, N), jnp.float32) * 0.5 + 0.5)
        D_param = jnp.ones((DI,), jnp.float32)
        dt = jnp.ones((DI,), jnp.float32) * 0.1
        B_param = jnp.ones((DI, N), jnp.float32) * 0.5
        C_param = jax.random.normal(ks[5], (DI, N), jnp.float32) * 0.1
        return {'x': x, 'norm_w': norm_w, 'in_proj_w': in_proj_w, 'in_proj_b': in_proj_b, 'conv_w': conv_w, 'conv_b': conv_b, 'out_proj_w': out_proj_w, 'out_proj_b': out_proj_b, 'A_log': A_log, 'D_param': D_param, 'dt': dt, 'B_param': B_param, 'C_param': C_param}
    _L1_attn_all = _L1_attn_setup()
    _L1_attn_in = {k: v for k, v in _L1_attn_all.items() if k in ('norm_w', 'in_proj_w', 'in_proj_b', 'conv_w', 'conv_b', 'out_proj_w', 'out_proj_b', 'A_log', 'D_param', 'dt', 'B_param', 'C_param')}
    del _L1_attn_all

    def _L1_ffn_setup():
        import jax, jax.numpy as jnp
        import numpy as np
        EMBED_DIM = 256
        HIDDEN_DIM = 1024
        NUM_EXPERTS = 8
        TOP_K = 2
        key = jax.random.key(seed)
        k_x, k_g, k_w1, k_w2 = jax.random.split(key, 4)
        x = jax.random.normal(k_x, (2, 128, EMBED_DIM), dtype=jnp.float32)
        gate_w = jax.random.normal(k_g, (NUM_EXPERTS, EMBED_DIM), dtype=jnp.float32) * (1.0 / np.sqrt(EMBED_DIM))
        w1 = jax.random.normal(k_w1, (NUM_EXPERTS, EMBED_DIM, HIDDEN_DIM), dtype=jnp.float32) * np.sqrt(2.0 / EMBED_DIM)
        b1 = jnp.zeros((NUM_EXPERTS, HIDDEN_DIM), dtype=jnp.float32)
        w2 = jax.random.normal(k_w2, (NUM_EXPERTS, HIDDEN_DIM, EMBED_DIM), dtype=jnp.float32) * np.sqrt(2.0 / HIDDEN_DIM)
        b2 = jnp.zeros((NUM_EXPERTS, EMBED_DIM), dtype=jnp.float32)
        return {'x': x, 'gate_w': gate_w, 'w1': w1, 'b1': b1, 'w2': w2, 'b2': b2}
    _L1_ffn_all = _L1_ffn_setup()
    _L1_ffn_in = {k: v for k, v in _L1_ffn_all.items() if k in ('gate_w', 'w1', 'b1', 'w2', 'b2')}
    del _L1_ffn_all

    def _L2_xattn_setup():
        import jax, jax.numpy as jnp
        import numpy as np
        HEADS = 8
        DIM_HEAD = 64
        SCALE = DIM_HEAD ** (-0.5)
        key = jax.random.key(seed)
        ks = jax.random.split(key, 7)
        B, Nq, Nc = (4, 512, 512)
        Dq, Dc = (256, 192)
        inner = HEADS * DIM_HEAD
        x = jax.random.normal(ks[0], (B, Nq, Dq), dtype=jnp.float32)
        context = jax.random.normal(ks[1], (B, Nc, Dc), dtype=jnp.float32)
        Wq = jax.random.normal(ks[2], (Dq, inner), dtype=jnp.float32) * Dq ** (-0.5)
        Wk = jax.random.normal(ks[3], (Dc, inner), dtype=jnp.float32) * Dc ** (-0.5)
        Wv = jax.random.normal(ks[4], (Dc, inner), dtype=jnp.float32) * Dc ** (-0.5)
        Wo = jax.random.normal(ks[5], (inner, Dq), dtype=jnp.float32) * inner ** (-0.5)
        bo = jax.random.normal(ks[6], (Dq,), dtype=jnp.float32) * 0.01
        return {'x': x, 'context': context, 'Wq': Wq, 'Wk': Wk, 'Wv': Wv, 'Wo': Wo, 'bo': bo}
    _L2_xattn_all = _L2_xattn_setup()
    _L2_xattn_in = {k: v for k, v in _L2_xattn_all.items() if k in ('Wq', 'Wk', 'Wv', 'Wo', 'bo')}
    del _L2_xattn_all

    def _L2_attn_setup():
        import jax, jax.numpy as jnp
        import numpy as np
        D_MODEL, D_STATE, D_CONV, EXPAND = (256, 16, 4, 2)
        D_INNER = EXPAND * D_MODEL
        BATCH, SEQ = (2, 256)
        EPS = 1e-08

        def _causal_dwconv(x_bcl, w, b):
            out = jax.lax.conv_general_dilated(x_bcl, w, window_strides=(1,), padding=[(D_CONV - 1, 0)], dimension_numbers=('NCH', 'OIH', 'NCH'), feature_group_count=D_INNER)
            return out + b[None, :, None]

        def _selective_scan(u, delta, A, B, C, D):
            dA = jnp.exp(delta[..., None] * A)
            dBu = delta[..., None] * B[:, :, None, :] * u[..., None]
            dA_t = jnp.moveaxis(dA, 1, 0)
            dBu_t = jnp.moveaxis(dBu, 1, 0)
            C_t = jnp.moveaxis(C, 1, 0)

            def step(h, inp):
                da, dbu, c = inp
                h = da * h + dbu
                y = jnp.einsum('bdn,bn->bd', h, c)
                return (h, y)
            h0 = jnp.zeros((u.shape[0], u.shape[2], A.shape[1]), u.dtype)
            _, ys = jax.lax.scan(step, h0, (dA_t, dBu_t, C_t))
            y = jnp.moveaxis(ys, 0, 1)
            return y + u * D
        key = jax.random.key(seed)
        ks = jax.random.split(key, 8)
        s = lambda fan: 1.0 / np.sqrt(fan)
        x = jax.random.normal(ks[0], (BATCH, SEQ, D_MODEL), jnp.float32)
        in_proj_w = jax.random.normal(ks[1], (2 * D_INNER, D_MODEL), jnp.float32) * s(D_MODEL)
        conv_w = jax.random.normal(ks[2], (D_INNER, 1, D_CONV), jnp.float32) * s(D_CONV)
        conv_b = jnp.zeros((D_INNER,), jnp.float32)
        x_proj_w = jax.random.normal(ks[3], (3 * D_STATE, D_INNER), jnp.float32) * s(D_INNER)
        dt_proj_w = jax.random.normal(ks[4], (D_INNER, D_STATE), jnp.float32) * s(D_STATE)
        dt_proj_b = jnp.zeros((D_INNER,), jnp.float32)
        A = jnp.tile(jnp.arange(1, D_STATE + 1, dtype=jnp.float32), (D_INNER, 1))
        A_log = jnp.log(A)
        D = jnp.ones((D_INNER,), jnp.float32)
        norm_w = jnp.ones((D_INNER,), jnp.float32)
        out_proj_w = jax.random.normal(ks[5], (D_MODEL, D_INNER), jnp.float32) * s(D_INNER)
        return dict(x=x, in_proj_w=in_proj_w, conv_w=conv_w, conv_b=conv_b, x_proj_w=x_proj_w, dt_proj_w=dt_proj_w, dt_proj_b=dt_proj_b, A_log=A_log, D=D, norm_w=norm_w, out_proj_w=out_proj_w)
    _L2_attn_all = _L2_attn_setup()
    _L2_attn_in = {k: v for k, v in _L2_attn_all.items() if k in ('in_proj_w', 'conv_w', 'conv_b', 'x_proj_w', 'dt_proj_w', 'dt_proj_b', 'A_log', 'D', 'norm_w', 'out_proj_w')}
    del _L2_attn_all

    def _L2_ffn_setup():
        import jax, jax.numpy as jnp
        import numpy as np
        E, H, I = (8, 256, 128)
        NG, TKG, TOPK = (4, 2, 4)
        SCALE = 2.5

        def _mlp(x, wg, wu, wd):
            return jax.nn.silu(x @ wg) * (x @ wu) @ wd
        key = jax.random.key(seed)
        ks = jax.random.split(key, 8)
        s = 0.02
        return {'hidden_states': jax.random.normal(ks[0], (32, 64, H), jnp.float32), 'gate_w': jax.random.normal(ks[1], (E, H), jnp.float32) * np.float32(np.sqrt(2.0 / H)), 'correction_bias': jnp.zeros((E,), jnp.float32), 'Wg': jax.random.normal(ks[2], (E, H, I), jnp.float32) * s, 'Wu': jax.random.normal(ks[3], (E, H, I), jnp.float32) * s, 'Wd': jax.random.normal(ks[4], (E, I, H), jnp.float32) * s, 'Wg_s': jax.random.normal(ks[5], (H, I), jnp.float32) * s, 'Wu_s': jax.random.normal(ks[6], (H, I), jnp.float32) * s, 'Wd_s': jax.random.normal(ks[7], (I, H), jnp.float32) * s}
    _L2_ffn_all = _L2_ffn_setup()
    _L2_ffn_in = {k: v for k, v in _L2_ffn_all.items() if k in ('gate_w', 'correction_bias', 'Wg', 'Wu', 'Wd', 'Wg_s', 'Wu_s', 'Wd_s')}
    del _L2_ffn_all

    def _L3_xattn_setup():
        import jax, jax.numpy as jnp
        import numpy as np
        DIM_IN, DIM_LAT, DIM_HEAD = (192, 256, 64)
        INNER = max(DIM_LAT, DIM_IN)
        HEADS = INNER // DIM_HEAD
        SCALE = DIM_HEAD ** (-0.5)
        RMS_EPS = 1e-08
        LN_EPS = 1e-05

        def layernorm(x, g, b):
            mu = jnp.mean(x, axis=-1, keepdims=True)
            var = jnp.mean((x - mu) ** 2, axis=-1, keepdims=True)
            return (x - mu) * jax.lax.rsqrt(var + LN_EPS) * g + b

        def rmsnorm(x, gamma):
            norm = jnp.sqrt(jnp.sum(x * x, axis=-1, keepdims=True)) * x.shape[-1] ** (-0.5)
            return x / jnp.maximum(norm, RMS_EPS) * gamma
        key = jax.random.key(seed)
        ks = jax.random.split(key, 12)
        b, n, m = (4, 1024, 128)
        x = jax.random.normal(ks[0], (b, n, DIM_IN), jnp.float32)
        latents = jax.random.normal(ks[1], (b, m, DIM_LAT), jnp.float32)
        mask = jax.random.randint(ks[2], (b, n), 0, 2).astype(bool)
        s = lambda k, sh, fan: jax.random.normal(k, sh, jnp.float32) * fan ** (-0.5)
        return {'x': x, 'latents': latents, 'mask': mask, 'ln_x_g': jnp.ones((DIM_IN,), jnp.float32), 'ln_x_b': jnp.zeros((DIM_IN,), jnp.float32), 'ln_l_g': jnp.ones((DIM_LAT,), jnp.float32), 'ln_l_b': jnp.zeros((DIM_LAT,), jnp.float32), 'qn_g': jnp.ones((DIM_HEAD,), jnp.float32), 'kn_g': jnp.ones((DIM_HEAD,), jnp.float32), 'Wq': s(ks[3], (INNER, DIM_LAT), DIM_LAT), 'Wkv': s(ks[4], (2 * INNER, DIM_IN), DIM_IN), 'Wlkv': s(ks[5], (2 * INNER, DIM_LAT), DIM_LAT), 'Wo': s(ks[6], (DIM_LAT, INNER), INNER), 'bo': jnp.zeros((DIM_LAT,), jnp.float32)}
    _L3_xattn_all = _L3_xattn_setup()
    _L3_xattn_in = {k: v for k, v in _L3_xattn_all.items() if k in ('ln_x_g', 'ln_x_b', 'ln_l_g', 'ln_l_b', 'qn_g', 'kn_g', 'Wq', 'Wkv', 'Wlkv', 'Wo', 'bo')}
    del _L3_xattn_all

    def _L3_attn_setup():
        import jax, jax.numpy as jnp
        import numpy as np
        B, S, E = (4, 256, 256)
        H = 16
        D = E // H
        key = jax.random.key(seed)
        kx, kq, kk, kv, ko = jax.random.split(key, 5)
        scale = 1.0 / np.sqrt(2.0 * E)
        return {'x': jax.random.normal(kx, (B, S, E), dtype=jnp.float32), 'Wq': jax.random.normal(kq, (E, E), dtype=jnp.float32) * scale, 'Wk': jax.random.normal(kk, (E, E), dtype=jnp.float32) * scale, 'Wv': jax.random.normal(kv, (E, E), dtype=jnp.float32) * scale, 'Wo': jax.random.normal(ko, (E, E), dtype=jnp.float32) * scale}
    _L3_attn_all = _L3_attn_setup()
    _L3_attn_in = {k: v for k, v in _L3_attn_all.items() if k in ('Wq', 'Wk', 'Wv', 'Wo')}
    del _L3_attn_all

    def _L3_ffn_setup():
        import jax, jax.numpy as jnp
        import numpy as np
        E = 8
        K = 2
        CAP_FACTOR = 1.0
        key = jax.random.key(seed)
        k0, k1, k2, k3 = jax.random.split(key, 4)
        B, S, M, H = (4, 512, 256, 1024)
        x = jax.random.normal(k0, (B, S, M), jnp.float32)
        wg = jax.random.normal(k1, (M, E), jnp.float32) * 0.02
        w1 = jax.random.normal(k2, (E, M, H), jnp.float32) * 0.02
        b1 = jnp.zeros((E, H), jnp.float32)
        w2 = jax.random.normal(k3, (E, H, M), jnp.float32) * 0.02
        b2 = jnp.zeros((E, M), jnp.float32)
        return {'x': x, 'wg': wg, 'w1': w1, 'b1': b1, 'w2': w2, 'b2': b2}
    _L3_ffn_all = _L3_ffn_setup()
    _L3_ffn_in = {k: v for k, v in _L3_ffn_all.items() if k in ('wg', 'w1', 'b1', 'w2', 'b2')}
    del _L3_ffn_all
    return {'x': x, 'ctx_768': ctx_768, 'mask_BxS2_bk0': mask_BxS2_bk0, 'L0_xattn_Wq': _L0_xattn_in['Wq'], 'L0_xattn_Wk': _L0_xattn_in['Wk'], 'L0_xattn_Wv': _L0_xattn_in['Wv'], 'L0_xattn_Wo': _L0_xattn_in['Wo'], 'L0_attn_ln_w': _L0_attn_in['ln_w'], 'L0_attn_ln_b': _L0_attn_in['ln_b'], 'L0_attn_in_proj_w': _L0_attn_in['in_proj_w'], 'L0_attn_conv_w': _L0_attn_in['conv_w'], 'L0_attn_conv_b': _L0_attn_in['conv_b'], 'L0_attn_dt_bias': _L0_attn_in['dt_bias'], 'L0_attn_A_log': _L0_attn_in['A_log'], 'L0_attn_D': _L0_attn_in['D'], 'L0_attn_norm_w': _L0_attn_in['norm_w'], 'L0_attn_out_proj_w': _L0_attn_in['out_proj_w'], 'L0_ffn_gate_w': _L0_ffn_in['gate_w'], 'L0_ffn_up_w': _L0_ffn_in['up_w'], 'L0_ffn_up_b': _L0_ffn_in['up_b'], 'L0_ffn_down_w': _L0_ffn_in['down_w'], 'L0_ffn_down_b': _L0_ffn_in['down_b'], 'L0_ffn_sh_up_w': _L0_ffn_in['sh_up_w'], 'L0_ffn_sh_up_b': _L0_ffn_in['sh_up_b'], 'L0_ffn_sh_down_w': _L0_ffn_in['sh_down_w'], 'L0_ffn_sh_down_b': _L0_ffn_in['sh_down_b'], 'L1_xattn_Wq': _L1_xattn_in['Wq'], 'L1_xattn_Wk': _L1_xattn_in['Wk'], 'L1_xattn_Wv': _L1_xattn_in['Wv'], 'L1_xattn_Wo': _L1_xattn_in['Wo'], 'L1_xattn_bo': _L1_xattn_in['bo'], 'L1_attn_norm_w': _L1_attn_in['norm_w'], 'L1_attn_in_proj_w': _L1_attn_in['in_proj_w'], 'L1_attn_in_proj_b': _L1_attn_in['in_proj_b'], 'L1_attn_conv_w': _L1_attn_in['conv_w'], 'L1_attn_conv_b': _L1_attn_in['conv_b'], 'L1_attn_out_proj_w': _L1_attn_in['out_proj_w'], 'L1_attn_out_proj_b': _L1_attn_in['out_proj_b'], 'L1_attn_A_log': _L1_attn_in['A_log'], 'L1_attn_D_param': _L1_attn_in['D_param'], 'L1_attn_dt': _L1_attn_in['dt'], 'L1_attn_B_param': _L1_attn_in['B_param'], 'L1_attn_C_param': _L1_attn_in['C_param'], 'L1_ffn_gate_w': _L1_ffn_in['gate_w'], 'L1_ffn_w1': _L1_ffn_in['w1'], 'L1_ffn_b1': _L1_ffn_in['b1'], 'L1_ffn_w2': _L1_ffn_in['w2'], 'L1_ffn_b2': _L1_ffn_in['b2'], 'L2_xattn_Wq': _L2_xattn_in['Wq'], 'L2_xattn_Wk': _L2_xattn_in['Wk'], 'L2_xattn_Wv': _L2_xattn_in['Wv'], 'L2_xattn_Wo': _L2_xattn_in['Wo'], 'L2_xattn_bo': _L2_xattn_in['bo'], 'L2_attn_in_proj_w': _L2_attn_in['in_proj_w'], 'L2_attn_conv_w': _L2_attn_in['conv_w'], 'L2_attn_conv_b': _L2_attn_in['conv_b'], 'L2_attn_x_proj_w': _L2_attn_in['x_proj_w'], 'L2_attn_dt_proj_w': _L2_attn_in['dt_proj_w'], 'L2_attn_dt_proj_b': _L2_attn_in['dt_proj_b'], 'L2_attn_A_log': _L2_attn_in['A_log'], 'L2_attn_D': _L2_attn_in['D'], 'L2_attn_norm_w': _L2_attn_in['norm_w'], 'L2_attn_out_proj_w': _L2_attn_in['out_proj_w'], 'L2_ffn_gate_w': _L2_ffn_in['gate_w'], 'L2_ffn_correction_bias': _L2_ffn_in['correction_bias'], 'L2_ffn_Wg': _L2_ffn_in['Wg'], 'L2_ffn_Wu': _L2_ffn_in['Wu'], 'L2_ffn_Wd': _L2_ffn_in['Wd'], 'L2_ffn_Wg_s': _L2_ffn_in['Wg_s'], 'L2_ffn_Wu_s': _L2_ffn_in['Wu_s'], 'L2_ffn_Wd_s': _L2_ffn_in['Wd_s'], 'L3_xattn_ln_x_g': _L3_xattn_in['ln_x_g'], 'L3_xattn_ln_x_b': _L3_xattn_in['ln_x_b'], 'L3_xattn_ln_l_g': _L3_xattn_in['ln_l_g'], 'L3_xattn_ln_l_b': _L3_xattn_in['ln_l_b'], 'L3_xattn_qn_g': _L3_xattn_in['qn_g'], 'L3_xattn_kn_g': _L3_xattn_in['kn_g'], 'L3_xattn_Wq': _L3_xattn_in['Wq'], 'L3_xattn_Wkv': _L3_xattn_in['Wkv'], 'L3_xattn_Wlkv': _L3_xattn_in['Wlkv'], 'L3_xattn_Wo': _L3_xattn_in['Wo'], 'L3_xattn_bo': _L3_xattn_in['bo'], 'L3_attn_Wq': _L3_attn_in['Wq'], 'L3_attn_Wk': _L3_attn_in['Wk'], 'L3_attn_Wv': _L3_attn_in['Wv'], 'L3_attn_Wo': _L3_attn_in['Wo'], 'L3_ffn_wg': _L3_ffn_in['wg'], 'L3_ffn_w1': _L3_ffn_in['w1'], 'L3_ffn_b1': _L3_ffn_in['b1'], 'L3_ffn_w2': _L3_ffn_in['w2'], 'L3_ffn_b2': _L3_ffn_in['b2']}

def reference(x, ctx_768, mask_BxS2_bk0, L0_xattn_Wq, L0_xattn_Wk, L0_xattn_Wv, L0_xattn_Wo, L0_attn_ln_w, L0_attn_ln_b, L0_attn_in_proj_w, L0_attn_conv_w, L0_attn_conv_b, L0_attn_dt_bias, L0_attn_A_log, L0_attn_D, L0_attn_norm_w, L0_attn_out_proj_w, L0_ffn_gate_w, L0_ffn_up_w, L0_ffn_up_b, L0_ffn_down_w, L0_ffn_down_b, L0_ffn_sh_up_w, L0_ffn_sh_up_b, L0_ffn_sh_down_w, L0_ffn_sh_down_b, L1_xattn_Wq, L1_xattn_Wk, L1_xattn_Wv, L1_xattn_Wo, L1_xattn_bo, L1_attn_norm_w, L1_attn_in_proj_w, L1_attn_in_proj_b, L1_attn_conv_w, L1_attn_conv_b, L1_attn_out_proj_w, L1_attn_out_proj_b, L1_attn_A_log, L1_attn_D_param, L1_attn_dt, L1_attn_B_param, L1_attn_C_param, L1_ffn_gate_w, L1_ffn_w1, L1_ffn_b1, L1_ffn_w2, L1_ffn_b2, L2_xattn_Wq, L2_xattn_Wk, L2_xattn_Wv, L2_xattn_Wo, L2_xattn_bo, L2_attn_in_proj_w, L2_attn_conv_w, L2_attn_conv_b, L2_attn_x_proj_w, L2_attn_dt_proj_w, L2_attn_dt_proj_b, L2_attn_A_log, L2_attn_D, L2_attn_norm_w, L2_attn_out_proj_w, L2_ffn_gate_w, L2_ffn_correction_bias, L2_ffn_Wg, L2_ffn_Wu, L2_ffn_Wd, L2_ffn_Wg_s, L2_ffn_Wu_s, L2_ffn_Wd_s, L3_xattn_ln_x_g, L3_xattn_ln_x_b, L3_xattn_ln_l_g, L3_xattn_ln_l_b, L3_xattn_qn_g, L3_xattn_kn_g, L3_xattn_Wq, L3_xattn_Wkv, L3_xattn_Wlkv, L3_xattn_Wo, L3_xattn_bo, L3_attn_Wq, L3_attn_Wk, L3_attn_Wv, L3_attn_Wo, L3_ffn_wg, L3_ffn_w1, L3_ffn_b1, L3_ffn_w2, L3_ffn_b2):
    import jax
    import jax.numpy as jnp

    def _L0_xattn_ref(q_tokens, kv_tokens, Wq, Wk, Wv, Wo):
        import jax, jax.numpy as jnp
        import numpy as np
        Q_DIM = 256
        KV_DIM = 192
        HEADS = 16
        DK = Q_DIM // HEADS
        B, T_q, _ = q_tokens.shape
        T_kv = kv_tokens.shape[1]
        q = q_tokens @ Wq.T
        k = kv_tokens @ Wk.T
        v = kv_tokens @ Wv.T
        q = q.reshape(B, T_q, HEADS, DK).transpose(0, 2, 1, 3)
        k = k.reshape(B, T_kv, HEADS, DK).transpose(0, 2, 1, 3)
        v = v.reshape(B, T_kv, HEADS, DK).transpose(0, 2, 1, 3)
        scale = 1.0 / jnp.sqrt(jnp.asarray(DK, q.dtype))
        attn = jnp.einsum('bhqd,bhkd->bhqk', q, k) * scale
        attn = jax.nn.softmax(attn, axis=-1)
        out = jnp.einsum('bhqk,bhkd->bhqd', attn, v)
        out = out.transpose(0, 2, 1, 3).reshape(B, T_q, Q_DIM)
        return out @ Wo.T

    def _L0_attn_ref(x, ln_w, ln_b, in_proj_w, conv_w, conv_b, dt_bias, A_log, D, norm_w, out_proj_w):
        import jax, jax.numpy as jnp
        import numpy as np
        D_MODEL, D_STATE, EXPAND, D_CONV, HEADDIM = (256, 128, 2, 4, 64)
        D_INNER = EXPAND * D_MODEL
        NHEADS = D_INNER // HEADDIM
        NGROUPS = 1
        CONV_DIM = D_INNER + 2 * NGROUPS * D_STATE
        D_IN_PROJ = 2 * D_INNER + 2 * NGROUPS * D_STATE + NHEADS
        BATCH, SEQ = (2, 1024)
        EPS = 1e-05

        def _mamba2(u, in_proj_w, conv_w, conv_b, dt_bias, A_log, Dp, norm_w, out_proj_w):
            b, l, _ = u.shape
            zxbcdt = u @ in_proj_w.T
            z, xBC, dt = jnp.split(zxbcdt, [D_INNER, D_INNER + CONV_DIM], axis=-1)
            xBC = jnp.transpose(xBC, (0, 2, 1))
            xBC = jax.lax.conv_general_dilated(xBC, conv_w[:, None, :], window_strides=(1,), padding=[(D_CONV - 1, 0)], feature_group_count=CONV_DIM, dimension_numbers=('NCH', 'OIH', 'NCH'))
            xBC = jax.nn.silu(jnp.transpose(xBC, (0, 2, 1)) + conv_b)
            x, Bm, Cm = jnp.split(xBC, [D_INNER, D_INNER + NGROUPS * D_STATE], axis=-1)
            dt = jax.nn.softplus(dt + dt_bias)
            A = -jnp.exp(A_log)
            xh = x.reshape(b, l, NHEADS, HEADDIM)
            dt_t, x_t = (jnp.moveaxis(dt, 1, 0), jnp.moveaxis(xh, 1, 0))
            B_t, C_t = (jnp.moveaxis(Bm, 1, 0), jnp.moveaxis(Cm, 1, 0))

            def step(h, inputs):
                dtk, xk, Bk, Ck = inputs
                decay = jnp.exp(dtk * A)
                h = h * decay[:, :, None, None] + dtk[:, :, None, None] * xk[..., None] * Bk[:, None, None, :]
                y = jnp.einsum('bhpn,bn->bhp', h, Ck)
                return (h, y)
            h0 = jnp.zeros((b, NHEADS, HEADDIM, D_STATE), u.dtype)
            _, ys = jax.lax.scan(step, h0, (dt_t, x_t, B_t, C_t))
            y = jnp.moveaxis(ys, 0, 1) + Dp[None, None, :, None] * xh
            y = y.reshape(b, l, D_INNER)
            y = y * jax.nn.silu(z)
            y = y * jax.lax.rsqrt(jnp.mean(y * y, axis=-1, keepdims=True) + EPS) * norm_w
            return y @ out_proj_w.T
        mu = jnp.mean(x, -1, keepdims=True)
        var = jnp.mean((x - mu) ** 2, -1, keepdims=True)
        xn = (x - mu) * jax.lax.rsqrt(var + EPS) * ln_w + ln_b
        return x + _mamba2(xn, in_proj_w, conv_w, conv_b, dt_bias, A_log, D, norm_w, out_proj_w)

    def _L0_ffn_ref(x, gate_w, up_w, up_b, down_w, down_b, sh_up_w, sh_up_b, sh_down_w, sh_down_b):
        import jax, jax.numpy as jnp
        import numpy as np
        D_MODEL = 256
        HIDDEN = 256
        NUM_EXPERTS = 8
        TOP_K = 2
        b, s, d = x.shape
        xf = x.reshape(-1, d)
        shared = jax.nn.silu(x @ sh_up_w + sh_up_b) @ sh_down_w + sh_down_b
        logits = xf @ gate_w.T
        scores = jax.nn.softmax(logits, axis=-1)
        topk_w, topk_i = jax.lax.top_k(scores, TOP_K)
        topk_w = topk_w / (topk_w.sum(axis=-1, keepdims=True) + 1e-20)
        comb = (jax.nn.one_hot(topk_i, NUM_EXPERTS, dtype=xf.dtype) * topk_w[..., None]).sum(axis=1)
        h = jnp.einsum('nd,edh->neh', xf, up_w) + up_b
        h = jax.nn.silu(h)
        ye = jnp.einsum('neh,ehd->ned', h, down_w) + down_b
        y = jnp.einsum('ned,ne->nd', ye, comb).reshape(b, s, d)
        return y + shared

    def _L1_xattn_ref(x, context, Wq, Wk, Wv, Wo, bo):
        import jax, jax.numpy as jnp
        import numpy as np
        HEADS = 8
        DIM_HEAD = 64
        QUERY_DIM = 256
        CONTEXT_DIM = 192
        INNER = HEADS * DIM_HEAD
        B, Sq, _ = x.shape
        h, d = (HEADS, DIM_HEAD)
        scale = d ** (-0.5)
        q = (x @ Wq).reshape(B, Sq, h, d).transpose(0, 2, 1, 3)
        k = (context @ Wk).reshape(B, -1, h, d).transpose(0, 2, 1, 3)
        v = (context @ Wv).reshape(B, -1, h, d).transpose(0, 2, 1, 3)
        scores = jnp.einsum('bhid,bhjd->bhij', q, k) * scale
        attn = jax.nn.softmax(scores, axis=-1)
        out = jnp.einsum('bhij,bhjd->bhid', attn, v)
        out = out.transpose(0, 2, 1, 3).reshape(B, Sq, h * d)
        return out @ Wo + bo

    def _L1_attn_ref(x, norm_w, in_proj_w, in_proj_b, conv_w, conv_b, out_proj_w, out_proj_b, A_log, D_param, dt, B_param, C_param):
        import jax, jax.numpy as jnp
        import numpy as np
        from jax import lax
        B, L, DM = (4, 256, 256)
        DI, N, KC = (512, 16, 4)
        EPS_NORM = 1e-06
        EPS_A = 1e-08

        def _mamba_block(x, norm_w, in_proj_w, in_proj_b, conv_w, conv_b, out_proj_w, out_proj_b, A_log, D_param, dt, B_param, C_param):
            b, l, _ = x.shape
            residual = x
            rms = lax.rsqrt(jnp.mean(x * x, axis=-1, keepdims=True) + EPS_NORM)
            xn = x * rms * norm_w
            xz = xn @ in_proj_w.T + in_proj_b
            x_ssm, gate = jnp.split(xz, 2, axis=-1)
            xc = x_ssm.transpose(0, 2, 1)
            xc = lax.conv_general_dilated(xc, conv_w, (1,), [(KC - 1, KC - 1)], dimension_numbers=('NCH', 'OIH', 'NCH'))
            xc = xc[:, :, :l] + conv_b[None, :, None]
            x_ssm = jax.nn.silu(xc.transpose(0, 2, 1))
            A = -jnp.exp(A_log)
            dts = jax.nn.sigmoid(dt)[:, None]
            A_bar = jnp.exp(dts * A)
            B_bar = (A_bar - 1.0) / (A + EPS_A) * B_param
            l_range = jnp.arange(l, dtype=x.dtype)
            A_pow = A_bar[:, :, None] ** l_range[None, None, :]
            K = jnp.einsum('dn,dn,dnl->dl', C_param, B_bar, A_pow)
            K = jnp.flip(K, axis=1)
            xcv = x_ssm.transpose(0, 2, 1)
            x_padded = jnp.pad(xcv, ((0, 0), (0, 0), (l - 1, 0)))
            ssm = lax.conv_general_dilated(x_padded, K[:, None, :], (1,), 'VALID', feature_group_count=K.shape[0], dimension_numbers=('NCH', 'OIH', 'NCH'))
            ssm = ssm.transpose(0, 2, 1) + x_ssm * D_param
            out = ssm * jax.nn.silu(gate)
            out = out @ out_proj_w.T + out_proj_b
            return residual + out
        return _mamba_block(x, norm_w, in_proj_w, in_proj_b, conv_w, conv_b, out_proj_w, out_proj_b, A_log, D_param, dt, B_param, C_param)

    def _L1_ffn_ref(x, gate_w, w1, b1, w2, b2):
        import jax, jax.numpy as jnp
        import numpy as np
        EMBED_DIM = 256
        HIDDEN_DIM = 1024
        NUM_EXPERTS = 8
        TOP_K = 2
        orig_shape = x.shape
        xt = x.reshape(-1, EMBED_DIM)
        logits = xt @ gate_w.T
        probs = jax.nn.softmax(logits, axis=-1)
        top_w, top_i = jax.lax.top_k(probs, TOP_K)
        top_w = top_w / (top_w.sum(axis=-1, keepdims=True) + 1e-09)
        h = jnp.einsum('td,ndh->tnh', xt, w1) + b1
        h = jax.nn.gelu(h, approximate=False)
        out_all = jnp.einsum('tnh,nhd->tnd', h, w2) + b2
        sel = jnp.take_along_axis(out_all, top_i[:, :, None], axis=1)
        out = (sel * top_w[:, :, None]).sum(axis=1)
        return out.reshape(orig_shape)

    def _L2_xattn_ref(x, context, Wq, Wk, Wv, Wo, bo):
        import jax, jax.numpy as jnp
        import numpy as np
        HEADS = 8
        DIM_HEAD = 64
        SCALE = DIM_HEAD ** (-0.5)
        B, Nq, _ = x.shape
        q = (x @ Wq).reshape(B, Nq, HEADS, DIM_HEAD)
        k = (context @ Wk).reshape(B, context.shape[1], HEADS, DIM_HEAD)
        v = (context @ Wv).reshape(B, context.shape[1], HEADS, DIM_HEAD)
        sim = jnp.einsum('bihd,bjhd->bhij', q, k) * SCALE
        attn = jax.nn.softmax(sim, axis=-1)
        out = jnp.einsum('bhij,bjhd->bihd', attn, v)
        out = out.reshape(B, Nq, HEADS * DIM_HEAD)
        return out @ Wo + bo

    def _L2_attn_ref(x, in_proj_w, conv_w, conv_b, x_proj_w, dt_proj_w, dt_proj_b, A_log, D, norm_w, out_proj_w):
        import jax, jax.numpy as jnp
        import numpy as np
        D_MODEL, D_STATE, D_CONV, EXPAND = (256, 16, 4, 2)
        D_INNER = EXPAND * D_MODEL
        BATCH, SEQ = (2, 256)
        EPS = 1e-08

        def _causal_dwconv(x_bcl, w, b):
            out = jax.lax.conv_general_dilated(x_bcl, w, window_strides=(1,), padding=[(D_CONV - 1, 0)], dimension_numbers=('NCH', 'OIH', 'NCH'), feature_group_count=D_INNER)
            return out + b[None, :, None]

        def _selective_scan(u, delta, A, B, C, D):
            dA = jnp.exp(delta[..., None] * A)
            dBu = delta[..., None] * B[:, :, None, :] * u[..., None]
            dA_t = jnp.moveaxis(dA, 1, 0)
            dBu_t = jnp.moveaxis(dBu, 1, 0)
            C_t = jnp.moveaxis(C, 1, 0)

            def step(h, inp):
                da, dbu, c = inp
                h = da * h + dbu
                y = jnp.einsum('bdn,bn->bd', h, c)
                return (h, y)
            h0 = jnp.zeros((u.shape[0], u.shape[2], A.shape[1]), u.dtype)
            _, ys = jax.lax.scan(step, h0, (dA_t, dBu_t, C_t))
            y = jnp.moveaxis(ys, 0, 1)
            return y + u * D
        xz = x @ in_proj_w.T
        xc, z = jnp.split(xz, 2, axis=-1)
        xc = _causal_dwconv(jnp.swapaxes(xc, 1, 2), conv_w, conv_b)
        xc = jax.nn.silu(jnp.swapaxes(xc, 1, 2))
        x_dbl = xc @ x_proj_w.T
        dlt, B, C = jnp.split(x_dbl, [D_STATE, 2 * D_STATE], axis=-1)
        delta = jax.nn.softplus(dlt @ dt_proj_w.T + dt_proj_b)
        A = -jnp.exp(A_log)
        y = _selective_scan(xc, delta, A, B, C, D)
        y = y * jax.nn.silu(z)
        y = y * jax.lax.rsqrt(jnp.mean(y * y, axis=-1, keepdims=True) + EPS) * norm_w
        return y @ out_proj_w.T

    def _L2_ffn_ref(hidden_states, gate_w, correction_bias, Wg, Wu, Wd, Wg_s, Wu_s, Wd_s):
        import jax, jax.numpy as jnp
        import numpy as np
        E, H, I = (8, 256, 128)
        NG, TKG, TOPK = (4, 2, 4)
        SCALE = 2.5

        def _mlp(x, wg, wu, wd):
            return jax.nn.silu(x @ wg) * (x @ wu) @ wd
        B, T, _ = hidden_states.shape
        x = hidden_states.reshape(-1, H)
        N = x.shape[0]
        logits = x @ gate_w.T
        scores = jax.nn.sigmoid(logits)
        scores_c = scores + correction_bias
        grp = scores_c.reshape(N, NG, E // NG)
        group_scores = jnp.sum(jax.lax.top_k(grp, 2)[0], axis=-1)
        grp_idx = jax.lax.top_k(group_scores, TKG)[1]
        group_mask = jnp.zeros_like(group_scores).at[jnp.arange(N)[:, None], grp_idx].set(1.0)
        score_mask = jnp.repeat(group_mask, E // NG, axis=-1) > 0.5
        scores_for_choice = jnp.where(score_mask, scores_c, 0.0)
        topk_idx = jax.lax.top_k(scores_for_choice, TOPK)[1]
        topk_w = jnp.take_along_axis(scores, topk_idx, axis=-1)
        topk_w = topk_w / (jnp.sum(topk_w, axis=-1, keepdims=True) + 1e-20)
        topk_w = topk_w * SCALE
        cw = jnp.sum(jax.nn.one_hot(topk_idx, E, dtype=topk_w.dtype) * topk_w[..., None], axis=1)
        g = jnp.einsum('nh,ehi->eni', x, Wg)
        u = jnp.einsum('nh,ehi->eni', x, Wu)
        y = jnp.einsum('eni,eih->enh', jax.nn.silu(g) * u, Wd)
        routed = jnp.einsum('enh,ne->nh', y, cw)
        out = routed + _mlp(x, Wg_s, Wu_s, Wd_s)
        return out.reshape(B, T, H)

    def _L3_xattn_ref(x, latents, mask, ln_x_g, ln_x_b, ln_l_g, ln_l_b, qn_g, kn_g, Wq, Wkv, Wlkv, Wo, bo):
        import jax, jax.numpy as jnp
        import numpy as np
        DIM_IN, DIM_LAT, DIM_HEAD = (192, 256, 64)
        INNER = max(DIM_LAT, DIM_IN)
        HEADS = INNER // DIM_HEAD
        SCALE = DIM_HEAD ** (-0.5)
        RMS_EPS = 1e-08
        LN_EPS = 1e-05

        def layernorm(x, g, b):
            mu = jnp.mean(x, axis=-1, keepdims=True)
            var = jnp.mean((x - mu) ** 2, axis=-1, keepdims=True)
            return (x - mu) * jax.lax.rsqrt(var + LN_EPS) * g + b

        def rmsnorm(x, gamma):
            norm = jnp.sqrt(jnp.sum(x * x, axis=-1, keepdims=True)) * x.shape[-1] ** (-0.5)
            return x / jnp.maximum(norm, RMS_EPS) * gamma
        b, n, _ = x.shape
        m = latents.shape[1]
        xn = layernorm(x, ln_x_g, ln_x_b)
        ln = layernorm(latents, ln_l_g, ln_l_b)
        q = ln @ Wq.T
        kv = jnp.concatenate([xn @ Wkv.T, ln @ Wlkv.T], axis=1)
        k, v = (kv[..., :INNER], kv[..., INNER:])
        split_heads = lambda t: t.reshape(t.shape[0], t.shape[1], HEADS, DIM_HEAD).transpose(0, 2, 1, 3)
        q, k, v = (split_heads(q), split_heads(k), split_heads(v))
        qn = rmsnorm(q, qn_g) * SCALE
        kn = rmsnorm(k, kn_g)
        attn = jnp.einsum('bhid,bhjd->bhij', qn, kn)
        full_mask = jnp.pad(mask, ((0, 0), (0, m)), constant_values=True)
        attn = jnp.where(full_mask[:, None, None, :], attn, -jnp.finfo(attn.dtype).max)
        attn = jax.nn.softmax(attn, axis=-1)
        out = jnp.einsum('bhij,bhjd->bhid', attn, v)
        out = out.transpose(0, 2, 1, 3).reshape(b, m, INNER)
        return out @ Wo.T + bo

    def _L3_attn_ref(x, Wq, Wk, Wv, Wo):
        import jax, jax.numpy as jnp
        import numpy as np
        B, S, E = (4, 256, 256)
        H = 16
        D = E // H
        b, s, e = x.shape

        def split_heads(t):
            return t.reshape(b, s, H, D).transpose(0, 2, 1, 3)
        q = split_heads(x @ Wq)
        k = split_heads(x @ Wk)
        v = split_heads(x @ Wv)
        qc = q - q.mean(axis=-1, keepdims=True)
        kc = k - k.mean(axis=-1, keepdims=True)
        cov = jnp.einsum('bhsd,bhtd->bhst', qc, kc) / D
        q_var = jnp.var(q, axis=-1, ddof=1)
        k_var = jnp.var(k, axis=-1, ddof=1)
        var_comp = q_var[..., :, None] * k_var[..., None, :] / D
        scores = cov + var_comp
        attn = jax.nn.softmax(scores, axis=-1)
        out = jnp.einsum('bhst,bhtd->bhsd', attn, v)
        out = out.transpose(0, 2, 1, 3).reshape(b, s, e)
        return out @ Wo

    def _L3_ffn_ref(x, wg, w1, b1, w2, b2):
        import jax, jax.numpy as jnp
        import numpy as np
        E = 8
        K = 2
        CAP_FACTOR = 1.0
        B, S, M = x.shape
        N = B * S
        capacity = int(CAP_FACTOR * K * N // E)
        xt = x.reshape(N, M)
        logits = xt @ wg
        scores = jax.nn.softmax(logits, axis=-1)
        topv, topi = jax.lax.top_k(scores, K)
        topv = topv / jnp.sum(topv, axis=-1, keepdims=True)
        masks = jax.nn.one_hot(topi.T, E, dtype=jnp.int32)
        flat = masks.reshape(K * N, E)
        locs = jnp.cumsum(flat, axis=0) - 1
        pos = jnp.sum(locs * flat, axis=-1).reshape(K, N).T
        valid = pos < capacity
        gate = topv * valid.astype(topv.dtype)
        pos_c = jnp.where(valid, pos, 0)
        xk = xt[:, None, :] * valid[..., None].astype(xt.dtype)
        disp = jnp.zeros((E, capacity, M), xt.dtype)
        disp = disp.at[topi, pos_c].add(xk)
        h = jax.nn.relu(jnp.einsum('ecm,emh->ech', disp, w1) + b1[:, None, :])
        y = jnp.einsum('ech,ehm->ecm', h, w2) + b2[:, None, :]
        out = jnp.sum(gate[..., None] * y[topi, pos_c], axis=1)
        return out.reshape(B, S, M)
    x = x + _L0_xattn_ref(_layernorm(x, axis=-1), ctx_768, L0_xattn_Wq, L0_xattn_Wk, L0_xattn_Wv, L0_xattn_Wo)
    x = x + _L0_attn_ref(_layernorm(x, axis=-1), L0_attn_ln_w, L0_attn_ln_b, L0_attn_in_proj_w, L0_attn_conv_w, L0_attn_conv_b, L0_attn_dt_bias, L0_attn_A_log, L0_attn_D, L0_attn_norm_w, L0_attn_out_proj_w)
    x = x + _L0_ffn_ref(_layernorm(x, axis=-1), L0_ffn_gate_w, L0_ffn_up_w, L0_ffn_up_b, L0_ffn_down_w, L0_ffn_down_b, L0_ffn_sh_up_w, L0_ffn_sh_up_b, L0_ffn_sh_down_w, L0_ffn_sh_down_b)
    x = x + _L1_xattn_ref(_layernorm(x, axis=-1), ctx_768, L1_xattn_Wq, L1_xattn_Wk, L1_xattn_Wv, L1_xattn_Wo, L1_xattn_bo)
    x = x + _L1_attn_ref(_layernorm(x, axis=-1), L1_attn_norm_w, L1_attn_in_proj_w, L1_attn_in_proj_b, L1_attn_conv_w, L1_attn_conv_b, L1_attn_out_proj_w, L1_attn_out_proj_b, L1_attn_A_log, L1_attn_D_param, L1_attn_dt, L1_attn_B_param, L1_attn_C_param)
    x = x + _L1_ffn_ref(_layernorm(x, axis=-1), L1_ffn_gate_w, L1_ffn_w1, L1_ffn_b1, L1_ffn_w2, L1_ffn_b2)
    x = x + _L2_xattn_ref(_layernorm(x, axis=-1), ctx_768, L2_xattn_Wq, L2_xattn_Wk, L2_xattn_Wv, L2_xattn_Wo, L2_xattn_bo)
    x = x + _L2_attn_ref(_layernorm(x, axis=-1), L2_attn_in_proj_w, L2_attn_conv_w, L2_attn_conv_b, L2_attn_x_proj_w, L2_attn_dt_proj_w, L2_attn_dt_proj_b, L2_attn_A_log, L2_attn_D, L2_attn_norm_w, L2_attn_out_proj_w)
    x = x + _L2_ffn_ref(_layernorm(x, axis=-1), L2_ffn_gate_w, L2_ffn_correction_bias, L2_ffn_Wg, L2_ffn_Wu, L2_ffn_Wd, L2_ffn_Wg_s, L2_ffn_Wu_s, L2_ffn_Wd_s)
    x = x + _L3_xattn_ref(ctx_768, _layernorm(x, axis=-1), mask_BxS2_bk0, L3_xattn_ln_x_g, L3_xattn_ln_x_b, L3_xattn_ln_l_g, L3_xattn_ln_l_b, L3_xattn_qn_g, L3_xattn_kn_g, L3_xattn_Wq, L3_xattn_Wkv, L3_xattn_Wlkv, L3_xattn_Wo, L3_xattn_bo)
    x = x + _L3_attn_ref(_layernorm(x, axis=-1), L3_attn_Wq, L3_attn_Wk, L3_attn_Wv, L3_attn_Wo)
    x = x + _L3_ffn_ref(_layernorm(x, axis=-1), L3_ffn_wg, L3_ffn_w1, L3_ffn_b1, L3_ffn_w2, L3_ffn_b2)
    return x

_drawn_inputs = setup_inputs


def setup_inputs(seed=0):
    import zlib

    import numpy as np

    out = dict(_drawn_inputs(seed))
    spreads = {'L0_attn_ln_w': (1.0, 0.2),
     'L0_attn_ln_b': (0.0, 0.1),
     'L0_attn_conv_b': (0.0, 0.1),
     'L0_attn_D': (1.0, 0.2),
     'L0_attn_norm_w': (1.0, 0.2),
     'L0_ffn_up_b': (0.0, 1.15),
     'L0_ffn_down_b': (0.0, 0.1),
     'L0_ffn_sh_up_b': (0.0, 0.323),
     'L0_ffn_sh_down_b': (0.0, 0.1),
     'L1_attn_norm_w': (1.0, 0.6),
     'L1_attn_in_proj_b': (0.0, 0.474),
     'L1_attn_conv_b': (0.0, 0.705),
     'L1_attn_out_proj_b': (0.0, 0.716),
     'L1_attn_D_param': (1.0, 0.6),
     'L1_attn_dt': (0.10000000149011612, 0.6),
     'L1_attn_B_param': (0.5, 0.6),
     'L1_ffn_b1': (0.0, 2.0),
     'L1_ffn_b2': (0.0, 2.0),
     'L2_attn_conv_b': (0.0, 0.715),
     'L2_attn_dt_proj_b': (0.0, 2.0),
     'L2_attn_D': (1.0, 0.6),
     'L2_attn_norm_w': (1.0, 0.6),
     'L2_ffn_correction_bias': (0.0, 0.8),
     'L3_xattn_ln_x_g': (1.0, 0.6),
     'L3_xattn_ln_x_b': (0.0, 2.0),
     'L3_xattn_ln_l_g': (1.0, 0.6),
     'L3_xattn_ln_l_b': (0.0, 2.0),
     'L3_xattn_qn_g': (1.0, 0.6),
     'L3_xattn_kn_g': (1.0, 0.6),
     'L3_xattn_bo': (0.0, 2.0),
     'L3_ffn_b1': (0.0, 2.0),
     'L3_ffn_b2': (0.0, 2.0)}
    factors = {'L1_xattn_bo': 2.86,
     'L1_attn_in_proj_w': 2.797,
     'L1_attn_conv_w': 4.063,
     'L1_attn_out_proj_w': 2.827,
     'L1_attn_A_log': 8.0,
     'L1_attn_C_param': 7.026,
     'L2_xattn_bo': 52.563,
     'L2_ffn_gate_w': 8.0,
     'L2_ffn_Wg': 8.0,
     'L2_ffn_Wu': 8.0,
     'L2_ffn_Wd': 8.0,
     'L2_ffn_Wg_s': 8.0,
     'L2_ffn_Wu_s': 8.0,
     'L2_ffn_Wd_s': 8.0,
     'L3_attn_Wq': 64.0,
     'L3_attn_Wk': 64.0,
     'L0_ffn_up_w': 2.819,
     'L2_xattn_Wq': 5.046,
     'L2_xattn_Wk': 4.135,
     'L2_attn_dt_proj_w': 4.337,
     'L2_attn_A_log': 5.207,
     'L3_xattn_Wq': 7.3,
     'L3_xattn_Wkv': 5.629,
     'L3_xattn_Wlkv': 5.859,
     'L3_xattn_Wo': 4.415,
     'L3_attn_Wv': 8.0,
     'L3_attn_Wo': 7.999,
     'L3_ffn_wg': 8.0,
     'L3_ffn_w1': 8.0,
     'L3_ffn_w2': 8.0}
    for name, (base, spread) in spreads.items():
        noise = np.random.default_rng([zlib.crc32(name.encode()), seed]).standard_normal(out[name].shape)
        drawn = base * np.exp(spread * noise) if base else spread * noise
        out[name] = jnp.asarray(drawn.astype(out[name].dtype))
    for name, factor in factors.items():
        out[name] = (out[name] * factor).astype(out[name].dtype)
    return out
```

```python
from contextlib import ExitStack, contextmanager

import numpy as np

import concourse.bass as bass
from concourse import mybir

ALU = mybir.AluOpType
ACT = mybir.ActivationFunctionType
AX = mybir.AxisListType
F32 = mybir.dt.float32
F32R = mybir.dt.float32r

P = 128
B, T, D = 16, 64, 256
N = B * T
S, DC = 1024, 192
CD = D // P
HALF = 512
SEMS = 40


class Core:

    def __init__(self, nc, dram, ctx):
        self.nc, self.dram = nc, dram
        sb = lambda name, shape: ctx.enter_context(nc.sbuf_tensor(name, shape, F32))
        self.sem_pool = [nc.alloc_semaphore(f"pool{i}") for i in range(SEMS)]
        self.xT = sb("xT", [P, CD, N])
        self.xn = sb("xn", [P, CD, N])
        self.ones = sb("ones", [P, P])
        self.ident = sb("ident", [P, P])
        self.count = 0
        self.weights = nc.alloc_semaphore("weights_landed")
        self.due = 0

    @contextmanager
    def stage(self, name, *signals):
        nc = self.nc
        self.count += 1
        tag = f"{name}{self.count}_"
        with ExitStack() as ctx:
            def sb(n, shape, dt=F32):
                return ctx.enter_context(nc.sbuf_tensor(tag + n, shape, dt))

            def ps(n, shape, dt=F32):
                return ctx.enter_context(nc.psum_tensor(tag + n, shape, dt))
            assert len(signals) <= SEMS
            yield (sb, ps, *self.sem_pool[:len(signals)])
        if signals:
            nums = [s.num for s in self.sem_pool[:len(signals)]]
            assert nums == list(range(nums[0], nums[0] + len(nums)))
            nc.all_engine_barrier(sems_to_clear=range(nums[0], nums[-1] + 1))


def load_constants(k):
    nc = k.nc
    with k.stage("load", "landed") as (sb, ps, landed):
        with nc.Block() as block:
            @block.sync
            def _(sp):
                sp.dma_start(k.xT[:], k.dram["xT"]).then_inc(landed, 16)
                sp.dma_start(k.ident[:], k.dram["ident"]).then_inc(landed, 16)
                sp.wait_ge(landed, 32)

            @block.vector
            def _(dve):
                dve.memset(k.ones[:], 1.0)


def store_result(k):
    nc = k.nc
    with k.stage("store", "stored") as (sb, ps, stored):
        with nc.Block() as block:
            @block.sync
            def _(sp):
                sp.dma_start(k.dram["outT"], k.xT[:]).then_inc(stored, 16)
                sp.wait_ge(stored, 16)


def layernorm(k, src, dst, eps, affine=None, centre=True, width=CD):
    nc = k.nc
    with k.stage("ln", "mean_ready", "centred", "squared", "var_ready", "shifted", "rooted", "inverted",
                 "scaled") as (
            sb, ps, mean_ready, centred, squared, var_ready, shifted, rooted, inverted, scaled):
        mean = ps("mean", [P, N])
        var = ps("var", [P, N])
        sq = sb("sq", [P, width, N])
        std = sb("std", [P, N])
        rstd = sb("rstd", [P, N])
        cen = sb("cen", [P, width, N]) if centre else None
        with nc.Block() as block:
            @block.tensor
            def _(pe):
                if centre:
                    for n in range(N // HALF):
                        for c in range(width):
                            mm = pe.matmul(mean[:, bass.ts(n, HALF)], k.ones[:], src[:, c, bass.ts(n, HALF)],
                                           start=c == 0, stop=c == width - 1)
                    mm.then_inc(mean_ready, 1)
                pe.wait_ge(squared, width)
                for n in range(N // HALF):
                    for c in range(width):
                        mm = pe.matmul(var[:, bass.ts(n, HALF)], k.ones[:], sq[:, c, bass.ts(n, HALF)],
                                       start=c == 0, stop=c == width - 1)
                mm.then_inc(var_ready, 1)

            @block.scalar
            def _(act):
                x = cen if centre else src
                for c in range(width):
                    if centre:
                        act.wait_ge(centred, c + 1)
                    act.activation(sq[:, c, :], x[:, c, :], ACT.Square).then_inc(squared, 1)
                act.wait_ge(shifted, 1)
                act.activation(std[:], std[:], ACT.Sqrt).then_inc(rooted, 1)

            @block.vector
            def _(dve):
                x = cen if centre else src
                if centre:
                    dve.wait_ge(mean_ready, 1)
                    for c in range(width):
                        dve.scalar_tensor_tensor(cen[:, c, :], mean[:], -1.0 / (width * P), src[:, c, :],
                                                 ALU.mult, ALU.add).then_inc(centred, 1)
                dve.wait_ge(var_ready, 1)
                dve.tensor_scalar(std[:], var[:], 1.0 / (width * P), eps, ALU.mult, ALU.add).then_inc(shifted, 1)
                dve.wait_ge(rooted, 1)
                dve.reciprocal(rstd[:], std[:]).then_inc(inverted, 1)
                dve.wait_ge(inverted, 1)
                if centre:
                    dve.wait_ge(centred, width)
                for c in range(width):
                    dve.tensor_tensor(dst[:, c, :], x[:, c, :], rstd[:], ALU.mult).then_inc(scaled, 1)
                if affine:
                    w, b = affine
                    dve.wait_ge(k.weights, k.due)
                    for c in range(width):
                        dve.wait_ge(scaled, c + 1)
                        if b is None:
                            dve.tensor_scalar(dst[:, c, :], dst[:, c, :], w[:, c:c + 1], None, ALU.mult)
                        else:
                            dve.tensor_scalar(dst[:, c, :], dst[:, c, :], w[:, c:c + 1], b[:, c:c + 1],
                                              ALU.mult, ALU.add)


def context_attention(k, name, heads, scale, bias):
    nc = k.nc
    slot = HALF // heads
    per = P // slot
    NC = HALF // P
    HQ = heads * T
    NJ = HQ // P
    NK = S // P
    W = per * T
    KR = DC - P
    with ExitStack() as ctx:
        keep = lambda n, shape: ctx.enter_context(nc.sbuf_tensor(f"{name}_{n}", shape, F32))
        qT = keep("qT", [P, NC, N])
        oT = keep("oT", [P, NC, N])
        wkT = keep("wkT", [P, NC, 2 * P])
        wv = keep("wv", [P, 2, HALF])
        wo = keep("wo", [P, NC, D])
        bo = keep("bo", [P, CD])
        with nc.sbuf_tensor(name + "_wq", [P, CD, HALF], F32) as wq:
            loads = [(wq[:], k.dram[name + "_Wq"]), (wkT[:], k.dram[name + "_WkT"]), (wv[:], k.dram[name + "_Wv"]),
                     (wo[:], k.dram[name + "_Wo"])]
            prefetch(k, *loads, *([(bo[:], k.dram[name + "_bo"])] if bias else []))
            layernorm(k, k.xT, k.xn, 1e-5)
            project(k, k.xn, wq, CD, NC, lambda act, m, n, bank: act.mul(qT[:, m, bass.ts(n, HALF)], bank, scale))

        with k.stage("att", "ctx0_landed", "ctx1_landed", "q_zero", "q_blocked", "split_step", "split_ready",
                     "q_folded", "q_high", "q_low", "scored", "maxed", "exped", "turned", "turned_v", "turned_a",
                     "mixed", "inverted", "normed", "mix_turned", "mix_taken", "projected", "proj_taken") as (
                sb, ps, ctx0_landed, ctx1_landed, q_zero, q_blocked, split_step, split_ready, q_folded, q_high,
                q_low, scored, maxed, exped, turned, turned_v, turned_a, mixed, inverted, normed, mix_turned,
                mix_taken, projected, proj_taken):
            landed = (ctx0_landed, ctx1_landed)
            cT = sb("cT", [P, 2, 2, S])
            cH = sb("cH", [P, 2, S], F32R)
            cL = sb("cL", [P, 2, S], F32R)
            cR = sb("cR", [P, 2, S], F32R)
            cN = sb("cN", [P, 2, NK, DC])
            qblk = sb("qblk", [P, 2, NC, W])
            qH = sb("qH", [P, 2, HQ], F32R)
            qL = sb("qL", [P, 2, HQ], F32R)
            pr = sb("pr", [P, 2, S])
            prT = sb("prT", [P, NK, P])
            nmax = sb("nmax", [P, NJ])
            total = sb("total", [P, NJ])
            inv = sb("inv", [P, NJ])
            mix = sb("mix", [P, 2, DC])
            mixT = sb("mixT", [P, 2, HQ])
            sc = ps("sc", [P, 2, S])
            tp = ps("tp", [P, NK, P])
            av = ps("av", [P, 2, HALF])
            chunk = tp[:].rearrange("p a b -> p (a b)")[:, 0:NC * W].rearrange("p (m w) -> p m w", m=NC)

            def every_batch(eng, run):
                with eng.Fori(0, B // 2 - 1) as i:
                    run(i * 2, 0, False)
                    run(i * 2 + 1, 1, False)
                run(B - 2, 0, False)
                run(B - 1, 1, True)

            with nc.Block() as block:
                @block.sync
                def _(sp):
                    def load(b, s):
                        sp.dma_start(cT[:, s, 0, :], k.dram["ctxT"][b, 0:P, :]).then_inc(landed[s], 16)
                        for g in range(2):
                            sp.dma_start(cT[g * KR:(g + 1) * KR, s, 1, :],
                                         k.dram["ctxT"][b, P:DC, :]).then_inc(landed[s], 16)
                        sp.dma_start(cN[:, s, :, :], k.dram["ctx"][b].rearrange("(j p) d -> p j d", p=P)
                                     ).then_inc(landed[s], 16)
                    load(0, 0)
                    load(1, 1)
                    with sp.Fori(1, B // 2) as i:
                        for s in range(2):
                            sp.wait_ge(mixed, (i * 2 + (s - 1)) * NJ)
                            load(i * 2 + s, s)

                @block.gpsimd
                def _(pool):
                    pool.memset(qblk[:], 0.0).then_inc(q_zero, 1)
                    pool.memset(mixT[:], 0.0).then_inc(q_zero, 1)
                    pool.wait_ge(q_zero, 2)

                    def block_q(b, s):
                        for g in range(per):
                            r = slice(g * slot, (g + 1) * slot)
                            pool.tensor_copy(qblk[r, s, :, bass.ts(g, T)],
                                             qT[r, :, bass.ds(b * T, T)]).then_inc(q_blocked, 1)
                        pool.wait_ge(q_blocked, (b + 1) * per)

                    def split(b, s, i):
                        pool.wait_ge(landed[s], i * 64 + 64)
                        x = cT[:, s, 0, :].rearrange("p (j q) -> p j q", q=P)
                        pool.tensor_tensor(cH[:, s].rearrange("p (j q) -> p j q", q=P), x, over(k.ones[:], 1, NK),
                                           ALU.mult).then_inc(split_step, 1)
                        pool.tensor_copy(cR[:, s], cT[:, s, 1, :]).then_inc(split_step, 1)
                        pool.wait_ge(split_step, b * 3 + 2)
                        pool.tensor_tensor(cL[:, s], cT[:, s, 0, :], cH[:, s].bitcast(F32), ALU.subtract
                                           ).then_inc(split_step, 1)
                        pool.wait_ge(split_step, b * 3 + 3)
                        pool.tensor_tensor(cR[KR:P, s], cT[KR:P, s, 1, :], cR[KR:P, s].bitcast(F32), ALU.subtract
                                           ).then_inc(split_ready, 1)
                        pool.wait_ge(split_ready, b + 1)

                    for s in range(2):
                        block_q(s, s)
                        split(s, s, 0)
                    with pool.Fori(1, B // 2) as i:
                        for s in range(2):
                            pool.wait_ge(q_folded, i * 2 + (s - 1))
                            block_q(i * 2 + s, s)
                            pool.wait_ge(scored, (i * 2 + (s - 1)) * NJ)
                            split(i * 2 + s, s, i)

                @block.tensor
                def _(pe):
                    def scores(b, s, j):
                        if j == 0:
                            pe.wait_ge(q_low, (b + 1) * 2)
                            pe.wait_ge(split_ready, b + 1)
                        if j >= 2:
                            pe.wait_ge(exped, b * NJ + (j - 1))
                        h0, h1, l0, l1 = (x[:, c, bass.ts(j, P)] for x in (qH, qL) for c in range(2))
                        for n in range(2):
                            to, at = sc[:, j % 2, bass.ts(n, HALF)], bass.ts(n, HALF)
                            pe.matmul(to, h0, cH[:, s, at], start=True, stop=False)
                            pe.matmul(to, h0, cL[:, s, at], start=False, stop=False)
                            pe.matmul(to, l0, cH[:, s, at], start=False, stop=False)
                            pe.matmul(to, h1, cR[:, s, at], start=False, stop=False)
                            mm = pe.matmul(to, l1, cR[:, s, at], start=False, stop=True)
                        mm.then_inc(scored, 1)

                    def fold(b, s):
                        pe.wait_ge(q_blocked, (b + 1) * per)
                        for m in range(NC):
                            for c in range(2):
                                mm = pe.matmul(sc[:, c, bass.ts(m, W)], wkT[:, m, bass.ts(c, P)],
                                               qblk[:, s, m, :], start=True, stop=True)
                        mm.then_inc(q_folded, 1)

                    def batch(b, s, last):
                        scores(b, s, 0)
                        for j in range(NJ + 1):
                            if j + 1 < NJ:
                                scores(b, s, j + 1)
                            if j >= 1:
                                pe.wait_ge(turned_v, b * NJ + j)
                                pe.wait_ge(turned_a, b * NJ + j)
                                if j >= 3:
                                    pe.wait_ge(mix_taken, b * NJ + (j - 2))
                                for n in range(NK):
                                    mm = pe.matmul(av[:, (j - 1) % 2, 0:DC], prT[:, n, :], cN[:, s, n, :],
                                                   start=n == 0, stop=n == NK - 1)
                                mm.then_inc(mixed, 1)
                            if j == NJ and not last:
                                fold(b + 1, 1 - s)
                            if j < NJ:
                                pe.wait_ge(exped, b * NJ + (j + 1))
                                if j == 0:
                                    pe.wait_ge(proj_taken, b + 1)
                                for n in range(NK):
                                    mm = pe.transpose(tp[:, n, :], pr[:, j % 2, bass.ts(n, P)], k.ident[:])
                                mm.then_inc(turned, 1)
                            if j >= 1:
                                pe.wait_ge(normed, b * NJ + j)
                                pe.transpose(av[:, (j - 1) % 2, DC:DC + P], mix[:, (j - 1) % 2, 0:P], k.ident[:])
                                pe.transpose(av[0:KR, (j - 1) % 2, DC + P:DC + 2 * P], mix[:, (j - 1) % 2, P:DC],
                                             k.ident[:]).then_inc(mix_turned, 1)
                        pe.wait_ge(mix_taken, b * NJ + NJ)
                        for m in range(NC):
                            pe.matmul(chunk[:, m, :], wv[:, 0, bass.ts(m, P)], mixT[:, 0, bass.ts(m, W)],
                                      start=True, stop=False)
                            mm = pe.matmul(chunk[:, m, :], wv[:, 1, bass.ts(m, P)], mixT[:, 1, bass.ts(m, W)],
                                           start=False, stop=True)
                        mm.then_inc(projected, 1)

                    fold(0, 0)
                    every_batch(pe, batch)

                @block.scalar
                def _(act):
                    def exp(b, j):
                        act.wait_ge(maxed, b * NJ + (j + 1))
                        act.activation(pr[:, j % 2, :], sc[:, j % 2, :], ACT.Exp, bias=nmax[:, j:j + 1],
                                       accum_out=total[:, j:j + 1]).then_inc(exped, 1)

                    def high(b):
                        act.wait_ge(q_folded, b + 1)
                        for c in range(2):
                            act.copy(qH[:, c, :], sc[:, c, 0:HQ]).then_inc(q_high, 1)

                    def batch(b, s, last):
                        exp(b, 0)
                        for j in range(NJ):
                            if j + 1 < NJ:
                                exp(b, j + 1)
                            act.wait_ge(turned, b * NJ + (j + 1))
                            act.copy(prT[:, 0:NK // 2, :], tp[:, 0:NK // 2, :]).then_inc(turned_a, 1)
                        if not last:
                            high(b + 1)
                        act.wait_ge(projected, b + 1)
                        for g in range(per):
                            r = slice(g * slot, (g + 1) * slot)
                            cp = act.copy(oT[r, :, bass.ds(b * T, T)], chunk[r, :, bass.ts(g, T)])
                        cp.then_inc(proj_taken, 1)

                    act.sem_inc(proj_taken, 1)
                    high(0)
                    every_batch(act, batch)

                @block.vector
                def _(dve):
                    def row_max(b, j):
                        dve.wait_ge(scored, b * NJ + (j + 1))
                        dve.tensor_reduce(nmax[:, j:j + 1], sc[:, j % 2, :], AX.X, ALU.max,
                                          negate=True).then_inc(maxed, 1)

                    def low(b):
                        for c in range(2):
                            dve.wait_ge(q_high, b * 2 + (c + 1))
                            dve.tensor_tensor(qL[:, c, :], sc[:, c, 0:HQ], qH[:, c, :].bitcast(F32),
                                              ALU.subtract).then_inc(q_low, 1)

                    def batch(b, s, last):
                        row_max(b, 0)
                        for j in range(NJ + 1):
                            if j + 1 < NJ:
                                row_max(b, j + 1)
                            if j >= 1:
                                dve.wait_ge(inverted, b * NJ + j)
                                dve.wait_ge(mixed, b * NJ + j)
                                dve.tensor_scalar(mix[:, (j - 1) % 2, :], av[:, (j - 1) % 2, 0:DC],
                                                  inv[:, j - 1:j], None, ALU.mult).then_inc(normed, 1)
                            if j < NJ:
                                dve.wait_ge(exped, b * NJ + (j + 1))
                                dve.reciprocal(inv[:, j:j + 1], total[:, j:j + 1]).then_inc(inverted, 1)
                                dve.wait_ge(turned, b * NJ + (j + 1))
                                dve.tensor_copy(prT[:, NK // 2:NK, :], tp[:, NK // 2:NK, :]).then_inc(turned_v, 1)
                            if j >= 1:
                                dve.wait_ge(mix_turned, b * NJ + j)
                                dve.tensor_copy(mixT[:, 0, bass.ts(j - 1, P)], av[:, (j - 1) % 2, DC:DC + P])
                                dve.tensor_copy(mixT[0:KR, 1, bass.ts(j - 1, P)],
                                                av[0:KR, (j - 1) % 2, DC + P:DC + 2 * P]).then_inc(mix_taken, 1)
                        if not last:
                            low(b + 1)

                    dve.wait_ge(q_zero, 2)
                    low(0)
                    every_batch(dve, batch)
        add_projection(k, oT, wo, NC, bias=bo if bias else None)


E = 8
NT = N // P


class Chain:

    def __init__(self, eng, sem, base=0):
        self.eng, self.sem, self.n, self.base = eng, sem, 0, base

    def mark(self, instruction):
        instruction.then_inc(self.sem, 1)
        self.n += 1

    def wait(self):
        self.eng.wait_ge(self.sem, self.base + self.n)

    def __call__(self, instruction):
        self.mark(instruction)
        self.wait()


def over(ap, axis, n):
    ap = ap.unsqueeze(axis)
    shape = list(ap.shape)
    shape[axis] = n
    return ap.broadcast_to(shape)


def gate(k, name, combT, top, softmax, eps, factor=1.0, grouped=False, capacity=None):
    nc = k.nc
    comb_dram = k.comb
    with k.stage("gate", "landed", "logits_ready", "scores_in", "scores_out", "counted", "valued", "comb_ready",
                 "turned", "copied", "stored", "step") as (
            sb, ps, landed, logits_ready, scores_in, scores_out, counted, valued, comb_ready, turned, copied,
            stored, step):
        gw = sb("gw", [P, CD, E])
        tri = sb("tri", [P, E * E])
        tri4 = sb("tri4", [P, 16])
        upto = sb("upto", [P, P])
        bias = sb("bias", [P, E])
        lg = sb("lg", [P, NT, E])
        pr = sb("pr", [P, NT, E])
        val = sb("val", [P, NT, E])
        ex = sb("ex", [P, NT, E])
        cmp = sb("cmp", [P, NT, E, E])
        eq = sb("eq", [P, NT, E, E])
        rank = sb("rank", [P, NT, E])
        mask = sb("mask", [P, 2, NT, E])
        row = sb("row", [P, 3, NT])
        comb = sb("comb", [P, NT, E])
        grp = sb("grp", [P, 3, NT, 4])
        pre = sb("pre", [P, 2 * NT, E])
        tot = sb("tot", [P, 2 * NT, E])
        ones = sb("ones", [P, 2 * NT])
        lg_ps = ps("lg_ps", [P, NT, E])
        cnt_ps = ps("cnt_ps", [P, 2 * NT, E])
        tot_ps = ps("tot_ps", [P, 2 * NT, E])
        ct_ps = ps("ct_ps", [P, N])
        with nc.Block() as block:
            @block.sync
            def _(sp):
                sp.dma_start(gw[:], k.dram[name + "_gate"]).then_inc(landed, 16)
                sp.dma_start(tri[:], k.dram["lower8"].partition_broadcast(P)).then_inc(landed, 16)
                sp.dma_start(tri4[:], k.dram["lower4"].partition_broadcast(P)).then_inc(landed, 16)
                sp.dma_start(upto[:], k.dram["upto"]).then_inc(landed, 16)
                if grouped:
                    sp.dma_start(bias[:], k.dram[name + "_cbias"].partition_broadcast(P)).then_inc(landed, 16)
                sp.wait_ge(copied, 1)
                sp.dma_start(comb_dram, combT[:]).then_inc(stored, 16)
                sp.wait_ge(stored, 16)

            @block.tensor
            def _(pe):
                pe.wait_ge(landed, 64 + 16 * grouped)
                for t in range(NT):
                    for c in range(CD):
                        mm = pe.matmul(lg_ps[:, t, :], k.xn[:, c, bass.ts(t, P)], gw[:, c, :],
                                       start=c == 0, stop=c == CD - 1)
                mm.then_inc(logits_ready, 1)
                if capacity:
                    pe.wait_ge(valued, 1)
                    flat = mask[:].rearrange("p a t e -> p (a t e)")
                    pe.matmul(cnt_ps[:].rearrange("p a e -> p (a e)"), upto[:], flat, start=True, stop=True)
                    pe.matmul(tot_ps[:].rearrange("p a e -> p (a e)"), k.ones[:], flat, start=True,
                              stop=True).then_inc(counted, 1)
                pe.wait_ge(comb_ready, 1)
                for t in range(NT):
                    mm = pe.transpose(ct_ps[0:E, bass.ts(t, P)], comb[:, t, :], k.ident[:])
                mm.then_inc(turned, 1)

            @block.scalar
            def _(act):
                if softmax:
                    act.wait_ge(scores_in, 1)
                    act.activation(ex[:], lg[:], ACT.Exp).then_inc(scores_out, 1)
                else:
                    act.wait_ge(logits_ready, 1)
                    act.activation(pr[:], lg_ps[:], ACT.Sigmoid).then_inc(scores_out, 1)

            @block.vector
            def _(dve):
                link = Chain(dve, step)
                tt = dve.tensor_tensor

                def ranks(out, v, e, lower):
                    mine, other = over(v, 3, e), over(v, 2, e)
                    c, q = (x[:].rearrange("p t a b -> p (t a b)")[:, 0:NT * e * e]
                            .rearrange("p (t a b) -> p t a b", t=NT, a=e) for x in (cmp, eq))
                    link(tt(c, other, mine, ALU.is_gt))
                    link(tt(q, other, mine, ALU.is_equal))
                    lw = lower.rearrange("p (a b) -> p a b", a=e)
                    link(tt(q, q, over(lw, 1, NT), ALU.mult))
                    link(tt(c, c, q, ALU.add))
                    link(dve.tensor_reduce(out, c, AX.X, ALU.add))

                dve.wait_ge(landed, 64 + 16 * grouped)
                if softmax:
                    dve.wait_ge(logits_ready, 1)
                    link(dve.tensor_reduce(row[:, 0, :], lg_ps[:], AX.X, ALU.max))
                    tt(lg[:], lg_ps[:], over(row[:, 0, :], 2, E), ALU.subtract).then_inc(scores_in, 1)
                    dve.wait_ge(scores_out, 1)
                    link(dve.tensor_reduce(row[:, 1, :], ex[:], AX.X, ALU.add))
                    link(dve.reciprocal(row[:, 2, :], row[:, 1, :]))
                    link(tt(pr[:], ex[:], over(row[:, 2, :], 2, E), ALU.mult))
                    choice = pr
                else:
                    dve.wait_ge(scores_out, 1)
                    link(tt(val[:], pr[:], over(bias[:], 1, NT), ALU.add))
                    pair = val[:].rearrange("p t (g j) -> p t g j", j=2)
                    link(tt(grp[:, 0, :, :], pair[:, :, :, 0], pair[:, :, :, 1], ALU.add))
                    ranks(grp[:, 1, :, :], grp[:, 0, :, :], 4, tri4[:])
                    link(dve.tensor_scalar(grp[:, 2, :, :], grp[:, 1, :, :], 1.5, None, ALU.is_lt))
                    link(tt(pair, pair, over(grp[:, 2, :, :], 3, 2), ALU.mult))
                    choice = val
                ranks(rank[:], choice[:], E, tri[:])
                if capacity:
                    link(dve.tensor_scalar(mask[:, 0], rank[:], 0.5, None, ALU.is_lt))
                    link(dve.tensor_scalar(mask[:, 1], rank[:], 1.5, None, ALU.is_lt))
                    tt(mask[:, 1], mask[:, 1], mask[:, 0], ALU.subtract).then_inc(valued, 1)
                    link(dve.memset(ones[:], 1.0))
                    dve.wait_ge(counted, 1)
                    link(dve.tensor_copy(tot[:], tot_ps[:]))
                    for e in range(E):
                        ins = dve.tensor_tensor_scan(pre[:, :, e], ones[:], tot[:, :, e], 0.0, ALU.mult, ALU.add)
                        ins.then_inc(step, 1)
                    link.n += E
                    dve.wait_ge(step, link.n)
                    link(tt(pre[:], pre[:], tot[:], ALU.subtract))
                    link(tt(pre[:], pre[:], cnt_ps[:], ALU.add))
                    link(dve.tensor_scalar(pre[:], pre[:], capacity + 0.5, None, ALU.is_lt))
                    m = mask[:].rearrange("p a t e -> p (a t) e")
                    link(tt(pre[:], pre[:], m, ALU.mult))
                    link(tt(rank[:], mask[:, 0], mask[:, 1], ALU.add))
                    chosen = rank
                else:
                    link(dve.tensor_scalar(rank[:], rank[:], top - 0.5, None, ALU.is_lt))
                    chosen = rank
                link(tt(lg[:], pr[:], chosen[:], ALU.mult))
                link(dve.tensor_reduce(row[:, 0, :], lg[:], AX.X, ALU.add))
                link(dve.tensor_scalar(row[:, 0, :], row[:, 0, :], eps, 1.0 / factor, ALU.add, ALU.mult))
                link(dve.reciprocal(row[:, 1, :], row[:, 0, :]))
                if capacity:
                    link(tt(rank[:], pre[:, 0:NT, :], pre[:, NT:2 * NT, :], ALU.add))
                    link(tt(lg[:], pr[:], rank[:], ALU.mult))
                tt(comb[:], lg[:], over(row[:, 1, :], 2, E), ALU.mult).then_inc(comb_ready, 1)
                dve.wait_ge(turned, 1)
                dve.tensor_copy(combT[:], ct_ps[0:E, :]).then_inc(copied, 1)


def experts(k, name, hidden, func, gated, up_bias, down_bias, shared, gate_args):
    nc = k.nc
    HC = hidden // P
    PER = HC * 2
    UP = 2 if gated else 1
    R = 4 // UP
    LAG = R // 2
    layernorm(k, k.xT, k.xn, 1e-5)
    with nc.sbuf_tensor(f"{name}_combT", [E, N], F32) as combT:
        gate(k, name, combT, **gate_args)
        with k.stage("moe", "landed0", "landed1", "shared_landed", "up_done", "activated", "scaled",
                     "down_done", "closed", "weighed") as (
                sb, ps, landed0, landed1, shared_landed, up_done, activated, scaled, down_done, closed,
                weighed):
            landed = (landed0, landed1)
            wu = sb("wu", [P, 2, UP * CD, hidden])
            wd = sb("wd", [P, 2, HC, D])
            bu = sb("bu", [P, 2, HC])
            cb = sb("cb", [P, 2, N])
            bd = sb("bd", [E, D])
            bs = sb("bs", [P, CD])
            h = sb("h", [P, R, HALF])
            hs = sb("hs", [P, R, HALF])
            up_ps = ps("up_ps", [P, R, UP, HALF])
            y_ps = ps("y_ps", [P, 4, HALF])
            per_load = 16 * (3 + up_bias)
            early = 16 * down_bias * (1 + shared)
            late = early + 16 * (2 + up_bias)
            PAIR = [(s, j) for s in range(2) for j in range(PER)]
            LONE = PAIR[:PER]

            with nc.Block() as block:
                def load(sp, e, s):
                    sp.dma_start(wu[:, s], k.dram[name + "_up"][e]).then_inc(landed[s], 16)
                    sp.dma_start(wd[:, s], k.dram[name + "_down"][e]).then_inc(landed[s], 16)
                    if up_bias:
                        sp.dma_start(bu[:, s], k.dram[name + "_upb"][e]).then_inc(landed[s], 16)
                    sp.dma_start(cb[:, s], k.comb[e].partition_broadcast(P)).then_inc(landed[s], 16)

                @block.sync
                def _(sp):
                    if down_bias:
                        sp.dma_start(bd[:], k.dram[name + "_downb"]).then_inc(shared_landed, 16)
                    if shared and down_bias:
                        sp.dma_start(bs[:], k.dram[name + "_sdownb"]).then_inc(shared_landed, 16)
                    load(sp, 0, 0)
                    load(sp, 1, 1)
                    with sp.Fori(1, E // 2) as i:
                        for s in range(2):
                            sp.wait_ge(down_done, (i * 2 + (s - 1)) * PER)
                            load(sp, i * 2 + s, s)
                    if shared:
                        sp.wait_ge(down_done, (E - 1) * PER)
                        sp.dma_start(wu[:, 0], k.dram[name + "_sup"]).then_inc(shared_landed, 16)
                        sp.dma_start(wd[:, 0], k.dram[name + "_sdown"]).then_inc(shared_landed, 16)
                        if up_bias:
                            sp.dma_start(bu[:, 0], k.dram[name + "_supb"]).then_inc(shared_landed, 16)

                @block.tensor
                def _(pe):
                    for u in range(4):
                        pe.matmul(y_ps[:, u, :], k.ident[:], k.xT[:, u // 2, bass.ts(u % 2, HALF)],
                                  start=True, stop=False)

                    def up(first, q, s, j):
                        pe.wait_ge(scaled, first + (q + 1))
                        for g in range(UP):
                            for c in range(CD):
                                mm = pe.matmul(up_ps[:, q % R, g, :], wu[:, s, g * CD + c, bass.ts(j // 2, P)],
                                               k.xn[:, c, bass.ts(j % 2, HALF)], start=c == 0, stop=c == CD - 1)
                        mm.then_inc(up_done, 1)

                    def down(first, q, s, j, last):
                        pe.wait_ge(scaled, first + (q + 1 + R))
                        for m in range(CD):
                            mm = pe.matmul(y_ps[:, 2 * m + j % 2, :], wd[:, s, j // 2, bass.ts(m, P)],
                                           hs[:, q % R, :], start=False, stop=last and j // 2 == HC - 1)
                        mm.then_inc(down_done, 1)

                    def run(items, first, arrive, last=False):
                        for q in range(len(items) + LAG):
                            if q < len(items):
                                s, j = items[q]
                                if j == 0:
                                    arrive(s)
                                up(first, q, s, j)
                            if q >= LAG:
                                down(first, q - LAG, *items[q - LAG], last)

                    with pe.Fori(0, E // 2) as i:
                        run(PAIR, i * (2 * PER), lambda s: pe.wait_ge(landed[s], i * per_load + per_load))
                    if shared:
                        run(LONE, E * PER, lambda s: pe.wait_ge(shared_landed, late), last=not down_bias)
                    if down_bias:
                        pe.wait_ge(shared_landed, early)
                        for u in range(4):
                            mm = pe.matmul(y_ps[:, u, :], bd[:, bass.ts(u // 2, P)],
                                           combT[:, bass.ts(u % 2, HALF)], start=False, stop=True)
                        mm.then_inc(closed, 1)

                @block.scalar
                def _(act):
                    act.sem_inc(scaled, R)

                    def run(items, first, arrive):
                        for q, (s, j) in enumerate(items):
                            if j == 0:
                                arrive(s)
                            act.wait_ge(up_done, first + (q + 1))
                            act.activation(h[:, q % R, :], up_ps[:, q % R, 0, :], func,
                                           bias=bu[:, s, j // 2:j // 2 + 1] if up_bias else 0.0
                                           ).then_inc(activated, 1)

                    with act.Fori(0, E // 2) as i:
                        run(PAIR, i * (2 * PER), lambda s: act.wait_ge(landed[s], i * per_load + per_load))
                    if shared:
                        run(LONE, E * PER, lambda s: act.wait_ge(shared_landed, late))
                    if down_bias:
                        act.wait_ge(closed, 1)
                    else:
                        act.wait_ge(down_done, (E + 1) * PER)
                    for u in range(4):
                        x = k.xT[:, u // 2, bass.ts(u % 2, HALF)]
                        if shared and down_bias:
                            act.activation(x, y_ps[:, u, :], ACT.Identity, bias=bs[:, u // 2:u // 2 + 1])
                        else:
                            act.copy(x, y_ps[:, u, :])

                @block.vector
                def _(dve):
                    def run(items, first, weighted):
                        for q, (s, j) in enumerate(items):
                            if j == 0:
                                weighted(s)
                            w = cb[:, s, bass.ts(j % 2, HALF)]
                            hq, hsq = h[:, q % R, :], hs[:, q % R, :]
                            dve.wait_ge(activated, first + (q + 1))
                            if gated:
                                dve.tensor_tensor(hq, hq, w, ALU.mult).then_inc(weighed, 1)
                                dve.wait_ge(weighed, first + (q + 1))
                                dve.tensor_tensor(hsq, hq, up_ps[:, q % R, 1, :], ALU.mult).then_inc(scaled, 1)
                            else:
                                dve.tensor_tensor(hsq, hq, w, ALU.mult).then_inc(scaled, 1)

                    with dve.Fori(0, E // 2) as i:
                        run(PAIR, i * (2 * PER), lambda s: dve.wait_ge(landed[s], i * per_load + per_load))
                    if shared:
                        for q in range(PER):
                            dve.wait_ge(activated, E * PER + q + 1)
                            if gated:
                                dve.tensor_tensor(hs[:, q % R, :], h[:, q % R, :], up_ps[:, q % R, 1, :],
                                                  ALU.mult).then_inc(scaled, 1)
                            else:
                                dve.tensor_copy(hs[:, q % R, :], h[:, q % R, :]).then_inc(scaled, 1)



def prefetch(k, *pairs):
    nc = k.nc
    k.due += 16 * len(pairs)
    with nc.Block() as block:
        @block.sync
        def _(sp):
            for to, of in pairs:
                sp.dma_start(to, of).then_inc(k.weights, 16)


def project(k, src, weights, chunks_in, tiles, drain):
    nc = k.nc
    RING = 4
    items = [(m, n) for m in range(tiles) for n in range(2)]
    with k.stage("proj", "ready", "taken") as (sb, ps, ready, taken):
        bank = ps("bank", [P, RING, HALF])
        with nc.Block() as block:
            @block.tensor
            def _(pe):
                pe.wait_ge(k.weights, k.due)
                for q, (m, n) in enumerate(items):
                    if q >= RING:
                        pe.wait_ge(taken, q - RING + 1)
                    for c in range(chunks_in):
                        mm = pe.matmul(bank[:, q % RING, :], weights[:, c, bass.ts(m, P)],
                                       src[:, c, bass.ts(n, HALF)], start=c == 0, stop=c == chunks_in - 1)
                    mm.then_inc(ready, 1)

            @block.scalar
            def _(act):
                act.wait_ge(k.weights, k.due)
                for q, (m, n) in enumerate(items):
                    act.wait_ge(ready, q + 1)
                    drain(act, m, n, bank[:, q % RING, :]).then_inc(taken, 1)


def add_projection(k, src, weights, chunks_in, more=None, bias=None):
    nc = k.nc
    with k.stage("out", "summed", "added") as (sb, ps, summed, added):
        y_ps = ps("y_ps", [P, 4, HALF])
        with nc.Block() as block:
            @block.tensor
            def _(pe):
                pe.wait_ge(k.weights, k.due)
                for u in range(CD * 2):
                    m, n = u // 2, u % 2
                    for c in range(chunks_in):
                        mm = pe.matmul(y_ps[:, u, :], weights[:, c, bass.ts(m, P)], src[:, c, bass.ts(n, HALF)],
                                       start=c == 0, stop=c == chunks_in - 1)
                    mm.then_inc(summed, 1)

            @block.vector
            def _(dve):
                dve.wait_ge(k.weights, k.due)
                for c in range(CD):
                    if more is not None:
                        dve.tensor_tensor(k.xT[:, c, :], k.xT[:, c, :], more[:, c, :], ALU.add).then_inc(added, 1)
                for u in range(CD * 2):
                    m, n = u // 2, u % 2
                    x = k.xT[:, m, bass.ts(n, HALF)]
                    if more is not None:
                        dve.wait_ge(added, m + 1)
                    dve.wait_ge(summed, u + 1)
                    dve.scalar_tensor_tensor(x, y_ps[:, u, :], bias[:, m:m + 1] if bias is not None else 0.0, x,
                                             ALU.add, ALU.add)


def by_batch(ap):
    return ap.rearrange("p (b t) -> p b t", t=T)


def causal_conv(k, raw, out, w, b, chunks_in):
    nc = k.nc
    with k.stage("conv", "tapped", "convolved") as (sb, ps, tapped, convolved):
        acc = sb("acc", [P, chunks_in, N])
        with nc.Block() as block:
            @block.vector
            def _(dve):
                dve.wait_ge(k.weights, k.due)
                for c in range(chunks_in):
                    dve.tensor_scalar(acc[:, c, :], raw[:, c, :], w[:, c, 3:4], b[:, c:c + 1],
                                      ALU.mult, ALU.add).then_inc(tapped, 1)
                for s in range(1, 4):
                    for c in range(chunks_in):
                        a, r = by_batch(acc[:, c, :]), by_batch(raw[:, c, :])
                        dve.wait_ge(tapped, (s - 1) * chunks_in + c + 1)
                        dve.scalar_tensor_tensor(a[:, :, s:], r[:, :, 0:T - s], w[:, c, 3 - s:4 - s], a[:, :, s:],
                                                 ALU.mult, ALU.add).then_inc(tapped, 1)

            @block.scalar
            def _(act):
                for c in range(chunks_in):
                    act.wait_ge(tapped, 3 * chunks_in + c + 1)
                    act.activation(out[:, c, :], acc[:, c, :], ACT.Silu)


def multiply(k, out, a, b, chunks_in):
    nc = k.nc
    with nc.Block() as block:
        @block.vector
        def _(dve):
            for c in range(chunks_in):
                dve.tensor_tensor(out[:, c, :], a[:, c, :], b[:, c, :], ALU.mult)


def state_space_duality(k):
    nc = k.nc
    H, DI = 8, 512
    IC = DI // P
    layernorm_src = k.xT
    with ExitStack() as ctx:
        keep = lambda n, shape: ctx.enter_context(nc.sbuf_tensor(f"ssd_{n}", shape, F32))
        win = keep("win", [P, CD, 11 * P])
        wout = keep("wout", [P, IC, D])
        cw = keep("cw", [P, 6, 4])
        cb = keep("cb", [P, 6])
        dcol = keep("dcol", [P, IC])
        nw = keep("nw", [P, IC])
        ln = keep("ln", [P, 2, CD])
        dtb = keep("dtb", [H, 2])
        sel = keep("sel", [H, H, P])
        bar = keep("bar", [P, P])
        fresh = keep("fresh", [H, N])
        u = keep("u", [P, CD, N])
        zs = keep("zs", [P, IC, N])
        y = keep("y", [P, IC, N])
        dt = keep("dt", [H, 2, N])
        xc = keep("xc", [P, 6, N])
        d = k.dram
        prefetch(k, (ln[:], d["L0_attn_ln"]), (win[:], d["L0_attn_in"]), (wout[:], d["L0_attn_out"]),
                 (cw[:], d["L0_attn_cw"]), (cb[:], d["L0_attn_cb"]), (dcol[:], d["L0_attn_D"]),
                 (nw[:], d["L0_attn_nw"]), (dtb[:], d["L0_attn_dt"]), (sel[:], d["pick8"]), (bar[:], d["bar"]),
                 (fresh[:], d["fresh"].partition_broadcast(H)))
        layernorm(k, layernorm_src, k.xn, 1e-5)
        layernorm(k, k.xn, u, 1e-5, affine=(ln[:, 0, :], ln[:, 1, :]))
        with nc.sbuf_tensor("ssd_raw", [P, 6, N], F32) as raw:
            def drain(act, m, n, bank):
                if m < IC:
                    return act.activation(zs[:, m, bass.ts(n, HALF)], bank, ACT.Silu)
                if m < IC + 6:
                    return act.copy(raw[:, m - IC, bass.ts(n, HALF)], bank)
                return act.activation(dt[:, 0, bass.ts(n, HALF)], bank[0:H, :], ACT.Identity, bias=dtb[:, 0:1])
            project(k, u, win, CD, 11, drain)
            causal_conv(k, raw, xc, cw, cb, 6)

        softplus(k, dt[:, 0:1], 1, rows=H)
        with k.stage("dt", "a_ready", "step") as (sb, ps, a_ready, step):
            t2 = sb("t2", [H, N])
            na = sb("na", [H, 1])
            with nc.Block() as block:
                @block.scalar
                def _(act):
                    act.activation(na[:], dtb[:, 1:2], ACT.Exp).then_inc(a_ready, 1)

                @block.vector
                def _(dve):
                    link = Chain(dve, step)
                    dve.wait_ge(a_ready, 1)
                    link(dve.tensor_scalar(t2[:], dt[:, 0, :], na[:, 0:1], -1.0, ALU.mult, ALU.mult))
                    dve.tensor_tensor_scan(dt[:, 1, :], fresh[:], t2[:], 0.0, ALU.mult, ALU.add)

        with k.stage("ssd", "tile_in", "grams", "cums", "cols_ready", "x_turned", "cols_taken", "diffed", "masked",
                     "decayed", "weighed", "x_scaled", "summed", "y_out") as (
                sb, ps, tile_in, grams, cums, cols_ready, x_turned, cols_taken, diffed, masked, decayed, weighed,
                x_scaled, summed, y_out):
            xin = sb("xin", [P, 2, 6, P])
            din = sb("din", [H, 2, 2, P])
            cols = sb("cols", [P, 2, 2 * H])
            dec = sb("dec", [P, 2, H, P])
            xdt = sb("xdt", [P, 2, DI])
            g_ps = ps("g_ps", [P, 2, HALF])
            c_ps = ps("c_ps", [P, H, P])
            x_ps = ps("x_ps", [P, 2, HALF])
            y_ps = ps("y_ps", [P, 2, HALF])
            with nc.Block() as block:
                @block.gpsimd
                def _(pool):
                    def take(t, s):
                        pool.tensor_copy(xin[:, s], xc[:, :, bass.ds(t * P, P)]).then_inc(tile_in, 1)
                        pool.tensor_copy(din[:, s], dt[:, :, bass.ds(t * P, P)]).then_inc(tile_in, 1)
                    take(0, 0)
                    take(1, 1)
                    with pool.Fori(1, NT // 2) as i:
                        for s in range(2):
                            pool.wait_ge(y_out, (i * 2 + (s - 1)) * IC)
                            take(i * 2 + s, s)

                @block.tensor
                def _(pe):
                    def before(t, s):
                        pe.wait_ge(tile_in, t * 2 + 2)
                        pe.matmul(g_ps[:, s, 0:P], xin[:, s, IC, :], xin[:, s, IC + 1, :], start=True, stop=True)
                        pe.transpose(g_ps[:, s, P:P + H], din[:, s, 1, :], k.ident[0:H, 0:H])
                        pe.transpose(g_ps[:, s, P + H:P + 2 * H], din[:, s, 0, :],
                                     k.ident[0:H, 0:H]).then_inc(cols_ready, 1)
                        pe.wait_ge(diffed, t + 1)
                        for h in range(H):
                            mm = pe.matmul(c_ps[:, h, :], sel[:, h, :], din[:, s, 1, :], start=True, stop=True)
                        mm.then_inc(cums, 1)
                        for c in range(IC):
                            mm = pe.transpose(x_ps[:, s, bass.ts(c, P)], xin[:, s, c, :], k.ident[:])
                        mm.then_inc(x_turned, 1)

                    def after(t, s):
                        pe.wait_ge(weighed, t + 1)
                        pe.wait_ge(x_scaled, t + 1)
                        for h in range(H):
                            r = slice((h % 2) * 64, (h % 2) * 64 + 64)
                            mm = pe.matmul(y_ps[r, s, bass.ts(h // 2, P)], xdt[:, s, bass.ts(h, 64)],
                                           dec[:, s, h, :], start=True, stop=True)
                        mm.then_inc(summed, 1)

                    with pe.Fori(0, NT // 2) as i:
                        before(i * 2, 0)
                        before(i * 2 + 1, 1)
                        after(i * 2, 0)
                        after(i * 2 + 1, 1)

                @block.scalar
                def _(act):
                    with act.Fori(0, NT // 2) as i:
                        for s in range(2):
                            act.wait_ge(masked, i * 2 + (s + 1))
                            act.activation(dec[:, s], dec[:, s], ACT.Exp).then_inc(decayed, 1)

                @block.vector
                def _(dve):
                    dve.sem_inc(diffed, 1)

                    def before(t, s):
                        dve.wait_ge(cols_ready, t + 1)
                        dve.tensor_copy(cols[:, s, :], g_ps[:, s, P:P + 2 * H]).then_inc(cols_taken, 1)
                        dve.wait_ge(cols_taken, t + 1)
                        dve.wait_ge(cums, t + 1)
                        dve.tensor_tensor(dec[:, s], c_ps[:], over(cols[:, s, 0:H], 2, P),
                                          ALU.subtract).then_inc(diffed, 1)
                        dve.wait_ge(x_turned, t + 1)
                        dve.tensor_tensor(xdt[:, s, :].rearrange("p (h q) -> p h q", h=H),
                                          x_ps[:, s, :].rearrange("p (h q) -> p h q", h=H),
                                          over(cols[:, s, H:2 * H], 2, 64), ALU.mult).then_inc(x_scaled, 1)
                        dve.wait_ge(diffed, t + 2)
                        dve.tensor_tensor(dec[:, s], dec[:, s], over(bar[:], 1, H), ALU.add).then_inc(masked, 1)

                    def after(t, s):
                        dve.wait_ge(decayed, t + 1)
                        dve.tensor_tensor(dec[:, s], dec[:, s], over(g_ps[:, s, 0:P], 1, H),
                                          ALU.mult).then_inc(weighed, 1)

                    def last(t, s):
                        dve.wait_ge(summed, t + 1)
                        for c in range(IC):
                            dve.scalar_tensor_tensor(y[:, c, bass.ds(t * P, P)], xin[:, s, c, :], dcol[:, c:c + 1],
                                                     y_ps[:, s, bass.ts(c, P)], ALU.mult, ALU.add
                                                     ).then_inc(y_out, 1)

                    with dve.Fori(0, NT // 2) as i:
                        for step_ in (before, after, last):
                            step_(i * 2, 0)
                            step_(i * 2 + 1, 1)
        multiply(k, y, y, zs, IC)
        layernorm(k, y, y, 1e-5, affine=(nw, None), centre=False, width=IC)
        add_projection(k, y, wout, IC, more=k.xn)


def long_convolution(k):
    nc = k.nc
    DI, NS = 512, 16
    IC = DI // P
    PAD = 3
    with ExitStack() as ctx:
        keep = lambda n, shape: ctx.enter_context(nc.sbuf_tensor(f"lc_{n}", shape, F32))
        win = keep("win", [P, CD, 2 * DI])
        wconv = keep("wconv", [P, IC, 4, DI])
        wout = keep("wout", [P, IC, D])
        nw = keep("nw", [P, CD])
        inb = keep("inb", [P, 2 * IC])
        cvb = keep("cvb", [P, IC])
        outb = keep("outb", [P, CD])
        par = keep("par", [P, 3, IC, NS])
        dts = keep("dts", [P, 2, IC])
        iota = keep("iota", [P, T])
        kern = keep("kern", [P, IC, T])
        gs = keep("gs", [P, IC, N])
        xs = keep("xs", [P, IC, N])
        d = k.dram
        nm = "L1_attn_"
        prefetch(k, (par[:], d[nm + "par"]), (dts[:], d[nm + "dts"]), (iota[:], d["lags"].partition_broadcast(P)),
                 (nw[:], d[nm + "nw"]), (win[:], d[nm + "in"]), (inb[:], d[nm + "inb"]),
                 (wconv[:], d[nm + "conv"]), (cvb[:], d[nm + "cvb"]), (wout[:], d[nm + "out"]),
                 (outb[:], d[nm + "outb"]))
        layernorm(k, k.xT, k.xn, 1e-5)
        with k.stage("kern", "act_in", "act_out", "step") as (sb, ps, act_in, act_out, step):
            a = sb("a", [P, IC, NS])
            x = sb("x", [P, IC, NS])
            th = sb("th", [P, IC, NS])
            sg = sb("sg", [P, IC])
            e = sb("e", [P, IC, T, NS])
            with nc.Block() as block:
                @block.scalar
                def _(act):
                    act.wait_ge(k.weights, k.due)
                    act.activation(a[:], par[:, 0], ACT.Exp)
                    act.activation(sg[:], dts[:, 0], ACT.Sigmoid).then_inc(act_out, 1)
                    act.wait_ge(act_in, 1)
                    act.activation(th[:], x[:], ACT.Tanh, scale=0.5).then_inc(act_out, 1)
                    act.wait_ge(act_in, 2)
                    for c in range(IC):
                        act.activation(e[:, c], e[:, c], ACT.Exp).then_inc(act_out, 1)

                @block.vector
                def _(dve):
                    link = Chain(dve, step)
                    tt = dve.tensor_tensor
                    dve.wait_ge(act_out, 1)
                    link(dve.tensor_scalar(a[:], a[:], -1.0, None, ALU.mult))
                    tt(x[:], a[:], over(sg[:], 2, NS), ALU.mult).then_inc(act_in, 1)
                    dve.wait_ge(act_in, 1)
                    for c in range(IC):
                        ins = tt(e[:, c], over(x[:, c], 1, T), over(iota[:], 2, NS), ALU.mult)
                    ins.then_inc(act_in, 1)
                    dve.wait_ge(act_out, 2)
                    dve.wait_ge(act_in, 2)
                    link(dve.tensor_scalar(x[:], th[:], -1.0, 1.0, ALU.mult, ALU.add))
                    link(dve.tensor_scalar(a[:], a[:], 1e-8, None, ALU.add))
                    link(tt(x[:], x[:], a[:], ALU.mult))
                    link(dve.reciprocal(a[:], x[:]))
                    link(tt(th[:], th[:], par[:, 1], ALU.mult))
                    link(tt(th[:], th[:], par[:, 2], ALU.mult))
                    link(dve.scalar_tensor_tensor(th[:], th[:], 2.0, a[:], ALU.mult, ALU.mult))
                    for c in range(IC):
                        dve.wait_ge(act_out, 3 + c)
                        link(tt(e[:, c], e[:, c], over(th[:, c], 1, T), ALU.mult))
                        link(dve.tensor_reduce(kern[:, c, :], e[:, c], AX.X, ALU.add))
                    dve.tensor_tensor(kern[:, :, 0:1], kern[:, :, 0:1], over(dts[:, 1], 2, 1), ALU.add)
        with nc.sbuf_tensor("lc_pad", [P, IC, B * (T + PAD)], F32) as pad:
            padded = pad[:].rearrange("p c (b t) -> p c b t", t=T + PAD)
            with nc.sbuf_tensor("lc_u", [P, CD, N], F32) as u:
                with nc.Block() as block:
                    @block.gpsimd
                    def _(pool):
                        pool.memset(pad[:], 0.0)
                layernorm(k, k.xn, u, 1e-6, affine=(nw, None), centre=False)

                def drain(act, m, n, bank):
                    if m < IC:
                        to = padded[:, m, n * B // 2:(n + 1) * B // 2, PAD:]
                        return act.activation(to, by_batch(bank), ACT.Identity, bias=inb[:, m:m + 1])
                    return act.activation(gs[:, m - IC, bass.ts(n, HALF)], bank, ACT.Silu, bias=inb[:, m:m + 1])
                project(k, u, win, CD, 2 * IC, drain)
            with k.stage("fullconv", "ready", "taken") as (sb, ps, ready, taken):
                bank = ps("bank", [P, 4, HALF])
                items = [(m, n) for m in range(IC) for n in range(2)]
                with nc.Block() as block:
                    @block.tensor
                    def _(pe):
                        for q, (m, n) in enumerate(items):
                            if q >= 4:
                                pe.wait_ge(taken, q - 3)
                            for c in range(IC):
                                for tap in range(4):
                                    mm = pe.matmul(bank[:, q % 4, :], wconv[:, c, tap, bass.ts(m, P)],
                                                   padded[:, c, n * B // 2:(n + 1) * B // 2, tap:tap + T],
                                                   start=c + tap == 0, stop=c == IC - 1 and tap == 3)
                            mm.then_inc(ready, 1)

                    @block.scalar
                    def _(act):
                        for q, (m, n) in enumerate(items):
                            act.wait_ge(ready, q + 1)
                            act.activation(xs[:, m, bass.ts(n, HALF)], bank[:, q % 4, :], ACT.Silu,
                                           bias=cvb[:, m:m + 1]).then_inc(taken, 1)
        with nc.sbuf_tensor("lc_y", [P, IC, N], F32) as y:
            with k.stage("lags", "lagged") as (sb, ps, lagged):
                with nc.Block() as block:
                    @block.vector
                    def _(dve):
                        for c in range(IC):
                            dve.tensor_scalar(y[:, c, :], xs[:, c, :], kern[:, c, 0:1], None,
                                              ALU.mult).then_inc(lagged, 1)
                        for lag in range(1, T):
                            for c in range(IC):
                                a, r = by_batch(y[:, c, :]), by_batch(xs[:, c, :])
                                dve.wait_ge(lagged, (lag - 1) * IC + c + 1)
                                dve.scalar_tensor_tensor(a[:, :, lag:], r[:, :, 0:T - lag], kern[:, c, lag:lag + 1],
                                                         a[:, :, lag:], ALU.mult, ALU.add).then_inc(lagged, 1)
            multiply(k, y, y, gs, IC)
            add_projection(k, y, wout, IC, more=k.xn, bias=outb)



def softplus(k, v, parts, rows=P):
    nc = k.nc
    with k.stage("softplus", "absed", "exped", "shifted", "logged", "topped", "lost") as (
            sb, ps, absed, exped, shifted, logged, topped, lost):
        e = sb("e", [rows, parts, N])
        w = sb("w", [rows, parts, N])
        with nc.Block() as block:
            @block.scalar
            def _(act):
                for c in range(parts):
                    act.wait_ge(absed, c + 1)
                    act.activation(e[:, c, :], e[:, c, :], ACT.Exp, scale=-1.0).then_inc(exped, 1)
                for c in range(parts):
                    act.wait_ge(lost, c + 1)
                    act.activation(w[:, c, :], w[:, c, :], ACT.Ln).then_inc(logged, 1)

            @block.vector
            def _(dve):
                for c in range(parts):
                    dve.tensor_scalar(w[:, c, :], v[:, c, :], 0.0, None, ALU.max).then_inc(topped, 1)
                for c in range(parts):
                    dve.wait_ge(topped, c + 1)
                    dve.scalar_tensor_tensor(e[:, c, :], w[:, c, :], 2.0, v[:, c, :], ALU.mult,
                                             ALU.subtract).then_inc(absed, 1)
                for c in range(parts):
                    dve.wait_ge(absed, c + 1)
                    dve.tensor_copy(v[:, c, :], w[:, c, :]).then_inc(topped, 1)
                for c in range(parts):
                    dve.wait_ge(exped, c + 1)
                    dve.wait_ge(topped, parts + c + 1)
                    dve.tensor_scalar(w[:, c, :], e[:, c, :], 1.0, None, ALU.add).then_inc(shifted, 1)
                for c in range(parts):
                    dve.wait_ge(shifted, c + 1)
                    dve.scalar_tensor_tensor(e[:, c, :], w[:, c, :], -1.0, e[:, c, :], ALU.add,
                                             ALU.subtract).then_inc(lost, 1)
                for c in range(parts):
                    dve.wait_ge(lost, c + 1)
                    dve.tensor_tensor(v[:, c, :], v[:, c, :], e[:, c, :], ALU.subtract).then_inc(shifted, 1)
                for c in range(parts):
                    dve.wait_ge(logged, c + 1)
                    dve.wait_ge(shifted, parts + c + 1)
                    dve.tensor_tensor(v[:, c, :], v[:, c, :], w[:, c, :], ALU.add)


def selective_scan(k):
    nc = k.nc
    DI, NS = 512, 16
    IC = DI // P
    HB = B // 2
    nm, d = "L2_attn_", k.dram
    with ExitStack() as ctx:
        keep = lambda n, shape: ctx.enter_context(nc.sbuf_tensor(f"scan_{n}", shape, F32))
        wout = keep("wout", [P, IC, D])
        nw = keep("nw", [P, IC])
        dcol = keep("dcol", [P, IC])
        alog = keep("alog", [P, IC * NS])
        zs = keep("zs", [P, IC, N])
        xc = keep("xc", [P, IC, N])
        delta = keep("delta", [P, IC, N])
        with ExitStack() as early:
            brief = lambda n, shape: early.enter_context(nc.sbuf_tensor(f"scan_{n}", shape, F32))
            win = brief("win", [P, CD, 2 * DI])
            wx = brief("wx", [P, IC, P])
            wdt = brief("wdt", [NS, 1, DI])
            cw = brief("cw", [P, IC, 4])
            cb = brief("cb", [P, IC])
            dtb = brief("dtb", [P, IC])
            raw = brief("raw", [P, IC, N])
            xd = brief("xd", [3 * NS, 1, N])
            prefetch(k, (win[:], d[nm + "in"]), (cw[:], d[nm + "cw"]), (cb[:], d[nm + "cb"]), (wx[:], d[nm + "x"]),
                     (wdt[:, 0, :], d[nm + "wdt"]), (dtb[:], d[nm + "dtb"]), (alog[:], d[nm + "A"]),
                     (dcol[:], d[nm + "D"]), (nw[:], d[nm + "nw"]), (wout[:], d[nm + "out"]))
            layernorm(k, k.xT, k.xn, 1e-5)

            def drain(act, m, n, bank):
                if m < IC:
                    return act.copy(raw[:, m, bass.ts(n, HALF)], bank)
                return act.activation(zs[:, m - IC, bass.ts(n, HALF)], bank, ACT.Silu)
            project(k, k.xn, win, CD, 2 * IC, drain)
            causal_conv(k, raw, xc, cw, cb, IC)
            project(k, xc, wx, IC, 1, lambda act, m, n, bank: act.copy(xd[:, 0, bass.ts(n, HALF)], bank[0:3 * NS, :]))
            with k.stage("bc", "stored") as (sb, ps, stored):
                with nc.Block() as block:
                    @block.sync
                    def _(sp):
                        sp.dma_start(k.bc, xd[NS:3 * NS, 0, :]).then_inc(stored, 16)
                        sp.wait_ge(stored, 16)
            project(k, xd[0:NS], wdt, 1, IC,
                    lambda act, m, n, bank: act.activation(delta[:, m, bass.ts(n, HALF)], bank, ACT.Identity,
                                                           bias=dtb[:, m:m + 1]))
        softplus(k, delta, IC)
        y = keep("y", [P, IC, N])
        with k.stage("scan", "rows_landed", "a_ready", "in_taken", "decay_out", "decay_ready", "drive_ready",
                     "scanned", "read_out", "summed", "y_out", "a_exped", "zeroed") as (
                sb, ps, rows_landed, a_ready, in_taken, decay_out, decay_ready, drive_ready, scanned, read_out,
                summed, y_out, a_exped, zeroed):
            RING = 4
            none = sb("none", [P, HB])
            bb = sb("bb", [P, NS, HALF])
            cc = sb("cc", [P, NS, HALF])
            av = sb("av", [P, IC * NS])
            dl = sb("dl", [P, HALF])
            ut = sb("ut", [P, HALF])
            ac = sb("ac", [P, NS])
            da = sb("da", [P, RING, HALF])
            db = sb("db", [P, RING, HALF])
            hh = sb("hh", [P, RING, HALF])
            hc = sb("hc", [P, RING, HALF])
            y_ps = ps("y_ps", [P, HALF])
            with nc.Block() as block:
                @block.sync
                def _(sp):
                    for g in range(2):
                        for n in range(NS):
                            if g:
                                sp.wait_ge(read_out, (IC - 1) * NS + n + 1 + RING)
                            for to, r in ((bb, n), (cc, NS + n)):
                                sp.dma_start(to[:, n, :], k.bc[r, bass.ts(g, HALF)].partition_broadcast(P)
                                             ).then_inc(rows_landed, 16)

                @block.scalar
                def _(act):
                    act.activation(av[:], alog[:], ACT.Exp).then_inc(a_exped, 1)
                    for g in range(2):
                        with act.Fori(0, IC) as c:
                            it = c + g * IC
                            act.wait_ge(in_taken, it * 3 + 3)
                            for n in range(NS):
                                q = it * NS + n
                                act.wait_ge(scanned, q + 1)
                                act.activation(da[:, n % RING, :], dl[:], ACT.Exp,
                                               scale=ac[:, n:n + 1]).then_inc(decay_out, 1)

                @block.gpsimd
                def _(pool):
                    pool.memset(none[:], 0.0).then_inc(zeroed, 1)
                    pool.wait_ge(zeroed, 1)
                    for g in range(2):
                        pool.wait_ge(rows_landed, (g + 1) * 2 * NS * 16)
                        with pool.Fori(0, IC) as c:
                            it = c + g * IC
                            pool.wait_ge(in_taken, it * 3 + 3)
                            for n in range(NS):
                                q = it * NS + n
                                pool.wait_ge(scanned, q + 1)
                                pool.tensor_tensor(db[:, n % RING, :], ut[:], bb[:, n, :],
                                                   ALU.mult).then_inc(drive_ready, 1)
                                pool.wait_ge(decay_out, q + 1)
                                pool.tensor_tensor(by_batch(da[:, n % RING, :])[:, :, 0], none[:], none[:],
                                                   ALU.mult).then_inc(decay_ready, 1)

                @block.vector
                def _(dve):
                    dve.sem_inc(scanned, RING)
                    dve.sem_inc(summed, RING)
                    dve.sem_inc(read_out, RING)
                    dve.wait_ge(a_exped, 1)
                    dve.tensor_scalar(av[:], av[:], -1.0, None, ALU.mult).then_inc(a_ready, 1)
                    dve.wait_ge(a_ready, 1)
                    for g in range(2):
                        dve.wait_ge(rows_landed, (g + 1) * 2 * NS * 16)
                        with dve.Fori(0, IC) as c:
                            it = c + g * IC
                            half = bass.ds(c * N + g * HALF, HALF)
                            flat = lambda t: t[:].rearrange("p c n -> p (c n)")[:, half]
                            dve.tensor_copy(dl[:], flat(delta)).then_inc(in_taken, 1)
                            dve.tensor_tensor(ut[:], flat(delta), flat(xc), ALU.mult).then_inc(in_taken, 1)
                            dve.tensor_copy(ac[:], av[:, bass.ds(c * NS, NS)]).then_inc(in_taken, 1)

                            def read(n):
                                q = it * NS + n
                                dve.wait_ge(scanned, q + 1 + RING)
                                dve.wait_ge(summed, q + 1)
                                dve.tensor_tensor(hc[:, n % RING, :], hh[:, n % RING, :], cc[:, n, :],
                                                  ALU.mult).then_inc(read_out, 1)

                            for n in range(NS):
                                q = it * NS + n
                                dve.wait_ge(decay_ready, q + 1)
                                dve.wait_ge(read_out, q + 1)
                                dve.wait_ge(drive_ready, q + 1)
                                dve.tensor_tensor_scan(hh[:, n % RING, :], da[:, n % RING, :], db[:, n % RING, :],
                                                       0.0, ALU.mult, ALU.add).then_inc(scanned, 1)
                                if n >= 1:
                                    read(n - 1)
                            read(NS - 1)
                            dve.wait_ge(summed, it * NS + NS + RING)
                            dve.tensor_copy(flat(y), y_ps[:]).then_inc(y_out, 1)

                @block.tensor
                def _(pe):
                    for g in range(2):
                        with pe.Fori(0, IC) as c:
                            it = c + g * IC
                            for n in range(NS):
                                pe.wait_ge(read_out, it * NS + (n + 1 + RING))
                                if n == 0:
                                    pe.wait_ge(y_out, it)
                                pe.matmul(y_ps[:], k.ident[:], hc[:, n % RING, :], start=n == 0,
                                          stop=n == NS - 1).then_inc(summed, 1)
        with k.stage("skip", "skipped") as (sb, ps, skipped):
            with nc.Block() as block:
                @block.vector
                def _(dve):
                    for c in range(IC):
                        dve.scalar_tensor_tensor(y[:, c, :], xc[:, c, :], dcol[:, c:c + 1], y[:, c, :], ALU.mult,
                                                 ALU.add).then_inc(skipped, 1)
                    for c in range(IC):
                        dve.wait_ge(skipped, c + 1)
                        dve.tensor_tensor(y[:, c, :], y[:, c, :], zs[:, c, :], ALU.mult)
        layernorm(k, y, y, 1e-8, affine=(nw, None), centre=False, width=IC)
        add_projection(k, y, wout, IC)



def correlation_attention(k):
    nc = k.nc
    heads, dk, slot = 16, 16, 32
    per, IC = P // slot, HALF // P
    nm, d = "L3_attn_", k.dram
    with ExitStack() as ctx:
        keep = lambda n, shape: ctx.enter_context(nc.sbuf_tensor(f"corr_{n}", shape, F32))
        wqk = keep("wqk", [P, CD, 2 * HALF])
        wv = keep("wv", [P, CD, HALF])
        wo = keep("wo", [P, IC, D])
        vmat = keep("vmat", [P, P])
        qk = keep("qk", [P, 2 * IC, N])
        oT = keep("oT", [P, IC, N])
        prefetch(k, (wqk[:], d[nm + "Wqk"]), (vmat[:], d["slotvar"]), (wv[:], d[nm + "Wv"]), (wo[:], d[nm + "Wo"]))
        layernorm(k, k.xT, k.xn, 1e-5)
        with k.stage("centre", "step") as (sb, ps, step):
            mean = sb("mean", [P, CD * 2 * heads])
            with nc.Block() as block:
                @block.vector
                def _(dve):
                    link = Chain(dve, step)
                    dve.wait_ge(k.weights, k.due)
                    w = wqk[:].rearrange("p c (h r) -> p (c h) r", r=slot)[:, :, 0:dk]
                    link(dve.tensor_reduce(mean[:], w, AX.X, ALU.add))
                    link(dve.tensor_scalar(mean[:], mean[:], 1.0 / dk, None, ALU.mult))
                    dve.tensor_tensor(w, w, over(mean[:], 2, dk), ALU.subtract)
        with k.stage("qk", "ready", "squared", "var_ready", "copied", "added") as (
                sb, ps, ready, squared, var_ready, copied, added):
            sq = sb("sq", [P, 2, HALF])
            bank = ps("bank", [P, 2, HALF])
            vbank = ps("vbank", [P, 2, HALF])
            items = [(m, n) for m in range(2 * IC) for n in range(2)]
            with nc.Block() as block:
                @block.tensor
                def _(pe):
                    for q in range(len(items) + 1):
                        if q < len(items):
                            m, n = items[q]
                            if q >= 2:
                                pe.wait_ge(squared, q - 1)
                            for c in range(CD):
                                mm = pe.matmul(bank[:, q % 2, :], wqk[:, c, bass.ts(m, P)],
                                               k.xn[:, c, bass.ts(n, HALF)], start=c == 0, stop=c == CD - 1)
                            mm.then_inc(ready, 1)
                        if q >= 1:
                            if q >= 3:
                                pe.wait_ge(added, q - 2)
                            pe.wait_ge(squared, q)
                            pe.matmul(vbank[:, (q - 1) % 2, :], vmat[:], sq[:, (q - 1) % 2, :], start=True,
                                      stop=True).then_inc(var_ready, 1)

                @block.scalar
                def _(act):
                    for q, (m, n) in enumerate(items):
                        act.wait_ge(ready, q + 1)
                        act.copy(qk[:, m, bass.ts(n, HALF)], bank[:, q % 2, :]).then_inc(copied, 1)
                        if q >= 2:
                            act.wait_ge(var_ready, q - 1)
                        act.activation(sq[:, q % 2, :], bank[:, q % 2, :], ACT.Square).then_inc(squared, 1)

                @block.vector
                def _(dve):
                    for q, (m, n) in enumerate(items):
                        x = qk[:, m, bass.ts(n, HALF)]
                        dve.wait_ge(copied, q + 1)
                        dve.wait_ge(var_ready, q + 1)
                        dve.tensor_tensor(x, x, vbank[:, q % 2, :], ALU.add).then_inc(added, 1)

        with k.stage("corr", "zeroed", "batch_in", "v_ready", "v_taken", "scored", "shifted", "exped", "normed",
                     "turned", "turned_v", "mixed", "out_taken", "step") as (
                sb, ps, zeroed, batch_in, v_ready, v_taken, scored, shifted, exped, normed, turned, turned_v,
                mixed, out_taken, step):
            W = per * T
            xb = sb("xb", [P, 2, CD, 2, T])
            qblk = sb("qblk", [P, 2, IC, W])
            vb = sb("vb", [P, 2, HALF])
            sm = sb("sm", [P, 2, 2 * IC, T])
            row = sb("row", [P, 2, 3, 2 * IC])
            pT = sb("pT", [P, IC, P])
            s_ps = ps("s_ps", [P, 2, 2 * IC, T])
            v_ps = ps("v_ps", [P, HALF])
            t_ps = ps("t_ps", [P, IC, P])
            o_ps = ps("o_ps", [P, 2, IC, P])
            with nc.Block() as block:
                @block.gpsimd
                def _(pool):
                    pool.memset(qblk[:], 0.0).then_inc(zeroed, 1)
                    pool.wait_ge(zeroed, 1)

                    def take(b, s):
                        if not (isinstance(b, int) and b == 0):
                            pool.wait_ge(batch_in, b * (per + 1))
                        pool.tensor_copy(xb[:, s], over(k.xn[:, :, bass.ds(b * T, T)], 2, 2)).then_inc(batch_in, 1)
                        pool.wait_ge(batch_in, b * (per + 1) + 1)
                        for g in range(per):
                            r = slice(g * slot, (g + 1) * slot)
                            pool.tensor_copy(qblk[r, s, :, bass.ts(g, T)],
                                             qk[r, 0:IC, bass.ds(b * T, T)]).then_inc(batch_in, 1)
                    take(0, 0)
                    take(1, 1)
                    with pool.Fori(1, B // 2) as i:
                        for s in range(2):
                            pool.wait_ge(scored, i * 2 + (s - 1))
                            take(i * 2 + s, s)

                @block.tensor
                def _(pe):
                    def before(b, s):
                        pe.wait_ge(batch_in, (b + 1) * (per + 1))
                        pe.wait_ge(v_taken, b + 1)
                        for c in range(CD):
                            mm = pe.matmul(v_ps[:], xb[:, s, c].rearrange("p a t -> p (a t)"), wv[:, c, :], start=c == 0, stop=c == CD - 1)
                        mm.then_inc(v_ready, 1)
                        for j in range(2 * IC):
                            mm = pe.matmul(s_ps[:, s, j, :], qblk[:, s, j // 2, bass.ts(j % 2, P)],
                                           qk[:, IC + j // 2, bass.ds(b * T, T)], start=True, stop=True)
                        mm.then_inc(scored, 1)

                    def after(b, s):
                        pe.wait_ge(normed, b + 1)
                        for m in range(IC):
                            mm = pe.transpose(t_ps[:, m, :], sm[:, s, 2 * m:2 * m + 2, :].rearrange(
                                "p a t -> p (a t)"), k.ident[:])
                        mm.then_inc(turned, 1)
                        pe.wait_ge(turned_v, b + 1)
                        pe.wait_ge(out_taken, b + 1)
                        for m in range(IC):
                            for a in range(2):
                                r = slice(a * T, (a + 1) * T)
                                mm = pe.matmul(o_ps[:, a, m, :], vb[r, s, bass.ts(m, P)], pT[r, m, :],
                                               start=True, stop=True)
                        mm.then_inc(mixed, 1)

                    with pe.Fori(0, B // 2) as i:
                        before(i * 2, 0)
                        before(i * 2 + 1, 1)
                        after(i * 2, 0)
                        after(i * 2 + 1, 1)

                @block.scalar
                def _(act):
                    act.sem_inc(v_taken, 1)
                    act.sem_inc(out_taken, 1)

                    with act.Fori(0, B // 2) as i:
                        for s in range(2):
                            b = i * 2 + s
                            act.wait_ge(v_ready, b + 1)
                            act.copy(vb[:, s, :], v_ps[:]).then_inc(v_taken, 1)
                        for s in range(2):
                            b = i * 2 + s
                            act.wait_ge(shifted, b + 1)
                            act.activation(sm[:, s], sm[:, s], ACT.Exp, scale=1.0 / dk).then_inc(exped, 1)
                        for s in range(2):
                            b = i * 2 + s
                            act.wait_ge(mixed, b + 1)
                            for g in range(per):
                                r = slice(g * slot, (g + 1) * slot)
                                cp = act.copy(oT[r, :, bass.ds(b * T, T)], o_ps[r, g // 2, :, bass.ts(g % 2, T)])
                            cp.then_inc(out_taken, 1)

                @block.vector
                def _(dve):
                    def norm(b, s, base):
                        dve.wait_ge(exped, b + 1)
                        dve.tensor_reduce(row[:, s, 1, :], sm[:, s], AX.X, ALU.add).then_inc(step, 1)
                        dve.wait_ge(step, base + 1)
                        dve.reciprocal(row[:, s, 2, :], row[:, s, 1, :]).then_inc(step, 1)
                        dve.wait_ge(step, base + 2)
                        dve.tensor_tensor(sm[:, s], sm[:, s], over(row[:, s, 2, :], 2, T),
                                          ALU.mult).then_inc(normed, 1)

                    with dve.Fori(0, B // 2) as i:
                        for s in range(2):
                            dve.wait_ge(scored, i * 2 + (s + 1))
                            dve.tensor_reduce(row[:, s, 0, :], s_ps[:, s], AX.X, ALU.max).then_inc(step, 1)
                            dve.wait_ge(step, i * 6 + (s + 1))
                            dve.tensor_tensor(sm[:, s], s_ps[:, s], over(row[:, s, 0, :], 2, T),
                                              ALU.subtract).then_inc(shifted, 1)
                        for s in range(2):
                            norm(i * 2 + s, s, i * 6 + (2 + 2 * s))
                        for s in range(2):
                            dve.wait_ge(turned, i * 2 + (s + 1))
                            dve.tensor_copy(pT[:], t_ps[:]).then_inc(turned_v, 1)
        add_projection(k, oT, wo, IC)


def masked_cross_attention(k):
    nc = k.nc
    heads, dk = 4, 64
    IC = heads * dk // P
    NK = S // P
    KEYS = S + T
    KR = DC - P
    nm, d = "L3_xattn_", k.dram
    with ExitStack() as ctx:
        keep = lambda n, shape: ctx.enter_context(nc.sbuf_tensor(f"mx_{n}", shape, F32))
        wq = keep("wq", [P, CD, IC * P])
        wl = keep("wl", [P, CD, 2 * IC * P])
        wc = keep("wc", [P, 2, 2 * IC * P])
        wo = keep("wo", [P, IC, D])
        bo = keep("bo", [P, CD])
        lnl = keep("lnl", [P, 2, CD])
        lnx = keep("lnx", [P, 2, 2])
        qg = keep("qg", [P, 2])
        pair = keep("pair", [P, P])
        lat = keep("lat", [P, CD, N])
        qT = keep("qT", [P, IC, N])
        oT = keep("oT", [P, IC, N])
        prefetch(k, (lnl[:], d[nm + "lnl"]), (lnx[:], d[nm + "lnx"]), (qg[:], d[nm + "qg"]), (pair[:], d["pair"]),
                 (wq[:], d[nm + "Wq"]), (wc[:], d[nm + "Wkv"]), (wl[:], d[nm + "Wlkv"]), (wo[:], d[nm + "Wo"]),
                 (bo[:], d[nm + "bo"]))
        with k.stage("mask", "landed", "cast", "ready", "stored") as (sb, ps, landed, cast, ready, stored):
            m8 = sb("m8", [B, S // 4], mybir.dt.uint32)
            mf = sb("mf", [B, S])
            with nc.Block() as block:
                @block.sync
                def _(sp):
                    sp.dma_start(m8[:], d["mask"]).then_inc(landed, 16)
                    sp.wait_ge(ready, 1)
                    sp.dma_start(k.bar_rows, mf[:]).then_inc(stored, 16)
                    sp.wait_ge(stored, 16)

                @block.vector
                def _(dve):
                    dve.wait_ge(landed, 16)
                    dve.tensor_copy(mf[:], m8[:].bitcast(mybir.dt.uint8)).then_inc(cast, 1)
                    dve.wait_ge(cast, 1)
                    dve.tensor_scalar(mf[:], mf[:], -1.0, 1e30, ALU.add, ALU.mult).then_inc(ready, 1)
        layernorm(k, k.xT, k.xn, 1e-5)
        layernorm(k, k.xn, lat, 1e-5, affine=(lnl[:, 0, :], lnl[:, 1, :]))
        with k.stage("fold", "bias_ready", "step") as (sb, ps, bias_ready, step):
            b_ps = ps("b_ps", [P, 2 * IC * P])
            with nc.Block() as block:
                @block.tensor
                def _(pe):
                    pe.wait_ge(k.weights, k.due)
                    pe.matmul(b_ps[KR:KR + 1, :], lnx[:, 1, 0:1], wc[:, 0, :], start=True, stop=False)
                    pe.matmul(b_ps[KR:KR + 1, :], lnx[0:KR, 1, 1:2], wc[0:KR, 1, :], start=False,
                              stop=True).then_inc(bias_ready, 1)

                @block.vector
                def _(dve):
                    dve.wait_ge(bias_ready, 1)
                    dve.tensor_scalar(wc[:, 0, :], wc[:, 0, :], lnx[:, 0, 0:1], None, ALU.mult)
                    dve.tensor_scalar(wc[0:KR, 1, :], wc[0:KR, 1, :], lnx[0:KR, 0, 1:2], None, ALU.mult)
                    dve.tensor_copy(wc[KR:KR + 1, 1, :], b_ps[KR:KR + 1, :])
                    dve.tensor_tensor(qg[:, 0:1], qg[:, 0:1], qg[:, 1:2], ALU.mult).then_inc(step, 1)
                    dve.wait_ge(step, 1)
                    dve.tensor_scalar(qg[:, 0:1], qg[:, 0:1], dk ** -0.5, None, ALU.mult)
        project(k, lat, wq, CD, IC, lambda act, m, n, bank: act.copy(qT[:, m, bass.ts(n, HALF)], bank))
        with k.stage("qnorm", "squared", "summed", "shifted", "rooted", "step") as (
                sb, ps, squared, summed, shifted, rooted, step):
            sq = sb("sq", [P, IC, N])
            n_ps = ps("n_ps", [P, IC, N])
            with nc.Block() as block:
                @block.scalar
                def _(act):
                    act.activation(sq[:], qT[:], ACT.Square).then_inc(squared, 1)
                    act.wait_ge(summed, 1)
                    act.activation(sq[:], n_ps[:], ACT.Sqrt, scale=1.0 / dk).then_inc(rooted, 1)

                @block.tensor
                def _(pe):
                    pe.wait_ge(squared, 1)
                    for c in range(IC):
                        for n in range(2):
                            mm = pe.matmul(n_ps[:, c, bass.ts(n, HALF)], pair[:], sq[:, c, bass.ts(n, HALF)],
                                           start=True, stop=True)
                    mm.then_inc(summed, 1)

                @block.vector
                def _(dve):
                    link = Chain(dve, step)
                    dve.wait_ge(rooted, 1)
                    link(dve.tensor_scalar(sq[:], sq[:], 1e-8, None, ALU.max))
                    link(dve.reciprocal(sq[:], sq[:]))
                    dve.scalar_tensor_tensor(qT[:], qT[:], qg[:, 0:1], sq[:], ALU.mult, ALU.mult)

        with k.stage("mx", "in0_landed", "in1_landed", "set_up", "batch_in", "var_ready", "rooted", "x_ready",
                     "x_turned", "kv_ready", "kv_taken", "key_squares", "sums_taken", "norms_out",
                     "keys_ready", "taken0", "taken1", "turned", "scored", "s_taken", "maxed", "exped", "inverted",
                     "mixed", "normed", "mix_turned", "out_taken", "step") as (
                sb, ps, in0_landed, in1_landed, set_up, batch_in, var_ready, rooted, x_ready, x_turned,
                kv_ready, kv_taken, key_squares, sums_taken, norms_out, keys_ready, taken0, taken1, turned, scored,
                s_taken, maxed, exped, inverted, mixed, normed, mix_turned, out_taken, step):
            landed = (in0_landed, in1_landed)
            taken = (taken0, taken1)
            KW = IC * P
            xN = sb("xN", [P, 2, NK, DC])
            nb = sb("nb", [P, 2, S])
            lb = sb("lb", [P, 2, CD, T])
            qblk = sb("qblk", [P, 2, IC, P])
            st = sb("st", [P, NK, 6])
            mv = sb("mv", [P, NK, 2])
            rs = sb("rs", [P, NK])
            xt = sb("xt", [P, 2, 2, P])
            kv = sb("kv", [P, NK + 1, 2 * KW])
            sq = sb("sq", [P, 2, KW])
            ssq = sb("ssq", [P, NK + 1, heads])
            rn = sb("rn", [P, NK + 1, heads])
            keysT = sb("keysT", [P, IC, (NK + 1) * P])
            sm = sb("sm", [P, IC, KEYS])
            pT = sb("pT", [P, NK + 1, P])
            col = sb("col", [P, 3, IC])
            mix = sb("mix", [P, IC, P])
            turn = ps("turn", [P, 2, HALF])
            kv_ps = ps("kv_ps", [P, 2, 2 * KW])
            s_ps = ps("s_ps", [P, 3, HALF])
            av = ps("av", [P, HALF])
            KT0, PT0, USES = NK, NK + 5, NK + 5 + 3 * IC
            KEY_GROUPS = ((0, 2), (2, 4), (4, 6), (6, 7), (7, NK + 1))
            PROB_GROUPS = ((0, 4), (4, 7), (7, NK + 1))
            TURNS = 5 + 3 * IC

            with nc.Block() as block:
                def free(eng, i, r):
                    eng.wait_ge(taken[r % 2], i * USES + (r // 2 + 1))

                @block.sync
                def _(sp):
                    def load(b, s):
                        sp.dma_start(xN[:, s], d["ctx"][b].rearrange("(j p) d -> p j d", p=P)
                                     ).then_inc(landed[s], 16)
                        sp.dma_start(nb[:, s], k.bar_rows[b].partition_broadcast(P)).then_inc(landed[s], 16)
                    load(0, 0)
                    load(1, 1)
                    with sp.Fori(1, B // 2) as i:
                        for s in range(2):
                            sp.wait_ge(mixed, (i * 2 + (s - 1)) * IC)
                            load(i * 2 + s, s)

                @block.gpsimd
                def _(pool):
                    pool.memset(qblk[:], 0.0).then_inc(set_up, 1)
                    pool.memset(xt[:], 1.0).then_inc(set_up, 1)
                    pool.memset(ssq[:], 1.0).then_inc(set_up, 1)
                    pool.wait_ge(set_up, 3)

                    def take(b, s):
                        if not (isinstance(b, int) and b == 0):
                            pool.wait_ge(batch_in, b * 3)
                        pool.tensor_copy(lb[:, s], lat[:, :, bass.ds(b * T, T)]).then_inc(batch_in, 1)
                        pool.wait_ge(batch_in, b * 3 + 1)
                        for g in range(2):
                            r = slice(g * dk, (g + 1) * dk)
                            pool.tensor_copy(qblk[r, s, :, bass.ts(g, T)],
                                             qT[r, :, bass.ds(b * T, T)]).then_inc(batch_in, 1)
                    take(0, 0)
                    take(1, 1)
                    with pool.Fori(1, B // 2) as i:
                        for s in range(2):
                            pool.wait_ge(mixed, (i * 2 + (s - 1)) * IC)
                            take(i * 2 + s, s)

                @block.tensor
                def _(pe):
                    pe.wait_ge(set_up, 3)

                    def project_keys(i, b, s, j):
                        q = b * (NK + 1) + j
                        pe.wait_ge(kv_taken, q + 1)
                        bank = kv_ps[:, (s * (NK + 1) + j) % 2, :]
                        if j < NK:
                            free(pe, i, s * USES + j + 2)
                            pe.matmul(bank, xt[:, j % 2, 0, :], wc[:, 0, :], start=True, stop=False)
                            mm = pe.matmul(bank, xt[0:KR + 1, j % 2, 1, :], wc[0:KR + 1, 1, :], start=False,
                                           stop=True)
                        else:
                            for c in range(CD):
                                mm = pe.matmul(bank[0:T, :], lb[:, s, c, :], wl[:, c, :], start=c == 0,
                                               stop=c == CD - 1)
                        mm.then_inc(kv_ready, 1)

                    def batch(i, s):
                        b = i * 2 + s
                        r0 = s * USES
                        pe.wait_ge(batch_in, (b + 1) * 3)
                        for j in range(NK + 1):
                            if j < NK:
                                pe.wait_ge(x_ready, b * NK + (j + 1))
                                free(pe, i, r0 + j)
                                to = turn[:, (r0 + j) % 2, :]
                                pe.transpose(to[:, 0:P], xN[:, s, j, 0:P], k.ident[:])
                                pe.transpose(to[0:KR, P:2 * P], xN[:, s, j, P:DC], k.ident[:]
                                             ).then_inc(x_turned, 1)
                            if j >= 1:
                                project_keys(i, b, s, j - 1)
                        project_keys(i, b, s, NK)
                        pe.wait_ge(keys_ready, b * 2 + 2)
                        for u, (j0, j1) in enumerate(KEY_GROUPS):
                            r = r0 + KT0 + u
                            free(pe, i, r)
                            for j in range(j0, j1):
                                rows = P if j < NK else T
                                for c in range(IC):
                                    at = c * 2 * P + (j - j0) * P
                                    mm = pe.transpose(turn[:, r % 2, at:at + rows],
                                                      kv[0:rows, j, bass.ts(c, P)], k.ident[0:rows, 0:rows])
                            mm.then_inc(turned, 1)

                        def scores(c):
                            pe.wait_ge(s_taken, b * IC + (c + 1))
                            for n, (at, w) in enumerate(((0, HALF), (HALF, HALF), (S, T))):
                                mm = pe.matmul(s_ps[:, n, 0:w], qblk[:, s, c, :], keysT[:, c, at:at + w],
                                               start=True, stop=True)
                            mm.then_inc(scored, 1)

                        free(pe, i, r0 + PT0)
                        free(pe, i, r0 + PT0 + 1)
                        scores(0)
                        scores(1)
                        for c in range(IC):
                            pe.wait_ge(exped, b * IC + (c + 1))
                            for g, (j0, j1) in enumerate(PROB_GROUPS):
                                r = r0 + PT0 + 3 * c + g
                                free(pe, i, r)
                                for j in range(j0, j1):
                                    rows = P if j < NK else T
                                    mm = pe.transpose(turn[0:rows, r % 2, bass.ts(j - j0, P)],
                                                      sm[:, c, j * P:j * P + rows], k.ident[:])
                                mm.then_inc(turned, 1)
                            free(pe, i, r0 + PT0 + 3 * c + 3)
                            free(pe, i, r0 + PT0 + 3 * c + 4)
                            pe.wait_ge(out_taken, b * IC + (c + 1))
                            for j in range(NK + 1):
                                rows = P if j < NK else T
                                mm = pe.matmul(av[:, 0:P], pT[0:rows, j, :],
                                               kv[0:rows, j, KW + c * P:KW + (c + 1) * P],
                                               start=j == 0, stop=j == NK)
                            mm.then_inc(mixed, 1)
                            pe.wait_ge(normed, b * IC + (c + 1))
                            pe.transpose(av[:, P:2 * P], mix[:, c, :], k.ident[:]).then_inc(mix_turned, 1)

                    with pe.Fori(0, B // 2) as i:
                        batch(i, 0)
                        batch(i, 1)

                @block.scalar
                def _(act):
                    act.sem_inc(kv_taken, 2)
                    act.sem_inc(taken0, 1)
                    act.sem_inc(taken1, 1)
                    act.sem_inc(s_taken, 1)
                    act.sem_inc(out_taken, 1)
                    act.wait_ge(set_up, 3)

                    def take_kv(b, s, j):
                        q = b * (NK + 1) + j
                        rows = P if j < NK else T
                        at = (s * (NK + 1) + j) % 2
                        act.wait_ge(kv_ready, q + 1)
                        act.wait_ge(sums_taken, q + 1)
                        act.activation(sq[0:rows, at, :], kv_ps[0:rows, at, 0:KW], ACT.Square
                                       ).then_inc(key_squares, 1)
                        act.copy(kv[0:rows, j, :], kv_ps[0:rows, at, :]).then_inc(kv_taken, 1)

                    def batch(i, s):
                        b = i * 2 + s
                        r0 = s * USES
                        act.wait_ge(var_ready, b + 1)
                        act.activation(rs[:], mv[:, :, 1], ACT.Sqrt).then_inc(rooted, 1)
                        for j in range(NK + 1):
                            if j < NK:
                                r = r0 + j
                                act.wait_ge(x_turned, b * NK + (j + 1))
                                act.copy(xt[:, j % 2, 0, :], turn[:, r % 2, 0:P])
                                act.copy(xt[0:KR, j % 2, 1, :], turn[0:KR, r % 2, P:2 * P]
                                         ).then_inc(taken[r % 2], 1)
                            if j >= 1:
                                take_kv(b, s, j - 1)
                        take_kv(b, s, NK)
                        act.wait_ge(sums_taken, b * (NK + 1) + (NK + 3))
                        act.activation(rn[:], ssq[:], ACT.Sqrt, scale=1.0 / dk).then_inc(norms_out, 1)
                        for c in range(IC):
                            act.wait_ge(maxed, b * IC + (c + 1))
                            act.activation(sm[:, c, :], sm[:, c, :], ACT.Exp, bias=col[:, 0, c:c + 1],
                                           accum_out=col[:, 1, c:c + 1]).then_inc(exped, 1)
                        for c in range(IC):
                            r = r0 + PT0 + 3 * c + 1
                            act.wait_ge(turned, b * TURNS + (5 + 3 * c + 2))
                            act.copy(pT[:, 4:7, :], turn[:, r % 2, 0:3 * P].rearrange("p (j q) -> p j q", q=P)
                                     ).then_inc(taken[r % 2], 1)

                    with act.Fori(0, B // 2) as i:
                        batch(i, 0)
                        batch(i, 1)

                @block.vector
                def _(dve):
                    dve.sem_inc(sums_taken, 2)
                    dve.wait_ge(set_up, 3)
                    STEPS = 2 * (NK + 9 + IC)

                    def batch(i, s, link):
                        b = i * 2 + s
                        r0 = s * USES
                        dve.wait_ge(landed[s], i * 32 + 32)
                        for j in range(NK):
                            link.mark(dve.bn_stats(st[:, j, :], xN[:, s, j, :]))
                        link.wait()
                        link.mark(dve.tensor_tensor(mv[:, :, 0], st[:, :, 1], st[:, :, 4], ALU.add))
                        link.mark(dve.tensor_tensor(mv[:, :, 1], st[:, :, 1], st[:, :, 4], ALU.subtract))
                        link(dve.tensor_tensor(rs[:], st[:, :, 2], st[:, :, 5], ALU.add))
                        link.mark(dve.tensor_scalar(mv[:, :, 0], mv[:, :, 0], 0.5, None, ALU.mult))
                        link.mark(dve.tensor_scalar(rs[:], rs[:], 1.0 / DC, 1e-5, ALU.mult, ALU.add))
                        link(dve.scalar_tensor_tensor(mv[:, :, 1], mv[:, :, 1], 0.25, mv[:, :, 1], ALU.mult,
                                                      ALU.mult))
                        dve.tensor_tensor(mv[:, :, 1], mv[:, :, 1], rs[:], ALU.add).then_inc(var_ready, 1)
                        dve.wait_ge(rooted, b + 1)
                        link(dve.reciprocal(rs[:], rs[:]))
                        for j in range(NK):
                            dve.tensor_scalar(xN[:, s, j, :], xN[:, s, j, :], mv[:, j, 0:1], rs[:, j:j + 1],
                                              ALU.subtract, ALU.mult).then_inc(x_ready, 1)
                        for j in range(NK + 1):
                            q = b * (NK + 1) + j
                            rows = P if j < NK else T
                            at = (s * (NK + 1) + j) % 2
                            dve.wait_ge(key_squares, q + 1)
                            dve.tensor_reduce(ssq[0:rows, j, :], sq[0:rows, at, :].rearrange("p (h q) -> p h q", q=dk),
                                              AX.X, ALU.add).then_inc(sums_taken, 1)
                        dve.wait_ge(norms_out, b + 1)
                        link(dve.tensor_scalar(rn[:], rn[:], 1e-8, None, ALU.max))
                        link(dve.reciprocal(rn[:], rn[:]))
                        for rows, js in ((P, slice(0, NK)), (T, slice(NK, NK + 1))):
                            keys = kv[0:rows, js, 0:KW].rearrange("p j (h q) -> p j h q", q=dk)
                            dve.tensor_tensor(keys, keys, over(rn[0:rows, js, :], 3, dk), ALU.mult
                                              ).then_inc(keys_ready, 1)
                        for u, (j0, j1) in enumerate(KEY_GROUPS):
                            r = r0 + KT0 + u
                            w = min(j1 * P, KEYS) - j0 * P
                            dve.wait_ge(turned, b * TURNS + (u + 1))
                            dve.tensor_copy(keysT[:, :, j0 * P:j0 * P + w],
                                            turn[:, r % 2, :].rearrange("p (c q) -> p c q", c=IC)[:, :, 0:w]
                                            ).then_inc(taken[r % 2], 1)
                        for c in range(IC):
                            dve.wait_ge(scored, b * IC + (c + 1))
                            dve.tensor_tensor(sm[:, c, 0:S], s_ps[:, 0:2, :].rearrange("p a q -> p (a q)"), nb[:, s],
                                              ALU.add)
                            dve.tensor_copy(sm[:, c, S:KEYS], s_ps[:, 2, 0:T]).then_inc(s_taken, 1)
                            dve.wait_ge(s_taken, b * IC + (c + 2))
                            dve.tensor_reduce(col[:, 0, c:c + 1], sm[:, c, :], AX.X, ALU.max, negate=True
                                              ).then_inc(maxed, 1)
                        for c in range(IC):
                            dve.wait_ge(exped, b * IC + (c + 1))
                            link(dve.reciprocal(col[:, 2, c:c + 1], col[:, 1, c:c + 1]))
                            r = r0 + PT0 + 3 * c
                            dve.wait_ge(turned, b * TURNS + (5 + 3 * c + 1))
                            dve.tensor_copy(pT[:, 0:4, :], turn[:, r % 2, :].rearrange("p (j q) -> p j q", q=P)
                                            ).then_inc(taken[r % 2], 1)
                            dve.wait_ge(turned, b * TURNS + (5 + 3 * c + 3))
                            dve.tensor_copy(pT[:, 7, :], turn[:, r % 2, 0:P])
                            dve.tensor_copy(pT[0:T, NK, :], turn[0:T, r % 2, P:2 * P]).then_inc(taken[r % 2], 1)
                            dve.wait_ge(mixed, b * IC + (c + 1))
                            dve.tensor_scalar(mix[:, c, :], av[:, 0:P], col[:, 2, c:c + 1], None, ALU.mult
                                              ).then_inc(normed, 1)
                            dve.wait_ge(mix_turned, b * IC + (c + 1))
                            for g in range(2):
                                r = slice(g * dk, (g + 1) * dk)
                                cp = dve.tensor_copy(oT[r, c, bass.ds(b * T, T)], av[r, P + g * T:P + (g + 1) * T])
                            cp.then_inc(out_taken, 1)

                    with dve.Fori(0, B // 2) as i:
                        link = Chain(dve, step, i * STEPS)
                        batch(i, 0, link)
                        batch(i, 1, link)
                        assert link.n == STEPS, link.n
        add_projection(k, oT, wo, IC, bias=bo)


def head_slots(w, heads):
    dk = w.shape[1] // heads
    out = np.zeros((w.shape[0], heads, HALF // heads), w.dtype)
    out[:, :, :dk] = w.reshape(w.shape[0], heads, dk)
    return out.reshape(w.shape[0], HALF)


def chunks(w):
    n = -(-w.shape[0] // P)
    out = np.zeros((n * P, w.shape[1]), w.dtype)
    out[:w.shape[0]] = w
    return np.ascontiguousarray(out.reshape(n, P, w.shape[1]).transpose(1, 0, 2))


def column(v):
    return np.ascontiguousarray(v.reshape(-1, P).T)


def layouts(x):
    a = {}
    a["xT"] = chunks(x["x"].reshape(N, D).T)
    a["ident"] = np.eye(P, dtype=np.float32)
    a["ctx"] = x["ctx_768"]
    a["ctxT"] = np.ascontiguousarray(x["ctx_768"].transpose(0, 2, 1))

    def xattn(name, heads, turned):
        g = lambda w: x[f"{name}_{w}"].T if turned else x[f"{name}_{w}"]
        a[name + "_Wq"] = chunks(head_slots(g("Wq"), heads))
        wk = head_slots(g("Wk"), heads).T
        a[name + "_WkT"] = chunks(np.concatenate([wk, wk[:, P:]], 1))
        a[name + "_Wv"] = chunks(head_slots(g("Wv"), heads))
        a[name + "_Wo"] = chunks(head_slots(g("Wo").T, heads).T)
    xattn("L0_xattn", 16, True)
    xattn("L1_xattn", 8, False)
    xattn("L2_xattn", 8, False)
    a["lower8"] = np.tril(np.ones((8, 8), np.float32), -1).reshape(64)
    a["lower4"] = np.tril(np.ones((4, 4), np.float32), -1).reshape(16)
    a["upto"] = np.triu(np.ones((P, P), np.float32))
    each = lambda w: np.stack([chunks(m) for m in w])
    cols = lambda w: np.stack([column(v) for v in w])
    a["L0_ffn_gate"] = chunks(x["L0_ffn_gate_w"].T)
    a["L0_ffn_up"], a["L0_ffn_down"] = each(x["L0_ffn_up_w"]), each(x["L0_ffn_down_w"])
    a["L0_ffn_upb"], a["L0_ffn_downb"] = cols(x["L0_ffn_up_b"]), x["L0_ffn_down_b"]
    a["L0_ffn_sup"], a["L0_ffn_sdown"] = chunks(x["L0_ffn_sh_up_w"]), chunks(x["L0_ffn_sh_down_w"])
    a["L0_ffn_supb"], a["L0_ffn_sdownb"] = column(x["L0_ffn_sh_up_b"]), column(x["L0_ffn_sh_down_b"])
    for name, gate_w in (("L1_ffn", x["L1_ffn_gate_w"].T), ("L3_ffn", x["L3_ffn_wg"])):
        a[name + "_gate"] = chunks(gate_w)
        a[name + "_up"], a[name + "_down"] = each(x[name + "_w1"]), each(x[name + "_w2"])
        a[name + "_upb"], a[name + "_downb"] = cols(x[name + "_b1"]), x[name + "_b2"]
    both = lambda g, u: np.concatenate([chunks(g), chunks(u)], 1)
    a["L2_ffn_gate"] = chunks(x["L2_ffn_gate_w"].T)
    a["L2_ffn_cbias"] = x["L2_ffn_correction_bias"]
    a["L2_ffn_up"] = np.stack([both(g, u) for g, u in zip(x["L2_ffn_Wg"], x["L2_ffn_Wu"])])
    a["L2_ffn_down"] = each(x["L2_ffn_Wd"])
    a["L2_ffn_sup"] = both(x["L2_ffn_Wg_s"], x["L2_ffn_Wu_s"])
    a["L2_ffn_sdown"] = chunks(x["L2_ffn_Wd_s"])
    a["pick8"] = np.repeat(np.eye(8, dtype=np.float32)[:, :, None], P, 2)
    s, t = np.arange(P)[:, None], np.arange(P)[None, :]
    a["bar"] = np.where((s // T == t // T) & (s <= t), 0.0, -1e30).astype(np.float32)
    a["fresh"] = (np.arange(N) % T != 0).astype(np.float32)
    a["lags"] = np.arange(T, dtype=np.float32)
    n = "L0_attn_"
    a[n + "in"] = chunks(np.pad(x[n + "in_proj_w"].T, ((0, 0), (0, 120))))
    a[n + "out"] = chunks(x[n + "out_proj_w"].T)
    a[n + "cw"], a[n + "cb"] = chunks(x[n + "conv_w"]), column(x[n + "conv_b"])
    a[n + "D"] = column(np.repeat(x[n + "D"], 64))
    a[n + "nw"] = column(x[n + "norm_w"])
    a[n + "ln"] = np.stack([column(x[n + "ln_w"]), column(x[n + "ln_b"])], 1)
    a[n + "dt"] = np.stack([x[n + "dt_bias"], x[n + "A_log"]], 1)
    n = "L1_attn_"
    a[n + "in"], a[n + "inb"] = chunks(x[n + "in_proj_w"].T), column(x[n + "in_proj_b"])
    a[n + "out"], a[n + "outb"] = chunks(x[n + "out_proj_w"].T), column(x[n + "out_proj_b"])
    a[n + "conv"] = x[n + "conv_w"].transpose(1, 2, 0).reshape(4, P, 4, 512).transpose(1, 0, 2, 3)
    a[n + "cvb"], a[n + "nw"] = column(x[n + "conv_b"]), column(x[n + "norm_w"])
    a[n + "par"] = np.stack([chunks(x[n + w]) for w in ("A_log", "B_param", "C_param")], 1)
    a[n + "dts"] = np.stack([column(x[n + "dt"]), column(x[n + "D_param"])], 1)
    n = "L2_attn_"
    a[n + "in"], a[n + "out"] = chunks(x[n + "in_proj_w"].T), chunks(x[n + "out_proj_w"].T)
    a[n + "cw"], a[n + "cb"] = chunks(x[n + "conv_w"][:, 0, :]), column(x[n + "conv_b"])
    a[n + "x"] = chunks(np.pad(x[n + "x_proj_w"].T, ((0, 0), (0, P - 48))))
    a[n + "wdt"], a[n + "dtb"] = x[n + "dt_proj_w"].T, column(x[n + "dt_proj_b"])
    a[n + "A"] = chunks(x[n + "A_log"]).reshape(P, 64)
    a[n + "D"], a[n + "nw"] = column(x[n + "D"]), column(x[n + "norm_w"])
    n = "L3_attn_"
    a[n + "Wqk"] = chunks(np.concatenate([head_slots(x[n + "Wq"], 16), head_slots(x[n + "Wk"], 16)], 1))
    a[n + "Wv"], a[n + "Wo"] = chunks(head_slots(x[n + "Wv"], 16)), chunks(head_slots(x[n + "Wo"].T, 16).T)
    r, c = np.arange(P)[:, None], np.arange(P)[None, :]
    a["slotvar"] = np.where((r // 32 == c // 32) & (r % 32 < 16) & (c % 32 == 16), 1.0 / 15, 0.0).astype(np.float32)
    a["pair"] = (r // 64 == c // 64).astype(np.float32)
    n = "L3_xattn_"
    a["mask"] = np.ascontiguousarray(x["mask_BxS2_bk0"]).view(np.uint32)
    for w in ("Wq", "Wkv", "Wlkv", "Wo"):
        a[n + w] = chunks(x[n + w].T)
    a[n + "bo"] = column(x[n + "bo"])
    a[n + "lnl"] = np.stack([column(x[n + "ln_l_g"]), column(x[n + "ln_l_b"])], 1)
    a[n + "lnx"] = np.stack([chunks(x[n + "ln_x_" + v][:, None])[:, :, 0] for v in "gb"], 1)
    a[n + "qg"] = np.stack([np.tile(x[n + v], 2) for v in ("qn_g", "kn_g")], 1)
    a["L1_xattn_bo"] = column(x["L1_xattn_bo"])
    a["L2_xattn_bo"] = column(x["L2_xattn_bo"])
    return a


CAPACITY = 2 * N // E
STEPS = [
    ("L3_attn", correlation_attention),
    ("L3_xattn", masked_cross_attention),
    ("L2_attn", selective_scan),
    ("L0_attn", state_space_duality),
    ("L1_attn", long_convolution),
    ("L0_ffn", lambda k: experts(k, "L0_ffn", 256, ACT.Silu, False, True, True, True,
                                 dict(top=2, softmax=True, eps=1e-20))),
    ("L1_ffn", lambda k: experts(k, "L1_ffn", 1024, ACT.Gelu, False, True, True, False,
                                 dict(top=2, softmax=True, eps=1e-9))),
    ("L2_ffn", lambda k: experts(k, "L2_ffn", 128, ACT.Silu, True, False, False, True,
                                 dict(top=4, softmax=False, eps=1e-20, factor=2.5, grouped=True))),
    ("L3_ffn", lambda k: experts(k, "L3_ffn", 1024, ACT.Relu, False, True, True, False,
                                 dict(top=2, softmax=True, eps=0.0, capacity=CAPACITY))),
    ("L0_xattn", lambda k: context_attention(k, "L0_xattn", 16, 16 ** -0.5, False)),
    ("L1_xattn", lambda k: context_attention(k, "L1_xattn", 8, 64 ** -0.5, True)),
    ("L2_xattn", lambda k: context_attention(k, "L2_xattn", 8, 64 ** -0.5, True)),
]


ORDER = ["L0_xattn", "L0_attn", "L0_ffn", "L1_xattn", "L1_attn", "L1_ffn", "L2_xattn", "L2_attn", "L2_ffn",
         "L3_xattn", "L3_attn", "L3_ffn"]


def build(nc, dram, steps=None):
    with ExitStack() as ctx:
        k = Core(nc, dram, ctx)
        k.comb = nc.dram_tensor("comb_rows", (E, N), F32).ap()
        load_constants(k)
        k.bc = nc.dram_tensor("state_rows", (32, N), F32).ap()
        k.bar_rows = nc.dram_tensor("bar_rows", (B, S), F32).ap()
        for name in ORDER:
            if steps is None or name in steps:
                dict(STEPS)[name](k)
        store_result(k)


def kernel(**inputs):
    import concourse.bacc as bacc
    from concourse.bass_utils import run_bass_kernel_spmd

    nc = bacc.Bacc("TRN2", target_bir_lowering=False, num_devices=1)
    arrays = {"in_" + n: np.ascontiguousarray(v) for n, v in layouts({n: np.asarray(v) for n, v in inputs.items()}).items()}
    dram = {n[3:]: nc.dram_tensor(n, v.shape, mybir.dt.from_np(v.dtype), kind="ExternalInput").ap()
            for n, v in arrays.items()}
    dram["outT"] = nc.dram_tensor("outT", (P, CD, N), F32, kind="ExternalOutput").ap()
    build(nc, dram)
    r = run_bass_kernel_spmd(nc, [arrays], core_ids=[0])
    out = r.results[0]["outT"]
    return np.ascontiguousarray(out.transpose(1, 0, 2).reshape(D, N).T.reshape(B, T, D))
```

```python
from contextlib import ExitStack, contextmanager

import numpy as np

import concourse.bass as bass
from concourse import mybir

ALU = mybir.AluOpType
ACT = mybir.ActivationFunctionType
AX = mybir.AxisListType
F32 = mybir.dt.float32
F32R = mybir.dt.float32r

P = 128
B, T, D = 16, 64, 256
N = B * T
S, DC = 1024, 192
CD = D // P
HALF = 512
SEMS = 40


class Core:

    def __init__(self, nc, dram, ctx):
        self.nc, self.dram = nc, dram
        sb = lambda name, shape: ctx.enter_context(nc.sbuf_tensor(name, shape, F32))
        self.sem_pool = [nc.alloc_semaphore(f"pool{i}") for i in range(SEMS)]
        self.xT = sb("xT", [P, CD, N])
        self.xn = sb("xn", [P, CD, N])
        self.ones = sb("ones", [P, P])
        self.ident = sb("ident", [P, P])
        self.count = 0
        self.weights = nc.alloc_semaphore("weights_landed")
        self.due = 0

    @contextmanager
    def stage(self, name, *signals):
        nc = self.nc
        self.count += 1
        tag = f"{name}{self.count}_"
        with ExitStack() as ctx:
            def sb(n, shape, dt=F32):
                return ctx.enter_context(nc.sbuf_tensor(tag + n, shape, dt))

            def ps(n, shape, dt=F32):
                return ctx.enter_context(nc.psum_tensor(tag + n, shape, dt))
            assert len(signals) <= SEMS
            yield (sb, ps, *self.sem_pool[:len(signals)])
        if signals:
            nums = [s.num for s in self.sem_pool[:len(signals)]]
            assert nums == list(range(nums[0], nums[0] + len(nums)))
            nc.all_engine_barrier(sems_to_clear=range(nums[0], nums[-1] + 1))


def load_constants(k):
    nc = k.nc
    with k.stage("load", "landed") as (sb, ps, landed):
        with nc.Block() as block:
            @block.sync
            def _(sp):
                sp.dma_start(k.xT[:], k.dram["xT"]).then_inc(landed, 16)
                sp.dma_start(k.ident[:], k.dram["ident"]).then_inc(landed, 16)
                sp.wait_ge(landed, 32)

            @block.vector
            def _(dve):
                dve.memset(k.ones[:], 1.0)


def store_result(k):
    nc = k.nc
    with k.stage("store", "stored") as (sb, ps, stored):
        with nc.Block() as block:
            @block.sync
            def _(sp):
                sp.dma_start(k.dram["outT"], k.xT[:]).then_inc(stored, 16)
                sp.wait_ge(stored, 16)


def layernorm(k, src, dst, eps, affine=None, centre=True, width=CD):
    nc = k.nc
    with k.stage("ln", "mean_ready", "centred", "squared", "var_ready", "shifted", "rooted",
                 "inverted", "scaled") as (
            sb, ps, mean_ready, centred, squared, var_ready, shifted, rooted, inverted, scaled):
        mean = ps("mean", [P, N])
        var = ps("var", [P, N])
        sq = sb("sq", [P, width, N])
        rstd = sb("rstd", [P, N])
        cen = sb("cen", [P, width, N]) if centre else None
        x = cen if centre else src
        items = [(n, c) for n in range(N // HALF) for c in range(width)]
        with nc.Block() as block:
            @block.tensor
            def _(pe):
                if centre:
                    for n, c in items:
                        mm = pe.matmul(mean[:, bass.ts(n, HALF)], k.ones[:], src[:, c, bass.ts(n, HALF)],
                                       start=c == 0, stop=c == width - 1)
                        if c == width - 1:
                            mm.then_inc(mean_ready, 1)
                for q, (n, c) in enumerate(items):
                    pe.wait_ge(squared, q + 1)
                    mm = pe.matmul(var[:, bass.ts(n, HALF)], k.ones[:], sq[:, c, bass.ts(n, HALF)],
                                   start=c == 0, stop=c == width - 1)
                    if c == width - 1:
                        mm.then_inc(var_ready, 1)

            @block.scalar
            def _(act):
                for q, (n, c) in enumerate(items):
                    if centre:
                        act.wait_ge(centred, q + 1)
                    act.activation(sq[:, c, bass.ts(n, HALF)], x[:, c, bass.ts(n, HALF)], ACT.Square,
                                   scale=(width * P) ** -0.5).then_inc(squared, 1)
                for n in range(N // HALF):
                    act.wait_ge(shifted, n + 1)
                    act.activation(rstd[:, bass.ts(n, HALF)], rstd[:, bass.ts(n, HALF)], ACT.Sqrt
                                   ).then_inc(rooted, 1)
            @block.vector
            def _(dve):
                if centre:
                    for n, c in items:
                        dve.wait_ge(mean_ready, n + 1)
                        dve.scalar_tensor_tensor(cen[:, c, bass.ts(n, HALF)], mean[:, bass.ts(n, HALF)],
                                                 -1.0 / (width * P), src[:, c, bass.ts(n, HALF)],
                                                 ALU.mult, ALU.add).then_inc(centred, 1)
                for n in range(N // HALF):
                    dve.wait_ge(var_ready, n + 1)
                    dve.tensor_scalar(rstd[:, bass.ts(n, HALF)], var[:, bass.ts(n, HALF)], eps, None,
                                      ALU.add).then_inc(shifted, 1)
                for n in range(N // HALF):
                    dve.wait_ge(rooted, n + 1)
                    dve.reciprocal(rstd[:, bass.ts(n, HALF)], rstd[:, bass.ts(n, HALF)]).then_inc(inverted, 1)
                if centre:
                    dve.wait_ge(centred, len(items))
                for q, (n, c) in enumerate(items):
                    at = bass.ts(n, HALF)
                    dve.wait_ge(inverted, n + 1)
                    if affine and affine[1] is None:
                        dve.scalar_tensor_tensor(dst[:, c, at], x[:, c, at], affine[0][:, c:c + 1], rstd[:, at],
                                                 ALU.mult, ALU.mult)
                    else:
                        dve.tensor_tensor(dst[:, c, at], x[:, c, at], rstd[:, at], ALU.mult).then_inc(scaled, 1)
                if affine and affine[1] is not None:
                    w, b = affine
                    dve.wait_ge(k.weights, k.due)
                    for q, (n, c) in enumerate(items):
                        dve.wait_ge(scaled, q + 1)
                        dve.tensor_scalar(dst[:, c, bass.ts(n, HALF)], dst[:, c, bass.ts(n, HALF)], w[:, c:c + 1],
                                          b[:, c:c + 1], ALU.mult, ALU.add)


def context_attention(k, name, heads, scale, bias):
    nc = k.nc
    slot = HALF // heads
    per = P // slot
    NC = HALF // P
    HQ = heads * T
    NJ = HQ // P
    NK = S // P
    W = per * T
    KR = DC - P
    with ExitStack() as ctx:
        keep = lambda n, shape: ctx.enter_context(nc.sbuf_tensor(f"{name}_{n}", shape, F32))
        qT = keep("qT", [P, NC, N])
        oT = keep("oT", [P, NC, N])
        wkT = keep("wkT", [P, NC, 2 * P])
        wv = keep("wv", [P, 2, HALF])
        wo = keep("wo", [P, NC, D])
        bo = keep("bo", [P, CD])
        with nc.sbuf_tensor(name + "_wq", [P, CD, HALF], F32) as wq:
            loads = [(wq[:], k.dram[name + "_Wq"]), (wkT[:], k.dram[name + "_WkT"]), (wv[:], k.dram[name + "_Wv"]),
                     (wo[:], k.dram[name + "_Wo"])]
            prefetch(k, *loads, *([(bo[:], k.dram[name + "_bo"])] if bias else []))
            layernorm(k, k.xT, k.xn, 1e-5)
            project(k, k.xn, wq, CD, NC, lambda act, m, n, bank: act.mul(qT[:, m, bass.ts(n, HALF)], bank, scale))

        with k.stage("att", "ctx0_landed", "ctx1_landed", "q_zero", "q_blocked", "split_step", "split_ready",
                     "q_folded", "q_high", "q_low", "scored", "maxed", "exped", "turned", "turned_v", "turned_a",
                     "mixed", "inverted", "normed", "mix_turned", "mix_taken", "projected", "proj_taken") as (
                sb, ps, ctx0_landed, ctx1_landed, q_zero, q_blocked, split_step, split_ready, q_folded, q_high,
                q_low, scored, maxed, exped, turned, turned_v, turned_a, mixed, inverted, normed, mix_turned,
                mix_taken, projected, proj_taken):
            landed = (ctx0_landed, ctx1_landed)
            cT = sb("cT", [P, 2, 2, S])
            cH = sb("cH", [P, 2, S], F32R)
            cL = sb("cL", [P, 2, S], F32R)
            cR = sb("cR", [P, 2, S], F32R)
            cN = sb("cN", [P, 2, NK, DC])
            qblk = sb("qblk", [P, 2, NC, W])
            qH = sb("qH", [P, 2, HQ], F32R)
            qL = sb("qL", [P, 2, HQ], F32R)
            pr = sb("pr", [P, 2, S])
            prT = sb("prT", [P, NK, P])
            nmax = sb("nmax", [P, NJ])
            total = sb("total", [P, NJ])
            inv = sb("inv", [P, NJ])
            mix = sb("mix", [P, 2, DC])
            mixT = sb("mixT", [P, 2, HQ])
            sc = ps("sc", [P, 2, S])
            tp = ps("tp", [P, NK, P])
            av = ps("av", [P, 2, HALF])
            chunk = tp[:].rearrange("p a b -> p (a b)")[:, 0:NC * W].rearrange("p (m w) -> p m w", m=NC)

            def every_batch(eng, run):
                with eng.Fori(0, B // 2 - 1) as i:
                    run(i * 2, 0, False)
                    run(i * 2 + 1, 1, False)
                run(B - 2, 0, False)
                run(B - 1, 1, True)

            with nc.Block() as block:
                @block.sync
                def _(sp):
                    def load(b, s):
                        sp.dma_start(cT[:, s, 0, :], k.dram["ctxT"][b, 0:P, :]).then_inc(landed[s], 16)
                        for g in range(2):
                            sp.dma_start(cT[g * KR:(g + 1) * KR, s, 1, :],
                                         k.dram["ctxT"][b, P:DC, :]).then_inc(landed[s], 16)
                        sp.dma_start(cN[:, s, :, :], k.dram["ctx"][b].rearrange("(j p) d -> p j d", p=P)
                                     ).then_inc(landed[s], 16)
                    load(0, 0)
                    load(1, 1)
                    with sp.Fori(1, B // 2) as i:
                        for s in range(2):
                            sp.wait_ge(mixed, (i * 2 + (s - 1)) * NJ)
                            load(i * 2 + s, s)

                @block.gpsimd
                def _(pool):
                    pool.memset(qblk[:], 0.0).then_inc(q_zero, 1)
                    pool.memset(mixT[:], 0.0).then_inc(q_zero, 1)
                    pool.wait_ge(q_zero, 2)

                    def block_q(b, s):
                        for g in range(per):
                            r = slice(g * slot, (g + 1) * slot)
                            pool.tensor_copy(qblk[r, s, :, bass.ts(g, T)],
                                             qT[r, :, bass.ds(b * T, T)]).then_inc(q_blocked, 1)
                        pool.wait_ge(q_blocked, (b + 1) * per)

                    def split(b, s, i):
                        pool.wait_ge(landed[s], i * 64 + 64)
                        x = cT[:, s, 0, :].rearrange("p (j q) -> p j q", q=P)
                        pool.tensor_tensor(cH[:, s].rearrange("p (j q) -> p j q", q=P), x, over(k.ones[:], 1, NK),
                                           ALU.mult).then_inc(split_step, 1)
                        x = cT[:, s, 1, :].rearrange("p (j q) -> p j q", q=P)
                        pool.tensor_tensor(cR[:, s].rearrange("p (j q) -> p j q", q=P), x, over(k.ones[:], 1, NK),
                                           ALU.mult).then_inc(split_step, 1)
                        pool.wait_ge(split_step, b * 3 + 2)
                        pool.tensor_tensor(cL[:, s], cT[:, s, 0, :], cH[:, s].bitcast(F32), ALU.subtract
                                           ).then_inc(split_step, 1)
                        pool.wait_ge(split_step, b * 3 + 3)
                        pool.tensor_tensor(cR[KR:P, s], cT[KR:P, s, 1, :], cR[KR:P, s].bitcast(F32), ALU.subtract
                                           ).then_inc(split_ready, 1)
                        pool.wait_ge(split_ready, b + 1)

                    for s in range(2):
                        block_q(s, s)
                        split(s, s, 0)
                    with pool.Fori(1, B // 2) as i:
                        for s in range(2):
                            pool.wait_ge(q_folded, i * 2 + (s - 1))
                            block_q(i * 2 + s, s)
                            pool.wait_ge(scored, (i * 2 + (s - 1)) * NJ)
                            split(i * 2 + s, s, i)

                @block.tensor
                def _(pe):
                    def scores(b, s, j):
                        if j == 0:
                            pe.wait_ge(q_low, (b + 1) * 2)
                            pe.wait_ge(split_ready, b + 1)
                        if j >= 2:
                            pe.wait_ge(exped, b * NJ + (j - 1))
                        h0, h1, l0, l1 = (x[:, c, bass.ts(j, P)] for x in (qH, qL) for c in range(2))
                        for n in range(2):
                            to, at = sc[:, j % 2, bass.ts(n, HALF)], bass.ts(n, HALF)
                            pe.matmul(to, h0, cH[:, s, at], start=True, stop=False)
                            pe.matmul(to, h0, cL[:, s, at], start=False, stop=False)
                            pe.matmul(to, l0, cH[:, s, at], start=False, stop=False)
                            pe.matmul(to, h1, cR[:, s, at], start=False, stop=False)
                            mm = pe.matmul(to, l1, cR[:, s, at], start=False, stop=True)
                        mm.then_inc(scored, 1)

                    def fold(b, s):
                        pe.wait_ge(q_blocked, (b + 1) * per)
                        for m in range(NC):
                            for c in range(2):
                                mm = pe.matmul(sc[:, c, bass.ts(m, W)], wkT[:, m, bass.ts(c, P)],
                                               qblk[:, s, m, :], start=True, stop=True)
                        mm.then_inc(q_folded, 1)

                    def batch(b, s, last):
                        scores(b, s, 0)
                        for j in range(NJ + 1):
                            if j + 1 < NJ:
                                scores(b, s, j + 1)
                            if j >= 1:
                                pe.wait_ge(turned_v, b * NJ + j)
                                pe.wait_ge(turned_a, b * NJ + j)
                                if j >= 3:
                                    pe.wait_ge(mix_taken, b * NJ + (j - 2))
                                for n in range(NK):
                                    mm = pe.matmul(av[:, (j - 1) % 2, 0:DC], prT[:, n, :], cN[:, s, n, :],
                                                   start=n == 0, stop=n == NK - 1)
                                mm.then_inc(mixed, 1)
                            if j == NJ and not last:
                                fold(b + 1, 1 - s)
                            if j < NJ:
                                pe.wait_ge(exped, b * NJ + (j + 1))
                                if j == 0:
                                    pe.wait_ge(proj_taken, b + 1)
                                for n in range(NK):
                                    mm = pe.transpose(tp[:, n, :], pr[:, j % 2, bass.ts(n, P)], k.ident[:])
                                mm.then_inc(turned, 1)
                            if j >= 1:
                                pe.wait_ge(normed, b * NJ + j)
                                pe.transpose(av[:, (j - 1) % 2, DC:DC + P], mix[:, (j - 1) % 2, 0:P], k.ident[:])
                                pe.transpose(av[0:KR, (j - 1) % 2, DC + P:DC + 2 * P], mix[:, (j - 1) % 2, P:DC],
                                             k.ident[:]).then_inc(mix_turned, 1)
                        pe.wait_ge(mix_taken, b * NJ + NJ)
                        for m in range(NC):
                            pe.matmul(chunk[:, m, :], wv[:, 0, bass.ts(m, P)], mixT[:, 0, bass.ts(m, W)],
                                      start=True, stop=False)
                            mm = pe.matmul(chunk[:, m, :], wv[:, 1, bass.ts(m, P)], mixT[:, 1, bass.ts(m, W)],
                                           start=False, stop=True)
                        mm.then_inc(projected, 1)

                    fold(0, 0)
                    every_batch(pe, batch)

                @block.scalar
                def _(act):
                    def exp(b, j):
                        act.wait_ge(maxed, b * NJ + (j + 1))
                        act.activation(pr[:, j % 2, :], sc[:, j % 2, :], ACT.Exp, bias=nmax[:, j:j + 1],
                                       accum_out=total[:, j:j + 1]).then_inc(exped, 1)

                    def high(b):
                        act.wait_ge(q_folded, b + 1)
                        for c in range(2):
                            act.copy(qH[:, c, :], sc[:, c, 0:HQ]).then_inc(q_high, 1)

                    def batch(b, s, last):
                        exp(b, 0)
                        for j in range(NJ):
                            if j + 1 < NJ:
                                exp(b, j + 1)
                            act.wait_ge(turned, b * NJ + (j + 1))
                            act.copy(prT[:, 0:NK // 2, :], tp[:, 0:NK // 2, :]).then_inc(turned_a, 1)
                        if not last:
                            high(b + 1)
                        act.wait_ge(projected, b + 1)
                        for g in range(per):
                            r = slice(g * slot, (g + 1) * slot)
                            cp = act.copy(oT[r, :, bass.ds(b * T, T)], chunk[r, :, bass.ts(g, T)])
                        cp.then_inc(proj_taken, 1)

                    act.sem_inc(proj_taken, 1)
                    high(0)
                    every_batch(act, batch)

                @block.vector
                def _(dve):
                    def row_max(b, j):
                        dve.wait_ge(scored, b * NJ + (j + 1))
                        dve.tensor_reduce(nmax[:, j:j + 1], sc[:, j % 2, :], AX.X, ALU.max,
                                          negate=True).then_inc(maxed, 1)

                    def low(b):
                        for c in range(2):
                            dve.wait_ge(q_high, b * 2 + (c + 1))
                            dve.tensor_tensor(qL[:, c, :], sc[:, c, 0:HQ], qH[:, c, :].bitcast(F32),
                                              ALU.subtract).then_inc(q_low, 1)

                    def batch(b, s, last):
                        row_max(b, 0)
                        for j in range(NJ + 1):
                            if j + 1 < NJ:
                                row_max(b, j + 1)
                            if j >= 1:
                                dve.wait_ge(inverted, b * NJ + j)
                                dve.wait_ge(mixed, b * NJ + j)
                                dve.tensor_scalar(mix[:, (j - 1) % 2, :], av[:, (j - 1) % 2, 0:DC],
                                                  inv[:, j - 1:j], None, ALU.mult).then_inc(normed, 1)
                            if j < NJ:
                                dve.wait_ge(exped, b * NJ + (j + 1))
                                dve.reciprocal(inv[:, j:j + 1], total[:, j:j + 1]).then_inc(inverted, 1)
                                dve.wait_ge(turned, b * NJ + (j + 1))
                                dve.tensor_copy(prT[:, NK // 2:NK, :], tp[:, NK // 2:NK, :]).then_inc(turned_v, 1)
                            if j >= 1:
                                dve.wait_ge(mix_turned, b * NJ + j)
                                dve.tensor_copy(mixT[:, 0, bass.ts(j - 1, P)], av[:, (j - 1) % 2, DC:DC + P])
                                dve.tensor_copy(mixT[0:KR, 1, bass.ts(j - 1, P)],
                                                av[0:KR, (j - 1) % 2, DC + P:DC + 2 * P]).then_inc(mix_taken, 1)
                        if not last:
                            low(b + 1)

                    dve.wait_ge(q_zero, 2)
                    low(0)
                    every_batch(dve, batch)
        add_projection(k, oT, wo, NC, bias=bo if bias else None)


E = 8
NT = N // P


class Chain:

    def __init__(self, eng, sem, base=0):
        self.eng, self.sem, self.n, self.base = eng, sem, 0, base

    def mark(self, instruction):
        instruction.then_inc(self.sem, 1)
        self.n += 1

    def wait(self):
        self.eng.wait_ge(self.sem, self.base + self.n)

    def __call__(self, instruction):
        self.mark(instruction)
        self.wait()


def over(ap, axis, n):
    ap = ap.unsqueeze(axis)
    shape = list(ap.shape)
    shape[axis] = n
    return ap.broadcast_to(shape)


def gate(k, name, combT, top, softmax, eps, factor=1.0, grouped=False, capacity=None):
    nc = k.nc
    comb_dram = k.comb
    with k.stage("gate", "landed", "logits_ready", "scores_in", "scores_out", "counted", "valued", "comb_ready",
                 "turned", "copied", "stored", "step", "cleared") as (
            sb, ps, landed, logits_ready, scores_in, scores_out, counted, valued, comb_ready, turned, copied,
            stored, step, cleared):
        gw = sb("gw", [P, CD, E])
        tri = sb("tri", [P, E * E])
        tri4 = sb("tri4", [P, 16])
        upto = sb("upto", [P, P])
        bias = sb("bias", [P, E])
        lg = sb("lg", [P, NT, E])
        pr = sb("pr", [P, NT, E])
        val = sb("val", [P, NT, E])
        ex = sb("ex", [P, NT, E])
        cmp = sb("cmp", [P, NT, E, E])
        eq = sb("eq", [P, NT, E, E])
        rank = sb("rank", [P, NT, E])
        mask = sb("mask", [P, 2, NT, E])
        row = sb("row", [P, 3, NT])
        comb = sb("comb", [P, NT, E])
        grp = sb("grp", [P, 3, NT, 4])
        pre = sb("pre", [P, 2 * NT, E])
        tot = sb("tot", [P, 2 * NT, E])
        ones = sb("ones", [P, 2 * NT])
        lg_ps = ps("lg_ps", [P, NT, E])
        cnt_ps = ps("cnt_ps", [P, 2 * NT, E])
        tot_ps = ps("tot_ps", [P, 2 * NT, E])
        ct_ps = ps("ct_ps", [P, N])
        with nc.Block() as block:
            @block.sync
            def _(sp):
                sp.dma_start(gw[:], k.dram[name + "_gate"]).then_inc(landed, 16)
                sp.dma_start(tri[:], k.dram["lower8"].partition_broadcast(P)).then_inc(landed, 16)
                sp.dma_start(tri4[:], k.dram["lower4"].partition_broadcast(P)).then_inc(landed, 16)
                sp.dma_start(upto[:], k.dram["upto"]).then_inc(landed, 16)
                if grouped:
                    sp.dma_start(bias[:], k.dram[name + "_cbias"].partition_broadcast(P)).then_inc(landed, 16)
                sp.wait_ge(copied, 1)
                sp.dma_start(comb_dram, combT[0:E, :]).then_inc(stored, 16)
                sp.wait_ge(stored, 16)

            @block.gpsimd
            def _(pool):
                pool.memset(combT[:], 0.0).then_inc(cleared, 1)

            @block.tensor
            def _(pe):
                pe.wait_ge(landed, 64 + 16 * grouped)
                for t in range(NT):
                    for c in range(CD):
                        mm = pe.matmul(lg_ps[:, t, :], k.xn[:, c, bass.ts(t, P)], gw[:, c, :],
                                       start=c == 0, stop=c == CD - 1)
                mm.then_inc(logits_ready, 1)
                if capacity:
                    pe.wait_ge(valued, 1)
                    flat = mask[:].rearrange("p a t e -> p (a t e)")
                    pe.matmul(cnt_ps[:].rearrange("p a e -> p (a e)"), upto[:], flat, start=True, stop=True)
                    pe.matmul(tot_ps[:].rearrange("p a e -> p (a e)"), k.ones[:], flat, start=True,
                              stop=True).then_inc(counted, 1)
                pe.wait_ge(comb_ready, 1)
                for t in range(NT):
                    mm = pe.transpose(ct_ps[0:E, bass.ts(t, P)], comb[:, t, :], k.ident[:])
                mm.then_inc(turned, 1)

            @block.scalar
            def _(act):
                if softmax:
                    act.wait_ge(scores_in, 1)
                    act.activation(ex[:], lg[:], ACT.Exp).then_inc(scores_out, 1)
                else:
                    act.wait_ge(logits_ready, 1)
                    act.activation(pr[:], lg_ps[:], ACT.Sigmoid).then_inc(scores_out, 1)

            @block.vector
            def _(dve):
                link = Chain(dve, step)
                tt = dve.tensor_tensor

                def ranks(out, v, e, lower):
                    mine, other = over(v, 3, e), over(v, 2, e)
                    c, q = (x[:].rearrange("p t a b -> p (t a b)")[:, 0:NT * e * e]
                            .rearrange("p (t a b) -> p t a b", t=NT, a=e) for x in (cmp, eq))
                    link(tt(c, other, mine, ALU.is_gt))
                    link(tt(q, other, mine, ALU.is_equal))
                    lw = lower.rearrange("p (a b) -> p a b", a=e)
                    link(tt(q, q, over(lw, 1, NT), ALU.mult))
                    link(tt(c, c, q, ALU.add))
                    link(dve.tensor_reduce(out, c, AX.X, ALU.add))

                dve.wait_ge(landed, 64 + 16 * grouped)
                if softmax:
                    dve.wait_ge(logits_ready, 1)
                    link(dve.tensor_reduce(row[:, 0, :], lg_ps[:], AX.X, ALU.max))
                    tt(lg[:], lg_ps[:], over(row[:, 0, :], 2, E), ALU.subtract).then_inc(scores_in, 1)
                    dve.wait_ge(scores_out, 1)
                    link(dve.tensor_reduce(row[:, 1, :], ex[:], AX.X, ALU.add))
                    link(dve.reciprocal(row[:, 2, :], row[:, 1, :]))
                    link(tt(pr[:], ex[:], over(row[:, 2, :], 2, E), ALU.mult))
                    choice = pr
                else:
                    dve.wait_ge(scores_out, 1)
                    link(tt(val[:], pr[:], over(bias[:], 1, NT), ALU.add))
                    pair = val[:].rearrange("p t (g j) -> p t g j", j=2)
                    link(tt(grp[:, 0, :, :], pair[:, :, :, 0], pair[:, :, :, 1], ALU.add))
                    ranks(grp[:, 1, :, :], grp[:, 0, :, :], 4, tri4[:])
                    link(dve.tensor_scalar(grp[:, 2, :, :], grp[:, 1, :, :], 1.5, None, ALU.is_lt))
                    link(tt(pair, pair, over(grp[:, 2, :, :], 3, 2), ALU.mult))
                    choice = val
                ranks(rank[:], choice[:], E, tri[:])
                if capacity:
                    link(dve.tensor_scalar(mask[:, 0], rank[:], 0.5, None, ALU.is_lt))
                    link(dve.tensor_scalar(mask[:, 1], rank[:], 1.5, None, ALU.is_lt))
                    tt(mask[:, 1], mask[:, 1], mask[:, 0], ALU.subtract).then_inc(valued, 1)
                    link(dve.memset(ones[:], 1.0))
                    dve.wait_ge(counted, 1)
                    link(dve.tensor_copy(tot[:], tot_ps[:]))
                    for e in range(E):
                        ins = dve.tensor_tensor_scan(pre[:, :, e], ones[:], tot[:, :, e], 0.0, ALU.mult, ALU.add)
                        ins.then_inc(step, 1)
                    link.n += E
                    dve.wait_ge(step, link.n)
                    link(tt(pre[:], pre[:], tot[:], ALU.subtract))
                    link(tt(pre[:], pre[:], cnt_ps[:], ALU.add))
                    link(dve.tensor_scalar(pre[:], pre[:], capacity + 0.5, None, ALU.is_lt))
                    m = mask[:].rearrange("p a t e -> p (a t) e")
                    link(tt(pre[:], pre[:], m, ALU.mult))
                    link(tt(rank[:], mask[:, 0], mask[:, 1], ALU.add))
                    chosen = rank
                else:
                    link(dve.tensor_scalar(rank[:], rank[:], top - 0.5, None, ALU.is_lt))
                    chosen = rank
                link(tt(lg[:], pr[:], chosen[:], ALU.mult))
                link(dve.tensor_reduce(row[:, 0, :], lg[:], AX.X, ALU.add))
                link(dve.tensor_scalar(row[:, 0, :], row[:, 0, :], eps, 1.0 / factor, ALU.add, ALU.mult))
                link(dve.reciprocal(row[:, 1, :], row[:, 0, :]))
                if capacity:
                    link(tt(rank[:], pre[:, 0:NT, :], pre[:, NT:2 * NT, :], ALU.add))
                    link(tt(lg[:], pr[:], rank[:], ALU.mult))
                tt(comb[:], lg[:], over(row[:, 1, :], 2, E), ALU.mult).then_inc(comb_ready, 1)
                dve.wait_ge(turned, 1)
                dve.wait_ge(cleared, 1)
                dve.tensor_copy(combT[0:E, :], ct_ps[0:E, :]).then_inc(copied, 1)


def split_weights(pool, k, ready, done, parts, raw):
    ones = k.ones[:]
    for (high, low), x in zip(parts, raw):
        tiles = lambda ap: ap.rearrange("p c (j q) -> p (c j) q", q=P)
        n = x.shape[1] * x.shape[2] // P
        pool.tensor_tensor(tiles(high), tiles(x), over(ones, 1, n), ALU.mult).then_inc(ready, 1)
    done(0)
    for (high, low), x in zip(parts, raw):
        last = pool.tensor_tensor(low, x, high.bitcast(F32), ALU.subtract)
    return last


def experts(k, name, hidden, func, gated, up_bias, down_bias, shared, gate_args):
    nc = k.nc
    HC = hidden // P
    PER = HC * 2
    UP = 2 if gated else 1
    RP = 4 // UP
    R = 4
    LAG = 2 + gated
    LAST = E if shared else E - 1
    with ExitStack() as ctx:
        keep = lambda n, shape, dt=F32: ctx.enter_context(nc.sbuf_tensor(f"{name}_{n}", shape, dt))
        combT = keep("combT", [P, N])
        wu = keep("wu", [P, 2, UP * CD, hidden])
        wd = keep("wd", [P, 2, HC, D])
        bd = keep("bd", [P, D])
        bs = keep("bs", [P, CD])
        first = [(t[:, e], k.dram[f"{name}_{n}"][e]) for e in range(2) for t, n in ((wu, "up"), (wd, "down"))]
        if down_bias:
            first.append((bd[:], k.dram[name + "_downb"]))
        if shared and down_bias:
            first.append((bs[:], k.dram[name + "_sdownb"]))
        prefetch(k, *first)
        layernorm(k, k.xT, k.xn, 1e-5)
        gate(k, name, combT, **gate_args)
        with k.stage("moe", "w0_landed", "w1_landed", "c0_landed", "c1_landed", "high_ready", "split_ready",
                     "x_high", "x_low", "up_done", "activated", "weighed", "high_taken", "scaled", "down_done",
                     "closed", "gated_in") as (
                sb, ps, w0_landed, w1_landed, c0_landed, c1_landed, high_ready, split_ready, x_high, x_low,
                up_done, activated, weighed, high_taken, scaled, down_done, closed, gated_in):
            w_landed, c_landed = (w0_landed, w1_landed), (c0_landed, c1_landed)
            wuH, wuL = (sb("wu" + n, [P, 2, UP * CD, hidden], F32R) for n in "HL")
            wdH, wdL = (sb("wd" + n, [P, 2, HC, D], F32R) for n in "HL")
            xH, xL = (sb("x" + n, [P, CD, N], F32R) for n in "HL")
            bu = sb("bu", [P, 2, HC])
            cb = sb("cb", [P, 2, N])
            h = sb("h", [P, R, HALF])
            hs = sb("hs", [P, R, HALF])
            hsH, hsL = (sb("hs" + n, [P, R, HALF], F32R) for n in "HL")
            up_ps = ps("up_ps", [P, RP, UP, HALF])
            y_ps = ps("y_ps", [P, 4, HALF])
            per_c = 16 * (1 + up_bias)
            PAIR = [(s, j) for s in range(2) for j in range(PER)]
            LONE = PAIR[:PER]

            with nc.Block() as block:
                @block.sync
                def _(sp):
                    def load_w(e, s):
                        is_shared = isinstance(e, int) and e == E
                        u = k.dram[name + "_sup"] if is_shared else k.dram[name + "_up"][e]
                        w = k.dram[name + "_sdown"] if is_shared else k.dram[name + "_down"][e]
                        sp.dma_start(wu[:, s], u).then_inc(w_landed[s], 16)
                        sp.dma_start(wd[:, s], w).then_inc(w_landed[s], 16)

                    def load_c(e, s):
                        if isinstance(e, int) and e == E:
                            if up_bias:
                                sp.dma_start(bu[:, s], k.dram[name + "_supb"]).then_inc(c_landed[s], 16)
                            return
                        sp.dma_start(cb[:, s], k.comb[e].partition_broadcast(P)).then_inc(c_landed[s], 16)
                        if up_bias:
                            sp.dma_start(bu[:, s], k.dram[name + "_upb"][e]).then_inc(c_landed[s], 16)

                    load_c(0, 0)
                    load_c(1, 1)
                    with sp.Fori(1, E // 2) as i:
                        for s in range(2):
                            e = i * 2 + s
                            sp.wait_ge(split_ready, e - 1)
                            load_w(e, s)
                            sp.wait_ge(down_done, (e - 1) * PER)
                            load_c(e, s)
                    if shared:
                        sp.wait_ge(split_ready, E - 1)
                        load_w(E, 0)
                        sp.wait_ge(down_done, (E - 1) * PER)
                        load_c(E, 0)

                @block.gpsimd
                def _(pool):
                    def split(e, s):
                        parts = ((wuH[:, s], wuL[:, s]), (wdH[:, s], wdL[:, s]))
                        split_weights(pool, k, high_ready, lambda _: pool.wait_ge(high_ready, (e + 1) * 2), parts,
                                      (wu[:, s], wd[:, s])).then_inc(split_ready, 1)

                    pool.wait_ge(k.weights, k.due)
                    split(0, 0)
                    split(1, 1)
                    with pool.Fori(1, E // 2) as i:
                        for s in range(2):
                            e = i * 2 + s
                            pool.wait_ge(down_done, (e - 1) * PER)
                            pool.wait_ge(w_landed[s], i * 32)
                            split(e, s)
                    if shared:
                        pool.wait_ge(down_done, (E - 1) * PER)
                        pool.wait_ge(w_landed[0], (E // 2) * 32)
                        split(E, 0)

                @block.tensor
                def _(pe):
                    for u in range(4):
                        pe.matmul(y_ps[:, u, :], k.ident[:], k.xT[:, u // 2, bass.ts(u % 2, HALF)],
                                  start=True, stop=False)
                    pe.wait_ge(x_low, CD)

                    def product(bank, wH, wL, rH, rL, start, stop):
                        pe.matmul(bank, wH, rH, start=start, stop=False)
                        pe.matmul(bank, wH, rL, start=False, stop=False)
                        return pe.matmul(bank, wL, rH, start=False, stop=stop)

                    def up(first, q, s, j):
                        pe.wait_ge(weighed, first + (q + 1))
                        at, half = bass.ts(j // 2, P), bass.ts(j % 2, HALF)
                        for g in range(UP):
                            for c in range(CD):
                                mm = product(up_ps[:, q % RP, g, :], wuH[:, s, g * CD + c, at],
                                             wuL[:, s, g * CD + c, at], xH[:, c, half], xL[:, c, half],
                                             c == 0, c == CD - 1)
                        mm.then_inc(up_done, 1)

                    def down(first, q, s, j, last):
                        pe.wait_ge(scaled, first + (q + 1))
                        for m in range(CD):
                            mm = product(y_ps[:, 2 * m + j % 2, :], wdH[:, s, j // 2, bass.ts(m, P)],
                                         wdL[:, s, j // 2, bass.ts(m, P)], hsH[:, q % R, :], hsL[:, q % R, :],
                                         False, last and j // 2 == HC - 1)
                        mm.then_inc(down_done, 1)

                    def run(items, first, arrive, last=False):
                        for q in range(len(items) + LAG):
                            if q < len(items):
                                s, j = items[q]
                                if j == 0:
                                    arrive(s)
                                up(first, q, s, j)
                            if q >= LAG:
                                down(first, q - LAG, *items[q - LAG], last)

                    with pe.Fori(0, E // 2) as i:
                        run(PAIR, i * (2 * PER), lambda s: pe.wait_ge(split_ready, i * 2 + (s + 1)))
                    if shared:
                        run(LONE, E * PER, lambda s: pe.wait_ge(split_ready, E + 1), last=not down_bias)
                    if down_bias:
                        pe.wait_ge(k.weights, k.due)
                        for u in range(4):
                            mm = pe.matmul(y_ps[:, u, :], bd[:, bass.ts(u // 2, P)], combT[:, bass.ts(u % 2, HALF)],
                                           start=False, stop=True)
                        mm.then_inc(closed, 1)

                @block.scalar
                def _(act):
                    act.copy(xH[:, 0, :], k.xn[:, 0, :]).then_inc(x_high, 1)
                    act.copy(xH[:, 1, :], k.xn[:, 1, :]).then_inc(x_high, 1)

                    def run(items, first, arrive):
                        for q in range(len(items) + 1):
                            if q < len(items):
                                s, j = items[q]
                                if j == 0:
                                    arrive(s)
                                act.wait_ge(up_done, first + (q + 1))
                                act.activation(h[:, q % R, :], up_ps[:, q % RP, 0, :], func,
                                               bias=bu[:, s, j // 2:j // 2 + 1] if up_bias else 0.0
                                               ).then_inc(activated, 1)
                            if q >= 1:
                                act.wait_ge(weighed, first + (q + RP))
                                act.copy(hsH[:, (q - 1) % R, :], hs[:, (q - 1) % R, :]).then_inc(high_taken, 1)

                    with act.Fori(0, E // 2) as i:
                        run(PAIR, i * (2 * PER), lambda s: act.wait_ge(c_landed[s], i * per_c + per_c))
                    if shared:
                        run(LONE, E * PER,
                            lambda s: act.wait_ge(c_landed[s], (E // 2) * per_c + 16) if up_bias else None)
                    if down_bias:
                        act.wait_ge(closed, 1)
                    else:
                        act.wait_ge(down_done, (LAST + 1) * PER)
                    for u in range(4):
                        x = k.xT[:, u // 2, bass.ts(u % 2, HALF)]
                        if shared and down_bias:
                            act.activation(x, y_ps[:, u, :], ACT.Identity, bias=bs[:, u // 2:u // 2 + 1])
                        else:
                            act.copy(x, y_ps[:, u, :])

                @block.vector
                def _(dve):
                    dve.sem_inc(weighed, RP)
                    for c in range(CD):
                        dve.wait_ge(x_high, c + 1)
                        dve.tensor_tensor(xL[:, c, :], k.xn[:, c, :], xH[:, c, :].bitcast(F32), ALU.subtract
                                          ).then_inc(x_low, 1)

                    def run(items, first, weighted):
                        for q in range(len(items) + 1):
                            if q < len(items):
                                s, j = items[q]
                                if j == 0 and weighted:
                                    weighted(s)
                                w = cb[:, s, bass.ts(j % 2, HALF)] if weighted else None
                                hq, hsq = h[:, q % R, :], hs[:, q % R, :]
                                dve.wait_ge(activated, first + (q + 1))
                                if gated and weighted:
                                    dve.tensor_tensor(hq, hq, w, ALU.mult).then_inc(gated_in, 1)
                                    dve.wait_ge(gated_in, first + (q + 1))
                                    dve.tensor_tensor(hsq, hq, up_ps[:, q % RP, 1, :], ALU.mult).then_inc(weighed, 1)
                                elif gated:
                                    dve.tensor_tensor(hsq, hq, up_ps[:, q % RP, 1, :], ALU.mult).then_inc(weighed, 1)
                                elif weighted:
                                    dve.tensor_tensor(hsq, hq, w, ALU.mult).then_inc(weighed, 1)
                                else:
                                    dve.tensor_copy(hsq, hq).then_inc(weighed, 1)
                            if q >= 1:
                                at = (q - 1) % R
                                dve.wait_ge(high_taken, first + q)
                                dve.tensor_tensor(hsL[:, at, :], hs[:, at, :], hsH[:, at, :].bitcast(F32),
                                                  ALU.subtract).then_inc(scaled, 1)

                    with dve.Fori(0, E // 2) as i:
                        run(PAIR, i * (2 * PER), lambda s: dve.wait_ge(c_landed[s], i * per_c + per_c))
                    if shared:
                        run(LONE, E * PER, None)


def prefetch(k, *pairs):
    nc = k.nc
    k.due += 16 * len(pairs)
    with nc.Block() as block:
        @block.sync
        def _(sp):
            for to, of in pairs:
                sp.dma_start(to, of).then_inc(k.weights, 16)


def project(k, src, weights, chunks_in, tiles, drain):
    nc = k.nc
    RING = 4
    items = [(m, n) for m in range(tiles) for n in range(2)]
    with k.stage("proj", "ready", "taken") as (sb, ps, ready, taken):
        bank = ps("bank", [P, RING, HALF])
        with nc.Block() as block:
            @block.tensor
            def _(pe):
                pe.wait_ge(k.weights, k.due)
                for q, (m, n) in enumerate(items):
                    if q >= RING:
                        pe.wait_ge(taken, q - RING + 1)
                    for c in range(chunks_in):
                        mm = pe.matmul(bank[:, q % RING, :], weights[:, c, bass.ts(m, P)],
                                       src[:, c, bass.ts(n, HALF)], start=c == 0, stop=c == chunks_in - 1)
                    mm.then_inc(ready, 1)

            @block.scalar
            def _(act):
                act.wait_ge(k.weights, k.due)
                for q, (m, n) in enumerate(items):
                    act.wait_ge(ready, q + 1)
                    drain(act, m, n, bank[:, q % RING, :]).then_inc(taken, 1)


def add_projection(k, src, weights, chunks_in, more=None, bias=None):
    nc = k.nc
    with k.stage("out", "summed", "added") as (sb, ps, summed, added):
        y_ps = ps("y_ps", [P, 4, HALF])
        with nc.Block() as block:
            @block.tensor
            def _(pe):
                pe.wait_ge(k.weights, k.due)
                for u in range(CD * 2):
                    m, n = u // 2, u % 2
                    for c in range(chunks_in):
                        mm = pe.matmul(y_ps[:, u, :], weights[:, c, bass.ts(m, P)], src[:, c, bass.ts(n, HALF)],
                                       start=c == 0, stop=c == chunks_in - 1)
                    mm.then_inc(summed, 1)

            @block.vector
            def _(dve):
                dve.wait_ge(k.weights, k.due)
                for c in range(CD):
                    if more is not None:
                        dve.tensor_tensor(k.xT[:, c, :], k.xT[:, c, :], more[:, c, :], ALU.add).then_inc(added, 1)
                for u in range(CD * 2):
                    m, n = u // 2, u % 2
                    x = k.xT[:, m, bass.ts(n, HALF)]
                    if more is not None:
                        dve.wait_ge(added, m + 1)
                    dve.wait_ge(summed, u + 1)
                    dve.scalar_tensor_tensor(x, y_ps[:, u, :], bias[:, m:m + 1] if bias is not None else 0.0, x,
                                             ALU.add, ALU.add)


def by_batch(ap):
    return ap.rearrange("p (b t) -> p b t", t=T)


def causal_conv(k, raw, out, w, b, chunks_in):
    nc = k.nc
    with k.stage("conv", "tapped", "convolved") as (sb, ps, tapped, convolved):
        acc = sb("acc", [P, chunks_in, N])
        with nc.Block() as block:
            @block.vector
            def _(dve):
                dve.wait_ge(k.weights, k.due)
                for c in range(chunks_in):
                    dve.tensor_scalar(acc[:, c, :], raw[:, c, :], w[:, c, 3:4], b[:, c:c + 1],
                                      ALU.mult, ALU.add).then_inc(tapped, 1)
                for s in range(1, 4):
                    for c in range(chunks_in):
                        a, r = by_batch(acc[:, c, :]), by_batch(raw[:, c, :])
                        dve.wait_ge(tapped, (s - 1) * chunks_in + c + 1)
                        dve.scalar_tensor_tensor(a[:, :, s:], r[:, :, 0:T - s], w[:, c, 3 - s:4 - s], a[:, :, s:],
                                                 ALU.mult, ALU.add).then_inc(tapped, 1)

            @block.scalar
            def _(act):
                for c in range(chunks_in):
                    act.wait_ge(tapped, 3 * chunks_in + c + 1)
                    act.activation(out[:, c, :], acc[:, c, :], ACT.Silu)


def multiply(k, out, a, b, chunks_in):
    nc = k.nc
    with nc.Block() as block:
        @block.vector
        def _(dve):
            for c in range(chunks_in):
                dve.tensor_tensor(out[:, c, :], a[:, c, :], b[:, c, :], ALU.mult)


def state_space_duality(k):
    nc = k.nc
    H, DI = 8, 512
    IC = DI // P
    layernorm_src = k.xT
    with ExitStack() as ctx:
        keep = lambda n, shape: ctx.enter_context(nc.sbuf_tensor(f"ssd_{n}", shape, F32))
        win = keep("win", [P, CD, 11 * P])
        wout = keep("wout", [P, IC, D])
        cw = keep("cw", [P, 6, 4])
        cb = keep("cb", [P, 6])
        dcol = keep("dcol", [P, IC])
        nw = keep("nw", [P, IC])
        ln = keep("ln", [P, 2, CD])
        dtb = keep("dtb", [H, 2])
        sel = keep("sel", [H, H, P])
        bar = keep("bar", [P, P])
        fresh = keep("fresh", [H, N])
        u = keep("u", [P, CD, N])
        zs = keep("zs", [P, IC, N])
        y = keep("y", [P, IC, N])
        dt = keep("dt", [H, 2, N])
        xc = keep("xc", [P, 6, N])
        d = k.dram
        prefetch(k, (ln[:], d["L0_attn_ln"]), (win[:], d["L0_attn_in"]), (wout[:], d["L0_attn_out"]),
                 (cw[:], d["L0_attn_cw"]), (cb[:], d["L0_attn_cb"]), (dcol[:], d["L0_attn_D"]),
                 (nw[:], d["L0_attn_nw"]), (dtb[:], d["L0_attn_dt"]), (sel[:], d["pick8"]), (bar[:], d["bar"]),
                 (fresh[:], d["fresh"].partition_broadcast(H)))
        layernorm(k, layernorm_src, k.xn, 1e-5)
        layernorm(k, k.xn, u, 1e-5, affine=(ln[:, 0, :], ln[:, 1, :]))
        with nc.sbuf_tensor("ssd_raw", [P, 6, N], F32) as raw:
            def drain(act, m, n, bank):
                if m < IC:
                    return act.activation(zs[:, m, bass.ts(n, HALF)], bank, ACT.Silu)
                if m < IC + 6:
                    return act.copy(raw[:, m - IC, bass.ts(n, HALF)], bank)
                return act.activation(dt[:, 0, bass.ts(n, HALF)], bank[0:H, :], ACT.Identity, bias=dtb[:, 0:1])
            project(k, u, win, CD, 11, drain)
            causal_conv(k, raw, xc, cw, cb, 6)

        softplus(k, dt[:, 0:1], 1, rows=H)
        with k.stage("dt", "a_ready", "step") as (sb, ps, a_ready, step):
            t2 = sb("t2", [H, N])
            na = sb("na", [H, 1])
            with nc.Block() as block:
                @block.scalar
                def _(act):
                    act.activation(na[:], dtb[:, 1:2], ACT.Exp).then_inc(a_ready, 1)

                @block.vector
                def _(dve):
                    link = Chain(dve, step)
                    dve.wait_ge(a_ready, 1)
                    link(dve.tensor_scalar(t2[:], dt[:, 0, :], na[:, 0:1], -1.0, ALU.mult, ALU.mult))
                    dve.tensor_tensor_scan(dt[:, 1, :], fresh[:], t2[:], 0.0, ALU.mult, ALU.add)

        with k.stage("ssd", "tile_in", "grams", "cums", "cols_ready", "x_turned", "cols_taken", "diffed", "masked",
                     "decayed", "weighed", "x_scaled", "summed", "y_out") as (
                sb, ps, tile_in, grams, cums, cols_ready, x_turned, cols_taken, diffed, masked, decayed, weighed,
                x_scaled, summed, y_out):
            xin = sb("xin", [P, 2, 6, P])
            din = sb("din", [H, 2, 2, P])
            cols = sb("cols", [P, 2, 2 * H])
            dec = sb("dec", [P, 2, H, P])
            xdt = sb("xdt", [P, 2, DI])
            g_ps = ps("g_ps", [P, 2, HALF])
            c_ps = ps("c_ps", [P, H, P])
            x_ps = ps("x_ps", [P, 2, HALF])
            y_ps = ps("y_ps", [P, 2, HALF])
            with nc.Block() as block:
                @block.gpsimd
                def _(pool):
                    def take(t, s):
                        pool.tensor_copy(xin[:, s], xc[:, :, bass.ds(t * P, P)]).then_inc(tile_in, 1)
                        pool.tensor_copy(din[:, s], dt[:, :, bass.ds(t * P, P)]).then_inc(tile_in, 1)
                    take(0, 0)
                    take(1, 1)
                    with pool.Fori(1, NT // 2) as i:
                        for s in range(2):
                            pool.wait_ge(y_out, (i * 2 + (s - 1)) * IC)
                            take(i * 2 + s, s)

                @block.tensor
                def _(pe):
                    def before(t, s):
                        pe.wait_ge(tile_in, t * 2 + 2)
                        pe.matmul(g_ps[:, s, 0:P], xin[:, s, IC, :], xin[:, s, IC + 1, :], start=True, stop=True)
                        pe.transpose(g_ps[:, s, P:P + H], din[:, s, 1, :], k.ident[0:H, 0:H])
                        pe.transpose(g_ps[:, s, P + H:P + 2 * H], din[:, s, 0, :],
                                     k.ident[0:H, 0:H]).then_inc(cols_ready, 1)
                        pe.wait_ge(diffed, t + 1)
                        for h in range(H):
                            mm = pe.matmul(c_ps[:, h, :], sel[:, h, :], din[:, s, 1, :], start=True, stop=True)
                        mm.then_inc(cums, 1)
                        for c in range(IC):
                            mm = pe.transpose(x_ps[:, s, bass.ts(c, P)], xin[:, s, c, :], k.ident[:])
                        mm.then_inc(x_turned, 1)

                    def after(t, s):
                        pe.wait_ge(weighed, t + 1)
                        pe.wait_ge(x_scaled, t + 1)
                        for h in range(H):
                            r = slice((h % 2) * 64, (h % 2) * 64 + 64)
                            mm = pe.matmul(y_ps[r, s, bass.ts(h // 2, P)], xdt[:, s, bass.ts(h, 64)],
                                           dec[:, s, h, :], start=True, stop=True)
                        mm.then_inc(summed, 1)

                    with pe.Fori(0, NT // 2) as i:
                        before(i * 2, 0)
                        before(i * 2 + 1, 1)
                        after(i * 2, 0)
                        after(i * 2 + 1, 1)

                @block.scalar
                def _(act):
                    with act.Fori(0, NT // 2) as i:
                        for s in range(2):
                            act.wait_ge(masked, i * 2 + (s + 1))
                            act.activation(dec[:, s], dec[:, s], ACT.Exp).then_inc(decayed, 1)

                @block.vector
                def _(dve):
                    dve.sem_inc(diffed, 1)

                    def before(t, s):
                        dve.wait_ge(cols_ready, t + 1)
                        dve.tensor_copy(cols[:, s, :], g_ps[:, s, P:P + 2 * H]).then_inc(cols_taken, 1)
                        dve.wait_ge(cols_taken, t + 1)
                        dve.wait_ge(cums, t + 1)
                        dve.tensor_tensor(dec[:, s], c_ps[:], over(cols[:, s, 0:H], 2, P),
                                          ALU.subtract).then_inc(diffed, 1)
                        dve.wait_ge(x_turned, t + 1)
                        dve.tensor_tensor(xdt[:, s, :].rearrange("p (h q) -> p h q", h=H),
                                          x_ps[:, s, :].rearrange("p (h q) -> p h q", h=H),
                                          over(cols[:, s, H:2 * H], 2, 64), ALU.mult).then_inc(x_scaled, 1)
                        dve.wait_ge(diffed, t + 2)
                        dve.tensor_tensor(dec[:, s], dec[:, s], over(bar[:], 1, H), ALU.add).then_inc(masked, 1)

                    def after(t, s):
                        dve.wait_ge(decayed, t + 1)
                        dve.tensor_tensor(dec[:, s], dec[:, s], over(g_ps[:, s, 0:P], 1, H),
                                          ALU.mult).then_inc(weighed, 1)

                    def last(t, s):
                        dve.wait_ge(summed, t + 1)
                        for c in range(IC):
                            dve.scalar_tensor_tensor(y[:, c, bass.ds(t * P, P)], xin[:, s, c, :], dcol[:, c:c + 1],
                                                     y_ps[:, s, bass.ts(c, P)], ALU.mult, ALU.add
                                                     ).then_inc(y_out, 1)

                    with dve.Fori(0, NT // 2) as i:
                        for step_ in (before, after, last):
                            step_(i * 2, 0)
                            step_(i * 2 + 1, 1)
        multiply(k, y, y, zs, IC)
        layernorm(k, y, y, 1e-5, affine=(nw, None), centre=False, width=IC)
        add_projection(k, y, wout, IC, more=k.xn)


def long_convolution(k):
    nc = k.nc
    DI, NS = 512, 16
    IC = DI // P
    PAD = 3
    with ExitStack() as ctx:
        keep = lambda n, shape: ctx.enter_context(nc.sbuf_tensor(f"lc_{n}", shape, F32))
        win = keep("win", [P, CD, 2 * DI])
        wconv = keep("wconv", [P, IC, 4, DI])
        wout = keep("wout", [P, IC, D])
        nw = keep("nw", [P, CD])
        inb = keep("inb", [P, 2 * IC])
        cvb = keep("cvb", [P, IC])
        outb = keep("outb", [P, CD])
        par = keep("par", [P, 3, IC, NS])
        dts = keep("dts", [P, 2, IC])
        iota = keep("iota", [P, T])
        kern = keep("kern", [P, IC, T])
        gs = keep("gs", [P, IC, N])
        xs = keep("xs", [P, IC, N])
        d = k.dram
        nm = "L1_attn_"
        prefetch(k, (par[:], d[nm + "par"]), (dts[:], d[nm + "dts"]), (iota[:], d["lags"].partition_broadcast(P)),
                 (nw[:], d[nm + "nw"]), (win[:], d[nm + "in"]), (inb[:], d[nm + "inb"]),
                 (wconv[:], d[nm + "conv"]), (cvb[:], d[nm + "cvb"]), (wout[:], d[nm + "out"]),
                 (outb[:], d[nm + "outb"]))
        layernorm(k, k.xT, k.xn, 1e-5)
        with k.stage("kern", "act_in", "act_out", "step") as (sb, ps, act_in, act_out, step):
            a = sb("a", [P, IC, NS])
            x = sb("x", [P, IC, NS])
            th = sb("th", [P, IC, NS])
            sg = sb("sg", [P, IC])
            e = sb("e", [P, IC, T, NS])
            with nc.Block() as block:
                @block.scalar
                def _(act):
                    act.wait_ge(k.weights, k.due)
                    act.activation(a[:], par[:, 0], ACT.Exp)
                    act.activation(sg[:], dts[:, 0], ACT.Sigmoid).then_inc(act_out, 1)
                    act.wait_ge(act_in, 1)
                    act.activation(th[:], x[:], ACT.Tanh, scale=0.5).then_inc(act_out, 1)
                    act.wait_ge(act_in, 2)
                    for c in range(IC):
                        act.activation(e[:, c], e[:, c], ACT.Exp).then_inc(act_out, 1)

                @block.vector
                def _(dve):
                    link = Chain(dve, step)
                    tt = dve.tensor_tensor
                    dve.wait_ge(act_out, 1)
                    link(dve.tensor_scalar(a[:], a[:], -1.0, None, ALU.mult))
                    tt(x[:], a[:], over(sg[:], 2, NS), ALU.mult).then_inc(act_in, 1)
                    dve.wait_ge(act_in, 1)
                    for c in range(IC):
                        ins = tt(e[:, c], over(x[:, c], 1, T), over(iota[:], 2, NS), ALU.mult)
                    ins.then_inc(act_in, 1)
                    dve.wait_ge(act_out, 2)
                    dve.wait_ge(act_in, 2)
                    link(dve.tensor_scalar(x[:], th[:], -1.0, 1.0, ALU.mult, ALU.add))
                    link(dve.tensor_scalar(a[:], a[:], 1e-8, None, ALU.add))
                    link(tt(x[:], x[:], a[:], ALU.mult))
                    link(dve.reciprocal(a[:], x[:]))
                    link(tt(th[:], th[:], par[:, 1], ALU.mult))
                    link(tt(th[:], th[:], par[:, 2], ALU.mult))
                    link(dve.scalar_tensor_tensor(th[:], th[:], 2.0, a[:], ALU.mult, ALU.mult))
                    for c in range(IC):
                        dve.wait_ge(act_out, 3 + c)
                        link(tt(e[:, c], e[:, c], over(th[:, c], 1, T), ALU.mult))
                        link(dve.tensor_reduce(kern[:, c, :], e[:, c], AX.X, ALU.add))
                    dve.tensor_tensor(kern[:, :, 0:1], kern[:, :, 0:1], over(dts[:, 1], 2, 1), ALU.add)
        with nc.sbuf_tensor("lc_pad", [P, IC, B * (T + PAD)], F32) as pad:
            padded = pad[:].rearrange("p c (b t) -> p c b t", t=T + PAD)
            with nc.sbuf_tensor("lc_u", [P, CD, N], F32) as u:
                with nc.Block() as block:
                    @block.gpsimd
                    def _(pool):
                        pool.memset(pad[:], 0.0)
                layernorm(k, k.xn, u, 1e-6, affine=(nw, None), centre=False)

                def drain(act, m, n, bank):
                    if m < IC:
                        to = padded[:, m, n * B // 2:(n + 1) * B // 2, PAD:]
                        return act.activation(to, by_batch(bank), ACT.Identity, bias=inb[:, m:m + 1])
                    return act.activation(gs[:, m - IC, bass.ts(n, HALF)], bank, ACT.Silu, bias=inb[:, m:m + 1])
                project(k, u, win, CD, 2 * IC, drain)
            with k.stage("fullconv", "ready", "taken") as (sb, ps, ready, taken):
                bank = ps("bank", [P, 4, HALF])
                items = [(m, n) for m in range(IC) for n in range(2)]
                with nc.Block() as block:
                    @block.tensor
                    def _(pe):
                        for q, (m, n) in enumerate(items):
                            if q >= 4:
                                pe.wait_ge(taken, q - 3)
                            for c in range(IC):
                                for tap in range(4):
                                    mm = pe.matmul(bank[:, q % 4, :], wconv[:, c, tap, bass.ts(m, P)],
                                                   padded[:, c, n * B // 2:(n + 1) * B // 2, tap:tap + T],
                                                   start=c + tap == 0, stop=c == IC - 1 and tap == 3)
                            mm.then_inc(ready, 1)

                    @block.scalar
                    def _(act):
                        for q, (m, n) in enumerate(items):
                            act.wait_ge(ready, q + 1)
                            act.activation(xs[:, m, bass.ts(n, HALF)], bank[:, q % 4, :], ACT.Silu,
                                           bias=cvb[:, m:m + 1]).then_inc(taken, 1)
        with nc.sbuf_tensor("lc_y", [P, IC, N], F32) as y:
            with k.stage("lags", "lagged") as (sb, ps, lagged):
                with nc.Block() as block:
                    @block.vector
                    def _(dve):
                        for c in range(IC):
                            dve.tensor_scalar(y[:, c, :], xs[:, c, :], kern[:, c, 0:1], None,
                                              ALU.mult).then_inc(lagged, 1)
                        for lag in range(1, T):
                            for c in range(IC):
                                a, r = by_batch(y[:, c, :]), by_batch(xs[:, c, :])
                                dve.wait_ge(lagged, (lag - 1) * IC + c + 1)
                                dve.scalar_tensor_tensor(a[:, :, lag:], r[:, :, 0:T - lag], kern[:, c, lag:lag + 1],
                                                         a[:, :, lag:], ALU.mult, ALU.add).then_inc(lagged, 1)
            multiply(k, y, y, gs, IC)
            add_projection(k, y, wout, IC, more=k.xn, bias=outb)



def softplus(k, v, parts, rows=P):
    nc = k.nc
    with k.stage("softplus", "absed", "exped", "shifted", "logged", "topped", "lost") as (
            sb, ps, absed, exped, shifted, logged, topped, lost):
        e = sb("e", [rows, parts, N])
        w = sb("w", [rows, parts, N])
        with nc.Block() as block:
            @block.scalar
            def _(act):
                for c in range(parts):
                    act.wait_ge(absed, c + 1)
                    act.activation(e[:, c, :], e[:, c, :], ACT.Exp, scale=-1.0).then_inc(exped, 1)
                for c in range(parts):
                    act.wait_ge(lost, c + 1)
                    act.activation(w[:, c, :], w[:, c, :], ACT.Ln).then_inc(logged, 1)

            @block.vector
            def _(dve):
                for c in range(parts):
                    dve.tensor_scalar(w[:, c, :], v[:, c, :], 0.0, None, ALU.max).then_inc(topped, 1)
                for c in range(parts):
                    dve.wait_ge(topped, c + 1)
                    dve.scalar_tensor_tensor(e[:, c, :], w[:, c, :], 2.0, v[:, c, :], ALU.mult,
                                             ALU.subtract).then_inc(absed, 1)
                for c in range(parts):
                    dve.wait_ge(absed, c + 1)
                    dve.tensor_copy(v[:, c, :], w[:, c, :]).then_inc(topped, 1)
                for c in range(parts):
                    dve.wait_ge(exped, c + 1)
                    dve.wait_ge(topped, parts + c + 1)
                    dve.tensor_scalar(w[:, c, :], e[:, c, :], 1.0, None, ALU.add).then_inc(shifted, 1)
                for c in range(parts):
                    dve.wait_ge(shifted, c + 1)
                    dve.scalar_tensor_tensor(e[:, c, :], w[:, c, :], -1.0, e[:, c, :], ALU.add,
                                             ALU.subtract).then_inc(lost, 1)
                for c in range(parts):
                    dve.wait_ge(lost, c + 1)
                    dve.tensor_tensor(v[:, c, :], v[:, c, :], e[:, c, :], ALU.subtract).then_inc(shifted, 1)
                for c in range(parts):
                    dve.wait_ge(logged, c + 1)
                    dve.wait_ge(shifted, parts + c + 1)
                    dve.tensor_tensor(v[:, c, :], v[:, c, :], w[:, c, :], ALU.add)


def selective_scan(k):
    nc = k.nc
    DI, NS = 512, 16
    IC = DI // P
    HB = B // 2
    nm, d = "L2_attn_", k.dram
    with ExitStack() as ctx:
        keep = lambda n, shape: ctx.enter_context(nc.sbuf_tensor(f"scan_{n}", shape, F32))
        wout = keep("wout", [P, IC, D])
        nw = keep("nw", [P, IC])
        dcol = keep("dcol", [P, IC])
        alog = keep("alog", [P, IC * NS])
        zs = keep("zs", [P, IC, N])
        xc = keep("xc", [P, IC, N])
        delta = keep("delta", [P, IC, N])
        with ExitStack() as early:
            brief = lambda n, shape: early.enter_context(nc.sbuf_tensor(f"scan_{n}", shape, F32))
            win = brief("win", [P, CD, 2 * DI])
            wx = brief("wx", [P, IC, P])
            wdt = brief("wdt", [NS, 1, DI])
            cw = brief("cw", [P, IC, 4])
            cb = brief("cb", [P, IC])
            dtb = brief("dtb", [P, IC])
            raw = brief("raw", [P, IC, N])
            xd = brief("xd", [3 * NS, 1, N])
            prefetch(k, (win[:], d[nm + "in"]), (cw[:], d[nm + "cw"]), (cb[:], d[nm + "cb"]), (wx[:], d[nm + "x"]),
                     (wdt[:, 0, :], d[nm + "wdt"]), (dtb[:], d[nm + "dtb"]), (alog[:], d[nm + "A"]),
                     (dcol[:], d[nm + "D"]), (nw[:], d[nm + "nw"]), (wout[:], d[nm + "out"]))
            layernorm(k, k.xT, k.xn, 1e-5)

            def drain(act, m, n, bank):
                if m < IC:
                    return act.copy(raw[:, m, bass.ts(n, HALF)], bank)
                return act.activation(zs[:, m - IC, bass.ts(n, HALF)], bank, ACT.Silu)
            project(k, k.xn, win, CD, 2 * IC, drain)
            causal_conv(k, raw, xc, cw, cb, IC)
            project(k, xc, wx, IC, 1, lambda act, m, n, bank: act.copy(xd[:, 0, bass.ts(n, HALF)], bank[0:3 * NS, :]))
            with k.stage("bc", "stored") as (sb, ps, stored):
                with nc.Block() as block:
                    @block.sync
                    def _(sp):
                        sp.dma_start(k.bc, xd[NS:3 * NS, 0, :]).then_inc(stored, 16)
                        sp.wait_ge(stored, 16)
            project(k, xd[0:NS], wdt, 1, IC,
                    lambda act, m, n, bank: act.activation(delta[:, m, bass.ts(n, HALF)], bank, ACT.Identity,
                                                           bias=dtb[:, m:m + 1]))
        softplus(k, delta, IC)
        y = keep("y", [P, IC, N])
        with k.stage("scan", "rows_landed", "a_ready", "in_taken", "decay_out", "decay_ready", "drive_ready",
                     "scanned", "read_out", "summed", "y_out", "a_exped", "zeroed") as (
                sb, ps, rows_landed, a_ready, in_taken, decay_out, decay_ready, drive_ready, scanned, read_out,
                summed, y_out, a_exped, zeroed):
            RING = 4
            none = sb("none", [P, HB])
            bb = sb("bb", [P, NS, HALF])
            cc = sb("cc", [P, NS, HALF])
            av = sb("av", [P, IC * NS])
            dl = sb("dl", [P, HALF])
            ut = sb("ut", [P, HALF])
            ac = sb("ac", [P, NS])
            da = sb("da", [P, RING, HALF])
            db = sb("db", [P, RING, HALF])
            hh = sb("hh", [P, RING, HALF])
            hc = sb("hc", [P, RING, HALF])
            y_ps = ps("y_ps", [P, HALF])
            with nc.Block() as block:
                @block.sync
                def _(sp):
                    for g in range(2):
                        for n in range(NS):
                            if g:
                                sp.wait_ge(read_out, (IC - 1) * NS + n + 1 + RING)
                            for to, r in ((bb, n), (cc, NS + n)):
                                sp.dma_start(to[:, n, :], k.bc[r, bass.ts(g, HALF)].partition_broadcast(P)
                                             ).then_inc(rows_landed, 16)

                @block.scalar
                def _(act):
                    act.activation(av[:], alog[:], ACT.Exp).then_inc(a_exped, 1)
                    for g in range(2):
                        with act.Fori(0, IC) as c:
                            it = c + g * IC
                            act.wait_ge(in_taken, it * 3 + 3)
                            for n in range(NS):
                                q = it * NS + n
                                act.wait_ge(scanned, q + 1)
                                act.activation(da[:, n % RING, :], dl[:], ACT.Exp,
                                               scale=ac[:, n:n + 1]).then_inc(decay_out, 1)

                @block.gpsimd
                def _(pool):
                    pool.memset(none[:], 0.0).then_inc(zeroed, 1)
                    pool.wait_ge(zeroed, 1)
                    for g in range(2):
                        pool.wait_ge(rows_landed, (g + 1) * 2 * NS * 16)
                        with pool.Fori(0, IC) as c:
                            it = c + g * IC
                            pool.wait_ge(in_taken, it * 3 + 3)
                            for n in range(NS):
                                q = it * NS + n
                                pool.wait_ge(scanned, q + 1)
                                pool.tensor_tensor(db[:, n % RING, :], ut[:], bb[:, n, :],
                                                   ALU.mult).then_inc(drive_ready, 1)
                                pool.wait_ge(decay_out, q + 1)
                                pool.tensor_tensor(by_batch(da[:, n % RING, :])[:, :, 0], none[:], none[:],
                                                   ALU.mult).then_inc(decay_ready, 1)

                @block.vector
                def _(dve):
                    dve.sem_inc(scanned, RING)
                    dve.sem_inc(summed, RING)
                    dve.sem_inc(read_out, RING)
                    dve.wait_ge(a_exped, 1)
                    dve.tensor_scalar(av[:], av[:], -1.0, None, ALU.mult).then_inc(a_ready, 1)
                    dve.wait_ge(a_ready, 1)
                    for g in range(2):
                        dve.wait_ge(rows_landed, (g + 1) * 2 * NS * 16)
                        with dve.Fori(0, IC) as c:
                            it = c + g * IC
                            half = bass.ds(c * N + g * HALF, HALF)
                            flat = lambda t: t[:].rearrange("p c n -> p (c n)")[:, half]
                            dve.tensor_copy(dl[:], flat(delta)).then_inc(in_taken, 1)
                            dve.tensor_tensor(ut[:], flat(delta), flat(xc), ALU.mult).then_inc(in_taken, 1)
                            dve.tensor_copy(ac[:], av[:, bass.ds(c * NS, NS)]).then_inc(in_taken, 1)

                            def read(n):
                                q = it * NS + n
                                dve.wait_ge(scanned, q + 1 + RING)
                                dve.wait_ge(summed, q + 1)
                                dve.tensor_tensor(hc[:, n % RING, :], hh[:, n % RING, :], cc[:, n, :],
                                                  ALU.mult).then_inc(read_out, 1)

                            for n in range(NS):
                                q = it * NS + n
                                dve.wait_ge(decay_ready, q + 1)
                                dve.wait_ge(read_out, q + 1)
                                dve.wait_ge(drive_ready, q + 1)
                                dve.tensor_tensor_scan(hh[:, n % RING, :], da[:, n % RING, :], db[:, n % RING, :],
                                                       0.0, ALU.mult, ALU.add).then_inc(scanned, 1)
                                if n >= 1:
                                    read(n - 1)
                            read(NS - 1)
                            dve.wait_ge(summed, it * NS + NS + RING)
                            dve.tensor_copy(flat(y), y_ps[:]).then_inc(y_out, 1)

                @block.tensor
                def _(pe):
                    for g in range(2):
                        with pe.Fori(0, IC) as c:
                            it = c + g * IC
                            for n in range(NS):
                                pe.wait_ge(read_out, it * NS + (n + 1 + RING))
                                if n == 0:
                                    pe.wait_ge(y_out, it)
                                pe.matmul(y_ps[:], k.ident[:], hc[:, n % RING, :], start=n == 0,
                                          stop=n == NS - 1).then_inc(summed, 1)
        with k.stage("skip", "skipped") as (sb, ps, skipped):
            with nc.Block() as block:
                @block.vector
                def _(dve):
                    for c in range(IC):
                        dve.scalar_tensor_tensor(y[:, c, :], xc[:, c, :], dcol[:, c:c + 1], y[:, c, :], ALU.mult,
                                                 ALU.add).then_inc(skipped, 1)
                    for c in range(IC):
                        dve.wait_ge(skipped, c + 1)
                        dve.tensor_tensor(y[:, c, :], y[:, c, :], zs[:, c, :], ALU.mult)
        layernorm(k, y, y, 1e-8, affine=(nw, None), centre=False, width=IC)
        add_projection(k, y, wout, IC)



def correlation_attention(k):
    nc = k.nc
    heads, dk, slot = 16, 16, 32
    per, IC = P // slot, HALF // P
    nm, d = "L3_attn_", k.dram
    with ExitStack() as ctx:
        keep = lambda n, shape: ctx.enter_context(nc.sbuf_tensor(f"corr_{n}", shape, F32))
        wqk = keep("wqk", [P, CD, 2 * HALF])
        wv = keep("wv", [P, CD, HALF])
        wo = keep("wo", [P, IC, D])
        vmat = keep("vmat", [P, P])
        qk = keep("qk", [P, 2 * IC, N])
        oT = keep("oT", [P, IC, N])
        prefetch(k, (wqk[:], d[nm + "Wqk"]), (vmat[:], d["slotvar"]), (wv[:], d[nm + "Wv"]), (wo[:], d[nm + "Wo"]))
        layernorm(k, k.xT, k.xn, 1e-5)
        with k.stage("centre", "step") as (sb, ps, step):
            mean = sb("mean", [P, CD * 2 * heads])
            with nc.Block() as block:
                @block.vector
                def _(dve):
                    link = Chain(dve, step)
                    dve.wait_ge(k.weights, k.due)
                    w = wqk[:].rearrange("p c (h r) -> p (c h) r", r=slot)[:, :, 0:dk]
                    link(dve.tensor_reduce(mean[:], w, AX.X, ALU.add))
                    link(dve.tensor_scalar(mean[:], mean[:], 1.0 / dk, None, ALU.mult))
                    dve.tensor_tensor(w, w, over(mean[:], 2, dk), ALU.subtract)
        with k.stage("qk", "ready", "squared", "var_ready", "copied", "added") as (
                sb, ps, ready, squared, var_ready, copied, added):
            sq = sb("sq", [P, 2, HALF])
            bank = ps("bank", [P, 2, HALF])
            vbank = ps("vbank", [P, 2, HALF])
            items = [(m, n) for m in range(2 * IC) for n in range(2)]
            with nc.Block() as block:
                @block.tensor
                def _(pe):
                    for q in range(len(items) + 1):
                        if q < len(items):
                            m, n = items[q]
                            if q >= 2:
                                pe.wait_ge(squared, q - 1)
                            for c in range(CD):
                                mm = pe.matmul(bank[:, q % 2, :], wqk[:, c, bass.ts(m, P)],
                                               k.xn[:, c, bass.ts(n, HALF)], start=c == 0, stop=c == CD - 1)
                            mm.then_inc(ready, 1)
                        if q >= 1:
                            if q >= 3:
                                pe.wait_ge(added, q - 2)
                            pe.wait_ge(squared, q)
                            pe.matmul(vbank[:, (q - 1) % 2, :], vmat[:], sq[:, (q - 1) % 2, :], start=True,
                                      stop=True).then_inc(var_ready, 1)

                @block.scalar
                def _(act):
                    for q, (m, n) in enumerate(items):
                        act.wait_ge(ready, q + 1)
                        act.copy(qk[:, m, bass.ts(n, HALF)], bank[:, q % 2, :]).then_inc(copied, 1)
                        if q >= 2:
                            act.wait_ge(var_ready, q - 1)
                        act.activation(sq[:, q % 2, :], bank[:, q % 2, :], ACT.Square).then_inc(squared, 1)

                @block.vector
                def _(dve):
                    for q, (m, n) in enumerate(items):
                        x = qk[:, m, bass.ts(n, HALF)]
                        dve.wait_ge(copied, q + 1)
                        dve.wait_ge(var_ready, q + 1)
                        dve.tensor_tensor(x, x, vbank[:, q % 2, :], ALU.add).then_inc(added, 1)

        with k.stage("corr", "zeroed", "batch_in", "v_ready", "v_taken", "scored", "shifted", "exped", "normed",
                     "turned", "turned_v", "mixed", "out_taken", "step") as (
                sb, ps, zeroed, batch_in, v_ready, v_taken, scored, shifted, exped, normed, turned, turned_v,
                mixed, out_taken, step):
            W = per * T
            xb = sb("xb", [P, 2, CD, 2, T])
            qblk = sb("qblk", [P, 2, IC, W])
            vb = sb("vb", [P, 2, HALF])
            sm = sb("sm", [P, 2, 2 * IC, T])
            row = sb("row", [P, 2, 3, 2 * IC])
            pT = sb("pT", [P, IC, P])
            s_ps = ps("s_ps", [P, 2, 2 * IC, T])
            v_ps = ps("v_ps", [P, HALF])
            t_ps = ps("t_ps", [P, IC, P])
            o_ps = ps("o_ps", [P, 2, IC, P])
            with nc.Block() as block:
                @block.gpsimd
                def _(pool):
                    pool.memset(qblk[:], 0.0).then_inc(zeroed, 1)
                    pool.wait_ge(zeroed, 1)

                    def take(b, s):
                        if not (isinstance(b, int) and b == 0):
                            pool.wait_ge(batch_in, b * (per + 1))
                        pool.tensor_copy(xb[:, s], over(k.xn[:, :, bass.ds(b * T, T)], 2, 2)).then_inc(batch_in, 1)
                        pool.wait_ge(batch_in, b * (per + 1) + 1)
                        for g in range(per):
                            r = slice(g * slot, (g + 1) * slot)
                            pool.tensor_copy(qblk[r, s, :, bass.ts(g, T)],
                                             qk[r, 0:IC, bass.ds(b * T, T)]).then_inc(batch_in, 1)
                    take(0, 0)
                    take(1, 1)
                    with pool.Fori(1, B // 2) as i:
                        for s in range(2):
                            pool.wait_ge(scored, i * 2 + (s - 1))
                            take(i * 2 + s, s)

                @block.tensor
                def _(pe):
                    def before(b, s):
                        pe.wait_ge(batch_in, (b + 1) * (per + 1))
                        pe.wait_ge(v_taken, b + 1)
                        for c in range(CD):
                            mm = pe.matmul(v_ps[:], xb[:, s, c].rearrange("p a t -> p (a t)"), wv[:, c, :], start=c == 0, stop=c == CD - 1)
                        mm.then_inc(v_ready, 1)
                        for j in range(2 * IC):
                            mm = pe.matmul(s_ps[:, s, j, :], qblk[:, s, j // 2, bass.ts(j % 2, P)],
                                           qk[:, IC + j // 2, bass.ds(b * T, T)], start=True, stop=True)
                        mm.then_inc(scored, 1)

                    def after(b, s):
                        pe.wait_ge(normed, b + 1)
                        for m in range(IC):
                            mm = pe.transpose(t_ps[:, m, :], sm[:, s, 2 * m:2 * m + 2, :].rearrange(
                                "p a t -> p (a t)"), k.ident[:])
                        mm.then_inc(turned, 1)
                        pe.wait_ge(turned_v, b + 1)
                        pe.wait_ge(out_taken, b + 1)
                        for m in range(IC):
                            for a in range(2):
                                r = slice(a * T, (a + 1) * T)
                                mm = pe.matmul(o_ps[:, a, m, :], vb[r, s, bass.ts(m, P)], pT[r, m, :],
                                               start=True, stop=True)
                        mm.then_inc(mixed, 1)

                    with pe.Fori(0, B // 2) as i:
                        before(i * 2, 0)
                        before(i * 2 + 1, 1)
                        after(i * 2, 0)
                        after(i * 2 + 1, 1)

                @block.scalar
                def _(act):
                    act.sem_inc(v_taken, 1)
                    act.sem_inc(out_taken, 1)

                    with act.Fori(0, B // 2) as i:
                        for s in range(2):
                            b = i * 2 + s
                            act.wait_ge(v_ready, b + 1)
                            act.copy(vb[:, s, :], v_ps[:]).then_inc(v_taken, 1)
                        for s in range(2):
                            b = i * 2 + s
                            act.wait_ge(shifted, b + 1)
                            act.activation(sm[:, s], sm[:, s], ACT.Exp, scale=1.0 / dk).then_inc(exped, 1)
                        for s in range(2):
                            b = i * 2 + s
                            act.wait_ge(mixed, b + 1)
                            for g in range(per):
                                r = slice(g * slot, (g + 1) * slot)
                                cp = act.copy(oT[r, :, bass.ds(b * T, T)], o_ps[r, g // 2, :, bass.ts(g % 2, T)])
                            cp.then_inc(out_taken, 1)

                @block.vector
                def _(dve):
                    def norm(b, s, base):
                        dve.wait_ge(exped, b + 1)
                        dve.tensor_reduce(row[:, s, 1, :], sm[:, s], AX.X, ALU.add).then_inc(step, 1)
                        dve.wait_ge(step, base + 1)
                        dve.reciprocal(row[:, s, 2, :], row[:, s, 1, :]).then_inc(step, 1)
                        dve.wait_ge(step, base + 2)
                        dve.tensor_tensor(sm[:, s], sm[:, s], over(row[:, s, 2, :], 2, T),
                                          ALU.mult).then_inc(normed, 1)

                    with dve.Fori(0, B // 2) as i:
                        for s in range(2):
                            dve.wait_ge(scored, i * 2 + (s + 1))
                            dve.tensor_reduce(row[:, s, 0, :], s_ps[:, s], AX.X, ALU.max).then_inc(step, 1)
                            dve.wait_ge(step, i * 6 + (s + 1))
                            dve.tensor_tensor(sm[:, s], s_ps[:, s], over(row[:, s, 0, :], 2, T),
                                              ALU.subtract).then_inc(shifted, 1)
                        for s in range(2):
                            norm(i * 2 + s, s, i * 6 + (2 + 2 * s))
                        for s in range(2):
                            dve.wait_ge(turned, i * 2 + (s + 1))
                            dve.tensor_copy(pT[:], t_ps[:]).then_inc(turned_v, 1)
        add_projection(k, oT, wo, IC)


def masked_cross_attention(k):
    nc = k.nc
    heads, dk = 4, 64
    IC = heads * dk // P
    NK = S // P
    KEYS = S + T
    KR = DC - P
    nm, d = "L3_xattn_", k.dram
    with ExitStack() as ctx:
        keep = lambda n, shape: ctx.enter_context(nc.sbuf_tensor(f"mx_{n}", shape, F32))
        wq = keep("wq", [P, CD, IC * P])
        wl = keep("wl", [P, CD, 2 * IC * P])
        wc = keep("wc", [P, 3, 2 * IC * P])
        wkH, wkL = (ctx.enter_context(nc.sbuf_tensor(f"mx_wk{n}", [P, 2, IC * P], F32R)) for n in "HL")
        wv = keep("wv", [P, 2, IC * P])
        bkb = keep("bkb", [P, IC * P])
        m8 = ctx.enter_context(nc.sbuf_tensor("mx_m8", [B, S // 4], mybir.dt.uint32))
        bars = ctx.enter_context(nc.sbuf_tensor("mx_bars", [P, S], F32R))
        wo = keep("wo", [P, IC, D])
        bo = keep("bo", [P, CD])
        lnl = keep("lnl", [P, 2, CD])
        lnx = keep("lnx", [P, 2, 3])
        qg = keep("qg", [P, 2])
        pair = keep("pair", [P, P])
        lat = keep("lat", [P, CD, N])
        qT = keep("qT", [P, IC, N])
        oT = keep("oT", [P, IC, N])
        prefetch(k, (lnl[:], d[nm + "lnl"]), (lnx[:], d[nm + "lnx"]), (qg[:], d[nm + "qg"]), (pair[:], d["pair"]),
                 (m8[:], d["mask"]), (wq[:], d[nm + "Wq"]), (wc[:], d[nm + "Wkv"]), (wl[:], d[nm + "Wlkv"]), (wo[:], d[nm + "Wo"]),
                 (bo[:], d[nm + "bo"]))
        layernorm(k, k.xT, k.xn, 1e-5)
        layernorm(k, k.xn, lat, 1e-5, affine=(lnl[:, 0, :], lnl[:, 1, :]))
        with k.stage("fold", "spread", "bias_ready", "scaled", "sums_ready", "centred", "split", "step",
                     "cleared", "cast") as (
                sb, ps, spread, bias_ready, scaled, sums_ready, centred, split, step, cleared, cast):
            bB = sb("bB", [P, 2, P])
            mf = sb("mf", [B, S])
            b_ps = ps("b_ps", [P, 2 * IC * P])
            s_ps = ps("s_ps", [P, 2 * IC * P])
            with nc.Block() as block:
                @block.tensor
                def _(pe):
                    pe.wait_ge(spread, 2)
                    for c in range(2):
                        mm = pe.matmul(b_ps[:], bB[:, c, :], wc[:, c, :], start=c == 0, stop=c == 1)
                    mm.then_inc(bias_ready, 1)
                    pe.wait_ge(scaled, 3)
                    for c in range(2):
                        mm = pe.matmul(s_ps[:], k.ones[:], wc[:, c, :], start=c == 0, stop=c == 1)
                    mm.then_inc(sums_ready, 1)

                @block.gpsimd
                def _(pool):
                    pool.memset(bars[:].bitcast(F32), 0.0).then_inc(cleared, 1)

                @block.vector
                def _(dve):
                    dve.wait_ge(k.weights, k.due)
                    for c in range(2):
                        dve.tensor_scalar(bB[:, c, :], k.ones[:], lnx[:, 1, c:c + 1], None, ALU.mult
                                          ).then_inc(spread, 1)
                    dve.tensor_copy(mf[:], m8[:].bitcast(mybir.dt.uint8)).then_inc(cast, 1)
                    dve.wait_ge(cleared, 1)
                    dve.wait_ge(cast, 1)
                    dve.tensor_scalar(bars[0:B, :], mf[:], -1.0, 1e30, ALU.add, ALU.mult)
                    dve.wait_ge(bias_ready, 1)
                    for c in range(3):
                        dve.tensor_scalar(wc[:, c, :], wc[:, c, :], lnx[:, 0, c:c + 1], None, ALU.mult
                                          ).then_inc(scaled, 1)
                    dve.tensor_copy(bkb[:], b_ps[:, 0:IC * P])
                    dve.wait_ge(sums_ready, 1)
                    dve.wait_ge(scaled, 3)
                    for c, rows in ((0, P), (1, KR), (2, P)):
                        dve.scalar_tensor_tensor(wc[0:rows, c, :], s_ps[0:rows, :], -1.0 / DC, wc[0:rows, c, :],
                                                 ALU.mult, ALU.add).then_inc(centred, 1)
                    dve.wait_ge(centred, 3)
                    for c in range(2):
                        dve.tensor_copy(wv[:, c, :], wc[:, c, IC * P:2 * IC * P]).then_inc(split, 1)
                    for c in range(2):
                        dve.tensor_copy(wkH[:, c, :], wc[:, 2 * c, 0:IC * P]).then_inc(split, 1)
                    dve.wait_ge(split, 4)
                    for c in range(2):
                        dve.tensor_tensor(wkL[:, c, :], wc[:, 2 * c, 0:IC * P], wkH[:, c, :].bitcast(F32),
                                          ALU.subtract)
                    dve.tensor_copy(wv[KR:KR + 1, 1, :], b_ps[KR:KR + 1, IC * P:2 * IC * P])
                    dve.tensor_tensor(qg[:, 0:1], qg[:, 0:1], qg[:, 1:2], ALU.mult).then_inc(step, 1)
                    dve.wait_ge(step, 1)
                    dve.tensor_scalar(qg[:, 0:1], qg[:, 0:1], dk ** -0.5, None, ALU.mult)
        project(k, lat, wq, CD, IC, lambda act, m, n, bank: act.copy(qT[:, m, bass.ts(n, HALF)], bank))
        with k.stage("qnorm", "squared", "summed", "shifted", "rooted", "step") as (
                sb, ps, squared, summed, shifted, rooted, step):
            sq = sb("sq", [P, IC, N])
            n_ps = ps("n_ps", [P, IC, N])
            with nc.Block() as block:
                @block.scalar
                def _(act):
                    act.activation(sq[:], qT[:], ACT.Square).then_inc(squared, 1)
                    act.wait_ge(summed, 1)
                    act.activation(sq[:], n_ps[:], ACT.Sqrt, scale=1.0 / dk).then_inc(rooted, 1)

                @block.tensor
                def _(pe):
                    pe.wait_ge(squared, 1)
                    for c in range(IC):
                        for n in range(2):
                            mm = pe.matmul(n_ps[:, c, bass.ts(n, HALF)], pair[:], sq[:, c, bass.ts(n, HALF)],
                                           start=True, stop=True)
                    mm.then_inc(summed, 1)

                @block.vector
                def _(dve):
                    link = Chain(dve, step)
                    dve.wait_ge(rooted, 1)
                    link(dve.tensor_scalar(sq[:], sq[:], 1e-8, None, ALU.max))
                    link(dve.reciprocal(sq[:], sq[:]))
                    dve.scalar_tensor_tensor(qT[:], qT[:], qg[:, 0:1], sq[:], ALU.mult, ALU.mult)

        attend_masked(k, wl, wkH, wkL, wv, bkb, bars, lat, qT, oT)
        add_projection(k, oT, wo, IC, bias=bo)


def attend_masked(k, wl, wkH, wkL, wv, bkb, bars, lat, qT, oT):
    nc = k.nc
    heads, dk = 4, 64
    IC = heads * dk // P
    KW = IC * P
    NK = S // P
    KEYS = S + T
    KR = DC - P
    G = NK // 2
    KUSES = G + 1
    PUSES = 3
    USES = KUSES + IC * PUSES
    d = k.dram
    with k.stage("mx", "t_landed", "n_landed", "set_up", "batch_in", "split_step",
                 "split_ready", "xs_ready", "var_ready", "var_rooted", "rs_ready", "kproj", "kp_taken", "squared",
                 "sums_ready", "sums_rooted", "keys_ready", "turned", "taken0", "taken1", "scored",
                 "maxed", "exped", "inverted", "mixed", "normed", "mix_turned", "mix_taken", "projected",
                 "out_taken", "step") as (
            sb, ps, t_landed, n_landed, set_up, batch_in, split_step, split_ready,
            xs_ready, var_ready, var_rooted, rs_ready, kproj, kp_taken, squared, sums_ready, sums_rooted,
            keys_ready, turned, taken0, taken1, scored, maxed, exped, inverted, mixed, normed,
            mix_turned, mix_taken, projected, out_taken, step):
        taken = (taken0, taken1)
        cT = sb("cT", [P, 2, S])
        cH = sb("cH", [P, 2, S], F32R)
        cL = sb("cL", [P, 2, S], F32R)
        cR = sb("cR", [P, 2, S], F32R)
        land = sb("land", [P, NK, DC])
        xs = sb("xs", [P, 2, NK, DC + 1])
        pick = sb("pick", [P, 2, P], F32R)
        lb = sb("lb", [P, 2, CD, T])
        qblk = sb("qblk", [P, 2, IC, P])
        st = sb("st", [P, NK, 6])
        mv = sb("mv", [P, NK, 2])
        rs = sb("rs", [P, 2, NK])
        kv = sb("kv", [P, NK + 1, KW])
        sq = sb("sq", [P, NK + 1, KW])
        rn = sb("rn", [P, NK + 1, heads])
        keysT = sb("keysT", [P, 2, IC, KEYS])
        vl = sb("vl", [P, 2, KW])
        sm = sb("sm", [P, IC, (NK + 1) * P])
        pT = sb("pT", [P, IC, NK + 1, P])
        col = sb("col", [P, 3, IC])
        mix = sb("mix", [P, DC + 1])
        mixT = sb("mixT", [P, 2, P])
        kp = ps("kp", [P, 2, HALF])
        tp = ps("tp", [P, 2, HALF])
        s_ps = ps("s_ps", [P, 3, HALF])
        av = ps("av", [P, HALF])

        def after(i, s):
            return (i, 1) if s == 0 else (i + 1, 0)

        def every_batch(eng, step_of):
            with eng.Fori(0, B // 2 - 1) as i:
                step_of(i, 0, 2)
                step_of(i, 1, 2)
            step_of(B // 2 - 1, 0, 1)
            step_of(B // 2 - 1, 1, 0)

        def bank_of(s, v):
            return (USES * s + v) % 2

        def nth(i, s, v):
            return i * USES + (USES * s + v) // 2

        with nc.Block() as block:
            @block.sync
            def _(sp):
                def load_t(b):
                    sp.dma_start(cT[:, 0, :], d["ctxT"][b, 0:P, :]).then_inc(t_landed, 16)
                    for g in range(2):
                        sp.dma_start(cT[g * KR:(g + 1) * KR, 1, :], d["ctxT"][b, P:DC, :]).then_inc(t_landed, 16)

                def load_n(b):
                    sp.dma_start(land[:], d["ctx"][b].rearrange("(j p) d -> p j d", p=P)).then_inc(n_landed, 16)

                load_t(0)
                load_n(0)
                sp.wait_ge(split_ready, 1)
                load_t(1)
                sp.wait_ge(xs_ready, 1)
                load_n(1)
                with sp.Fori(1, B // 2) as i:
                    for s in range(2):
                        b = i * 2 + s
                        sp.wait_ge(split_ready, b)
                        load_t(b)
                        sp.wait_ge(xs_ready, b)
                        load_n(b)

            @block.gpsimd
            def _(pool):
                pool.memset(qblk[:], 0.0).then_inc(set_up, 1)
                pool.memset(kv[:, NK, :], 1.0).then_inc(set_up, 1)
                pool.memset(pT[:, :, NK, :], 0.0).then_inc(set_up, 1)
                pool.memset(vl[:], 0.0).then_inc(set_up, 1)
                pool.memset(mixT[:, 1, :], 0.0).then_inc(set_up, 1)
                pool.memset(xs[:, :, :, DC:DC + 1], 1.0).then_inc(set_up, 1)
                pool.memset(sm[:, :, KEYS:], 0.0).then_inc(set_up, 1)
                pool.wait_ge(set_up, 7)

                def take(b, s):
                    pool.tensor_copy(lb[:, s], lat[:, :, bass.ds(b * T, T)]).then_inc(batch_in, 1)
                    pool.tensor_copy(pick[:, s, :], k.ident[:, bass.ds(b, 1)].broadcast_to([P, P])).then_inc(batch_in, 1)
                    pool.wait_ge(batch_in, b * 4 + 2)
                    for g in range(2):
                        r = slice(g * dk, (g + 1) * dk)
                        pool.tensor_copy(qblk[r, s, :, bass.ts(g, T)],
                                         qT[r, :, bass.ds(b * T, T)]).then_inc(batch_in, 1)
                    pool.wait_ge(batch_in, b * 4 + 4)

                def scale(b, s):
                    pool.wait_ge(rs_ready, b + 1)
                    pool.tensor_tensor(xs[:, s, :, 0:DC], land[:], over(rs[:, s, :], 2, DC), ALU.mult
                                       ).then_inc(xs_ready, 1)
                    pool.wait_ge(xs_ready, b + 1)

                def split(b, s):
                    pool.wait_ge(t_landed, b * 48 + 48)
                    x = cT[:, 0, :].rearrange("p (j q) -> p j q", q=P)
                    pool.tensor_tensor(cH[:, s].rearrange("p (j q) -> p j q", q=P), x, over(k.ones[:], 1, NK),
                                       ALU.mult).then_inc(split_step, 1)
                    pool.tensor_copy(cR[:, s], cT[:, 1, :]).then_inc(split_step, 1)
                    pool.wait_ge(split_step, b * 3 + 2)
                    pool.tensor_tensor(cL[:, s], cT[:, 0, :], cH[:, s].bitcast(F32), ALU.subtract
                                       ).then_inc(split_step, 1)
                    pool.wait_ge(split_step, b * 3 + 3)
                    pool.tensor_tensor(cR[KR:P, s], cT[KR:P, 1, :], cR[KR:P, s].bitcast(F32), ALU.subtract
                                       ).then_inc(split_ready, 1)
                    pool.wait_ge(split_ready, b + 1)

                def batch(i, s, more):
                    b = i * 2 + s
                    if more >= 1:
                        pool.wait_ge(out_taken, b * IC + 1)
                        scale(b + 1, 1 - s)
                        take(b + 1, 1 - s)
                    if more >= 2:
                        pool.wait_ge(kproj, (b + 1) * KUSES)
                        split(b + 2, s)

                take(0, 0)
                split(0, 0)
                scale(0, 0)
                split(1, 1)
                every_batch(pool, batch)

            @block.tensor
            def _(pe):
                def free(i, s, v):
                    pe.wait_ge(taken[bank_of(s, v)], nth(i, s, v) + 1)

                def copied(i, s, v):
                    pe.wait_ge(taken[bank_of(s, v)], nth(i, s, v) + 2)

                def project_keys(i, s, g):
                    q = (i * 2 + s) * KUSES + g
                    pe.wait_ge(kp_taken, q + 1)
                    if g == 0:
                        pe.wait_ge(split_ready, i * 2 + (s + 1))
                    if g == G:
                        pe.wait_ge(batch_in, (i * 2 + s) * 4 + 4)
                    to = kp[:, (s * KUSES + g) % 2, :]
                    if g < G:
                        for t in range(2):
                            at, bank = bass.ts(2 * g + t, P), to[:, bass.ts(t, KW)]
                            pe.matmul(bank, cH[:, s, at], wkH[:, 0, :], start=True, stop=False)
                            pe.matmul(bank, cH[:, s, at], wkL[:, 0, :], start=False, stop=False)
                            pe.matmul(bank, cL[:, s, at], wkH[:, 0, :], start=False, stop=False)
                            pe.matmul(bank, cR[:, s, at], wkH[:, 1, :], start=False, stop=False)
                            mm = pe.matmul(bank, cR[:, s, at], wkL[:, 1, :], start=False, stop=True)
                    else:
                        for c in range(CD):
                            mm = pe.matmul(to[0:T, :], lb[:, s, c, :], wl[:, c, :], start=c == 0, stop=c == CD - 1)
                    mm.then_inc(kproj, 1)

                def turn_keys(i, s, v):
                    if v == 0:
                        pe.wait_ge(keys_ready, i * 2 + (s + 1))
                    free(i, s, v)
                    to = tp[:, bank_of(s, v), :]
                    for c in range(IC):
                        for t in range(2 if v < G else 1):
                            mm = pe.transpose(to[:, c * 2 * P + t * P:c * 2 * P + (t + 1) * P],
                                              kv[:, 2 * v + t, bass.ts(c, P)], k.ident[:])
                    mm.then_inc(turned, 1)

                def scores(i, s, c):
                    b = i * 2 + s
                    if c == 0:
                        copied(i, s, KUSES - 2)
                        copied(i, s, KUSES - 1)
                    if c:
                        pe.wait_ge(exped, b * IC + c)
                    for n in range(2):
                        pe.matmul(s_ps[:, n, :], qblk[:, s, c, :], keysT[:, s, c, bass.ts(n, HALF)],
                                  start=True, stop=False)
                        pe.matmul(s_ps[:, n, :], pick[:, s, :], bars[:, bass.ts(n, HALF)], start=False, stop=True)
                    mm = pe.matmul(s_ps[:, 2, 0:T], qblk[:, s, c, :], keysT[:, s, c, S:KEYS], start=True, stop=True)
                    mm.then_inc(scored, 1)

                def turn_probs(i, s, c):
                    pe.wait_ge(exped, (i * 2 + s) * IC + (c + 1))
                    for g in range(PUSES):
                        v = KUSES + PUSES * c + g
                        free(i, s, v)
                        for t in range(4 if g < 2 else 1):
                            j = 4 * g + t
                            mm = pe.transpose(tp[:, bank_of(s, v), bass.ts(t, P)], sm[:, c, bass.ts(j, P)], k.ident[:])
                        mm.then_inc(turned, 1)

                def mix_rows(i, s, c):
                    b = i * 2 + s
                    for g in (1, 2):
                        copied(i, s, KUSES + PUSES * c + g)
                    pe.wait_ge(xs_ready, b + 1)
                    pe.wait_ge(out_taken, b * IC + (c + 1))
                    for j in range(NK):
                        mm = pe.matmul(av[:, 0:DC + 1], pT[:, c, j, :], xs[:, s, j, :], start=j == 0, stop=j == NK - 1)
                    mm.then_inc(mixed, 1)

                def turn_mix(i, s, c):
                    pe.wait_ge(normed, (i * 2 + s) * IC + (c + 1))
                    pe.transpose(av[:, 2 * P:3 * P], mix[:, 0:P], k.ident[:])
                    pe.transpose(av[0:KR + 1, 3 * P:4 * P], mix[:, P:DC + 1], k.ident[:]).then_inc(mix_turned, 1)

                def project_mix(i, s, c):
                    pe.wait_ge(mix_taken, (i * 2 + s) * IC + (c + 1))
                    pe.matmul(av[:, 0:P], wv[:, 0, bass.ts(c, P)], mixT[:, 0, :], start=True, stop=False)
                    pe.matmul(av[:, 0:P], wv[:, 1, bass.ts(c, P)], mixT[:, 1, :], start=False, stop=False)
                    pe.matmul(av[:, 0:P], vl[:, s, bass.ts(c, P)], pT[:, c, NK, :], start=False, stop=True
                              ).then_inc(projected, 1)

                def batch(i, s, more):
                    ahead = after(i, s)
                    scores(i, s, 0)
                    if more:
                        project_keys(*ahead, 0)
                        project_keys(*ahead, 1)
                    scores(i, s, 1)
                    if more:
                        project_keys(*ahead, 2)
                    turn_probs(i, s, 0)
                    if more:
                        project_keys(*ahead, 3)
                        project_keys(*ahead, 4)
                    mix_rows(i, s, 0)
                    turn_probs(i, s, 1)
                    turn_mix(i, s, 0)
                    project_mix(i, s, 0)
                    mix_rows(i, s, 1)
                    if more:
                        turn_keys(*ahead, 0)
                        turn_keys(*ahead, 1)
                    turn_mix(i, s, 1)
                    if more:
                        turn_keys(*ahead, 2)
                        turn_keys(*ahead, 3)
                    project_mix(i, s, 1)
                    if more:
                        turn_keys(*ahead, 4)

                pe.wait_ge(set_up, 7)
                for g in range(KUSES):
                    project_keys(0, 0, g)
                for v in range(KUSES):
                    turn_keys(0, 0, v)
                every_batch(pe, batch)

            def copy_keys(eng, copy, mine, i, s, v):
                if bank_of(s, v) != mine:
                    return
                eng.wait_ge(turned, i * (2 * USES) + (USES * s + v + 1))
                w = 2 * P if v < G else T
                copy(keysT[:, s, :, v * 2 * P:v * 2 * P + w],
                     tp[:, mine, :].rearrange("p (c q) -> p c q", c=IC)[:, :, 0:w]).then_inc(taken[mine], 1)

            def copy_probs(eng, copy, mine, i, s, c):
                for g in range(PUSES):
                    v = KUSES + PUSES * c + g
                    if bank_of(s, v) != mine:
                        continue
                    eng.wait_ge(turned, i * (2 * USES) + (USES * s + v + 1))
                    if g < 2:
                        copy(pT[:, c, 4 * g:4 * g + 4, :], tp[:, mine, :].rearrange("p (j q) -> p j q", q=P)
                             ).then_inc(taken[mine], 1)
                    else:
                        copy(pT[0:T, c, NK, :], tp[0:T, mine, 0:P]).then_inc(taken[mine], 1)

            @block.scalar
            def _(act):
                act.sem_inc(taken0, 1)
                act.sem_inc(out_taken, 1)
                act.wait_ge(set_up, 7)

                def exp(i, s, c):
                    act.wait_ge(maxed, (i * 2 + s) * IC + (c + 1))
                    act.activation(sm[:, c, 0:KEYS], s_ps[:].rearrange("p a q -> p (a q)")[:, 0:KEYS], ACT.Exp, bias=col[:, 0, c:c + 1],
                                   accum_out=col[:, 1, c:c + 1]).then_inc(exped, 1)

                def square(i, s, part):
                    b = i * 2 + s
                    act.wait_ge(kp_taken, b * KUSES + 2 + (2, KUSES)[part])
                    j = (slice(0, 4), slice(4, NK + 1))[part]
                    act.activation(sq[:, j, :], kv[:, j, :], ACT.Square).then_inc(squared, 1)

                def root_var(i, s):
                    act.wait_ge(var_ready, i * 2 + (s + 1))
                    act.activation(mv[:, :, 1], mv[:, :, 1], ACT.Sqrt).then_inc(var_rooted, 1)

                def root_sums(i, s):
                    act.wait_ge(sums_ready, (i * 2 + s) * 2 + 2)
                    act.activation(rn[:], rn[:], ACT.Sqrt, scale=1.0 / dk).then_inc(sums_rooted, 1)

                def take_mix(i, s, c):
                    act.wait_ge(mix_turned, (i * 2 + s) * IC + (c + 1))
                    act.copy(mixT[:, 0, :], av[:, 2 * P:3 * P])
                    act.copy(mixT[0:KR + 1, 1, :], av[0:KR + 1, 3 * P:4 * P]).then_inc(mix_taken, 1)

                def take_out(i, s, c):
                    b = i * 2 + s
                    act.wait_ge(projected, b * IC + (c + 1))
                    for g in range(2):
                        r = slice(g * dk, (g + 1) * dk)
                        cp = act.copy(oT[r, c, bass.ds(b * T, T)], av[r, bass.ts(g, T)])
                    cp.then_inc(out_taken, 1)

                def batch(i, s, more):
                    ahead = after(i, s)
                    exp(i, s, 0)
                    if more:
                        square(*ahead, 0)
                    exp(i, s, 1)
                    copy_probs(act, act.copy, 0, i, s, 0)
                    if more:
                        square(*ahead, 1)
                        root_sums(*ahead)
                    copy_probs(act, act.copy, 0, i, s, 1)
                    take_mix(i, s, 0)
                    take_out(i, s, 0)
                    if more:
                        copy_keys(act, act.copy, 0, *ahead, 0)
                        copy_keys(act, act.copy, 0, *ahead, 1)
                    take_mix(i, s, 1)
                    if more:
                        copy_keys(act, act.copy, 0, *ahead, 2)
                        copy_keys(act, act.copy, 0, *ahead, 3)
                    take_out(i, s, 1)
                    if more == 2:
                        root_var(i + 1, s)
                    if more:
                        copy_keys(act, act.copy, 0, *ahead, 4)

                root_var(0, 0)
                square(0, 0, 0)
                square(0, 0, 1)
                root_sums(0, 0)
                root_var(0, 1)
                for v in range(KUSES):
                    copy_keys(act, act.copy, 0, 0, 0, v)
                every_batch(act, batch)

            @block.vector
            def _(dve):
                dve.sem_inc(taken1, 1)
                dve.sem_inc(kp_taken, 2)
                dve.wait_ge(set_up, 7)

                def stats(i, s, link, part):
                    if part == 0:
                        dve.wait_ge(n_landed, (i * 2 + s) * 16 + 16)
                    for j in range(part * NK // 2, (part + 1) * NK // 2):
                        link.mark(dve.bn_stats(st[:, j, :], land[:, j, :]))

                def variance(link):
                    link.wait()
                    link.mark(dve.tensor_tensor(mv[:, :, 0], st[:, :, 1], st[:, :, 4], ALU.subtract))
                    link(dve.tensor_tensor(mv[:, :, 1], st[:, :, 2], st[:, :, 5], ALU.add))
                    link.mark(dve.scalar_tensor_tensor(mv[:, :, 0], mv[:, :, 0], 0.25, mv[:, :, 0], ALU.mult,
                                                       ALU.mult))
                    link(dve.tensor_scalar(mv[:, :, 1], mv[:, :, 1], 1.0 / DC, 1e-5, ALU.mult, ALU.add))
                    dve.tensor_tensor(mv[:, :, 1], mv[:, :, 1], mv[:, :, 0], ALU.add).then_inc(var_ready, 1)

                def invert_std(i, s):
                    dve.wait_ge(var_rooted, i * 2 + (s + 1))
                    dve.reciprocal(rs[:, s, :], mv[:, :, 1]).then_inc(rs_ready, 1)

                def take_keys(i, s, g):
                    b = i * 2 + s
                    if g == 0:
                        dve.wait_ge(rs_ready, b + 1)
                    dve.wait_ge(kproj, b * KUSES + (g + 1))
                    at = kp[:, (s * KUSES + g) % 2, :]
                    if g < G:
                        for t in range(2):
                            j = 2 * g + t
                            cp = dve.scalar_tensor_tensor(kv[:, j, :], at[:, bass.ts(t, KW)], rs[:, s, j:j + 1],
                                                          bkb[:], ALU.mult, ALU.add)
                    else:
                        dve.tensor_copy(kv[0:T, NK, :], at[0:T, 0:KW])
                        cp = dve.tensor_copy(vl[0:T, s, :], at[0:T, KW:2 * KW])
                    cp.then_inc(kp_taken, 1)

                def sums(i, s, part):
                    dve.wait_ge(squared, (i * 2 + s) * 2 + (part + 1))
                    j = (slice(0, 4), slice(4, NK + 1))[part]
                    dve.tensor_reduce(rn[:, j, :], sq[:, j, :].rearrange("p j (h q) -> p j h q", q=dk), AX.X, ALU.add
                                      ).then_inc(sums_ready, 1)

                def norm_keys(i, s, link):
                    dve.wait_ge(sums_rooted, i * 2 + (s + 1))
                    link(dve.tensor_scalar(rn[:], rn[:], 1e-8, None, ALU.max))
                    link(dve.reciprocal(rn[:], rn[:]))
                    keys = kv[:].rearrange("p j (h q) -> p j h q", q=dk)
                    dve.tensor_tensor(keys, keys, over(rn[:], 3, dk), ALU.mult).then_inc(keys_ready, 1)

                def row_max(i, s, c):
                    b = i * 2 + s
                    dve.wait_ge(scored, b * IC + (c + 1))
                    dve.tensor_reduce(col[:, 0, c:c + 1], s_ps[:].rearrange("p a q -> p (a q)")[:, 0:KEYS], AX.X,
                                      ALU.max, negate=True).then_inc(maxed, 1)

                def scale_latents(i, s, c):
                    b = i * 2 + s
                    dve.wait_ge(exped, b * IC + (c + 1))
                    dve.reciprocal(col[:, 2, c:c + 1], col[:, 1, c:c + 1]).then_inc(inverted, 1)
                    dve.wait_ge(inverted, b * (2 * IC) + (2 * c + 1))
                    dve.tensor_scalar(sm[:, c, S:KEYS], sm[:, c, S:KEYS], col[:, 2, c:c + 1], None, ALU.mult
                                      ).then_inc(inverted, 1)

                def norm_mix(i, s, c):
                    dve.wait_ge(mixed, (i * 2 + s) * IC + (c + 1))
                    dve.tensor_scalar(mix[:], av[:, 0:DC + 1], col[:, 2, c:c + 1], None, ALU.mult
                                      ).then_inc(normed, 1)

                CHAINED = NK + 4 + 2

                def batch(i, s, more):
                    ahead = after(i, s)
                    link = Chain(dve, step, (i * 2 + s) * CHAINED + (2 * (NK + 4) + 2))
                    row_max(i, s, 0)
                    if more:
                        take_keys(*ahead, 0)
                        take_keys(*ahead, 1)
                    scale_latents(i, s, 0)
                    row_max(i, s, 1)
                    if more:
                        take_keys(*ahead, 2)
                    copy_probs(dve, dve.tensor_copy, 1, i, s, 0)
                    if more == 2:
                        stats(i + 1, s, link, 0)
                    if more:
                        take_keys(*ahead, 3)
                        take_keys(*ahead, 4)
                        sums(*ahead, 0)
                    if more == 2:
                        stats(i + 1, s, link, 1)
                    scale_latents(i, s, 1)
                    if more:
                        sums(*ahead, 1)
                    copy_probs(dve, dve.tensor_copy, 1, i, s, 1)
                    norm_mix(i, s, 0)
                    if more:
                        norm_keys(*ahead, link)
                    if more == 2:
                        variance(link)
                    norm_mix(i, s, 1)
                    if more:
                        for v in range(KUSES):
                            copy_keys(dve, dve.tensor_copy, 1, *ahead, v)
                    if more == 2:
                        invert_std(i + 1, s)

                link = Chain(dve, step)
                for part in range(2):
                    stats(0, 0, link, part)
                variance(link)
                invert_std(0, 0)
                for g in range(KUSES):
                    take_keys(0, 0, g)
                for part in range(2):
                    sums(0, 0, part)
                norm_keys(0, 0, link)
                for part in range(2):
                    stats(0, 1, link, part)
                variance(link)
                invert_std(0, 1)
                for v in range(KUSES):
                    copy_keys(dve, dve.tensor_copy, 1, 0, 0, v)
                assert link.n == 2 * (NK + 4) + 2, link.n
                every_batch(dve, batch)


def head_slots(w, heads):
    dk = w.shape[1] // heads
    out = np.zeros((w.shape[0], heads, HALF // heads), w.dtype)
    out[:, :, :dk] = w.reshape(w.shape[0], heads, dk)
    return out.reshape(w.shape[0], HALF)


def chunks(w):
    n = -(-w.shape[0] // P)
    out = np.zeros((n * P, w.shape[1]), w.dtype)
    out[:w.shape[0]] = w
    return np.ascontiguousarray(out.reshape(n, P, w.shape[1]).transpose(1, 0, 2))


def column(v):
    return np.ascontiguousarray(v.reshape(-1, P).T)


def layouts(x):
    a = {}
    a["xT"] = chunks(x["x"].reshape(N, D).T)
    a["ident"] = np.eye(P, dtype=np.float32)
    a["ctx"] = x["ctx_768"]
    a["ctxT"] = np.ascontiguousarray(x["ctx_768"].transpose(0, 2, 1))

    def xattn(name, heads, turned):
        g = lambda w: x[f"{name}_{w}"].T if turned else x[f"{name}_{w}"]
        a[name + "_Wq"] = chunks(head_slots(g("Wq"), heads))
        wk = head_slots(g("Wk"), heads).T
        a[name + "_WkT"] = chunks(np.concatenate([wk, wk[:, P:]], 1))
        a[name + "_Wv"] = chunks(head_slots(g("Wv"), heads))
        a[name + "_Wo"] = chunks(head_slots(g("Wo").T, heads).T)
    xattn("L0_xattn", 16, True)
    xattn("L1_xattn", 8, False)
    xattn("L2_xattn", 8, False)
    a["lower8"] = np.tril(np.ones((8, 8), np.float32), -1).reshape(64)
    a["lower4"] = np.tril(np.ones((4, 4), np.float32), -1).reshape(16)
    a["upto"] = np.triu(np.ones((P, P), np.float32))
    each = lambda w: np.stack([chunks(m) for m in w])
    cols = lambda w: np.stack([column(v) for v in w])
    a["L0_ffn_gate"] = chunks(x["L0_ffn_gate_w"].T)
    a["L0_ffn_up"], a["L0_ffn_down"] = each(x["L0_ffn_up_w"]), each(x["L0_ffn_down_w"])
    a["L0_ffn_upb"], a["L0_ffn_downb"] = cols(x["L0_ffn_up_b"]), np.pad(x["L0_ffn_down_b"], ((0, P - E), (0, 0)))
    a["L0_ffn_sup"], a["L0_ffn_sdown"] = chunks(x["L0_ffn_sh_up_w"]), chunks(x["L0_ffn_sh_down_w"])
    a["L0_ffn_supb"], a["L0_ffn_sdownb"] = column(x["L0_ffn_sh_up_b"]), column(x["L0_ffn_sh_down_b"])
    for name, gate_w in (("L1_ffn", x["L1_ffn_gate_w"].T), ("L3_ffn", x["L3_ffn_wg"])):
        a[name + "_gate"] = chunks(gate_w)
        a[name + "_up"], a[name + "_down"] = each(x[name + "_w1"]), each(x[name + "_w2"])
        a[name + "_upb"], a[name + "_downb"] = cols(x[name + "_b1"]), np.pad(x[name + "_b2"], ((0, P - E), (0, 0)))
    both = lambda g, u: np.concatenate([chunks(g), chunks(u)], 1)
    a["L2_ffn_gate"] = chunks(x["L2_ffn_gate_w"].T)
    a["L2_ffn_cbias"] = x["L2_ffn_correction_bias"]
    a["L2_ffn_up"] = np.stack([both(g, u) for g, u in zip(x["L2_ffn_Wg"], x["L2_ffn_Wu"])])
    a["L2_ffn_down"] = each(x["L2_ffn_Wd"])
    a["L2_ffn_sup"] = both(x["L2_ffn_Wg_s"], x["L2_ffn_Wu_s"])
    a["L2_ffn_sdown"] = chunks(x["L2_ffn_Wd_s"])
    a["pick8"] = np.repeat(np.eye(8, dtype=np.float32)[:, :, None], P, 2)
    s, t = np.arange(P)[:, None], np.arange(P)[None, :]
    a["bar"] = np.where((s // T == t // T) & (s <= t), 0.0, -1e30).astype(np.float32)
    a["fresh"] = (np.arange(N) % T != 0).astype(np.float32)
    a["lags"] = np.arange(T, dtype=np.float32)
    n = "L0_attn_"
    a[n + "in"] = chunks(np.pad(x[n + "in_proj_w"].T, ((0, 0), (0, 120))))
    a[n + "out"] = chunks(x[n + "out_proj_w"].T)
    a[n + "cw"], a[n + "cb"] = chunks(x[n + "conv_w"]), column(x[n + "conv_b"])
    a[n + "D"] = column(np.repeat(x[n + "D"], 64))
    a[n + "nw"] = column(x[n + "norm_w"])
    a[n + "ln"] = np.stack([column(x[n + "ln_w"]), column(x[n + "ln_b"])], 1)
    a[n + "dt"] = np.stack([x[n + "dt_bias"], x[n + "A_log"]], 1)
    n = "L1_attn_"
    a[n + "in"], a[n + "inb"] = chunks(x[n + "in_proj_w"].T), column(x[n + "in_proj_b"])
    a[n + "out"], a[n + "outb"] = chunks(x[n + "out_proj_w"].T), column(x[n + "out_proj_b"])
    a[n + "conv"] = x[n + "conv_w"].transpose(1, 2, 0).reshape(4, P, 4, 512).transpose(1, 0, 2, 3)
    a[n + "cvb"], a[n + "nw"] = column(x[n + "conv_b"]), column(x[n + "norm_w"])
    a[n + "par"] = np.stack([chunks(x[n + w]) for w in ("A_log", "B_param", "C_param")], 1)
    a[n + "dts"] = np.stack([column(x[n + "dt"]), column(x[n + "D_param"])], 1)
    n = "L2_attn_"
    a[n + "in"], a[n + "out"] = chunks(x[n + "in_proj_w"].T), chunks(x[n + "out_proj_w"].T)
    a[n + "cw"], a[n + "cb"] = chunks(x[n + "conv_w"][:, 0, :]), column(x[n + "conv_b"])
    a[n + "x"] = chunks(np.pad(x[n + "x_proj_w"].T, ((0, 0), (0, P - 48))))
    a[n + "wdt"], a[n + "dtb"] = x[n + "dt_proj_w"].T, column(x[n + "dt_proj_b"])
    a[n + "A"] = chunks(x[n + "A_log"]).reshape(P, 64)
    a[n + "D"], a[n + "nw"] = column(x[n + "D"]), column(x[n + "norm_w"])
    n = "L3_attn_"
    a[n + "Wqk"] = chunks(np.concatenate([head_slots(x[n + "Wq"], 16), head_slots(x[n + "Wk"], 16)], 1))
    a[n + "Wv"], a[n + "Wo"] = chunks(head_slots(x[n + "Wv"], 16)), chunks(head_slots(x[n + "Wo"].T, 16).T)
    r, c = np.arange(P)[:, None], np.arange(P)[None, :]
    a["slotvar"] = np.where((r // 32 == c // 32) & (r % 32 < 16) & (c % 32 == 16), 1.0 / 15, 0.0).astype(np.float32)
    a["pair"] = (r // 64 == c // 64).astype(np.float32)
    n = "L3_xattn_"
    a["mask"] = np.ascontiguousarray(x["mask_BxS2_bk0"]).view(np.uint32)
    for w in ("Wq", "Wlkv", "Wo"):
        a[n + w] = chunks(x[n + w].T)
    twice = lambda w: chunks(np.concatenate([w[:P], w[P:], np.zeros((2 * P - DC, w.shape[1]), w.dtype), w[P:], w[P:]]))
    a[n + "Wkv"] = twice(x[n + "Wkv"].T)
    a[n + "bo"] = column(x[n + "bo"])
    a[n + "lnl"] = np.stack([column(x[n + "ln_l_g"]), column(x[n + "ln_l_b"])], 1)
    a[n + "lnx"] = np.stack([twice(x[n + "ln_x_" + v][:, None])[:, :, 0] for v in "gb"], 1)
    a[n + "qg"] = np.stack([np.tile(x[n + v], 2) for v in ("qn_g", "kn_g")], 1)
    a["L1_xattn_bo"] = column(x["L1_xattn_bo"])
    a["L2_xattn_bo"] = column(x["L2_xattn_bo"])
    return a


CAPACITY = 2 * N // E
STEPS = [
    ("L3_attn", correlation_attention),
    ("L3_xattn", masked_cross_attention),
    ("L2_attn", selective_scan),
    ("L0_attn", state_space_duality),
    ("L1_attn", long_convolution),
    ("L0_ffn", lambda k: experts(k, "L0_ffn", 256, ACT.Silu, False, True, True, True,
                                 dict(top=2, softmax=True, eps=1e-20))),
    ("L1_ffn", lambda k: experts(k, "L1_ffn", 1024, ACT.Gelu, False, True, True, False,
                                 dict(top=2, softmax=True, eps=1e-9))),
    ("L2_ffn", lambda k: experts(k, "L2_ffn", 128, ACT.Silu, True, False, False, True,
                                 dict(top=4, softmax=False, eps=1e-20, factor=2.5, grouped=True))),
    ("L3_ffn", lambda k: experts(k, "L3_ffn", 1024, ACT.Relu, False, True, True, False,
                                 dict(top=2, softmax=True, eps=0.0, capacity=CAPACITY))),
    ("L0_xattn", lambda k: context_attention(k, "L0_xattn", 16, 16 ** -0.5, False)),
    ("L1_xattn", lambda k: context_attention(k, "L1_xattn", 8, 64 ** -0.5, True)),
    ("L2_xattn", lambda k: context_attention(k, "L2_xattn", 8, 64 ** -0.5, True)),
]


ORDER = ["L0_xattn", "L0_attn", "L0_ffn", "L1_xattn", "L1_attn", "L1_ffn", "L2_xattn", "L2_attn", "L2_ffn",
         "L3_xattn", "L3_attn", "L3_ffn"]


def build(nc, dram, steps=None):
    with ExitStack() as ctx:
        k = Core(nc, dram, ctx)
        k.comb = nc.dram_tensor("comb_rows", (E, N), F32).ap()
        load_constants(k)
        k.bc = nc.dram_tensor("state_rows", (32, N), F32).ap()
        for name in ORDER:
            if steps is None or name in steps:
                dict(STEPS)[name](k)
        store_result(k)


def kernel(**inputs):
    import concourse.bacc as bacc
    from concourse.bass_utils import run_bass_kernel_spmd

    nc = bacc.Bacc("TRN2", target_bir_lowering=False, num_devices=1)
    arrays = {"in_" + n: np.ascontiguousarray(v) for n, v in layouts({n: np.asarray(v) for n, v in inputs.items()}).items()}
    dram = {n[3:]: nc.dram_tensor(n, v.shape, mybir.dt.from_np(v.dtype), kind="ExternalInput").ap()
            for n, v in arrays.items()}
    dram["outT"] = nc.dram_tensor("outT", (P, CD, N), F32, kind="ExternalOutput").ap()
    build(nc, dram)
    r = run_bass_kernel_spmd(nc, [arrays], core_ids=[0])
    out = r.results[0]["outT"]
    return np.ascontiguousarray(out.transpose(1, 0, 2).reshape(D, N).T.reshape(B, T, D))
```

```python
from contextlib import ExitStack, contextmanager

import numpy as np

import concourse.bass as bass
from concourse import mybir

ALU = mybir.AluOpType
ACT = mybir.ActivationFunctionType
AX = mybir.AxisListType
F32 = mybir.dt.float32
F32R = mybir.dt.float32r

P = 128
B, T, D = 16, 64, 256
N = B * T
S, DC = 1024, 192
CD = D // P
HALF = 512
SEMS = 40


class Core:

    def __init__(self, nc, dram, ctx):
        self.nc, self.dram = nc, dram
        sb = lambda name, shape: ctx.enter_context(nc.sbuf_tensor(name, shape, F32))
        self.sem_pool = [nc.alloc_semaphore(f"pool{i}") for i in range(SEMS)]
        self.xT = sb("xT", [P, CD, N])
        self.xn = sb("xn", [P, CD, N])
        self.ones = sb("ones", [P, P])
        self.ident = sb("ident", [P, P])
        self.count = 0
        self.weights = nc.alloc_semaphore("weights_landed")
        self.due = 0

    @contextmanager
    def stage(self, name, *signals):
        nc = self.nc
        self.count += 1
        tag = f"{name}{self.count}_"
        with ExitStack() as ctx:
            def sb(n, shape, dt=F32):
                return ctx.enter_context(nc.sbuf_tensor(tag + n, shape, dt))

            def ps(n, shape, dt=F32):
                return ctx.enter_context(nc.psum_tensor(tag + n, shape, dt))
            assert len(signals) <= SEMS
            yield (sb, ps, *self.sem_pool[:len(signals)])
        if signals:
            nums = [s.num for s in self.sem_pool[:len(signals)]]
            assert nums == list(range(nums[0], nums[0] + len(nums)))
            nc.all_engine_barrier(sems_to_clear=range(nums[0], nums[-1] + 1))


def load_constants(k):
    nc = k.nc
    with k.stage("load", "landed") as (sb, ps, landed):
        with nc.Block() as block:
            @block.sync
            def _(sp):
                sp.dma_start(k.xT[:], k.dram["xT"]).then_inc(landed, 16)
                sp.dma_start(k.ident[:], k.dram["ident"]).then_inc(landed, 16)
                sp.wait_ge(landed, 32)

            @block.vector
            def _(dve):
                dve.memset(k.ones[:], 1.0)


def store_result(k):
    nc = k.nc
    with k.stage("store", "stored") as (sb, ps, stored):
        with nc.Block() as block:
            @block.sync
            def _(sp):
                sp.dma_start(k.dram["outT"], k.xT[:]).then_inc(stored, 16)
                sp.wait_ge(stored, 16)


def layernorm(k, src, dst, eps, affine=None, centre=True, width=CD):
    nc = k.nc
    with k.stage("ln", "mean_ready", "centred", "squared", "var_ready", "shifted", "rooted",
                 "inverted", "scaled") as (
            sb, ps, mean_ready, centred, squared, var_ready, shifted, rooted, inverted, scaled):
        mean = ps("mean", [P, N])
        var = ps("var", [P, N])
        sq = sb("sq", [P, width, N])
        rstd = sb("rstd", [P, N])
        cen = sb("cen", [P, width, N]) if centre else None
        x = cen if centre else src
        items = [(n, c) for n in range(N // HALF) for c in range(width)]
        with nc.Block() as block:
            @block.tensor
            def _(pe):
                if centre:
                    for n, c in items:
                        mm = pe.matmul(mean[:, bass.ts(n, HALF)], k.ones[:], src[:, c, bass.ts(n, HALF)],
                                       start=c == 0, stop=c == width - 1)
                        if c == width - 1:
                            mm.then_inc(mean_ready, 1)
                for q, (n, c) in enumerate(items):
                    pe.wait_ge(squared, q + 1)
                    mm = pe.matmul(var[:, bass.ts(n, HALF)], k.ones[:], sq[:, c, bass.ts(n, HALF)],
                                   start=c == 0, stop=c == width - 1)
                    if c == width - 1:
                        mm.then_inc(var_ready, 1)

            @block.scalar
            def _(act):
                for q, (n, c) in enumerate(items):
                    if centre:
                        act.wait_ge(centred, q + 1)
                    act.activation(sq[:, c, bass.ts(n, HALF)], x[:, c, bass.ts(n, HALF)], ACT.Square,
                                   scale=(width * P) ** -0.5).then_inc(squared, 1)
                for n in range(N // HALF):
                    act.wait_ge(shifted, n + 1)
                    act.activation(rstd[:, bass.ts(n, HALF)], rstd[:, bass.ts(n, HALF)], ACT.Sqrt
                                   ).then_inc(rooted, 1)
            @block.vector
            def _(dve):
                if centre:
                    for n, c in items:
                        dve.wait_ge(mean_ready, n + 1)
                        dve.scalar_tensor_tensor(cen[:, c, bass.ts(n, HALF)], mean[:, bass.ts(n, HALF)],
                                                 -1.0 / (width * P), src[:, c, bass.ts(n, HALF)],
                                                 ALU.mult, ALU.add).then_inc(centred, 1)
                for n in range(N // HALF):
                    dve.wait_ge(var_ready, n + 1)
                    dve.tensor_scalar(rstd[:, bass.ts(n, HALF)], var[:, bass.ts(n, HALF)], eps, None,
                                      ALU.add).then_inc(shifted, 1)
                for n in range(N // HALF):
                    dve.wait_ge(rooted, n + 1)
                    dve.reciprocal(rstd[:, bass.ts(n, HALF)], rstd[:, bass.ts(n, HALF)]).then_inc(inverted, 1)
                if centre:
                    dve.wait_ge(centred, len(items))
                for q, (n, c) in enumerate(items):
                    at = bass.ts(n, HALF)
                    dve.wait_ge(inverted, n + 1)
                    if affine and affine[1] is None:
                        dve.scalar_tensor_tensor(dst[:, c, at], x[:, c, at], affine[0][:, c:c + 1], rstd[:, at],
                                                 ALU.mult, ALU.mult)
                    else:
                        dve.tensor_tensor(dst[:, c, at], x[:, c, at], rstd[:, at], ALU.mult).then_inc(scaled, 1)
                if affine and affine[1] is not None:
                    w, b = affine
                    dve.wait_ge(k.weights, k.due)
                    for q, (n, c) in enumerate(items):
                        dve.wait_ge(scaled, q + 1)
                        dve.tensor_scalar(dst[:, c, bass.ts(n, HALF)], dst[:, c, bass.ts(n, HALF)], w[:, c:c + 1],
                                          b[:, c:c + 1], ALU.mult, ALU.add)


def every_batch(eng, run):
    with eng.Fori(0, B // 2 - 1) as i:
        run(i * 2, 0, False)
        run(i * 2 + 1, 1, False)
    run(B - 2, 0, False)
    run(B - 1, 1, True)


def context_attention(k, name, heads, scale, bias):
    nc = k.nc
    slot = HALF // heads
    per = P // slot
    NC = HALF // P
    HQ = heads * T
    NJ = HQ // P
    NP = NJ // 2
    NK = S // P
    W = per * T
    KR = DC - P
    with ExitStack() as ctx:
        keep = lambda n, shape: ctx.enter_context(nc.sbuf_tensor(f"{name}_{n}", shape, F32))
        qT = keep("qT", [P, NC, N])
        oT = keep("oT", [P, NC, N])
        wkT = keep("wkT", [P, NC, 2 * P])
        wv = keep("wv", [P, 2, HALF])
        wo = keep("wo", [P, NC, D])
        bo = keep("bo", [P, CD])
        with nc.sbuf_tensor(name + "_wq", [P, CD, HALF], F32) as wq:
            loads = [(wq[:], k.dram[name + "_Wq"]), (wkT[:], k.dram[name + "_WkT"]), (wv[:], k.dram[name + "_Wv"]),
                     (wo[:], k.dram[name + "_Wo"])]
            prefetch(k, *loads, *([(bo[:], k.dram[name + "_bo"])] if bias else []))
            layernorm(k, k.xT, k.xn, 1e-5)
            project(k, k.xn, wq, CD, NC, lambda act, m, n, bank: act.mul(qT[:, m, bass.ts(n, HALF)], bank, scale))

        with k.stage("att", "t_landed", "n_landed", "q_zero", "q_blocked", "step_t", "step_n", "t_split", "n_split",
                     "q_folded", "q_high", "q_low", "scored", "maxed", "exped", "inverted", "normed", "turned",
                     "probs_high", "probs_low", "mixed", "mix_taken", "projected", "proj_taken") as (
                sb, ps, t_landed, n_landed, q_zero, q_blocked, step_t, step_n, t_split, n_split, q_folded, q_high,
                q_low, scored, maxed, exped, inverted, normed, turned, probs_high, probs_low, mixed, mix_taken,
                projected, proj_taken):
            cT = sb("cT", [P, 2, S])
            cH = sb("cH", [P, 2, S], F32R)
            cL = sb("cL", [P, 2, S], F32R)
            cR = sb("cR", [P, 2, S], F32R)
            cN = sb("cN", [P, NK, DC])
            nH = sb("nH", [P, 2, NK, P], F32R)
            nL = sb("nL", [P, 2, NK, P], F32R)
            nR = sb("nR", [P, 2, NK, P], F32R)
            qblk = sb("qblk", [P, 2, NC, W])
            qH = sb("qH", [P, 2, HQ], F32R)
            qL = sb("qL", [P, 2, HQ], F32R)
            pr = sb("pr", [P, 2, S])
            pH = sb("pH", [P, NK, 2, P], F32R)
            pL = sb("pL", [P, NK, 2, P], F32R)
            nmax = sb("nmax", [P, NJ])
            total = sb("total", [P, NJ])
            inv = sb("inv", [P, NJ])
            mixT = sb("mixT", [P, 2, HQ])
            sc = ps("sc", [P, 2, S])
            tp = ps("tp", [P, NK, P])
            av = ps("av", [P, 2, 2, 2 * P])
            chunk = tp[:].rearrange("p a b -> p (a b)")[:, 0:NC * W].rearrange("p (m w) -> p m w", m=NC)
            BANK = NK // 2

            with nc.Block() as block:
                @block.sync
                def _(sp):
                    def load_t(b):
                        sp.dma_start(cT[:, 0, :], k.dram["ctxT"][b, 0:P, :]).then_inc(t_landed, 16)
                        for g in range(2):
                            sp.dma_start(cT[g * KR:(g + 1) * KR, 1, :], k.dram["ctxT"][b, P:DC, :]
                                         ).then_inc(t_landed, 16)

                    def load_n(b):
                        sp.dma_start(cN[:], k.dram["ctx"][b].rearrange("(j p) d -> p j d", p=P)
                                     ).then_inc(n_landed, 16)
                    load_t(0)
                    load_n(0)
                    with sp.Fori(1, B) as b:
                        sp.wait_ge(t_split, b)
                        load_t(b)
                        sp.wait_ge(n_split, b)
                        load_n(b)

                @block.gpsimd
                def _(pool):
                    pool.memset(qblk[:], 0.0).then_inc(q_zero, 1)
                    pool.wait_ge(q_zero, 1)

                    def block_q(b, s):
                        for g in range(per):
                            r = slice(g * slot, (g + 1) * slot)
                            pool.tensor_copy(qblk[r, s, :, bass.ts(g, T)],
                                             qT[r, :, bass.ds(b * T, T)]).then_inc(q_blocked, 1)
                        pool.wait_ge(q_blocked, (b + 1) * per)

                    def high(to, of):
                        return pool.tensor_tensor(to, of, over(k.ones[:, 0:to.shape[2]], 1, NK), ALU.mult)

                    tiles = lambda ap: ap.rearrange("p (j q) -> p j q", q=P)

                    def split(b, s):
                        pool.wait_ge(t_landed, b * 48 + 48)
                        high(tiles(cH[:, s]), tiles(cT[:, 0, :])).then_inc(step_t, 1)
                        high(tiles(cR[:, s]), tiles(cT[:, 1, :])).then_inc(step_t, 1)
                        pool.wait_ge(step_t, b * 3 + 2)
                        pool.tensor_tensor(cL[:, s], cT[:, 0, :], cH[:, s].bitcast(F32), ALU.subtract
                                           ).then_inc(step_t, 1)
                        pool.wait_ge(step_t, b * 3 + 3)
                        pool.tensor_tensor(cR[KR:P, s], cT[KR:P, 1, :], cR[KR:P, s].bitcast(F32), ALU.subtract
                                           ).then_inc(t_split, 1)
                        pool.wait_ge(t_split, b + 1)
                        pool.wait_ge(n_landed, b * 16 + 16)
                        high(nH[:, s], cN[:, :, 0:P]).then_inc(step_n, 1)
                        high(nR[:, s, :, 0:KR], cN[:, :, P:DC]).then_inc(step_n, 1)
                        pool.wait_ge(step_n, b * 3 + 2)
                        pool.tensor_tensor(nL[:, s], cN[:, :, 0:P], nH[:, s].bitcast(F32), ALU.subtract
                                           ).then_inc(step_n, 1)
                        pool.wait_ge(step_n, b * 3 + 3)
                        pool.tensor_tensor(nR[:, s, :, KR:P], cN[:, :, P:DC], nR[:, s, :, 0:KR].bitcast(F32),
                                           ALU.subtract).then_inc(n_split, 1)
                        pool.wait_ge(n_split, b + 1)

                    for s in range(2):
                        block_q(s, s)
                        split(s, s)
                    with pool.Fori(1, B // 2) as i:
                        for s in range(2):
                            pool.wait_ge(mixed, (i * 2 + (s - 1)) * NP)
                            block_q(i * 2 + s, s)
                            split(i * 2 + s, s)

                @block.tensor
                def _(pe):
                    def fold(b, s):
                        pe.wait_ge(q_blocked, (b + 1) * per)
                        for m in range(NC):
                            for c in range(2):
                                mm = pe.matmul(sc[:, c, bass.ts(m, W)], wkT[:, m, bass.ts(c, P)],
                                               qblk[:, s, m, :], start=True, stop=True)
                        mm.then_inc(q_folded, 1)

                    def scores(b, s, j):
                        if j == 0:
                            pe.wait_ge(q_low, (b + 1) * 2)
                            pe.wait_ge(t_split, b + 1)
                        if j >= 2:
                            pe.wait_ge(exped, b * NJ + (j - 1))
                        h0, h1, l0, l1 = (x[:, c, bass.ts(j, P)] for x in (qH, qL) for c in range(2))
                        for n in range(2):
                            to, at = sc[:, j % 2, bass.ts(n, HALF)], bass.ts(n, HALF)
                            pe.matmul(to, h0, cH[:, s, at], start=True, stop=False)
                            pe.matmul(to, h0, cL[:, s, at], start=False, stop=False)
                            pe.matmul(to, l0, cH[:, s, at], start=False, stop=False)
                            pe.matmul(to, h1, cR[:, s, at], start=False, stop=False)
                            mm = pe.matmul(to, l1, cR[:, s, at], start=False, stop=True)
                        mm.then_inc(scored, 1)

                    def turn(b, j):
                        pe.wait_ge(normed, b * NJ + (j + 1))
                        if j == 0:
                            pe.wait_ge(proj_taken, b + 1)
                        else:
                            pe.wait_ge(probs_low, (b * NJ + j) * 2)
                        for n in range(NK):
                            mm = pe.transpose(tp[:, n, :], pr[:, j % 2, bass.ts(n, P)], k.ident[:])
                            if n % BANK == BANK - 1:
                                mm.then_inc(turned, 1)

                    def mix(b, s, p):
                        pe.wait_ge(probs_low, (b * NJ + (2 * p + 2)) * 2)
                        if p == 0:
                            pe.wait_ge(n_split, b + 1)
                        if p >= 2:
                            pe.wait_ge(mix_taken, b * NP + (p - 1))
                        for c in range(2):
                            to = av[:, p % 2, c, :]
                            passes = ((nH, pH), (nH, pL), (nL, pH)) if c == 0 else ((nR, pH), (nR, pL))
                            for n in range(NK):
                                for t, (of, w) in enumerate(passes):
                                    mm = pe.matmul(to, of[:, s, n, :], w[:, n].rearrange("p a q -> p (a q)"),
                                                   start=n + t == 0, stop=n == NK - 1 and t == len(passes) - 1)
                        mm.then_inc(mixed, 1)

                    def project_mix(b):
                        pe.wait_ge(mix_taken, b * NP + NP)
                        for m in range(NC):
                            pe.matmul(chunk[:, m, :], wv[:, 0, bass.ts(m, P)], mixT[:, 0, bass.ts(m, W)],
                                      start=True, stop=False)
                            mm = pe.matmul(chunk[:, m, :], wv[:, 1, bass.ts(m, P)], mixT[:, 1, bass.ts(m, W)],
                                           start=False, stop=True)
                        mm.then_inc(projected, 1)

                    def batch(b, s, last):
                        for p in range(NP):
                            turn(b, 2 * p)
                            if p + 1 < NP:
                                scores(b, s, 2 * p + 2)
                            elif not last:
                                pe.wait_ge(exped, b * NJ + NJ)
                                fold(b + 1, 1 - s)
                            turn(b, 2 * p + 1)
                            if p + 1 < NP:
                                scores(b, s, 2 * p + 3)
                            mix(b, s, p)
                        if not last:
                            scores(b + 1, 1 - s, 0)
                            scores(b + 1, 1 - s, 1)
                        project_mix(b)

                    fold(0, 0)
                    scores(0, 0, 0)
                    scores(0, 0, 1)
                    every_batch(pe, batch)

                @block.scalar
                def _(act):
                    def exp(b, j):
                        act.wait_ge(maxed, b * NJ + (j + 1))
                        act.activation(pr[:, j % 2, :], sc[:, j % 2, :], ACT.Exp, bias=nmax[:, j:j + 1],
                                       accum_out=total[:, j:j + 1]).then_inc(exped, 1)

                    def high_q(b):
                        act.wait_ge(q_folded, b + 1)
                        for c in range(2):
                            act.copy(qH[:, c, :], sc[:, c, 0:HQ]).then_inc(q_high, 1)

                    def high_probs(b, j):
                        for h in range(2):
                            n = slice(h * BANK, (h + 1) * BANK)
                            act.wait_ge(turned, (b * NJ + j) * 2 + (h + 1))
                            act.copy(pH[:, n, j % 2, :], tp[:, n, :]).then_inc(probs_high, 1)

                    def take_mix(b, p):
                        act.wait_ge(mixed, b * NP + (p + 1))
                        act.copy(mixT[:, :, bass.ts(p, 2 * P)], av[:, p % 2]).then_inc(mix_taken, 1)

                    def batch(b, s, last):
                        for j in range(NJ):
                            if j % 2 == 0 and j >= 2:
                                exp(b, j + 1)
                                take_mix(b, j // 2 - 1)
                            high_probs(b, j)
                            if j % 2 and j + 1 < NJ:
                                exp(b, j + 1)
                        if not last:
                            high_q(b + 1)
                        take_mix(b, NP - 1)
                        if not last:
                            exp(b + 1, 0)
                            exp(b + 1, 1)
                        act.wait_ge(projected, b + 1)
                        for g in range(per):
                            r = slice(g * slot, (g + 1) * slot)
                            cp = act.copy(oT[r, :, bass.ds(b * T, T)], chunk[r, :, bass.ts(g, T)])
                        cp.then_inc(proj_taken, 1)

                    act.sem_inc(proj_taken, 1)
                    high_q(0)
                    exp(0, 0)
                    exp(0, 1)
                    every_batch(act, batch)

                @block.vector
                def _(dve):
                    def row_max(b, j):
                        dve.wait_ge(scored, b * NJ + (j + 1))
                        dve.tensor_reduce(nmax[:, j:j + 1], sc[:, j % 2, :], AX.X, ALU.max,
                                          negate=True).then_inc(maxed, 1)

                    def low_q(b):
                        for c in range(2):
                            dve.wait_ge(q_high, b * 2 + (c + 1))
                            dve.tensor_tensor(qL[:, c, :], sc[:, c, 0:HQ], qH[:, c, :].bitcast(F32),
                                              ALU.subtract).then_inc(q_low, 1)

                    def invert(b, j):
                        dve.wait_ge(exped, b * NJ + (j + 1))
                        dve.reciprocal(inv[:, j:j + 1], total[:, j:j + 1]).then_inc(inverted, 1)
                        dve.wait_ge(inverted, b * NJ + (j + 1))
                        dve.tensor_scalar(pr[:, j % 2, :], pr[:, j % 2, :], inv[:, j:j + 1], None, ALU.mult
                                          ).then_inc(normed, 1)

                    def low_probs(b, j):
                        for h in range(2):
                            n = slice(h * BANK, (h + 1) * BANK)
                            dve.wait_ge(probs_high, (b * NJ + j) * 2 + (h + 1))
                            dve.tensor_tensor(pL[:, n, j % 2, :], tp[:, n, :], pH[:, n, j % 2, :].bitcast(F32),
                                              ALU.subtract).then_inc(probs_low, 1)

                    def batch(b, s, last):
                        for j in range(NJ):
                            if j % 2 == 0:
                                if j >= 2:
                                    row_max(b, j + 1)
                                invert(b, j + 1)
                            low_probs(b, j)
                            if j % 2 and j + 1 < NJ:
                                row_max(b, j + 1)
                                invert(b, j + 1)
                        if not last:
                            low_q(b + 1)
                            row_max(b + 1, 0)
                            row_max(b + 1, 1)
                            invert(b + 1, 0)

                    low_q(0)
                    row_max(0, 0)
                    row_max(0, 1)
                    invert(0, 0)
                    every_batch(dve, batch)
        add_projection(k, oT, wo, NC, bias=bo if bias else None)


E = 8
NT = N // P


class Chain:

    def __init__(self, eng, sem, base=0):
        self.eng, self.sem, self.n, self.base = eng, sem, 0, base

    def mark(self, instruction):
        instruction.then_inc(self.sem, 1)
        self.n += 1

    def wait(self):
        self.eng.wait_ge(self.sem, self.base + self.n)

    def __call__(self, instruction):
        self.mark(instruction)
        self.wait()


def over(ap, axis, n):
    ap = ap.unsqueeze(axis)
    shape = list(ap.shape)
    shape[axis] = n
    return ap.broadcast_to(shape)


def gate(k, name, combT, meanwhile, top, softmax, eps, factor=1.0, grouped=False, capacity=None):
    nc = k.nc
    comb_dram = k.comb
    with k.stage("gate", "landed", "logits_ready", "scores_in", "scores_out", "counted", "valued", "comb_ready",
                 "turned", "copied", "stored", "step", "cleared",
                 "aside") as (
            sb, ps, landed, logits_ready, scores_in, scores_out, counted, valued, comb_ready, turned, copied,
            stored, step, cleared, aside):
        gw = sb("gw", [P, CD, E])
        tri = sb("tri", [P, E * E])
        tri4 = sb("tri4", [P, 16])
        upto = sb("upto", [P, P])
        bias = sb("bias", [P, E])
        lg = sb("lg", [P, NT, E])
        pr = sb("pr", [P, NT, E])
        val = sb("val", [P, NT, E])
        ex = sb("ex", [P, NT, E])
        cmp = sb("cmp", [P, NT, E, E])
        eq = sb("eq", [P, NT, E, E])
        rank = sb("rank", [P, NT, E])
        mask = sb("mask", [P, 2, NT, E])
        row = sb("row", [P, 3, NT])
        comb = sb("comb", [P, NT, E])
        grp = sb("grp", [P, 3, NT, 4])
        pre = sb("pre", [P, 2 * NT, E])
        tot = sb("tot", [P, 2 * NT, E])
        ones = sb("ones", [P, 2 * NT])
        lg_ps = ps("lg_ps", [P, NT, E])
        cnt_ps = ps("cnt_ps", [P, 2 * NT, E])
        tot_ps = ps("tot_ps", [P, 2 * NT, E])
        ct_ps = ps("ct_ps", [P, N])
        with nc.Block() as block:
            @block.sync
            def _(sp):
                sp.dma_start(gw[:], k.dram[name + "_gate"]).then_inc(landed, 16)
                sp.dma_start(tri[:], k.dram["lower8"].partition_broadcast(P)).then_inc(landed, 16)
                sp.dma_start(tri4[:], k.dram["lower4"].partition_broadcast(P)).then_inc(landed, 16)
                sp.dma_start(upto[:], k.dram["upto"]).then_inc(landed, 16)
                if grouped:
                    sp.dma_start(bias[:], k.dram[name + "_cbias"].partition_broadcast(P)).then_inc(landed, 16)
                sp.wait_ge(copied, 1)
                sp.dma_start(comb_dram, combT[0:E, :]).then_inc(stored, 16)
                sp.wait_ge(stored, 16)

            @block.gpsimd
            def _(pool):
                pool.memset(combT[:], 0.0).then_inc(cleared, 1)
                meanwhile(pool, aside)

            @block.tensor
            def _(pe):
                pe.wait_ge(landed, 64 + 16 * grouped)
                for t in range(NT):
                    for c in range(CD):
                        mm = pe.matmul(lg_ps[:, t, :], k.xn[:, c, bass.ts(t, P)], gw[:, c, :],
                                       start=c == 0, stop=c == CD - 1)
                mm.then_inc(logits_ready, 1)
                if capacity:
                    pe.wait_ge(valued, 1)
                    flat = mask[:].rearrange("p a t e -> p (a t e)")
                    pe.matmul(cnt_ps[:].rearrange("p a e -> p (a e)"), upto[:], flat, start=True, stop=True)
                    pe.matmul(tot_ps[:].rearrange("p a e -> p (a e)"), k.ones[:], flat, start=True,
                              stop=True).then_inc(counted, 1)
                pe.wait_ge(comb_ready, 1)
                for t in range(NT):
                    mm = pe.transpose(ct_ps[0:E, bass.ts(t, P)], comb[:, t, :], k.ident[:])
                mm.then_inc(turned, 1)

            @block.scalar
            def _(act):
                if softmax:
                    act.wait_ge(scores_in, 1)
                    act.activation(ex[:], lg[:], ACT.Exp).then_inc(scores_out, 1)
                else:
                    act.wait_ge(logits_ready, 1)
                    act.activation(pr[:], lg_ps[:], ACT.Sigmoid).then_inc(scores_out, 1)

            @block.vector
            def _(dve):
                link = Chain(dve, step)
                tt = dve.tensor_tensor

                def ranks(out, v, e, lower):
                    mine, other = over(v, 3, e), over(v, 2, e)
                    c, q = (x[:].rearrange("p t a b -> p (t a b)")[:, 0:NT * e * e]
                            .rearrange("p (t a b) -> p t a b", t=NT, a=e) for x in (cmp, eq))
                    link(tt(c, other, mine, ALU.is_gt))
                    link(tt(q, other, mine, ALU.is_equal))
                    lw = lower.rearrange("p (a b) -> p a b", a=e)
                    link(tt(q, q, over(lw, 1, NT), ALU.mult))
                    link(tt(c, c, q, ALU.add))
                    link(dve.tensor_reduce(out, c, AX.X, ALU.add))

                dve.wait_ge(landed, 64 + 16 * grouped)
                if softmax:
                    dve.wait_ge(logits_ready, 1)
                    link(dve.tensor_reduce(row[:, 0, :], lg_ps[:], AX.X, ALU.max))
                    tt(lg[:], lg_ps[:], over(row[:, 0, :], 2, E), ALU.subtract).then_inc(scores_in, 1)
                    dve.wait_ge(scores_out, 1)
                    link(dve.tensor_reduce(row[:, 1, :], ex[:], AX.X, ALU.add))
                    link(dve.reciprocal(row[:, 2, :], row[:, 1, :]))
                    link(tt(pr[:], ex[:], over(row[:, 2, :], 2, E), ALU.mult))
                    choice = pr
                else:
                    dve.wait_ge(scores_out, 1)
                    link(tt(val[:], pr[:], over(bias[:], 1, NT), ALU.add))
                    pair = val[:].rearrange("p t (g j) -> p t g j", j=2)
                    link(tt(grp[:, 0, :, :], pair[:, :, :, 0], pair[:, :, :, 1], ALU.add))
                    ranks(grp[:, 1, :, :], grp[:, 0, :, :], 4, tri4[:])
                    link(dve.tensor_scalar(grp[:, 2, :, :], grp[:, 1, :, :], 1.5, None, ALU.is_lt))
                    link(tt(pair, pair, over(grp[:, 2, :, :], 3, 2), ALU.mult))
                    choice = val
                ranks(rank[:], choice[:], E, tri[:])
                if capacity:
                    link(dve.tensor_scalar(mask[:, 0], rank[:], 0.5, None, ALU.is_lt))
                    link(dve.tensor_scalar(mask[:, 1], rank[:], 1.5, None, ALU.is_lt))
                    tt(mask[:, 1], mask[:, 1], mask[:, 0], ALU.subtract).then_inc(valued, 1)
                    link(dve.memset(ones[:], 1.0))
                    dve.wait_ge(counted, 1)
                    link(dve.tensor_copy(tot[:], tot_ps[:]))
                    for e in range(E):
                        ins = dve.tensor_tensor_scan(pre[:, :, e], ones[:], tot[:, :, e], 0.0, ALU.mult, ALU.add)
                        ins.then_inc(step, 1)
                    link.n += E
                    dve.wait_ge(step, link.n)
                    link(tt(pre[:], pre[:], tot[:], ALU.subtract))
                    link(tt(pre[:], pre[:], cnt_ps[:], ALU.add))
                    link(dve.tensor_scalar(pre[:], pre[:], capacity + 0.5, None, ALU.is_lt))
                    m = mask[:].rearrange("p a t e -> p (a t) e")
                    link(tt(pre[:], pre[:], m, ALU.mult))
                    link(tt(rank[:], mask[:, 0], mask[:, 1], ALU.add))
                    chosen = rank
                else:
                    link(dve.tensor_scalar(rank[:], rank[:], top - 0.5, None, ALU.is_lt))
                    chosen = rank
                link(tt(lg[:], pr[:], chosen[:], ALU.mult))
                link(dve.tensor_reduce(row[:, 0, :], lg[:], AX.X, ALU.add))
                link(dve.tensor_scalar(row[:, 0, :], row[:, 0, :], eps, 1.0 / factor, ALU.add, ALU.mult))
                link(dve.reciprocal(row[:, 1, :], row[:, 0, :]))
                if capacity:
                    link(tt(rank[:], pre[:, 0:NT, :], pre[:, NT:2 * NT, :], ALU.add))
                    link(tt(lg[:], pr[:], rank[:], ALU.mult))
                tt(comb[:], lg[:], over(row[:, 1, :], 2, E), ALU.mult).then_inc(comb_ready, 1)
                dve.wait_ge(turned, 1)
                dve.wait_ge(cleared, 1)
                dve.tensor_copy(combT[0:E, :], ct_ps[0:E, :]).then_inc(copied, 1)


def split_weights(pool, k, high_ready, count, parts, raw):
    tiles = lambda ap: ap.rearrange("p c (j q) -> p (c j) q", q=P)
    for (high, low), x in zip(parts, raw):
        n = x.shape[1] * x.shape[2] // P
        pool.tensor_tensor(tiles(high), tiles(x), over(k.ones[:], 1, n), ALU.mult).then_inc(high_ready, 1)
    pool.wait_ge(high_ready, count)
    for (high, low), x in zip(parts, raw):
        last = pool.tensor_tensor(low, x, high.bitcast(F32), ALU.subtract)
    return last


def experts(k, name, hidden, func, gated, up_bias, down_bias, shared, gate_args):
    nc = k.nc
    HC = hidden // P
    PER = HC * 2
    UP = 2 if gated else 1
    RP = 4 // UP
    R = 4
    LAG = 2 + gated
    LAST = E if shared else E - 1
    with ExitStack() as ctx:
        keep = lambda n, shape, dt=F32: ctx.enter_context(nc.sbuf_tensor(f"{name}_{n}", shape, dt))
        combT = keep("combT", [P, N])
        wu = keep("wu", [P, 2, UP * CD, hidden])
        wd = keep("wd", [P, 2, HC, D])
        bd = keep("bd", [P, D])
        bs = keep("bs", [P, CD])
        first = [(t[:, e], k.dram[f"{name}_{n}"][e]) for e in range(2) for t, n in ((wu, "up"), (wd, "down"))]
        if down_bias:
            first.append((bd[:], k.dram[name + "_downb"]))
        if shared and down_bias:
            first.append((bs[:], k.dram[name + "_sdownb"]))
        prefetch(k, *first)
        layernorm(k, k.xT, k.xn, 1e-5)
        wuH, wuL = (keep("wu" + n, [P, 2, UP * CD, hidden], F32R) for n in "HL")
        wdH, wdL = (keep("wd" + n, [P, 2, HC, D], F32R) for n in "HL")

        def split(pool, e, s, high_ready):
            return split_weights(pool, k, high_ready, (e + 1) * 2, ((wuH[:, s], wuL[:, s]), (wdH[:, s], wdL[:, s])),
                                 (wu[:, s], wd[:, s]))

        def split_first(pool, high_ready):
            pool.wait_ge(k.weights, k.due)
            split(pool, 0, 0, high_ready)
        gate(k, name, combT, split_first, **gate_args)
        with k.stage("moe", "w0_landed", "w1_landed", "c0_landed", "c1_landed", "high_ready", "split_ready",
                     "x_high", "x_low", "up_done", "activated", "weighed", "high_taken", "scaled", "down_done",
                     "closed", "gated_in") as (
                sb, ps, w0_landed, w1_landed, c0_landed, c1_landed, high_ready, split_ready, x_high, x_low,
                up_done, activated, weighed, high_taken, scaled, down_done, closed, gated_in):
            w_landed, c_landed = (w0_landed, w1_landed), (c0_landed, c1_landed)
            xH, xL = (sb("x" + n, [P, CD, N], F32R) for n in "HL")
            bu = sb("bu", [P, 2, HC])
            cb = sb("cb", [P, 2, N])
            h = sb("h", [P, R, HALF])
            hs = sb("hs", [P, R, HALF])
            hsH, hsL = (sb("hs" + n, [P, R, HALF], F32R) for n in "HL")
            up_ps = ps("up_ps", [P, RP, UP, HALF])
            y_ps = ps("y_ps", [P, 4, HALF])
            per_c = 16 * (1 + up_bias)
            PAIR = [(s, j) for s in range(2) for j in range(PER)]
            LONE = PAIR[:PER]

            with nc.Block() as block:
                @block.sync
                def _(sp):
                    def load_w(e, s):
                        is_shared = isinstance(e, int) and e == E
                        u = k.dram[name + "_sup"] if is_shared else k.dram[name + "_up"][e]
                        w = k.dram[name + "_sdown"] if is_shared else k.dram[name + "_down"][e]
                        sp.dma_start(wu[:, s], u).then_inc(w_landed[s], 16)
                        sp.dma_start(wd[:, s], w).then_inc(w_landed[s], 16)

                    def load_c(e, s):
                        if isinstance(e, int) and e == E:
                            if up_bias:
                                sp.dma_start(bu[:, s], k.dram[name + "_supb"]).then_inc(c_landed[s], 16)
                            return
                        sp.dma_start(cb[:, s], k.comb[e].partition_broadcast(P)).then_inc(c_landed[s], 16)
                        if up_bias:
                            sp.dma_start(bu[:, s], k.dram[name + "_upb"][e]).then_inc(c_landed[s], 16)

                    load_c(0, 0)
                    load_c(1, 1)
                    with sp.Fori(1, E // 2) as i:
                        for s in range(2):
                            e = i * 2 + s
                            sp.wait_ge(split_ready, e - 1)
                            load_w(e, s)
                            sp.wait_ge(down_done, (e - 1) * PER)
                            load_c(e, s)
                    if shared:
                        sp.wait_ge(split_ready, E - 1)
                        load_w(E, 0)
                        sp.wait_ge(down_done, (E - 1) * PER)
                        load_c(E, 0)

                @block.gpsimd
                def _(pool):
                    pool.sem_inc(high_ready, 2)
                    pool.sem_inc(split_ready, 1)
                    split(pool, 1, 1, high_ready).then_inc(split_ready, 1)
                    with pool.Fori(1, E // 2) as i:
                        for s in range(2):
                            e = i * 2 + s
                            pool.wait_ge(down_done, (e - 1) * PER)
                            pool.wait_ge(w_landed[s], i * 32)
                            split(pool, e, s, high_ready).then_inc(split_ready, 1)
                    if shared:
                        pool.wait_ge(down_done, (E - 1) * PER)
                        pool.wait_ge(w_landed[0], (E // 2) * 32)
                        split(pool, E, 0, high_ready).then_inc(split_ready, 1)

                @block.tensor
                def _(pe):
                    for u in range(4):
                        pe.matmul(y_ps[:, u, :], k.ident[:], k.xT[:, u // 2, bass.ts(u % 2, HALF)],
                                  start=True, stop=False)
                    pe.wait_ge(x_low, CD)

                    def product(bank, wH, wL, rH, rL, start, stop):
                        pe.matmul(bank, wH, rH, start=start, stop=False)
                        pe.matmul(bank, wH, rL, start=False, stop=False)
                        return pe.matmul(bank, wL, rH, start=False, stop=stop)

                    def up(first, q, s, j):
                        pe.wait_ge(weighed, first + (q + 1))
                        at, half = bass.ts(j // 2, P), bass.ts(j % 2, HALF)
                        for g in range(UP):
                            for c in range(CD):
                                mm = product(up_ps[:, q % RP, g, :], wuH[:, s, g * CD + c, at],
                                             wuL[:, s, g * CD + c, at], xH[:, c, half], xL[:, c, half],
                                             c == 0, c == CD - 1)
                        mm.then_inc(up_done, 1)

                    def down(first, q, s, j, last):
                        pe.wait_ge(scaled, first + (q + 1))
                        for m in range(CD):
                            mm = product(y_ps[:, 2 * m + j % 2, :], wdH[:, s, j // 2, bass.ts(m, P)],
                                         wdL[:, s, j // 2, bass.ts(m, P)], hsH[:, q % R, :], hsL[:, q % R, :],
                                         False, last and j // 2 == HC - 1)
                        mm.then_inc(down_done, 1)

                    def run(items, first, arrive, last=False):
                        for q in range(len(items) + LAG):
                            if q < len(items):
                                s, j = items[q]
                                if j == 0:
                                    arrive(s)
                                up(first, q, s, j)
                            if q >= LAG:
                                down(first, q - LAG, *items[q - LAG], last)

                    with pe.Fori(0, E // 2) as i:
                        run(PAIR, i * (2 * PER), lambda s: pe.wait_ge(split_ready, i * 2 + (s + 1)))
                    if shared:
                        run(LONE, E * PER, lambda s: pe.wait_ge(split_ready, E + 1), last=not down_bias)
                    if down_bias:
                        pe.wait_ge(k.weights, k.due)
                        for u in range(4):
                            mm = pe.matmul(y_ps[:, u, :], bd[:, bass.ts(u // 2, P)], combT[:, bass.ts(u % 2, HALF)],
                                           start=False, stop=True)
                        mm.then_inc(closed, 1)

                @block.scalar
                def _(act):
                    act.copy(xH[:, 0, :], k.xn[:, 0, :]).then_inc(x_high, 1)
                    act.copy(xH[:, 1, :], k.xn[:, 1, :]).then_inc(x_high, 1)

                    def run(items, first, arrive):
                        for q in range(len(items) + 1):
                            if q < len(items):
                                s, j = items[q]
                                if j == 0:
                                    arrive(s)
                                act.wait_ge(up_done, first + (q + 1))
                                act.activation(h[:, q % R, :], up_ps[:, q % RP, 0, :], func,
                                               bias=bu[:, s, j // 2:j // 2 + 1] if up_bias else 0.0
                                               ).then_inc(activated, 1)
                            if q >= 1:
                                act.wait_ge(weighed, first + (q + RP))
                                act.copy(hsH[:, (q - 1) % R, :], hs[:, (q - 1) % R, :]).then_inc(high_taken, 1)

                    with act.Fori(0, E // 2) as i:
                        run(PAIR, i * (2 * PER), lambda s: act.wait_ge(c_landed[s], i * per_c + per_c))
                    if shared:
                        run(LONE, E * PER,
                            lambda s: act.wait_ge(c_landed[s], (E // 2) * per_c + 16) if up_bias else None)
                    if down_bias:
                        act.wait_ge(closed, 1)
                    else:
                        act.wait_ge(down_done, (LAST + 1) * PER)
                    for u in range(4):
                        x = k.xT[:, u // 2, bass.ts(u % 2, HALF)]
                        if shared and down_bias:
                            act.activation(x, y_ps[:, u, :], ACT.Identity, bias=bs[:, u // 2:u // 2 + 1])
                        else:
                            act.copy(x, y_ps[:, u, :])

                @block.vector
                def _(dve):
                    dve.sem_inc(weighed, RP)
                    for c in range(CD):
                        dve.wait_ge(x_high, c + 1)
                        dve.tensor_tensor(xL[:, c, :], k.xn[:, c, :], xH[:, c, :].bitcast(F32), ALU.subtract
                                          ).then_inc(x_low, 1)

                    def run(items, first, weighted):
                        for q in range(len(items) + 1):
                            if q < len(items):
                                s, j = items[q]
                                if j == 0 and weighted:
                                    weighted(s)
                                w = cb[:, s, bass.ts(j % 2, HALF)] if weighted else None
                                hq, hsq = h[:, q % R, :], hs[:, q % R, :]
                                dve.wait_ge(activated, first + (q + 1))
                                if gated and weighted:
                                    dve.tensor_tensor(hq, hq, w, ALU.mult).then_inc(gated_in, 1)
                                    dve.wait_ge(gated_in, first + (q + 1))
                                    dve.tensor_tensor(hsq, hq, up_ps[:, q % RP, 1, :], ALU.mult).then_inc(weighed, 1)
                                elif gated:
                                    dve.tensor_tensor(hsq, hq, up_ps[:, q % RP, 1, :], ALU.mult).then_inc(weighed, 1)
                                elif weighted:
                                    dve.tensor_tensor(hsq, hq, w, ALU.mult).then_inc(weighed, 1)
                                else:
                                    dve.tensor_copy(hsq, hq).then_inc(weighed, 1)
                            if q >= 1:
                                at = (q - 1) % R
                                dve.wait_ge(high_taken, first + q)
                                dve.tensor_tensor(hsL[:, at, :], hs[:, at, :], hsH[:, at, :].bitcast(F32),
                                                  ALU.subtract).then_inc(scaled, 1)

                    with dve.Fori(0, E // 2) as i:
                        run(PAIR, i * (2 * PER), lambda s: dve.wait_ge(c_landed[s], i * per_c + per_c))
                    if shared:
                        run(LONE, E * PER, None)


def prefetch(k, *pairs):
    nc = k.nc
    k.due += 16 * len(pairs)
    with nc.Block() as block:
        @block.sync
        def _(sp):
            for to, of in pairs:
                sp.dma_start(to, of).then_inc(k.weights, 16)


def project(k, src, weights, chunks_in, tiles, drain):
    nc = k.nc
    RING = 4
    items = [(m, n) for m in range(tiles) for n in range(2)]
    with k.stage("proj", "ready", "taken") as (sb, ps, ready, taken):
        bank = ps("bank", [P, RING, HALF])
        with nc.Block() as block:
            @block.tensor
            def _(pe):
                pe.wait_ge(k.weights, k.due)
                for q, (m, n) in enumerate(items):
                    if q >= RING:
                        pe.wait_ge(taken, q - RING + 1)
                    for c in range(chunks_in):
                        mm = pe.matmul(bank[:, q % RING, :], weights[:, c, bass.ts(m, P)],
                                       src[:, c, bass.ts(n, HALF)], start=c == 0, stop=c == chunks_in - 1)
                    mm.then_inc(ready, 1)

            @block.scalar
            def _(act):
                act.wait_ge(k.weights, k.due)
                for q, (m, n) in enumerate(items):
                    act.wait_ge(ready, q + 1)
                    drain(act, m, n, bank[:, q % RING, :]).then_inc(taken, 1)


def add_projection(k, src, weights, chunks_in, more=None, bias=None):
    nc = k.nc
    with k.stage("out", "summed", "added") as (sb, ps, summed, added):
        y_ps = ps("y_ps", [P, 4, HALF])
        with nc.Block() as block:
            @block.tensor
            def _(pe):
                pe.wait_ge(k.weights, k.due)
                for u in range(CD * 2):
                    m, n = u // 2, u % 2
                    for c in range(chunks_in):
                        mm = pe.matmul(y_ps[:, u, :], weights[:, c, bass.ts(m, P)], src[:, c, bass.ts(n, HALF)],
                                       start=c == 0, stop=c == chunks_in - 1)
                    mm.then_inc(summed, 1)

            @block.vector
            def _(dve):
                dve.wait_ge(k.weights, k.due)
                for c in range(CD):
                    if more is not None:
                        dve.tensor_tensor(k.xT[:, c, :], k.xT[:, c, :], more[:, c, :], ALU.add).then_inc(added, 1)
                for u in range(CD * 2):
                    m, n = u // 2, u % 2
                    x = k.xT[:, m, bass.ts(n, HALF)]
                    if more is not None:
                        dve.wait_ge(added, m + 1)
                    dve.wait_ge(summed, u + 1)
                    dve.scalar_tensor_tensor(x, y_ps[:, u, :], bias[:, m:m + 1] if bias is not None else 0.0, x,
                                             ALU.add, ALU.add)


def by_batch(ap):
    return ap.rearrange("p (b t) -> p b t", t=T)


def causal_conv(k, raw, out, w, b, chunks_in):
    nc = k.nc
    with k.stage("conv", "tapped", "convolved") as (sb, ps, tapped, convolved):
        acc = sb("acc", [P, chunks_in, N])
        with nc.Block() as block:
            @block.vector
            def _(dve):
                dve.wait_ge(k.weights, k.due)
                for c in range(chunks_in):
                    dve.tensor_scalar(acc[:, c, :], raw[:, c, :], w[:, c, 3:4], b[:, c:c + 1],
                                      ALU.mult, ALU.add).then_inc(tapped, 1)
                for s in range(1, 4):
                    for c in range(chunks_in):
                        a, r = by_batch(acc[:, c, :]), by_batch(raw[:, c, :])
                        dve.wait_ge(tapped, (s - 1) * chunks_in + c + 1)
                        dve.scalar_tensor_tensor(a[:, :, s:], r[:, :, 0:T - s], w[:, c, 3 - s:4 - s], a[:, :, s:],
                                                 ALU.mult, ALU.add).then_inc(tapped, 1)

            @block.scalar
            def _(act):
                for c in range(chunks_in):
                    act.wait_ge(tapped, 3 * chunks_in + c + 1)
                    act.activation(out[:, c, :], acc[:, c, :], ACT.Silu)


def multiply(k, out, a, b, chunks_in):
    nc = k.nc
    with nc.Block() as block:
        @block.vector
        def _(dve):
            for c in range(chunks_in):
                dve.tensor_tensor(out[:, c, :], a[:, c, :], b[:, c, :], ALU.mult)


def state_space_duality(k):
    nc = k.nc
    H, DI = 8, 512
    IC = DI // P
    with ExitStack() as ctx:
        keep = lambda n, shape: ctx.enter_context(nc.sbuf_tensor(f"ssd_{n}", shape, F32))
        win = keep("win", [P, CD, 11 * P])
        wout = keep("wout", [P, IC, D])
        cw = keep("cw", [P, 6, 4])
        cb = keep("cb", [P, 6])
        dcol = keep("dcol", [P, IC])
        nw = keep("nw", [P, IC])
        ln = keep("ln", [P, 2, CD])
        dtb = keep("dtb", [H, 2])
        sel = keep("sel", [H, H, P])
        bar = keep("bar", [P, P])
        fresh = keep("fresh", [H, N])
        u = keep("u", [P, CD, N])
        zs = keep("zs", [P, IC, N])
        y = keep("y", [P, IC, N])
        dt = keep("dt", [H, 2, N])
        xc = keep("xc", [P, 6, N])
        d = k.dram
        prefetch(k, (ln[:], d["L0_attn_ln"]), (win[:], d["L0_attn_in"]), (wout[:], d["L0_attn_out"]),
                 (cw[:], d["L0_attn_cw"]), (cb[:], d["L0_attn_cb"]), (dcol[:], d["L0_attn_D"]),
                 (nw[:], d["L0_attn_nw"]), (dtb[:], d["L0_attn_dt"]), (sel[:], d["pick8"]), (bar[:], d["bar"]),
                 (fresh[:], d["fresh"].partition_broadcast(H)))
        layernorm(k, k.xT, k.xn, 1e-5)
        layernorm(k, k.xn, u, 1e-5, affine=(ln[:, 0, :], ln[:, 1, :]))
        with nc.sbuf_tensor("ssd_raw", [P, 6, N], F32) as raw:
            def drain(act, m, n, bank):
                if m < IC:
                    return act.activation(zs[:, m, bass.ts(n, HALF)], bank, ACT.Silu)
                if m < IC + 6:
                    return act.copy(raw[:, m - IC, bass.ts(n, HALF)], bank)
                return act.activation(dt[:, 0, bass.ts(n, HALF)], bank[0:H, :], ACT.Identity, bias=dtb[:, 0:1])
            project(k, u, win, CD, 11, drain)
            causal_conv(k, raw, xc, cw, cb, 6)

        softplus(k, dt[:, 0:1], 1, rows=H)
        with k.stage("dt", "a_ready", "step") as (sb, ps, a_ready, step):
            t2 = sb("t2", [H, N])
            na = sb("na", [H, 1])
            with nc.Block() as block:
                @block.scalar
                def _(act):
                    act.activation(na[:], dtb[:, 1:2], ACT.Exp).then_inc(a_ready, 1)

                @block.vector
                def _(dve):
                    link = Chain(dve, step)
                    dve.wait_ge(a_ready, 1)
                    link(dve.tensor_scalar(t2[:], dt[:, 0, :], na[:, 0:1], -1.0, ALU.mult, ALU.mult))
                    dve.tensor_tensor_scan(dt[:, 1, :], fresh[:], t2[:], 0.0, ALU.mult, ALU.add)

        with k.stage("ssd", "tile_in", "grams", "cums", "cols_ready", "x_turned", "cols_taken", "diffed", "masked",
                     "decayed", "weighed", "x_scaled", "summed", "y_out") as (
                sb, ps, tile_in, grams, cums, cols_ready, x_turned, cols_taken, diffed, masked, decayed, weighed,
                x_scaled, summed, y_out):
            xin = sb("xin", [P, 2, 6, P])
            din = sb("din", [H, 2, 2, P])
            cols = sb("cols", [P, 2, 2 * H])
            dec = sb("dec", [P, 2, H, P])
            xdt = sb("xdt", [P, 2, DI])
            g_ps = ps("g_ps", [P, 2, HALF])
            c_ps = ps("c_ps", [P, H, P])
            x_ps = ps("x_ps", [P, 2, HALF])
            y_ps = ps("y_ps", [P, 2, HALF])
            with nc.Block() as block:
                @block.gpsimd
                def _(pool):
                    def take(t, s):
                        pool.tensor_copy(xin[:, s], xc[:, :, bass.ds(t * P, P)]).then_inc(tile_in, 1)
                        pool.tensor_copy(din[:, s], dt[:, :, bass.ds(t * P, P)]).then_inc(tile_in, 1)
                    take(0, 0)
                    take(1, 1)
                    with pool.Fori(1, NT // 2) as i:
                        for s in range(2):
                            pool.wait_ge(y_out, (i * 2 + (s - 1)) * IC)
                            take(i * 2 + s, s)

                @block.tensor
                def _(pe):
                    def before(t, s):
                        pe.wait_ge(tile_in, t * 2 + 2)
                        pe.matmul(g_ps[:, s, 0:P], xin[:, s, IC, :], xin[:, s, IC + 1, :], start=True, stop=True)
                        pe.transpose(g_ps[:, s, P:P + H], din[:, s, 1, :], k.ident[0:H, 0:H])
                        pe.transpose(g_ps[:, s, P + H:P + 2 * H], din[:, s, 0, :],
                                     k.ident[0:H, 0:H]).then_inc(cols_ready, 1)
                        pe.wait_ge(diffed, t + 1)
                        for h in range(H):
                            mm = pe.matmul(c_ps[:, h, :], sel[:, h, :], din[:, s, 1, :], start=True, stop=True)
                        mm.then_inc(cums, 1)
                        for c in range(IC):
                            mm = pe.transpose(x_ps[:, s, bass.ts(c, P)], xin[:, s, c, :], k.ident[:])
                        mm.then_inc(x_turned, 1)

                    def after(t, s):
                        pe.wait_ge(weighed, t + 1)
                        pe.wait_ge(x_scaled, t + 1)
                        for h in range(H):
                            r = slice((h % 2) * 64, (h % 2) * 64 + 64)
                            mm = pe.matmul(y_ps[r, s, bass.ts(h // 2, P)], xdt[:, s, bass.ts(h, 64)],
                                           dec[:, s, h, :], start=True, stop=True)
                        mm.then_inc(summed, 1)

                    with pe.Fori(0, NT // 2) as i:
                        before(i * 2, 0)
                        before(i * 2 + 1, 1)
                        after(i * 2, 0)
                        after(i * 2 + 1, 1)

                @block.scalar
                def _(act):
                    with act.Fori(0, NT // 2) as i:
                        for s in range(2):
                            act.wait_ge(masked, i * 2 + (s + 1))
                            act.activation(dec[:, s], dec[:, s], ACT.Exp).then_inc(decayed, 1)

                @block.vector
                def _(dve):
                    dve.sem_inc(diffed, 1)

                    def before(t, s):
                        dve.wait_ge(cols_ready, t + 1)
                        dve.tensor_copy(cols[:, s, :], g_ps[:, s, P:P + 2 * H]).then_inc(cols_taken, 1)
                        dve.wait_ge(cols_taken, t + 1)
                        dve.wait_ge(cums, t + 1)
                        dve.tensor_tensor(dec[:, s], c_ps[:], over(cols[:, s, 0:H], 2, P),
                                          ALU.subtract).then_inc(diffed, 1)
                        dve.wait_ge(x_turned, t + 1)
                        dve.tensor_tensor(xdt[:, s, :].rearrange("p (h q) -> p h q", h=H),
                                          x_ps[:, s, :].rearrange("p (h q) -> p h q", h=H),
                                          over(cols[:, s, H:2 * H], 2, 64), ALU.mult).then_inc(x_scaled, 1)
                        dve.wait_ge(diffed, t + 2)
                        dve.tensor_tensor(dec[:, s], dec[:, s], over(bar[:], 1, H), ALU.add).then_inc(masked, 1)

                    def after(t, s):
                        dve.wait_ge(decayed, t + 1)
                        dve.tensor_tensor(dec[:, s], dec[:, s], over(g_ps[:, s, 0:P], 1, H),
                                          ALU.mult).then_inc(weighed, 1)

                    def last(t, s):
                        dve.wait_ge(summed, t + 1)
                        for c in range(IC):
                            dve.scalar_tensor_tensor(y[:, c, bass.ds(t * P, P)], xin[:, s, c, :], dcol[:, c:c + 1],
                                                     y_ps[:, s, bass.ts(c, P)], ALU.mult, ALU.add
                                                     ).then_inc(y_out, 1)

                    with dve.Fori(0, NT // 2) as i:
                        for step_ in (before, after, last):
                            step_(i * 2, 0)
                            step_(i * 2 + 1, 1)
        multiply(k, y, y, zs, IC)
        layernorm(k, y, y, 1e-5, affine=(nw, None), centre=False, width=IC)
        add_projection(k, y, wout, IC, more=k.xn)


def long_convolution(k):
    nc = k.nc
    DI, NS = 512, 16
    IC = DI // P
    PAD = 3
    with ExitStack() as ctx:
        keep = lambda n, shape: ctx.enter_context(nc.sbuf_tensor(f"lc_{n}", shape, F32))
        win = keep("win", [P, CD, 2 * DI])
        wconv = keep("wconv", [P, IC, 4, DI])
        wout = keep("wout", [P, IC, D])
        nw = keep("nw", [P, CD])
        inb = keep("inb", [P, 2 * IC])
        cvb = keep("cvb", [P, IC])
        outb = keep("outb", [P, CD])
        par = keep("par", [P, 3, IC, NS])
        dts = keep("dts", [P, 2, IC])
        iota = keep("iota", [P, T])
        kern = keep("kern", [P, IC, T])
        gs = keep("gs", [P, IC, N])
        xs = keep("xs", [P, IC, N])
        y = keep("y", [P, IC, N])
        d = k.dram
        nm = "L1_attn_"
        prefetch(k, (par[:], d[nm + "par"]), (dts[:], d[nm + "dts"]), (iota[:], d["lags"].partition_broadcast(P)),
                 (nw[:], d[nm + "nw"]), (win[:], d[nm + "in"]), (inb[:], d[nm + "inb"]),
                 (wconv[:], d[nm + "conv"]), (cvb[:], d[nm + "cvb"]), (wout[:], d[nm + "out"]),
                 (outb[:], d[nm + "outb"]))
        layernorm(k, k.xT, k.xn, 1e-5)
        with k.stage("kern", "act_in", "act_out", "step") as (sb, ps, act_in, act_out, step):
            a = sb("a", [P, IC, NS])
            x = sb("x", [P, IC, NS])
            th = sb("th", [P, IC, NS])
            sg = sb("sg", [P, IC])
            e = sb("e", [P, IC, T, NS])
            with nc.Block() as block:
                @block.scalar
                def _(act):
                    act.wait_ge(k.weights, k.due)
                    act.activation(a[:], par[:, 0], ACT.Exp)
                    act.activation(sg[:], dts[:, 0], ACT.Sigmoid).then_inc(act_out, 1)
                    act.wait_ge(act_in, 1)
                    act.activation(th[:], x[:], ACT.Tanh, scale=0.5).then_inc(act_out, 1)
                    act.wait_ge(act_in, 2)
                    for c in range(IC):
                        act.activation(e[:, c], e[:, c], ACT.Exp).then_inc(act_out, 1)

                @block.vector
                def _(dve):
                    link = Chain(dve, step)
                    tt = dve.tensor_tensor
                    dve.wait_ge(act_out, 1)
                    link(dve.tensor_scalar(a[:], a[:], -1.0, None, ALU.mult))
                    tt(x[:], a[:], over(sg[:], 2, NS), ALU.mult).then_inc(act_in, 1)
                    dve.wait_ge(act_in, 1)
                    for c in range(IC):
                        ins = tt(e[:, c], over(x[:, c], 1, T), over(iota[:], 2, NS), ALU.mult)
                    ins.then_inc(act_in, 1)
                    dve.wait_ge(act_out, 2)
                    dve.wait_ge(act_in, 2)
                    link(dve.tensor_scalar(x[:], th[:], -1.0, 1.0, ALU.mult, ALU.add))
                    link(dve.tensor_scalar(a[:], a[:], 1e-8, None, ALU.add))
                    link(tt(x[:], x[:], a[:], ALU.mult))
                    link(dve.reciprocal(a[:], x[:]))
                    link(tt(th[:], th[:], par[:, 1], ALU.mult))
                    link(tt(th[:], th[:], par[:, 2], ALU.mult))
                    link(dve.scalar_tensor_tensor(th[:], th[:], 2.0, a[:], ALU.mult, ALU.mult))
                    for c in range(IC):
                        dve.wait_ge(act_out, 3 + c)
                        link(tt(e[:, c], e[:, c], over(th[:, c], 1, T), ALU.mult))
                        link(dve.tensor_reduce(kern[:, c, :], e[:, c], AX.X, ALU.add))
                    dve.tensor_tensor(kern[:, :, 0:1], kern[:, :, 0:1], over(dts[:, 1], 2, 1), ALU.add)
        with nc.sbuf_tensor("lc_pad", [P, IC, B * (T + PAD)], F32) as pad:
            padded = pad[:].rearrange("p c (b t) -> p c b t", t=T + PAD)
            with nc.sbuf_tensor("lc_u", [P, CD, N], F32) as u:
                with nc.Block() as block:
                    @block.gpsimd
                    def _(pool):
                        pool.memset(pad[:], 0.0)
                layernorm(k, k.xn, u, 1e-6, affine=(nw, None), centre=False)

                def drain(act, m, n, bank):
                    if m < IC:
                        to = padded[:, m, n * B // 2:(n + 1) * B // 2, PAD:]
                        return act.activation(to, by_batch(bank), ACT.Identity, bias=inb[:, m:m + 1])
                    return act.activation(gs[:, m - IC, bass.ts(n, HALF)], bank, ACT.Silu, bias=inb[:, m:m + 1])
                project(k, u, win, CD, 2 * IC, drain)
            with k.stage("fullconv", "ready", "taken", "lagged", "diag_ready", "diag_used") as (
                    sb, ps, ready, taken, lagged, diag_ready, diag_used):
                RING = 4
                bank = ps("bank", [P, 4, HALF])
                last = ps("last", [P, 2, HALF])
                diag = sb("diag", [P, RING, P])
                items = [(m, n) for m in range(IC) for n in range(2)]
                halves = lambda ap, n: by_batch(ap[:, bass.ts(n, HALF)])
                with nc.Block() as block:
                    @block.tensor
                    def _(pe):
                        for q, (m, n) in enumerate(items):
                            if q >= 4:
                                pe.wait_ge(taken, q - 3)
                            for c in range(IC):
                                for tap in range(4):
                                    mm = pe.matmul(bank[:, q % 4, :], wconv[:, c, tap, bass.ts(m, P)],
                                                   padded[:, c, n * B // 2:(n + 1) * B // 2, tap:tap + T],
                                                   start=c + tap == 0, stop=c == IC - 1 and tap == 3)
                            mm.then_inc(ready, 1)
                        pe.wait_ge(taken, len(items))
                        for lag in range(T):
                            pe.wait_ge(diag_ready, lag + 1)
                            for n in range(2):
                                x, to = halves(xs[:, IC - 1, :], n), by_batch(last[:, n, :])
                                mm = pe.matmul(to[:, :, lag:], diag[:, lag % RING, :], x[:, :, 0:T - lag],
                                               start=lag == 0, stop=lag == T - 1)
                            mm.then_inc(diag_used, 1)

                    @block.scalar
                    def _(act):
                        for q, (m, n) in enumerate(items):
                            act.wait_ge(ready, q + 1)
                            act.activation(xs[:, m, bass.ts(n, HALF)], bank[:, q % 4, :], ACT.Silu,
                                           bias=cvb[:, m:m + 1]).then_inc(taken, 1)
                        for lag in range(T):
                            if lag >= RING:
                                act.wait_ge(diag_used, lag - RING + 1)
                            act.activation(diag[:, lag % RING, :], k.ident[:], ACT.Identity,
                                           scale=kern[:, IC - 1, lag:lag + 1]).then_inc(diag_ready, 1)

                    @block.vector
                    def _(dve):
                        for c in range(IC - 1):
                            for lag in range(T):
                                for n in range(2):
                                    a, r = halves(y[:, c, :], n), halves(xs[:, c, :], n)
                                    if lag == 0:
                                        dve.wait_ge(taken, 2 * c + n + 1)
                                        dve.tensor_scalar(a, r, kern[:, c, 0:1], None, ALU.mult).then_inc(lagged, 1)
                                    else:
                                        dve.wait_ge(lagged, (c * T + lag - 1) * 2 + n + 1)
                                        dve.scalar_tensor_tensor(a[:, :, lag:], r[:, :, 0:T - lag],
                                                                 kern[:, c, lag:lag + 1], a[:, :, lag:],
                                                                 ALU.mult, ALU.add).then_inc(lagged, 1)
                            dve.wait_ge(lagged, (c + 1) * T * 2)
                            dve.tensor_tensor(y[:, c, :], y[:, c, :], gs[:, c, :], ALU.mult)
                        dve.wait_ge(diag_used, T)
                        dve.tensor_tensor(y[:, IC - 1, :], last[:].rearrange("p n q -> p (n q)"), gs[:, IC - 1, :],
                                          ALU.mult)
        add_projection(k, y, wout, IC, more=k.xn, bias=outb)


def softplus(k, v, parts, rows=P):
    nc = k.nc
    with k.stage("softplus", "absed", "exped", "shifted", "logged", "topped", "lost") as (
            sb, ps, absed, exped, shifted, logged, topped, lost):
        e = sb("e", [rows, parts, N])
        w = sb("w", [rows, parts, N])
        with nc.Block() as block:
            @block.scalar
            def _(act):
                for c in range(parts):
                    act.wait_ge(absed, c + 1)
                    act.activation(e[:, c, :], e[:, c, :], ACT.Exp, scale=-1.0).then_inc(exped, 1)
                for c in range(parts):
                    act.wait_ge(lost, c + 1)
                    act.activation(w[:, c, :], w[:, c, :], ACT.Ln).then_inc(logged, 1)

            @block.vector
            def _(dve):
                for c in range(parts):
                    dve.tensor_scalar(w[:, c, :], v[:, c, :], 0.0, None, ALU.max).then_inc(topped, 1)
                for c in range(parts):
                    dve.wait_ge(topped, c + 1)
                    dve.scalar_tensor_tensor(e[:, c, :], w[:, c, :], 2.0, v[:, c, :], ALU.mult,
                                             ALU.subtract).then_inc(absed, 1)
                for c in range(parts):
                    dve.wait_ge(absed, c + 1)
                    dve.tensor_copy(v[:, c, :], w[:, c, :]).then_inc(topped, 1)
                for c in range(parts):
                    dve.wait_ge(exped, c + 1)
                    dve.wait_ge(topped, parts + c + 1)
                    dve.tensor_scalar(w[:, c, :], e[:, c, :], 1.0, None, ALU.add).then_inc(shifted, 1)
                for c in range(parts):
                    dve.wait_ge(shifted, c + 1)
                    dve.scalar_tensor_tensor(e[:, c, :], w[:, c, :], -1.0, e[:, c, :], ALU.add,
                                             ALU.subtract).then_inc(lost, 1)
                for c in range(parts):
                    dve.wait_ge(lost, c + 1)
                    dve.tensor_tensor(v[:, c, :], v[:, c, :], e[:, c, :], ALU.subtract).then_inc(shifted, 1)
                for c in range(parts):
                    dve.wait_ge(logged, c + 1)
                    dve.wait_ge(shifted, parts + c + 1)
                    dve.tensor_tensor(v[:, c, :], v[:, c, :], w[:, c, :], ALU.add)


def selective_scan(k):
    nc = k.nc
    DI, NS = 512, 16
    IC = DI // P
    HB = B // 2
    nm, d = "L2_attn_", k.dram
    with ExitStack() as ctx:
        keep = lambda n, shape: ctx.enter_context(nc.sbuf_tensor(f"scan_{n}", shape, F32))
        wout = keep("wout", [P, IC, D])
        nw = keep("nw", [P, IC])
        dcol = keep("dcol", [P, IC])
        alog = keep("alog", [P, IC * NS])
        zs = keep("zs", [P, IC, N])
        xc = keep("xc", [P, IC, N])
        delta = keep("delta", [P, IC, N])
        with ExitStack() as early:
            brief = lambda n, shape: early.enter_context(nc.sbuf_tensor(f"scan_{n}", shape, F32))
            win = brief("win", [P, CD, 2 * DI])
            wx = brief("wx", [P, IC, P])
            wdt = brief("wdt", [NS, 1, DI])
            cw = brief("cw", [P, IC, 4])
            cb = brief("cb", [P, IC])
            dtb = brief("dtb", [P, IC])
            raw = brief("raw", [P, IC, N])
            xd = brief("xd", [3 * NS, 1, N])
            prefetch(k, (win[:], d[nm + "in"]), (cw[:], d[nm + "cw"]), (cb[:], d[nm + "cb"]), (wx[:], d[nm + "x"]),
                     (wdt[:, 0, :], d[nm + "wdt"]), (dtb[:], d[nm + "dtb"]), (alog[:], d[nm + "A"]),
                     (dcol[:], d[nm + "D"]), (nw[:], d[nm + "nw"]), (wout[:], d[nm + "out"]))
            layernorm(k, k.xT, k.xn, 1e-5)

            def drain(act, m, n, bank):
                if m < IC:
                    return act.copy(raw[:, m, bass.ts(n, HALF)], bank)
                return act.activation(zs[:, m - IC, bass.ts(n, HALF)], bank, ACT.Silu)
            project(k, k.xn, win, CD, 2 * IC, drain)
            causal_conv(k, raw, xc, cw, cb, IC)
            project(k, xc, wx, IC, 1, lambda act, m, n, bank: act.copy(xd[:, 0, bass.ts(n, HALF)], bank[0:3 * NS, :]))
            with k.stage("bc", "stored") as (sb, ps, stored):
                with nc.Block() as block:
                    @block.sync
                    def _(sp):
                        sp.dma_start(k.bc, xd[NS:3 * NS, 0, :]).then_inc(stored, 16)
                        sp.wait_ge(stored, 16)
            project(k, xd[0:NS], wdt, 1, IC,
                    lambda act, m, n, bank: act.activation(delta[:, m, bass.ts(n, HALF)], bank, ACT.Identity,
                                                           bias=dtb[:, m:m + 1]))
        bb = keep("bb", [P, NS, HALF])
        cc = keep("cc", [P, NS, HALF])
        state_rows = [(bb, n, n) for n in range(NS)] + [(cc, n, NS + n) for n in range(NS)]
        prefetch(k, *((to[:, n, :], k.bc[r, 0:HALF].partition_broadcast(P)) for to, n, r in state_rows))
        softplus(k, delta, IC)
        y = keep("y", [P, IC, N])
        with k.stage("scan", "rows_landed", "a_ready", "in_taken", "decay_out", "decay_ready", "drive_ready",
                     "scanned", "read_out", "summed", "y_out", "a_exped", "zeroed") as (
                sb, ps, rows_landed, a_ready, in_taken, decay_out, decay_ready, drive_ready, scanned, read_out,
                summed, y_out, a_exped, zeroed):
            RING = 4
            none = sb("none", [P, HB])
            av = sb("av", [P, IC * NS])
            dl = sb("dl", [P, HALF])
            ut = sb("ut", [P, HALF])
            ac = sb("ac", [P, NS])
            da = sb("da", [P, RING, HALF])
            db = sb("db", [P, RING, HALF])
            hh = sb("hh", [P, RING, HALF])
            hc = sb("hc", [P, RING, HALF])
            y_ps = ps("y_ps", [P, HALF])
            with nc.Block() as block:
                @block.sync
                def _(sp):
                    for n in range(NS):
                        sp.wait_ge(read_out, (IC - 1) * NS + n + 1 + RING)
                        for to, r in ((bb, n), (cc, NS + n)):
                            sp.dma_start(to[:, n, :], k.bc[r, HALF:N].partition_broadcast(P)
                                         ).then_inc(rows_landed, 16)

                @block.scalar
                def _(act):
                    act.activation(av[:], alog[:], ACT.Exp).then_inc(a_exped, 1)
                    for g in range(2):
                        with act.Fori(0, IC) as c:
                            it = c + g * IC
                            act.wait_ge(in_taken, it * 3 + 3)
                            for n in range(NS):
                                q = it * NS + n
                                act.wait_ge(scanned, q + 1)
                                act.activation(da[:, n % RING, :], dl[:], ACT.Exp,
                                               scale=ac[:, n:n + 1]).then_inc(decay_out, 1)

                @block.gpsimd
                def _(pool):
                    pool.memset(none[:], 0.0).then_inc(zeroed, 1)
                    pool.wait_ge(zeroed, 1)
                    for g in range(2):
                        if g == 0:
                            pool.wait_ge(k.weights, k.due)
                        else:
                            pool.wait_ge(rows_landed, 2 * NS * 16)
                        with pool.Fori(0, IC) as c:
                            it = c + g * IC
                            pool.wait_ge(in_taken, it * 3 + 3)
                            for n in range(NS):
                                q = it * NS + n
                                pool.wait_ge(scanned, q + 1)
                                pool.tensor_tensor(db[:, n % RING, :], ut[:], bb[:, n, :],
                                                   ALU.mult).then_inc(drive_ready, 1)
                                pool.wait_ge(decay_out, q + 1)
                                pool.tensor_tensor(by_batch(da[:, n % RING, :])[:, :, 0], none[:], none[:],
                                                   ALU.mult).then_inc(decay_ready, 1)

                @block.vector
                def _(dve):
                    dve.sem_inc(scanned, RING)
                    dve.sem_inc(summed, RING)
                    dve.sem_inc(read_out, RING)
                    dve.sem_inc(y_out, 1)
                    dve.wait_ge(a_exped, 1)
                    dve.tensor_scalar(av[:], av[:], -1.0, None, ALU.mult).then_inc(a_ready, 1)
                    dve.wait_ge(a_ready, 1)
                    for g in range(2):
                        if g == 0:
                            dve.wait_ge(k.weights, k.due)
                        else:
                            dve.wait_ge(rows_landed, 2 * NS * 16)
                        with dve.Fori(0, IC) as c:
                            it = c + g * IC
                            half = bass.ds(c * N + g * HALF, HALF)
                            flat = lambda t: t[:].rearrange("p c n -> p (c n)")[:, half]
                            dve.tensor_copy(dl[:], flat(delta)).then_inc(in_taken, 1)
                            dve.tensor_tensor(ut[:], flat(delta), flat(xc), ALU.mult).then_inc(in_taken, 1)
                            dve.tensor_copy(ac[:], av[:, bass.ds(c * NS, NS)]).then_inc(in_taken, 1)

                            def read(n):
                                q = it * NS + n
                                dve.wait_ge(scanned, q + 1 + RING)
                                dve.wait_ge(summed, q + 1)
                                dve.tensor_tensor(hc[:, n % RING, :], hh[:, n % RING, :], cc[:, n, :],
                                                  ALU.mult).then_inc(read_out, 1)

                            for n in range(NS):
                                q = it * NS + n
                                dve.wait_ge(decay_ready, q + 1)
                                dve.wait_ge(read_out, q + 1)
                                dve.wait_ge(drive_ready, q + 1)
                                dve.tensor_tensor_scan(hh[:, n % RING, :], da[:, n % RING, :], db[:, n % RING, :],
                                                       0.0, ALU.mult, ALU.add).then_inc(scanned, 1)
                                if n >= 1:
                                    read(n - 1)
                            read(NS - 1)
                            dve.wait_ge(summed, it * NS + NS + RING)
                            dve.tensor_copy(flat(y), y_ps[:]).then_inc(y_out, 1)

                @block.tensor
                def _(pe):
                    for g in range(2):
                        with pe.Fori(0, IC) as c:
                            it = c + g * IC
                            for n in range(NS):
                                pe.wait_ge(read_out, it * NS + (n + 1 + RING))
                                if n == 0:
                                    pe.wait_ge(y_out, it + 1)
                                pe.matmul(y_ps[:], k.ident[:], hc[:, n % RING, :], start=n == 0,
                                          stop=n == NS - 1).then_inc(summed, 1)
        with k.stage("skip", "skipped") as (sb, ps, skipped):
            with nc.Block() as block:
                @block.vector
                def _(dve):
                    for c in range(IC):
                        dve.scalar_tensor_tensor(y[:, c, :], xc[:, c, :], dcol[:, c:c + 1], y[:, c, :], ALU.mult,
                                                 ALU.add).then_inc(skipped, 1)
                    for c in range(IC):
                        dve.wait_ge(skipped, c + 1)
                        dve.tensor_tensor(y[:, c, :], y[:, c, :], zs[:, c, :], ALU.mult)
        layernorm(k, y, y, 1e-8, affine=(nw, None), centre=False, width=IC)
        add_projection(k, y, wout, IC)



def correlation_attention(k):
    nc = k.nc
    heads, dk, slot = 16, 16, 32
    per, IC = P // slot, HALF // P
    nm, d = "L3_attn_", k.dram
    with ExitStack() as ctx:
        keep = lambda n, shape: ctx.enter_context(nc.sbuf_tensor(f"corr_{n}", shape, F32))
        wqk = keep("wqk", [P, CD, 2 * HALF])
        wv = keep("wv", [P, CD, HALF])
        wo = keep("wo", [P, IC, D])
        vmat = keep("vmat", [P, P])
        qk = keep("qk", [P, 2 * IC, N])
        oT = keep("oT", [P, IC, N])
        prefetch(k, (wqk[:], d[nm + "Wqk"]), (vmat[:], d["slotvar"]), (wv[:], d[nm + "Wv"]), (wo[:], d[nm + "Wo"]))
        layernorm(k, k.xT, k.xn, 1e-5)
        with k.stage("centre", "step") as (sb, ps, step):
            mean = sb("mean", [P, CD * 2 * heads])
            with nc.Block() as block:
                @block.vector
                def _(dve):
                    link = Chain(dve, step)
                    dve.wait_ge(k.weights, k.due)
                    w = wqk[:].rearrange("p c (h r) -> p (c h) r", r=slot)[:, :, 0:dk]
                    link(dve.tensor_reduce(mean[:], w, AX.X, ALU.add))
                    link(dve.tensor_scalar(mean[:], mean[:], 1.0 / dk, None, ALU.mult))
                    dve.tensor_tensor(w, w, over(mean[:], 2, dk), ALU.subtract)
        with k.stage("qk", "ready", "squared", "var_ready", "copied", "added") as (
                sb, ps, ready, squared, var_ready, copied, added):
            sq = sb("sq", [P, 2, HALF])
            bank = ps("bank", [P, 2, HALF])
            vbank = ps("vbank", [P, 2, HALF])
            items = [(m, n) for m in range(2 * IC) for n in range(2)]
            with nc.Block() as block:
                @block.tensor
                def _(pe):
                    for q in range(len(items) + 1):
                        if q < len(items):
                            m, n = items[q]
                            if q >= 2:
                                pe.wait_ge(squared, q - 1)
                            for c in range(CD):
                                mm = pe.matmul(bank[:, q % 2, :], wqk[:, c, bass.ts(m, P)],
                                               k.xn[:, c, bass.ts(n, HALF)], start=c == 0, stop=c == CD - 1)
                            mm.then_inc(ready, 1)
                        if q >= 1:
                            if q >= 3:
                                pe.wait_ge(added, q - 2)
                            pe.wait_ge(squared, q)
                            pe.matmul(vbank[:, (q - 1) % 2, :], vmat[:], sq[:, (q - 1) % 2, :], start=True,
                                      stop=True).then_inc(var_ready, 1)

                @block.scalar
                def _(act):
                    for q, (m, n) in enumerate(items):
                        act.wait_ge(ready, q + 1)
                        act.copy(qk[:, m, bass.ts(n, HALF)], bank[:, q % 2, :]).then_inc(copied, 1)
                        if q >= 2:
                            act.wait_ge(var_ready, q - 1)
                        act.activation(sq[:, q % 2, :], bank[:, q % 2, :], ACT.Square).then_inc(squared, 1)

                @block.vector
                def _(dve):
                    for q, (m, n) in enumerate(items):
                        x = qk[:, m, bass.ts(n, HALF)]
                        dve.wait_ge(copied, q + 1)
                        dve.wait_ge(var_ready, q + 1)
                        dve.tensor_tensor(x, x, vbank[:, q % 2, :], ALU.add).then_inc(added, 1)

        with k.stage("corr", "zeroed", "batch_in", "v_ready", "v_taken", "scored", "shifted", "exped", "normed",
                     "turned", "turned_v", "mixed", "out_taken", "step") as (
                sb, ps, zeroed, batch_in, v_ready, v_taken, scored, shifted, exped, normed, turned, turned_v,
                mixed, out_taken, step):
            W = per * T
            xb = sb("xb", [P, 2, CD, 2, T])
            qblk = sb("qblk", [P, 2, IC, W])
            vb = sb("vb", [P, 2, HALF])
            sm = sb("sm", [P, 2, 2 * IC, T])
            row = sb("row", [P, 2, 3, 2 * IC])
            pT = sb("pT", [P, IC, 2, P])
            s_ps = ps("s_ps", [P, 2, 2 * IC, T])
            v_ps = ps("v_ps", [P, HALF])
            t_ps = ps("t_ps", [P, IC, P])
            o_ps = ps("o_ps", [P, IC, 2, P])
            with nc.Block() as block:
                @block.gpsimd
                def _(pool):
                    pool.memset(pT[:], 0.0).then_inc(zeroed, 1)
                    pool.memset(qblk[:], 0.0).then_inc(zeroed, 1)
                    pool.wait_ge(zeroed, 2)

                    def take(b, s):
                        if not (isinstance(b, int) and b == 0):
                            pool.wait_ge(batch_in, b * (per + 1))
                        pool.tensor_copy(xb[:, s], over(k.xn[:, :, bass.ds(b * T, T)], 2, 2)).then_inc(batch_in, 1)
                        pool.wait_ge(batch_in, b * (per + 1) + 1)
                        for g in range(per):
                            r = slice(g * slot, (g + 1) * slot)
                            pool.tensor_copy(qblk[r, s, :, bass.ts(g, T)],
                                             qk[r, 0:IC, bass.ds(b * T, T)]).then_inc(batch_in, 1)
                    take(0, 0)
                    take(1, 1)
                    with pool.Fori(1, B // 2) as i:
                        for s in range(2):
                            pool.wait_ge(scored, i * 2 + (s - 1))
                            take(i * 2 + s, s)

                @block.tensor
                def _(pe):
                    def values(b, s):
                        pe.wait_ge(batch_in, (b + 1) * (per + 1))
                        pe.wait_ge(v_taken, b + 1)
                        for c in range(CD):
                            mm = pe.matmul(v_ps[:], xb[:, s, c].rearrange("p a t -> p (a t)"), wv[:, c, :],
                                           start=c == 0, stop=c == CD - 1)
                        mm.then_inc(v_ready, 1)

                    def scores(b, s):
                        for j in range(2 * IC):
                            mm = pe.matmul(s_ps[:, s, j, :], qblk[:, s, j // 2, bass.ts(j % 2, P)],
                                           qk[:, IC + j // 2, bass.ds(b * T, T)], start=True, stop=True)
                        mm.then_inc(scored, 1)

                    def turn(b, s):
                        pe.wait_ge(normed, b + 1)
                        for m in range(IC):
                            mm = pe.transpose(t_ps[:, m, :], sm[:, s, 2 * m:2 * m + 2, :].rearrange(
                                "p a t -> p (a t)"), k.ident[:])
                        mm.then_inc(turned, 1)

                    def mix(b, s):
                        pe.wait_ge(turned_v, b + 1)
                        pe.wait_ge(out_taken, b + 1)
                        for m in range(IC):
                            mm = pe.matmul(o_ps[:, m].rearrange("p a q -> p (a q)"), vb[:, s, bass.ts(m, P)],
                                           pT[:, m].rearrange("p a q -> p (a q)"), start=True, stop=True)
                        mm.then_inc(mixed, 1)

                    def batch(b, s, last):
                        if not last:
                            values(b + 1, 1 - s)
                        turn(b, s)
                        if not last:
                            scores(b + 1, 1 - s)
                        mix(b, s)

                    values(0, 0)
                    scores(0, 0)
                    every_batch(pe, batch)

                @block.scalar
                def _(act):
                    act.sem_inc(v_taken, 1)
                    act.sem_inc(out_taken, 1)

                    def before(b, s):
                        act.wait_ge(v_ready, b + 1)
                        act.copy(vb[:, s, :], v_ps[:]).then_inc(v_taken, 1)
                        act.wait_ge(shifted, b + 1)
                        act.activation(sm[:, s], sm[:, s], ACT.Exp, scale=1.0 / dk).then_inc(exped, 1)

                    def batch(b, s, last):
                        if not last:
                            before(b + 1, 1 - s)
                        act.wait_ge(mixed, b + 1)
                        for g in range(per):
                            r = slice(g * slot, (g + 1) * slot)
                            cp = act.copy(oT[r, :, bass.ds(b * T, T)], o_ps[r, :, g // 2, bass.ts(g % 2, T)])
                        cp.then_inc(out_taken, 1)

                    before(0, 0)
                    every_batch(act, batch)

                @block.vector
                def _(dve):
                    def shift(b, s):
                        dve.wait_ge(scored, b + 1)
                        dve.tensor_reduce(row[:, s, 0, :], s_ps[:, s], AX.X, ALU.max).then_inc(step, 1)
                        dve.wait_ge(step, b * 3 + 1)
                        dve.tensor_tensor(sm[:, s], s_ps[:, s], over(row[:, s, 0, :], 2, T),
                                          ALU.subtract).then_inc(shifted, 1)

                    def norm(b, s):
                        dve.wait_ge(exped, b + 1)
                        dve.tensor_reduce(row[:, s, 1, :], sm[:, s], AX.X, ALU.add).then_inc(step, 1)
                        dve.wait_ge(step, b * 3 + 2)
                        dve.reciprocal(row[:, s, 2, :], row[:, s, 1, :]).then_inc(step, 1)
                        dve.wait_ge(step, b * 3 + 3)
                        dve.tensor_tensor(sm[:, s], sm[:, s], over(row[:, s, 2, :], 2, T),
                                          ALU.mult).then_inc(normed, 1)

                    def batch(b, s, last):
                        norm(b, s)
                        dve.wait_ge(turned, b + 1)
                        dve.tensor_copy(pT[0:T, :, 0, :], t_ps[0:T])
                        dve.tensor_copy(pT[T:P, :, 1, :], t_ps[T:P]).then_inc(turned_v, 1)
                        if not last:
                            shift(b + 1, 1 - s)

                    dve.wait_ge(zeroed, 2)
                    shift(0, 0)
                    every_batch(dve, batch)
        add_projection(k, oT, wo, IC)


def masked_cross_attention(k):
    nc = k.nc
    heads, dk = 4, 64
    IC = heads * dk // P
    NK = S // P
    KEYS = S + T
    KR = DC - P
    nm, d = "L3_xattn_", k.dram
    with ExitStack() as ctx:
        keep = lambda n, shape: ctx.enter_context(nc.sbuf_tensor(f"mx_{n}", shape, F32))
        wq = keep("wq", [P, CD, IC * P])
        wl = keep("wl", [P, CD, 2 * IC * P])
        wc = keep("wc", [P, 3, 2 * IC * P])
        wkH, wkL = (ctx.enter_context(nc.sbuf_tensor(f"mx_wk{n}", [P, 2, IC * P], F32R)) for n in "HL")
        wv = keep("wv", [P, 2, IC * P])
        bkb = keep("bkb", [P, IC * P])
        m8 = ctx.enter_context(nc.sbuf_tensor("mx_m8", [B, S // 4], mybir.dt.uint32))
        bars = ctx.enter_context(nc.sbuf_tensor("mx_bars", [P, S], F32R))
        wo = keep("wo", [P, IC, D])
        bo = keep("bo", [P, CD])
        lnl = keep("lnl", [P, 2, CD])
        lnx = keep("lnx", [P, 2, 3])
        qg = keep("qg", [P, 2])
        pair = keep("pair", [P, P])
        lat = keep("lat", [P, CD, N])
        qT = keep("qT", [P, IC, N])
        oT = keep("oT", [P, IC, N])
        prefetch(k, (lnl[:], d[nm + "lnl"]), (lnx[:], d[nm + "lnx"]), (qg[:], d[nm + "qg"]), (pair[:], d["pair"]),
                 (m8[:], d["mask"]), (wq[:], d[nm + "Wq"]), (wc[:], d[nm + "Wkv"]), (wl[:], d[nm + "Wlkv"]),
                 (wo[:], d[nm + "Wo"]),
                 (bo[:], d[nm + "bo"]))
        layernorm(k, k.xT, k.xn, 1e-5)
        layernorm(k, k.xn, lat, 1e-5, affine=(lnl[:, 0, :], lnl[:, 1, :]))
        with k.stage("fold", "spread", "bias_ready", "scaled", "sums_ready", "centred", "split", "step",
                     "cleared", "cast") as (
                sb, ps, spread, bias_ready, scaled, sums_ready, centred, split, step, cleared, cast):
            bB = sb("bB", [P, 2, P])
            mf = sb("mf", [B, S])
            b_ps = ps("b_ps", [P, 2 * IC * P])
            s_ps = ps("s_ps", [P, 2 * IC * P])
            with nc.Block() as block:
                @block.tensor
                def _(pe):
                    pe.wait_ge(spread, 2)
                    for c in range(2):
                        mm = pe.matmul(b_ps[:], bB[:, c, :], wc[:, c, :], start=c == 0, stop=c == 1)
                    mm.then_inc(bias_ready, 1)
                    pe.wait_ge(scaled, 3)
                    for c in range(2):
                        mm = pe.matmul(s_ps[:], k.ones[:], wc[:, c, :], start=c == 0, stop=c == 1)
                    mm.then_inc(sums_ready, 1)

                @block.gpsimd
                def _(pool):
                    pool.memset(bars[:].bitcast(F32), 0.0).then_inc(cleared, 1)

                @block.vector
                def _(dve):
                    dve.wait_ge(k.weights, k.due)
                    for c in range(2):
                        dve.tensor_scalar(bB[:, c, :], k.ones[:], lnx[:, 1, c:c + 1], None, ALU.mult
                                          ).then_inc(spread, 1)
                    dve.tensor_copy(mf[:], m8[:].bitcast(mybir.dt.uint8)).then_inc(cast, 1)
                    dve.wait_ge(cleared, 1)
                    dve.wait_ge(cast, 1)
                    dve.tensor_scalar(bars[0:B, :], mf[:], -1.0, 1e30, ALU.add, ALU.mult)
                    dve.wait_ge(bias_ready, 1)
                    for c in range(3):
                        dve.tensor_scalar(wc[:, c, :], wc[:, c, :], lnx[:, 0, c:c + 1], None, ALU.mult
                                          ).then_inc(scaled, 1)
                    dve.tensor_copy(bkb[:], b_ps[:, 0:IC * P])
                    dve.wait_ge(sums_ready, 1)
                    dve.wait_ge(scaled, 3)
                    for c, rows in ((0, P), (1, KR), (2, P)):
                        dve.scalar_tensor_tensor(wc[0:rows, c, :], s_ps[0:rows, :], -1.0 / DC, wc[0:rows, c, :],
                                                 ALU.mult, ALU.add).then_inc(centred, 1)
                    dve.wait_ge(centred, 3)
                    for c in range(2):
                        dve.tensor_copy(wv[:, c, :], wc[:, c, IC * P:2 * IC * P]).then_inc(split, 1)
                    for c in range(2):
                        dve.tensor_copy(wkH[:, c, :], wc[:, 2 * c, 0:IC * P]).then_inc(split, 1)
                    dve.wait_ge(split, 4)
                    for c in range(2):
                        dve.tensor_tensor(wkL[:, c, :], wc[:, 2 * c, 0:IC * P], wkH[:, c, :].bitcast(F32),
                                          ALU.subtract)
                    dve.tensor_copy(wv[KR:KR + 1, 1, :], b_ps[KR:KR + 1, IC * P:2 * IC * P])
                    dve.tensor_tensor(qg[:, 0:1], qg[:, 0:1], qg[:, 1:2], ALU.mult).then_inc(step, 1)
                    dve.wait_ge(step, 1)
                    dve.tensor_scalar(qg[:, 0:1], qg[:, 0:1], dk ** -0.5, None, ALU.mult)
        project(k, lat, wq, CD, IC, lambda act, m, n, bank: act.copy(qT[:, m, bass.ts(n, HALF)], bank))
        with k.stage("qnorm", "squared", "summed", "rooted", "step") as (sb, ps, squared, summed, rooted, step):
            sq = sb("sq", [P, IC, N])
            n_ps = ps("n_ps", [P, IC, N])
            with nc.Block() as block:
                @block.scalar
                def _(act):
                    act.activation(sq[:], qT[:], ACT.Square).then_inc(squared, 1)
                    act.wait_ge(summed, 1)
                    act.activation(sq[:], n_ps[:], ACT.Sqrt, scale=1.0 / dk).then_inc(rooted, 1)

                @block.tensor
                def _(pe):
                    pe.wait_ge(squared, 1)
                    for c in range(IC):
                        for n in range(2):
                            mm = pe.matmul(n_ps[:, c, bass.ts(n, HALF)], pair[:], sq[:, c, bass.ts(n, HALF)],
                                           start=True, stop=True)
                    mm.then_inc(summed, 1)

                @block.vector
                def _(dve):
                    link = Chain(dve, step)
                    dve.wait_ge(rooted, 1)
                    link(dve.tensor_scalar(sq[:], sq[:], 1e-8, None, ALU.max))
                    link(dve.reciprocal(sq[:], sq[:]))
                    dve.scalar_tensor_tensor(qT[:], qT[:], qg[:, 0:1], sq[:], ALU.mult, ALU.mult)

        attend_masked(k, wl, wkH, wkL, wv, bkb, bars, lat, qT, oT)
        add_projection(k, oT, wo, IC, bias=bo)


def attend_masked(k, wl, wkH, wkL, wv, bkb, bars, lat, qT, oT):
    nc = k.nc
    heads, dk = 4, 64
    IC = heads * dk // P
    KW = IC * P
    NK = S // P
    KEYS = S + T
    KR = DC - P
    G = NK // 2
    KUSES = G + 1
    PUSES = 3
    USES = KUSES + IC * PUSES
    d = k.dram
    with k.stage("mx", "t_landed", "n_landed", "set_up", "batch_in", "split_step",
                 "split_ready", "xs_ready", "var_ready", "var_rooted", "rs_ready", "kproj", "kp_taken", "squared",
                 "sums_ready", "sums_rooted", "keys_ready", "turned", "taken0", "taken1", "scored",
                 "maxed", "exped", "inverted", "mixed", "normed", "mix_turned", "mix_taken", "projected",
                 "out_taken", "step") as (
            sb, ps, t_landed, n_landed, set_up, batch_in, split_step, split_ready,
            xs_ready, var_ready, var_rooted, rs_ready, kproj, kp_taken, squared, sums_ready, sums_rooted,
            keys_ready, turned, taken0, taken1, scored, maxed, exped, inverted, mixed, normed,
            mix_turned, mix_taken, projected, out_taken, step):
        taken = (taken0, taken1)
        cT = sb("cT", [P, 2, S])
        cH = sb("cH", [P, 2, S], F32R)
        cL = sb("cL", [P, 2, S], F32R)
        cR = sb("cR", [P, 2, S], F32R)
        land = sb("land", [P, NK, DC])
        xs = sb("xs", [P, 2, NK, DC + 1])
        pick = sb("pick", [P, 2, P], F32R)
        lb = sb("lb", [P, 2, CD, T])
        qblk = sb("qblk", [P, 2, IC, P])
        st = sb("st", [P, NK, 6])
        mv = sb("mv", [P, NK, 2])
        rs = sb("rs", [P, 2, NK])
        kv = sb("kv", [P, NK + 1, KW])
        sq = sb("sq", [P, NK + 1, KW])
        rn = sb("rn", [P, NK + 1, heads])
        keysT = sb("keysT", [P, 2, IC, KEYS])
        vl = sb("vl", [P, 2, KW])
        sm = sb("sm", [P, IC, (NK + 1) * P])
        pT = sb("pT", [P, IC, NK + 1, P])
        col = sb("col", [P, 3, IC])
        mix = sb("mix", [P, DC + 1])
        mixT = sb("mixT", [P, 2, P])
        kp = ps("kp", [P, 2, HALF])
        tp = ps("tp", [P, 2, HALF])
        s_ps = ps("s_ps", [P, 3, HALF])
        av = ps("av", [P, HALF])

        def after(i, s):
            return (i, 1) if s == 0 else (i + 1, 0)

        def every_batch(eng, step_of):
            with eng.Fori(0, B // 2 - 1) as i:
                step_of(i, 0, 2)
                step_of(i, 1, 2)
            step_of(B // 2 - 1, 0, 1)
            step_of(B // 2 - 1, 1, 0)

        def bank_of(s, v):
            return (USES * s + v) % 2

        def nth(i, s, v):
            return i * USES + (USES * s + v) // 2

        with nc.Block() as block:
            @block.sync
            def _(sp):
                def load_t(b):
                    sp.dma_start(cT[:, 0, :], d["ctxT"][b, 0:P, :]).then_inc(t_landed, 16)
                    for g in range(2):
                        sp.dma_start(cT[g * KR:(g + 1) * KR, 1, :], d["ctxT"][b, P:DC, :]).then_inc(t_landed, 16)

                def load_n(b):
                    sp.dma_start(land[:], d["ctx"][b].rearrange("(j p) d -> p j d", p=P)).then_inc(n_landed, 16)

                load_t(0)
                load_n(0)
                sp.wait_ge(split_ready, 1)
                load_t(1)
                sp.wait_ge(xs_ready, 1)
                load_n(1)
                with sp.Fori(1, B // 2) as i:
                    for s in range(2):
                        b = i * 2 + s
                        sp.wait_ge(split_ready, b)
                        load_t(b)
                        sp.wait_ge(xs_ready, b)
                        load_n(b)

            @block.gpsimd
            def _(pool):
                pool.memset(qblk[:], 0.0).then_inc(set_up, 1)
                pool.memset(kv[:, NK, :], 1.0).then_inc(set_up, 1)
                pool.memset(pT[:, :, NK, :], 0.0).then_inc(set_up, 1)
                pool.memset(vl[:], 0.0).then_inc(set_up, 1)
                pool.memset(mixT[:, 1, :], 0.0).then_inc(set_up, 1)
                pool.memset(xs[:, :, :, DC:DC + 1], 1.0).then_inc(set_up, 1)
                pool.memset(sm[:, :, KEYS:], 0.0).then_inc(set_up, 1)
                pool.wait_ge(set_up, 7)

                def take(b, s):
                    pool.tensor_copy(lb[:, s], lat[:, :, bass.ds(b * T, T)]).then_inc(batch_in, 1)
                    pool.tensor_copy(pick[:, s, :], k.ident[:, bass.ds(b, 1)].broadcast_to([P, P])
                                     ).then_inc(batch_in, 1)
                    pool.wait_ge(batch_in, b * 4 + 2)
                    for g in range(2):
                        r = slice(g * dk, (g + 1) * dk)
                        pool.tensor_copy(qblk[r, s, :, bass.ts(g, T)],
                                         qT[r, :, bass.ds(b * T, T)]).then_inc(batch_in, 1)
                    pool.wait_ge(batch_in, b * 4 + 4)

                def scale(b, s):
                    pool.wait_ge(rs_ready, b + 1)
                    pool.tensor_tensor(xs[:, s, :, 0:DC], land[:], over(rs[:, s, :], 2, DC), ALU.mult
                                       ).then_inc(xs_ready, 1)
                    pool.wait_ge(xs_ready, b + 1)

                def split(b, s):
                    pool.wait_ge(t_landed, b * 48 + 48)
                    x = cT[:, 0, :].rearrange("p (j q) -> p j q", q=P)
                    pool.tensor_tensor(cH[:, s].rearrange("p (j q) -> p j q", q=P), x, over(k.ones[:], 1, NK),
                                       ALU.mult).then_inc(split_step, 1)
                    pool.tensor_copy(cR[:, s], cT[:, 1, :]).then_inc(split_step, 1)
                    pool.wait_ge(split_step, b * 3 + 2)
                    pool.tensor_tensor(cL[:, s], cT[:, 0, :], cH[:, s].bitcast(F32), ALU.subtract
                                       ).then_inc(split_step, 1)
                    pool.wait_ge(split_step, b * 3 + 3)
                    pool.tensor_tensor(cR[KR:P, s], cT[KR:P, 1, :], cR[KR:P, s].bitcast(F32), ALU.subtract
                                       ).then_inc(split_ready, 1)
                    pool.wait_ge(split_ready, b + 1)

                def batch(i, s, more):
                    b = i * 2 + s
                    if more >= 1:
                        pool.wait_ge(out_taken, b * IC + 1)
                        scale(b + 1, 1 - s)
                        take(b + 1, 1 - s)
                    if more >= 2:
                        pool.wait_ge(kproj, (b + 1) * KUSES)
                        split(b + 2, s)

                take(0, 0)
                split(0, 0)
                scale(0, 0)
                split(1, 1)
                every_batch(pool, batch)

            @block.tensor
            def _(pe):
                def free(i, s, v):
                    pe.wait_ge(taken[bank_of(s, v)], nth(i, s, v) + 1)

                def copied(i, s, v):
                    pe.wait_ge(taken[bank_of(s, v)], nth(i, s, v) + 2)

                def project_keys(i, s, g):
                    q = (i * 2 + s) * KUSES + g
                    pe.wait_ge(kp_taken, q + 1)
                    if g == 0:
                        pe.wait_ge(split_ready, i * 2 + (s + 1))
                    if g == G:
                        pe.wait_ge(batch_in, (i * 2 + s) * 4 + 4)
                    to = kp[:, (s * KUSES + g) % 2, :]
                    if g < G:
                        for t in range(2):
                            at, bank = bass.ts(2 * g + t, P), to[:, bass.ts(t, KW)]
                            pe.matmul(bank, cH[:, s, at], wkH[:, 0, :], start=True, stop=False)
                            pe.matmul(bank, cH[:, s, at], wkL[:, 0, :], start=False, stop=False)
                            pe.matmul(bank, cL[:, s, at], wkH[:, 0, :], start=False, stop=False)
                            pe.matmul(bank, cR[:, s, at], wkH[:, 1, :], start=False, stop=False)
                            mm = pe.matmul(bank, cR[:, s, at], wkL[:, 1, :], start=False, stop=True)
                    else:
                        for c in range(CD):
                            mm = pe.matmul(to[0:T, :], lb[:, s, c, :], wl[:, c, :], start=c == 0, stop=c == CD - 1)
                    mm.then_inc(kproj, 1)

                def turn_keys(i, s, v):
                    if v == 0:
                        pe.wait_ge(keys_ready, i * 2 + (s + 1))
                    free(i, s, v)
                    to = tp[:, bank_of(s, v), :]
                    for c in range(IC):
                        for t in range(2 if v < G else 1):
                            mm = pe.transpose(to[:, c * 2 * P + t * P:c * 2 * P + (t + 1) * P],
                                              kv[:, 2 * v + t, bass.ts(c, P)], k.ident[:])
                    mm.then_inc(turned, 1)

                def scores(i, s, c):
                    b = i * 2 + s
                    if c == 0:
                        copied(i, s, KUSES - 2)
                        copied(i, s, KUSES - 1)
                    if c:
                        pe.wait_ge(exped, b * IC + c)
                    for n in range(2):
                        pe.matmul(s_ps[:, n, :], qblk[:, s, c, :], keysT[:, s, c, bass.ts(n, HALF)],
                                  start=True, stop=False)
                        pe.matmul(s_ps[:, n, :], pick[:, s, :], bars[:, bass.ts(n, HALF)], start=False, stop=True)
                    mm = pe.matmul(s_ps[:, 2, 0:T], qblk[:, s, c, :], keysT[:, s, c, S:KEYS], start=True, stop=True)
                    mm.then_inc(scored, 1)

                def turn_probs(i, s, c):
                    pe.wait_ge(exped, (i * 2 + s) * IC + (c + 1))
                    for g in range(PUSES):
                        v = KUSES + PUSES * c + g
                        free(i, s, v)
                        for t in range(4 if g < 2 else 1):
                            j = 4 * g + t
                            mm = pe.transpose(tp[:, bank_of(s, v), bass.ts(t, P)], sm[:, c, bass.ts(j, P)], k.ident[:])
                        mm.then_inc(turned, 1)

                def mix_rows(i, s, c):
                    b = i * 2 + s
                    for g in (1, 2):
                        copied(i, s, KUSES + PUSES * c + g)
                    pe.wait_ge(xs_ready, b + 1)
                    pe.wait_ge(out_taken, b * IC + (c + 1))
                    for j in range(NK):
                        mm = pe.matmul(av[:, 0:DC + 1], pT[:, c, j, :], xs[:, s, j, :], start=j == 0, stop=j == NK - 1)
                    mm.then_inc(mixed, 1)

                def turn_mix(i, s, c):
                    pe.wait_ge(normed, (i * 2 + s) * IC + (c + 1))
                    pe.transpose(av[:, 2 * P:3 * P], mix[:, 0:P], k.ident[:])
                    pe.transpose(av[0:KR + 1, 3 * P:4 * P], mix[:, P:DC + 1], k.ident[:]).then_inc(mix_turned, 1)

                def project_mix(i, s, c):
                    pe.wait_ge(mix_taken, (i * 2 + s) * IC + (c + 1))
                    pe.matmul(av[:, 0:P], wv[:, 0, bass.ts(c, P)], mixT[:, 0, :], start=True, stop=False)
                    pe.matmul(av[:, 0:P], wv[:, 1, bass.ts(c, P)], mixT[:, 1, :], start=False, stop=False)
                    pe.matmul(av[:, 0:P], vl[:, s, bass.ts(c, P)], pT[:, c, NK, :], start=False, stop=True
                              ).then_inc(projected, 1)

                def batch(i, s, more):
                    ahead = after(i, s)
                    scores(i, s, 0)
                    if more:
                        project_keys(*ahead, 0)
                        project_keys(*ahead, 1)
                    scores(i, s, 1)
                    if more:
                        project_keys(*ahead, 2)
                    turn_probs(i, s, 0)
                    if more:
                        project_keys(*ahead, 3)
                        project_keys(*ahead, 4)
                    mix_rows(i, s, 0)
                    turn_probs(i, s, 1)
                    turn_mix(i, s, 0)
                    project_mix(i, s, 0)
                    mix_rows(i, s, 1)
                    if more:
                        turn_keys(*ahead, 0)
                        turn_keys(*ahead, 1)
                    turn_mix(i, s, 1)
                    if more:
                        turn_keys(*ahead, 2)
                        turn_keys(*ahead, 3)
                    project_mix(i, s, 1)
                    if more:
                        turn_keys(*ahead, 4)

                pe.wait_ge(set_up, 7)
                for g in range(KUSES):
                    project_keys(0, 0, g)
                for v in range(KUSES):
                    turn_keys(0, 0, v)
                every_batch(pe, batch)

            def copy_keys(eng, copy, mine, i, s, v):
                if bank_of(s, v) != mine:
                    return
                eng.wait_ge(turned, i * (2 * USES) + (USES * s + v + 1))
                w = 2 * P if v < G else T
                copy(keysT[:, s, :, v * 2 * P:v * 2 * P + w],
                     tp[:, mine, :].rearrange("p (c q) -> p c q", c=IC)[:, :, 0:w]).then_inc(taken[mine], 1)

            def copy_probs(eng, copy, mine, i, s, c):
                for g in range(PUSES):
                    v = KUSES + PUSES * c + g
                    if bank_of(s, v) != mine:
                        continue
                    eng.wait_ge(turned, i * (2 * USES) + (USES * s + v + 1))
                    if g < 2:
                        copy(pT[:, c, 4 * g:4 * g + 4, :], tp[:, mine, :].rearrange("p (j q) -> p j q", q=P)
                             ).then_inc(taken[mine], 1)
                    else:
                        copy(pT[0:T, c, NK, :], tp[0:T, mine, 0:P]).then_inc(taken[mine], 1)

            @block.scalar
            def _(act):
                act.sem_inc(taken0, 1)
                act.sem_inc(out_taken, 1)
                act.wait_ge(set_up, 7)

                def exp(i, s, c):
                    act.wait_ge(maxed, (i * 2 + s) * IC + (c + 1))
                    act.activation(sm[:, c, 0:KEYS], s_ps[:].rearrange("p a q -> p (a q)")[:, 0:KEYS], ACT.Exp,
                                   bias=col[:, 0, c:c + 1],
                                   accum_out=col[:, 1, c:c + 1]).then_inc(exped, 1)

                def square(i, s, part):
                    b = i * 2 + s
                    act.wait_ge(kp_taken, b * KUSES + 2 + (2, KUSES)[part])
                    j = (slice(0, 4), slice(4, NK + 1))[part]
                    act.activation(sq[:, j, :], kv[:, j, :], ACT.Square).then_inc(squared, 1)

                def root_var(i, s):
                    act.wait_ge(var_ready, i * 2 + (s + 1))
                    act.activation(mv[:, :, 1], mv[:, :, 1], ACT.Sqrt).then_inc(var_rooted, 1)

                def root_sums(i, s):
                    act.wait_ge(sums_ready, (i * 2 + s) * 2 + 2)
                    act.activation(rn[:], rn[:], ACT.Sqrt, scale=1.0 / dk).then_inc(sums_rooted, 1)

                def take_mix(i, s, c):
                    act.wait_ge(mix_turned, (i * 2 + s) * IC + (c + 1))
                    act.copy(mixT[:, 0, :], av[:, 2 * P:3 * P])
                    act.copy(mixT[0:KR + 1, 1, :], av[0:KR + 1, 3 * P:4 * P]).then_inc(mix_taken, 1)

                def take_out(i, s, c):
                    b = i * 2 + s
                    act.wait_ge(projected, b * IC + (c + 1))
                    for g in range(2):
                        r = slice(g * dk, (g + 1) * dk)
                        cp = act.copy(oT[r, c, bass.ds(b * T, T)], av[r, bass.ts(g, T)])
                    cp.then_inc(out_taken, 1)

                def batch(i, s, more):
                    ahead = after(i, s)
                    exp(i, s, 0)
                    if more:
                        square(*ahead, 0)
                    exp(i, s, 1)
                    copy_probs(act, act.copy, 0, i, s, 0)
                    if more:
                        square(*ahead, 1)
                        root_sums(*ahead)
                    copy_probs(act, act.copy, 0, i, s, 1)
                    take_mix(i, s, 0)
                    take_out(i, s, 0)
                    if more:
                        copy_keys(act, act.copy, 0, *ahead, 0)
                        copy_keys(act, act.copy, 0, *ahead, 1)
                    take_mix(i, s, 1)
                    if more:
                        copy_keys(act, act.copy, 0, *ahead, 2)
                        copy_keys(act, act.copy, 0, *ahead, 3)
                    take_out(i, s, 1)
                    if more == 2:
                        root_var(i + 1, s)
                    if more:
                        copy_keys(act, act.copy, 0, *ahead, 4)

                root_var(0, 0)
                square(0, 0, 0)
                square(0, 0, 1)
                root_sums(0, 0)
                root_var(0, 1)
                for v in range(KUSES):
                    copy_keys(act, act.copy, 0, 0, 0, v)
                every_batch(act, batch)

            @block.vector
            def _(dve):
                dve.sem_inc(taken1, 1)
                dve.sem_inc(kp_taken, 2)
                dve.wait_ge(set_up, 7)

                def stats(i, s, link, part):
                    if part == 0:
                        dve.wait_ge(n_landed, (i * 2 + s) * 16 + 16)
                    for j in range(part * NK // 2, (part + 1) * NK // 2):
                        link.mark(dve.bn_stats(st[:, j, :], land[:, j, :]))

                def variance(link):
                    link.wait()
                    link.mark(dve.tensor_tensor(mv[:, :, 0], st[:, :, 1], st[:, :, 4], ALU.subtract))
                    link(dve.tensor_tensor(mv[:, :, 1], st[:, :, 2], st[:, :, 5], ALU.add))
                    link.mark(dve.scalar_tensor_tensor(mv[:, :, 0], mv[:, :, 0], 0.25, mv[:, :, 0], ALU.mult,
                                                       ALU.mult))
                    link(dve.tensor_scalar(mv[:, :, 1], mv[:, :, 1], 1.0 / DC, 1e-5, ALU.mult, ALU.add))
                    dve.tensor_tensor(mv[:, :, 1], mv[:, :, 1], mv[:, :, 0], ALU.add).then_inc(var_ready, 1)

                def invert_std(i, s):
                    dve.wait_ge(var_rooted, i * 2 + (s + 1))
                    dve.reciprocal(rs[:, s, :], mv[:, :, 1]).then_inc(rs_ready, 1)

                def take_keys(i, s, g):
                    b = i * 2 + s
                    if g == 0:
                        dve.wait_ge(rs_ready, b + 1)
                    dve.wait_ge(kproj, b * KUSES + (g + 1))
                    at = kp[:, (s * KUSES + g) % 2, :]
                    if g < G:
                        for t in range(2):
                            j = 2 * g + t
                            cp = dve.scalar_tensor_tensor(kv[:, j, :], at[:, bass.ts(t, KW)], rs[:, s, j:j + 1],
                                                          bkb[:], ALU.mult, ALU.add)
                    else:
                        dve.tensor_copy(kv[0:T, NK, :], at[0:T, 0:KW])
                        cp = dve.tensor_copy(vl[0:T, s, :], at[0:T, KW:2 * KW])
                    cp.then_inc(kp_taken, 1)

                def sums(i, s, part):
                    dve.wait_ge(squared, (i * 2 + s) * 2 + (part + 1))
                    j = (slice(0, 4), slice(4, NK + 1))[part]
                    dve.tensor_reduce(rn[:, j, :], sq[:, j, :].rearrange("p j (h q) -> p j h q", q=dk), AX.X, ALU.add
                                      ).then_inc(sums_ready, 1)

                def norm_keys(i, s, link):
                    dve.wait_ge(sums_rooted, i * 2 + (s + 1))
                    link(dve.tensor_scalar(rn[:], rn[:], 1e-8, None, ALU.max))
                    link(dve.reciprocal(rn[:], rn[:]))
                    keys = kv[:].rearrange("p j (h q) -> p j h q", q=dk)
                    dve.tensor_tensor(keys, keys, over(rn[:], 3, dk), ALU.mult).then_inc(keys_ready, 1)

                def row_max(i, s, c):
                    b = i * 2 + s
                    dve.wait_ge(scored, b * IC + (c + 1))
                    dve.tensor_reduce(col[:, 0, c:c + 1], s_ps[:].rearrange("p a q -> p (a q)")[:, 0:KEYS], AX.X,
                                      ALU.max, negate=True).then_inc(maxed, 1)

                def scale_latents(i, s, c):
                    b = i * 2 + s
                    dve.wait_ge(exped, b * IC + (c + 1))
                    dve.reciprocal(col[:, 2, c:c + 1], col[:, 1, c:c + 1]).then_inc(inverted, 1)
                    dve.wait_ge(inverted, b * (2 * IC) + (2 * c + 1))
                    dve.tensor_scalar(sm[:, c, S:KEYS], sm[:, c, S:KEYS], col[:, 2, c:c + 1], None, ALU.mult
                                      ).then_inc(inverted, 1)

                def norm_mix(i, s, c):
                    dve.wait_ge(mixed, (i * 2 + s) * IC + (c + 1))
                    dve.tensor_scalar(mix[:], av[:, 0:DC + 1], col[:, 2, c:c + 1], None, ALU.mult
                                      ).then_inc(normed, 1)

                CHAINED = NK + 4 + 2

                def batch(i, s, more):
                    ahead = after(i, s)
                    link = Chain(dve, step, (i * 2 + s) * CHAINED + (2 * (NK + 4) + 2))
                    row_max(i, s, 0)
                    if more:
                        take_keys(*ahead, 0)
                        take_keys(*ahead, 1)
                    scale_latents(i, s, 0)
                    row_max(i, s, 1)
                    if more:
                        take_keys(*ahead, 2)
                    copy_probs(dve, dve.tensor_copy, 1, i, s, 0)
                    if more == 2:
                        stats(i + 1, s, link, 0)
                    if more:
                        take_keys(*ahead, 3)
                        take_keys(*ahead, 4)
                        sums(*ahead, 0)
                    if more == 2:
                        stats(i + 1, s, link, 1)
                    scale_latents(i, s, 1)
                    if more:
                        sums(*ahead, 1)
                    copy_probs(dve, dve.tensor_copy, 1, i, s, 1)
                    norm_mix(i, s, 0)
                    if more:
                        norm_keys(*ahead, link)
                    if more == 2:
                        variance(link)
                    norm_mix(i, s, 1)
                    if more:
                        for v in range(KUSES):
                            copy_keys(dve, dve.tensor_copy, 1, *ahead, v)
                    if more == 2:
                        invert_std(i + 1, s)

                link = Chain(dve, step)
                for part in range(2):
                    stats(0, 0, link, part)
                variance(link)
                invert_std(0, 0)
                for g in range(KUSES):
                    take_keys(0, 0, g)
                for part in range(2):
                    sums(0, 0, part)
                norm_keys(0, 0, link)
                for part in range(2):
                    stats(0, 1, link, part)
                variance(link)
                invert_std(0, 1)
                for v in range(KUSES):
                    copy_keys(dve, dve.tensor_copy, 1, 0, 0, v)
                assert link.n == 2 * (NK + 4) + 2, link.n
                every_batch(dve, batch)


def head_slots(w, heads):
    dk = w.shape[1] // heads
    out = np.zeros((w.shape[0], heads, HALF // heads), w.dtype)
    out[:, :, :dk] = w.reshape(w.shape[0], heads, dk)
    return out.reshape(w.shape[0], HALF)


def chunks(w):
    n = -(-w.shape[0] // P)
    out = np.zeros((n * P, w.shape[1]), w.dtype)
    out[:w.shape[0]] = w
    return np.ascontiguousarray(out.reshape(n, P, w.shape[1]).transpose(1, 0, 2))


def column(v):
    return np.ascontiguousarray(v.reshape(-1, P).T)


def layouts(x):
    a = {}
    a["xT"] = chunks(x["x"].reshape(N, D).T)
    a["ident"] = np.eye(P, dtype=np.float32)
    a["ctx"] = x["ctx_768"]
    a["ctxT"] = np.ascontiguousarray(x["ctx_768"].transpose(0, 2, 1))

    def xattn(name, heads, turned):
        g = lambda w: x[f"{name}_{w}"].T if turned else x[f"{name}_{w}"]
        a[name + "_Wq"] = chunks(head_slots(g("Wq"), heads))
        wk = head_slots(g("Wk"), heads).T
        a[name + "_WkT"] = chunks(np.concatenate([wk, wk[:, P:]], 1))
        wv = head_slots(g("Wv"), heads)
        a[name + "_Wv"] = chunks(np.concatenate([wv, wv[P:]], 0))
        a[name + "_Wo"] = chunks(head_slots(g("Wo").T, heads).T)
    xattn("L0_xattn", 16, True)
    xattn("L1_xattn", 8, False)
    xattn("L2_xattn", 8, False)
    a["lower8"] = np.tril(np.ones((8, 8), np.float32), -1).reshape(64)
    a["lower4"] = np.tril(np.ones((4, 4), np.float32), -1).reshape(16)
    a["upto"] = np.triu(np.ones((P, P), np.float32))
    each = lambda w: np.stack([chunks(m) for m in w])
    cols = lambda w: np.stack([column(v) for v in w])
    a["L0_ffn_gate"] = chunks(x["L0_ffn_gate_w"].T)
    a["L0_ffn_up"], a["L0_ffn_down"] = each(x["L0_ffn_up_w"]), each(x["L0_ffn_down_w"])
    a["L0_ffn_upb"], a["L0_ffn_downb"] = cols(x["L0_ffn_up_b"]), np.pad(x["L0_ffn_down_b"], ((0, P - E), (0, 0)))
    a["L0_ffn_sup"], a["L0_ffn_sdown"] = chunks(x["L0_ffn_sh_up_w"]), chunks(x["L0_ffn_sh_down_w"])
    a["L0_ffn_supb"], a["L0_ffn_sdownb"] = column(x["L0_ffn_sh_up_b"]), column(x["L0_ffn_sh_down_b"])
    for name, gate_w in (("L1_ffn", x["L1_ffn_gate_w"].T), ("L3_ffn", x["L3_ffn_wg"])):
        a[name + "_gate"] = chunks(gate_w)
        a[name + "_up"], a[name + "_down"] = each(x[name + "_w1"]), each(x[name + "_w2"])
        a[name + "_upb"], a[name + "_downb"] = cols(x[name + "_b1"]), np.pad(x[name + "_b2"], ((0, P - E), (0, 0)))
    both = lambda g, u: np.concatenate([chunks(g), chunks(u)], 1)
    a["L2_ffn_gate"] = chunks(x["L2_ffn_gate_w"].T)
    a["L2_ffn_cbias"] = x["L2_ffn_correction_bias"]
    a["L2_ffn_up"] = np.stack([both(g, u) for g, u in zip(x["L2_ffn_Wg"], x["L2_ffn_Wu"])])
    a["L2_ffn_down"] = each(x["L2_ffn_Wd"])
    a["L2_ffn_sup"] = both(x["L2_ffn_Wg_s"], x["L2_ffn_Wu_s"])
    a["L2_ffn_sdown"] = chunks(x["L2_ffn_Wd_s"])
    a["pick8"] = np.repeat(np.eye(8, dtype=np.float32)[:, :, None], P, 2)
    s, t = np.arange(P)[:, None], np.arange(P)[None, :]
    a["bar"] = np.where((s // T == t // T) & (s <= t), 0.0, -1e30).astype(np.float32)
    a["fresh"] = (np.arange(N) % T != 0).astype(np.float32)
    a["lags"] = np.arange(T, dtype=np.float32)
    n = "L0_attn_"
    a[n + "in"] = chunks(np.pad(x[n + "in_proj_w"].T, ((0, 0), (0, 120))))
    a[n + "out"] = chunks(x[n + "out_proj_w"].T)
    a[n + "cw"], a[n + "cb"] = chunks(x[n + "conv_w"]), column(x[n + "conv_b"])
    a[n + "D"] = column(np.repeat(x[n + "D"], 64))
    a[n + "nw"] = column(x[n + "norm_w"])
    a[n + "ln"] = np.stack([column(x[n + "ln_w"]), column(x[n + "ln_b"])], 1)
    a[n + "dt"] = np.stack([x[n + "dt_bias"], x[n + "A_log"]], 1)
    n = "L1_attn_"
    a[n + "in"], a[n + "inb"] = chunks(x[n + "in_proj_w"].T), column(x[n + "in_proj_b"])
    a[n + "out"], a[n + "outb"] = chunks(x[n + "out_proj_w"].T), column(x[n + "out_proj_b"])
    a[n + "conv"] = x[n + "conv_w"].transpose(1, 2, 0).reshape(4, P, 4, 512).transpose(1, 0, 2, 3)
    a[n + "cvb"], a[n + "nw"] = column(x[n + "conv_b"]), column(x[n + "norm_w"])
    a[n + "par"] = np.stack([chunks(x[n + w]) for w in ("A_log", "B_param", "C_param")], 1)
    a[n + "dts"] = np.stack([column(x[n + "dt"]), column(x[n + "D_param"])], 1)
    n = "L2_attn_"
    a[n + "in"], a[n + "out"] = chunks(x[n + "in_proj_w"].T), chunks(x[n + "out_proj_w"].T)
    a[n + "cw"], a[n + "cb"] = chunks(x[n + "conv_w"][:, 0, :]), column(x[n + "conv_b"])
    a[n + "x"] = chunks(np.pad(x[n + "x_proj_w"].T, ((0, 0), (0, P - 48))))
    a[n + "wdt"], a[n + "dtb"] = x[n + "dt_proj_w"].T, column(x[n + "dt_proj_b"])
    a[n + "A"] = chunks(x[n + "A_log"]).reshape(P, 64)
    a[n + "D"], a[n + "nw"] = column(x[n + "D"]), column(x[n + "norm_w"])
    n = "L3_attn_"
    a[n + "Wqk"] = chunks(np.concatenate([head_slots(x[n + "Wq"], 16), head_slots(x[n + "Wk"], 16)], 1))
    a[n + "Wv"], a[n + "Wo"] = chunks(head_slots(x[n + "Wv"], 16)), chunks(head_slots(x[n + "Wo"].T, 16).T)
    r, c = np.arange(P)[:, None], np.arange(P)[None, :]
    a["slotvar"] = np.where((r // 32 == c // 32) & (r % 32 < 16) & (c % 32 == 16), 1.0 / 15, 0.0).astype(np.float32)
    a["pair"] = (r // 64 == c // 64).astype(np.float32)
    n = "L3_xattn_"
    a["mask"] = np.ascontiguousarray(x["mask_BxS2_bk0"]).view(np.uint32)
    for w in ("Wq", "Wlkv", "Wo"):
        a[n + w] = chunks(x[n + w].T)
    twice = lambda w: chunks(np.concatenate([w[:P], w[P:], np.zeros((2 * P - DC, w.shape[1]), w.dtype), w[P:], w[P:]]))
    a[n + "Wkv"] = twice(x[n + "Wkv"].T)
    a[n + "bo"] = column(x[n + "bo"])
    a[n + "lnl"] = np.stack([column(x[n + "ln_l_g"]), column(x[n + "ln_l_b"])], 1)
    a[n + "lnx"] = np.stack([twice(x[n + "ln_x_" + v][:, None])[:, :, 0] for v in "gb"], 1)
    a[n + "qg"] = np.stack([np.tile(x[n + v], 2) for v in ("qn_g", "kn_g")], 1)
    a["L1_xattn_bo"] = column(x["L1_xattn_bo"])
    a["L2_xattn_bo"] = column(x["L2_xattn_bo"])
    return a


CAPACITY = 2 * N // E
STEPS = {
    "L0_xattn": lambda k: context_attention(k, "L0_xattn", 16, 16 ** -0.5, False),
    "L0_attn": state_space_duality,
    "L0_ffn": lambda k: experts(k, "L0_ffn", 256, ACT.Silu, False, True, True, True,
                                dict(top=2, softmax=True, eps=1e-20)),
    "L1_xattn": lambda k: context_attention(k, "L1_xattn", 8, 64 ** -0.5, True),
    "L1_attn": long_convolution,
    "L1_ffn": lambda k: experts(k, "L1_ffn", 1024, ACT.Gelu, False, True, True, False,
                                dict(top=2, softmax=True, eps=1e-9)),
    "L2_xattn": lambda k: context_attention(k, "L2_xattn", 8, 64 ** -0.5, True),
    "L2_attn": selective_scan,
    "L2_ffn": lambda k: experts(k, "L2_ffn", 128, ACT.Silu, True, False, False, True,
                                dict(top=4, softmax=False, eps=1e-20, factor=2.5, grouped=True)),
    "L3_xattn": masked_cross_attention,
    "L3_attn": correlation_attention,
    "L3_ffn": lambda k: experts(k, "L3_ffn", 1024, ACT.Relu, False, True, True, False,
                                dict(top=2, softmax=True, eps=0.0, capacity=CAPACITY)),
}


def build(nc, dram, steps=None):
    with ExitStack() as ctx:
        k = Core(nc, dram, ctx)
        k.comb = nc.dram_tensor("comb_rows", (E, N), F32).ap()
        k.bc = nc.dram_tensor("state_rows", (32, N), F32).ap()
        load_constants(k)
        for name, step in STEPS.items():
            if steps is None or name in steps:
                step(k)
        store_result(k)


def kernel(**inputs):
    import concourse.bacc as bacc
    from concourse.bass_utils import run_bass_kernel_spmd

    nc = bacc.Bacc("TRN2", target_bir_lowering=False, num_devices=1)
    inputs = {n: np.asarray(v) for n, v in inputs.items()}
    arrays = {"in_" + n: np.ascontiguousarray(v) for n, v in layouts(inputs).items()}
    dram = {n[3:]: nc.dram_tensor(n, v.shape, mybir.dt.from_np(v.dtype), kind="ExternalInput").ap()
            for n, v in arrays.items()}
    dram["outT"] = nc.dram_tensor("outT", (P, CD, N), F32, kind="ExternalOutput").ap()
    build(nc, dram)
    r = run_bass_kernel_spmd(nc, [arrays], core_ids=[0])
    out = r.results[0]["outT"]
    return np.ascontiguousarray(out.transpose(1, 0, 2).reshape(D, N).T.reshape(B, T, D))
```
